# Optimizing a Trainium2 kernel written in Bass

```python
import numpy as np
import jax
import jax.numpy as jnp

def _softmax(x, axis=-1):
    return jax.nn.softmax(x, axis=axis)

def _gelu(x):
    return jax.nn.gelu(x, approximate=True)

def _silu(x):
    return jax.nn.silu(x)

def _sigmoid(x):
    return jax.nn.sigmoid(x)

def _layernorm(x, axis=-1, eps=1e-05):
    m = jnp.mean(x, axis=axis, keepdims=True)
    v = jnp.var(x, axis=axis, keepdims=True)
    return (x - m) / jnp.sqrt(v + eps)

def _scatter_add(tgt, idx, src, axis=0):
    return tgt.at[idx].add(src)

def _segment_sum(src, seg, n):
    return jax.ops.segment_sum(src, seg, n)
kernel_name = 'mk_decoder_preln_d2_seqx_r8_cb2079'

def setup_inputs(seed: int=0):
    np.random.seed(seed)
    _w = jnp.asarray

    def _rec_inputs():
        import jax
        import jax.numpy as jnp
        _rk = jax.random.key(seed)
        x = -0.0002928 + 1 * jax.random.normal(jax.random.fold_in(_rk, 1), (4, 512, 128), jnp.float32)
        _lenS = 512 - jax.random.randint(jax.random.fold_in(_rk, 7), (4,), 0, max(1, 512 // 4) + 1, jnp.int32)
        _lenS2 = 77 - jax.random.randint(jax.random.fold_in(_rk, 8), (4,), 0, max(1, 77 // 4) + 1, jnp.int32)
        _ctx_1024P = jax.random.normal(jax.random.fold_in(_rk, 11), (4, 16, 128), jnp.float32)
        _ctx_1024c = jax.random.dirichlet(jax.random.fold_in(_rk, 511), 0.3 * jnp.ones((16,), jnp.float32), (4, 77))
        _ctx_1024t = jnp.einsum('bsk,bkd->bsd', _ctx_1024c, _ctx_1024P)
        _ctx_1024t = _ctx_1024t * jax.lax.rsqrt(jnp.mean(jnp.square(_ctx_1024t)) + 1e-12) * 0.953939
        ctx_1024 = -1.39393e-06 + 0.999914 * (_ctx_1024t + 0.3 * jax.random.normal(jax.random.fold_in(_rk, 611), (4, 77, 128), jnp.float32))
        _validS = jnp.arange(512)[None, :] < _lenS[:, None]
        _validS2 = jnp.arange(77)[None, :] < _lenS2[:, None]
        _causal = jnp.tril(jnp.ones((512, 512), dtype=bool))
        mask_Bx1x1xS2_ik0 = jnp.where(jnp.broadcast_to(_validS2[:, None, None, :], (4, 1, 1, 77)), 0, 1).astype(jnp.int32)
        mask_1x1xSxS2_ik0 = jnp.where(jnp.broadcast_to(_validS2[0:1, None, None, :], (1, 1, 512, 77)), 0, 1).astype(jnp.int32)
        return (x, ctx_1024, mask_Bx1x1xS2_ik0, mask_1x1xSxS2_ik0)
    x, ctx_1024, mask_Bx1x1xS2_ik0, mask_1x1xSxS2_ik0 = _rec_inputs()

    def _L0_attn_setup():
        import jax, jax.numpy as jnp
        import numpy as np
        D_MODEL = 128
        N_HEADS = 16
        D_HEAD = D_MODEL // N_HEADS
        B, T = (2, 256)
        key = jax.random.key(seed)
        ks = jax.random.split(key, 8)
        s = 1.0 / np.sqrt(D_MODEL)
        return {'x': jax.random.normal(ks[0], (B, T, D_MODEL), dtype=jnp.float32), 'ln_g': jnp.ones((D_MODEL,), jnp.float32), 'ln_b': jnp.zeros((D_MODEL,), jnp.float32), 'w_qkv': jax.random.normal(ks[1], (D_MODEL, 3 * D_MODEL), jnp.float32) * s, 'b_qkv': jnp.zeros((3 * D_MODEL,), jnp.float32), 'w_gate': jax.random.normal(ks[2], (D_MODEL, D_MODEL), jnp.float32) * s, 'b_gate': jnp.zeros((D_MODEL,), jnp.float32), 'w_proj': jax.random.normal(ks[3], (D_MODEL, D_MODEL), jnp.float32) * s, 'b_proj': jnp.zeros((D_MODEL,), jnp.float32)}
    _L0_attn_all = _L0_attn_setup()
    _L0_attn_in = {k: v for k, v in _L0_attn_all.items() if k in ('ln_g', 'ln_b', 'w_qkv', 'b_qkv', 'w_gate', 'b_gate', 'w_proj', 'b_proj')}
    del _L0_attn_all

    def _L0_xattn_setup():
        import jax, jax.numpy as jnp
        import numpy as np
        E, H = (128, 16)
        N, S, T = (2, 256, 256)
        key = jax.random.key(seed)
        ks = jax.random.split(key, 8)
        scale = 1.0 / np.sqrt(E)
        q = jax.random.normal(ks[0], (N, S, E), dtype=jnp.float32)
        k = jax.random.normal(ks[1], (N, T, E), dtype=jnp.float32)
        v = jax.random.normal(ks[2], (N, T, E), dtype=jnp.float32)
        pad_mask = jax.random.randint(ks[3], (N, 1, 1, T), 0, 2, dtype=jnp.int32)
        subsq_mask = jnp.tril(jnp.ones((S, T), dtype=jnp.int32))[None, None]
        Wq = jax.random.normal(ks[4], (E, E), dtype=jnp.float32) * scale
        Wk = jax.random.normal(ks[5], (E, E), dtype=jnp.float32) * scale
        Wv = jax.random.normal(ks[6], (E, E), dtype=jnp.float32) * scale
        bq = jnp.zeros((E,), dtype=jnp.float32)
        bk = jnp.zeros((E,), dtype=jnp.float32)
        bv = jnp.zeros((E,), dtype=jnp.float32)
        return {'query': q, 'key': k, 'value': v, 'pad_mask': pad_mask, 'subsq_mask': subsq_mask, 'Wq': Wq, 'bq': bq, 'Wk': Wk, 'bk': bk, 'Wv': Wv, 'bv': bv}
    _L0_xattn_all = _L0_xattn_setup()
    _L0_xattn_in = {k: v for k, v in _L0_xattn_all.items() if k in ('Wq', 'bq', 'Wk', 'bk', 'Wv', 'bv')}
    del _L0_xattn_all

    def _L0_ffn_setup():
        import jax, jax.numpy as jnp
        import numpy as np
        B, S, DIM = (2, 256, 128)
        HID = 256
        E, NSH, TOPK = (8, 2, 2)

        def _ffn(x, w1, w2, w3):
            return jax.nn.silu(x @ w1.T) * (x @ w3.T) @ w2.T
        key = jax.random.key(seed)
        ks = jax.random.split(key, 8)
        sc = 0.02
        return {'x': jax.random.normal(ks[0], (B, S, DIM), jnp.float32), 'router_w': jax.random.normal(ks[1], (E, DIM), jnp.float32) * sc, 'expert_bias': jnp.zeros((E,), jnp.float32), 'w1': jax.random.normal(ks[2], (E, HID, DIM), jnp.float32) * sc, 'w3': jax.random.normal(ks[3], (E, HID, DIM), jnp.float32) * sc, 'w2': jax.random.normal(ks[4], (E, DIM, HID), jnp.float32) * sc, 'sw1': jax.random.normal(ks[5], (NSH, HID, DIM), jnp.float32) * sc, 'sw3': jax.random.normal(ks[6], (NSH, HID, DIM), jnp.float32) * sc, 'sw2': jax.random.normal(ks[7], (NSH, DIM, HID), jnp.float32) * sc}
    _L0_ffn_all = _L0_ffn_setup()
    _L0_ffn_in = {k: v for k, v in _L0_ffn_all.items() if k in ('router_w', 'expert_bias', 'w1', 'w3', 'w2', 'sw1', 'sw3', 'sw2')}
    del _L0_ffn_all

    def _L1_attn_setup():
        import jax, jax.numpy as jnp
        import numpy as np
        D_MODEL = 128
        H = 16
        DH = 64
        FFN = 512
        CHUNK = 64
        LN_EPS = 1e-05

        def layer_norm(x, w, b):
            mu = x.mean(-1, keepdims=True)
            var = x.var(-1, keepdims=True)
            return (x - mu) * jax.lax.rsqrt(var + LN_EPS) * w + b

        def l2_normalize(x):
            n = jnp.sqrt(jnp.sum(x * x, axis=-1, keepdims=True))
            return x / jnp.maximum(n, 1e-12)

        def chunk_gla(q, k, v, alpha, C=CHUNK):
            B, Hh, N, D = q.shape
            nc = N // C
            q = q.reshape(B, Hh, nc, C, D)
            k = k.reshape(B, Hh, nc, C, D)
            v = v.reshape(B, Hh, nc, C, D)
            alpha = alpha.reshape(B, Hh, nc, C, D)
            log_a = jnp.log(jnp.maximum(alpha, 1e-06))
            la_cum = jnp.cumsum(log_a, axis=3)
            la_mean = la_cum.mean(-1)
            tril = jnp.tril(jnp.ones((C, C), dtype=q.dtype))
            decay = jnp.exp(la_mean[..., :, None] - la_mean[..., None, :]) * tril
            attn_intra = jnp.einsum('bhncd,bhnmd->bhncm', q, k) * decay
            o_intra = jnp.einsum('bhncm,bhnmd->bhncd', attn_intra, v)
            decay_to_end = jnp.exp(la_cum[:, :, :, -1:, :] - la_cum)
            kv_chunk = jnp.einsum('bhncf,bhnce->bhnfe', k * decay_to_end, v)
            chunk_decay = jnp.exp(log_a.sum(3))
            q_dec = q * jnp.exp(la_cum)

            def step(S, inp):
                qd, kv, cd = inp
                o = jnp.einsum('bhcd,bhde->bhce', qd, S)
                S_new = S * cd[:, :, :, None] + kv
                return (S_new, o)
            S0 = jnp.zeros((B, Hh, D, D), dtype=q.dtype)
            _, o_inter = jax.lax.scan(step, S0, (jnp.moveaxis(q_dec, 2, 0), jnp.moveaxis(kv_chunk, 2, 0), jnp.moveaxis(chunk_decay, 2, 0)))
            o_inter = jnp.moveaxis(o_inter, 0, 2)
            return (o_intra + o_inter).reshape(B, Hh, N, D)
        key = jax.random.key(seed)
        ks = jax.random.split(key, 16)
        s = 0.02
        td = H * DH
        return {'x': jax.random.normal(ks[0], (2, 512, D_MODEL), dtype=jnp.float32), 'Wq': jax.random.normal(ks[1], (D_MODEL, td), dtype=jnp.float32) * s, 'Wk': jax.random.normal(ks[2], (D_MODEL, td), dtype=jnp.float32) * s, 'Wv': jax.random.normal(ks[3], (D_MODEL, td), dtype=jnp.float32) * s, 'Wg': jax.random.normal(ks[4], (D_MODEL, td), dtype=jnp.float32) * s, 'bg': jnp.full((td,), -0.5, dtype=jnp.float32), 'Wo': jax.random.normal(ks[5], (td, D_MODEL), dtype=jnp.float32) * s, 'ln1_w': jnp.ones((D_MODEL,), jnp.float32), 'ln1_b': jnp.zeros((D_MODEL,), jnp.float32), 'ln2_w': jnp.ones((D_MODEL,), jnp.float32), 'ln2_b': jnp.zeros((D_MODEL,), jnp.float32), 'W1': jax.random.normal(ks[6], (D_MODEL, FFN), dtype=jnp.float32) * s, 'b1': jnp.zeros((FFN,), jnp.float32), 'W2': jax.random.normal(ks[7], (FFN, D_MODEL), dtype=jnp.float32) * s, 'b2': jnp.zeros((D_MODEL,), jnp.float32)}
    _L1_attn_all = _L1_attn_setup()
    _L1_attn_in = {k: v for k, v in _L1_attn_all.items() if k in ('Wq', 'Wk', 'Wv', 'Wg', 'bg', 'Wo', 'ln1_w', 'ln1_b', 'ln2_w', 'ln2_b', 'W1', 'b1', 'W2', 'b2')}
    del _L1_attn_all

    def _L1_xattn_setup():
        import jax, jax.numpy as jnp
        import numpy as np
        B, L_ENC, L_DEC, D = (16, 64, 128, 128)
        key = jax.random.key(seed)
        k1, k2, k3, k4, k5, k6 = jax.random.split(key, 6)
        encoder_hc = jax.random.normal(k1, (B, L_ENC, D), dtype=jnp.float32)
        decoder_hq = jax.random.normal(k2, (B, L_DEC, D), dtype=jnp.float32)
        w_sim = jax.random.normal(k3, (3 * D,), dtype=jnp.float32) * 0.02
        b_sim = jax.random.normal(k4, (1,), dtype=jnp.float32) * 0.02
        W_qv = jax.random.normal(k5, (4 * D, D), dtype=jnp.float32) * 0.02
        b_qv = jax.random.normal(k6, (D,), dtype=jnp.float32) * 0.02
        return {'encoder_hc': encoder_hc, 'decoder_hq': decoder_hq, 'w_sim': w_sim, 'b_sim': b_sim, 'W_qv': W_qv, 'b_qv': b_qv}
    _L1_xattn_all = _L1_xattn_setup()
    _L1_xattn_in = {k: v for k, v in _L1_xattn_all.items() if k in ('w_sim', 'b_sim', 'W_qv', 'b_qv')}
    del _L1_xattn_all

    def _L1_ffn_setup():
        import jax, jax.numpy as jnp
        import numpy as np
        B, S, D = (8, 64, 128)
        H = 16
        DFF = 512
        E = 4
        K = 2
        EPS = 1e-05

        def _layernorm(x, w, b):
            m = x.mean(-1, keepdims=True)
            v = ((x - m) ** 2).mean(-1, keepdims=True)
            return (x - m) / jnp.sqrt(v + EPS) * w + b

        def _encoder_layer(x, iw, ib, ow, ob, l1w, l1b, l2w, l2b, n1w, n1b, n2w, n2b):
            b, s, d = x.shape
            hd = d // H
            qkv = x @ iw.T + ib
            q, k, v = jnp.split(qkv, 3, axis=-1)
            rs = lambda t: t.reshape(b, s, H, hd).transpose(0, 2, 1, 3)
            q, k, v = (rs(q), rs(k), rs(v))
            scale = jnp.asarray(hd, x.dtype) ** 0.5
            scores = jnp.einsum('bhqd,bhkd->bhqk', q, k) / scale
            attn = jax.nn.softmax(scores, axis=-1)
            o = jnp.einsum('bhqk,bhkd->bhqd', attn, v).transpose(0, 2, 1, 3).reshape(b, s, d)
            o = o @ ow.T + ob
            x = _layernorm(x + o, n1w, n1b)
            ff = jax.nn.relu(x @ l1w.T + l1b) @ l2w.T + l2b
            return _layernorm(x + ff, n2w, n2b)
        key = jax.random.key(seed)
        ks = jax.random.split(key, 12)
        g = lambda k, shape: jax.random.normal(k, shape, dtype=jnp.float32) * 0.02
        return {'x': jax.random.normal(ks[0], (B, S, D), dtype=jnp.float32), 'in_proj_w': g(ks[1], (E, 3 * D, D)), 'in_proj_b': g(ks[2], (E, 3 * D)), 'out_proj_w': g(ks[3], (E, D, D)), 'out_proj_b': g(ks[4], (E, D)), 'ln1_w': jnp.ones((E, D), jnp.float32), 'ln1_b': jnp.zeros((E, D), jnp.float32), 'lin1_w': g(ks[5], (E, DFF, D)), 'lin1_b': g(ks[6], (E, DFF)), 'lin2_w': g(ks[7], (E, D, DFF)), 'lin2_b': g(ks[8], (E, D)), 'ln2_w': jnp.ones((E, D), jnp.float32), 'ln2_b': jnp.zeros((E, D), jnp.float32), 'gate_w': g(ks[9], (E, D)), 'gate_b': g(ks[10], (E,))}
    _L1_ffn_all = _L1_ffn_setup()
    _L1_ffn_in = {k: v for k, v in _L1_ffn_all.items() if k in ('in_proj_w', 'in_proj_b', 'out_proj_w', 'out_proj_b', 'ln1_w', 'ln1_b', 'lin1_w', 'lin1_b', 'lin2_w', 'lin2_b', 'ln2_w', 'ln2_b', 'gate_w', 'gate_b')}
    del _L1_ffn_all
    return {'x': x, 'ctx_1024': ctx_1024, 'mask_Bx1x1xS2_ik0': mask_Bx1x1xS2_ik0, 'mask_1x1xSxS2_ik0': mask_1x1xSxS2_ik0, 'L0_attn_ln_g': _L0_attn_in['ln_g'], 'L0_attn_ln_b': _L0_attn_in['ln_b'], 'L0_attn_w_qkv': _L0_attn_in['w_qkv'], 'L0_attn_b_qkv': _L0_attn_in['b_qkv'], 'L0_attn_w_gate': _L0_attn_in['w_gate'], 'L0_attn_b_gate': _L0_attn_in['b_gate'], 'L0_attn_w_proj': _L0_attn_in['w_proj'], 'L0_attn_b_proj': _L0_attn_in['b_proj'], 'L0_xattn_Wq': _L0_xattn_in['Wq'], 'L0_xattn_bq': _L0_xattn_in['bq'], 'L0_xattn_Wk': _L0_xattn_in['Wk'], 'L0_xattn_bk': _L0_xattn_in['bk'], 'L0_xattn_Wv': _L0_xattn_in['Wv'], 'L0_xattn_bv': _L0_xattn_in['bv'], 'L0_ffn_router_w': _L0_ffn_in['router_w'], 'L0_ffn_expert_bias': _L0_ffn_in['expert_bias'], 'L0_ffn_w1': _L0_ffn_in['w1'], 'L0_ffn_w3': _L0_ffn_in['w3'], 'L0_ffn_w2': _L0_ffn_in['w2'], 'L0_ffn_sw1': _L0_ffn_in['sw1'], 'L0_ffn_sw3': _L0_ffn_in['sw3'], 'L0_ffn_sw2': _L0_ffn_in['sw2'], 'L1_attn_Wq': _L1_attn_in['Wq'], 'L1_attn_Wk': _L1_attn_in['Wk'], 'L1_attn_Wv': _L1_attn_in['Wv'], 'L1_attn_Wg': _L1_attn_in['Wg'], 'L1_attn_bg': _L1_attn_in['bg'], 'L1_attn_Wo': _L1_attn_in['Wo'], 'L1_attn_ln1_w': _L1_attn_in['ln1_w'], 'L1_attn_ln1_b': _L1_attn_in['ln1_b'], 'L1_attn_ln2_w': _L1_attn_in['ln2_w'], 'L1_attn_ln2_b': _L1_attn_in['ln2_b'], 'L1_attn_W1': _L1_attn_in['W1'], 'L1_attn_b1': _L1_attn_in['b1'], 'L1_attn_W2': _L1_attn_in['W2'], 'L1_attn_b2': _L1_attn_in['b2'], 'L1_xattn_w_sim': _L1_xattn_in['w_sim'], 'L1_xattn_b_sim': _L1_xattn_in['b_sim'], 'L1_xattn_W_qv': _L1_xattn_in['W_qv'], 'L1_xattn_b_qv': _L1_xattn_in['b_qv'], 'L1_ffn_in_proj_w': _L1_ffn_in['in_proj_w'], 'L1_ffn_in_proj_b': _L1_ffn_in['in_proj_b'], 'L1_ffn_out_proj_w': _L1_ffn_in['out_proj_w'], 'L1_ffn_out_proj_b': _L1_ffn_in['out_proj_b'], 'L1_ffn_ln1_w': _L1_ffn_in['ln1_w'], 'L1_ffn_ln1_b': _L1_ffn_in['ln1_b'], 'L1_ffn_lin1_w': _L1_ffn_in['lin1_w'], 'L1_ffn_lin1_b': _L1_ffn_in['lin1_b'], 'L1_ffn_lin2_w': _L1_ffn_in['lin2_w'], 'L1_ffn_lin2_b': _L1_ffn_in['lin2_b'], 'L1_ffn_ln2_w': _L1_ffn_in['ln2_w'], 'L1_ffn_ln2_b': _L1_ffn_in['ln2_b'], 'L1_ffn_gate_w': _L1_ffn_in['gate_w'], 'L1_ffn_gate_b': _L1_ffn_in['gate_b']}

def reference(x, ctx_1024, mask_Bx1x1xS2_ik0, mask_1x1xSxS2_ik0, L0_attn_ln_g, L0_attn_ln_b, L0_attn_w_qkv, L0_attn_b_qkv, L0_attn_w_gate, L0_attn_b_gate, L0_attn_w_proj, L0_attn_b_proj, L0_xattn_Wq, L0_xattn_bq, L0_xattn_Wk, L0_xattn_bk, L0_xattn_Wv, L0_xattn_bv, L0_ffn_router_w, L0_ffn_expert_bias, L0_ffn_w1, L0_ffn_w3, L0_ffn_w2, L0_ffn_sw1, L0_ffn_sw3, L0_ffn_sw2, L1_attn_Wq, L1_attn_Wk, L1_attn_Wv, L1_attn_Wg, L1_attn_bg, L1_attn_Wo, L1_attn_ln1_w, L1_attn_ln1_b, L1_attn_ln2_w, L1_attn_ln2_b, L1_attn_W1, L1_attn_b1, L1_attn_W2, L1_attn_b2, L1_xattn_w_sim, L1_xattn_b_sim, L1_xattn_W_qv, L1_xattn_b_qv, L1_ffn_in_proj_w, L1_ffn_in_proj_b, L1_ffn_out_proj_w, L1_ffn_out_proj_b, L1_ffn_ln1_w, L1_ffn_ln1_b, L1_ffn_lin1_w, L1_ffn_lin1_b, L1_ffn_lin2_w, L1_ffn_lin2_b, L1_ffn_ln2_w, L1_ffn_ln2_b, L1_ffn_gate_w, L1_ffn_gate_b):
    import jax
    import jax.numpy as jnp

    def _L0_attn_ref(x, ln_g, ln_b, w_qkv, b_qkv, w_gate, b_gate, w_proj, b_proj):
        import jax, jax.numpy as jnp
        import numpy as np
        D_MODEL = 128
        N_HEADS = 16
        D_HEAD = D_MODEL // N_HEADS
        B, T = (2, 256)
        Bb, Tt, Dd = x.shape
        H, dh = (N_HEADS, D_HEAD)
        mu = jnp.mean(x, axis=-1, keepdims=True)
        var = jnp.mean((x - mu) ** 2, axis=-1, keepdims=True)
        x_norm = (x - mu) / jnp.sqrt(var + 1e-05) * ln_g + ln_b
        qkv = x_norm @ w_qkv + b_qkv
        q, k, v = jnp.split(qkv, 3, axis=-1)
        gate_sig = jax.nn.sigmoid(x @ w_gate + b_gate)
        gate_norm = gate_sig / (jnp.mean(gate_sig, axis=-1, keepdims=True) + 1e-05)
        q = q * gate_norm
        k = k * gate_norm

        def to_heads(t):
            return t.reshape(Bb, Tt, H, dh).transpose(0, 2, 1, 3)
        q, k, v = (to_heads(q), to_heads(k), to_heads(v))
        q = jax.nn.elu(q) + 1.0
        k = jax.nn.elu(k) + 1.0
        kv = jnp.einsum('bhtd,bhtm->bhtdm', k, v)
        kv_cumsum = jnp.cumsum(kv, axis=2)
        out_num = jnp.einsum('bhtd,bhtdm->bhtm', q, kv_cumsum)
        k_cumsum = jnp.cumsum(k, axis=2)
        out_den = jnp.einsum('bhtd,bhtd->bht', q, k_cumsum)[..., None] + 1e-05
        out = out_num / out_den
        out = out.transpose(0, 2, 1, 3).reshape(Bb, Tt, Dd)
        return out @ w_proj + b_proj

    def _L0_xattn_ref(query, key, value, pad_mask, subsq_mask, Wq, bq, Wk, bk, Wv, bv):
        import jax, jax.numpy as jnp
        import numpy as np
        E, H = (128, 16)
        N, S, T = (2, 256, 256)
        n, s, e = query.shape
        t = value.shape[1]
        d = e // H
        q = (query @ Wq.T + bq).reshape(n, s, H, d).transpose(0, 2, 1, 3)
        k = (key @ Wk.T + bk).reshape(n, t, H, d).transpose(0, 2, 1, 3)
        v = (value @ Wv.T + bv).reshape(n, t, H, d).transpose(0, 2, 1, 3)
        att = jnp.einsum('bhsd,bhtd->bhst', q, k) / jnp.sqrt(jnp.float32(d))
        att = jnp.where(pad_mask == 0, jnp.float32(-1000000000.0), att)
        att = jnp.where(subsq_mask == 0, jnp.float32(-1000000000.0), att)
        prob = jax.nn.softmax(att, axis=-1)
        out = jnp.einsum('bhst,bhtd->bhsd', prob, v)
        return out.transpose(0, 2, 1, 3).reshape(n, s, e)

    def _L0_ffn_ref(x, router_w, expert_bias, w1, w3, w2, sw1, sw3, sw2):
        import jax, jax.numpy as jnp
        import numpy as np
        B, S, DIM = (2, 256, 128)
        HID = 256
        E, NSH, TOPK = (8, 2, 2)

        def _ffn(x, w1, w2, w3):
            return jax.nn.silu(x @ w1.T) * (x @ w3.T) @ w2.T
        bs, sl, d = x.shape
        xf = x.reshape(-1, d)
        shared = jnp.zeros_like(xf)
        for i in range(sw1.shape[0]):
            shared = shared + _ffn(xf, sw1[i], sw2[i], sw3[i])
        logits = xf @ router_w.T + expert_bias
        rw, sel = jax.lax.top_k(logits, TOPK)
        rw = jax.nn.softmax(rw.astype(jnp.float32), axis=-1).astype(x.dtype)
        onehot = jax.nn.one_hot(sel, E, dtype=x.dtype)
        combine = jnp.einsum('tk,tke->te', rw, onehot)

        def body(acc, ew):
            e1, e3, e2, cw = ew
            acc = acc + cw[:, None] * _ffn(xf, e1, e2, e3)
            return (acc, None)
        out, _ = jax.lax.scan(body, jnp.zeros_like(xf), (w1, w3, w2, combine.T))
        out = out + shared
        return out.reshape(bs, sl, -1)

    def _L1_attn_ref(x, Wq, Wk, Wv, Wg, bg, Wo, ln1_w, ln1_b, ln2_w, ln2_b, W1, b1, W2, b2):
        import jax, jax.numpy as jnp
        import numpy as np
        D_MODEL = 128
        H = 16
        DH = 64
        FFN = 512
        CHUNK = 64
        LN_EPS = 1e-05

        def layer_norm(x, w, b):
            mu = x.mean(-1, keepdims=True)
            var = x.var(-1, keepdims=True)
            return (x - mu) * jax.lax.rsqrt(var + LN_EPS) * w + b

        def l2_normalize(x):
            n = jnp.sqrt(jnp.sum(x * x, axis=-1, keepdims=True))
            return x / jnp.maximum(n, 1e-12)

        def chunk_gla(q, k, v, alpha, C=CHUNK):
            B, Hh, N, D = q.shape
            nc = N // C
            q = q.reshape(B, Hh, nc, C, D)
            k = k.reshape(B, Hh, nc, C, D)
            v = v.reshape(B, Hh, nc, C, D)
            alpha = alpha.reshape(B, Hh, nc, C, D)
            log_a = jnp.log(jnp.maximum(alpha, 1e-06))
            la_cum = jnp.cumsum(log_a, axis=3)
            la_mean = la_cum.mean(-1)
            tril = jnp.tril(jnp.ones((C, C), dtype=q.dtype))
            decay = jnp.exp(la_mean[..., :, None] - la_mean[..., None, :]) * tril
            attn_intra = jnp.einsum('bhncd,bhnmd->bhncm', q, k) * decay
            o_intra = jnp.einsum('bhncm,bhnmd->bhncd', attn_intra, v)
            decay_to_end = jnp.exp(la_cum[:, :, :, -1:, :] - la_cum)
            kv_chunk = jnp.einsum('bhncf,bhnce->bhnfe', k * decay_to_end, v)
            chunk_decay = jnp.exp(log_a.sum(3))
            q_dec = q * jnp.exp(la_cum)

            def step(S, inp):
                qd, kv, cd = inp
                o = jnp.einsum('bhcd,bhde->bhce', qd, S)
                S_new = S * cd[:, :, :, None] + kv
                return (S_new, o)
            S0 = jnp.zeros((B, Hh, D, D), dtype=q.dtype)
            _, o_inter = jax.lax.scan(step, S0, (jnp.moveaxis(q_dec, 2, 0), jnp.moveaxis(kv_chunk, 2, 0), jnp.moveaxis(chunk_decay, 2, 0)))
            o_inter = jnp.moveaxis(o_inter, 0, 2)
            return (o_intra + o_inter).reshape(B, Hh, N, D)
        B, N, _ = x.shape
        xn = layer_norm(x, ln1_w, ln1_b)
        q = (xn @ Wq).reshape(B, N, H, DH).transpose(0, 2, 1, 3)
        k = (xn @ Wk).reshape(B, N, H, DH).transpose(0, 2, 1, 3)
        v = (xn @ Wv).reshape(B, N, H, DH).transpose(0, 2, 1, 3)
        q = l2_normalize(q)
        k = l2_normalize(k)
        alpha = jax.nn.sigmoid(xn @ Wg + bg).reshape(B, N, H, DH).transpose(0, 2, 1, 3)
        o = chunk_gla(q, k, v, alpha)
        o = o.transpose(0, 2, 1, 3).reshape(B, N, H * DH)
        x = x + o @ Wo
        h = layer_norm(x, ln2_w, ln2_b)
        x = x + jax.nn.gelu(h @ W1 + b1, approximate=False) @ W2 + b2
        return x

    def _L1_xattn_ref(encoder_hc, decoder_hq, w_sim, b_sim, W_qv, b_qv):
        import jax, jax.numpy as jnp
        import numpy as np
        B, L_ENC, L_DEC, D = (16, 64, 128, 128)
        d = encoder_hc.shape[-1]
        w1, w2, w3 = (w_sim[:d], w_sim[d:2 * d], w_sim[2 * d:])
        Sim = (encoder_hc @ w1)[:, :, None] + (decoder_hq @ w2)[:, None, :] + jnp.einsum('bid,bjd->bij', encoder_hc * w3, decoder_hq) + b_sim[0]
        A = jax.nn.softmax(Sim, axis=2)
        hq_hat = jnp.einsum('bij,bjd->bid', A, decoder_hq)
        Batt = jax.nn.softmax(jnp.max(Sim, axis=2), axis=1)
        hc_bar = jnp.einsum('bi,bid->bd', Batt, encoder_hc)[:, None, :]
        hc_hat = jnp.broadcast_to(hc_bar, encoder_hc.shape)
        feats = jnp.concatenate([encoder_hc, hq_hat, encoder_hc * hq_hat, encoder_hc * hc_hat], axis=-1)
        hcq = feats @ W_qv + b_qv
        return hcq

    def _L1_ffn_ref(x, in_proj_w, in_proj_b, out_proj_w, out_proj_b, ln1_w, ln1_b, lin1_w, lin1_b, lin2_w, lin2_b, ln2_w, ln2_b, gate_w, gate_b):
        import jax, jax.numpy as jnp
        import numpy as np
        B, S, D = (8, 64, 128)
        H = 16
        DFF = 512
        E = 4
        K = 2
        EPS = 1e-05

        def _layernorm(x, w, b):
            m = x.mean(-1, keepdims=True)
            v = ((x - m) ** 2).mean(-1, keepdims=True)
            return (x - m) / jnp.sqrt(v + EPS) * w + b

        def _encoder_layer(x, iw, ib, ow, ob, l1w, l1b, l2w, l2b, n1w, n1b, n2w, n2b):
            b, s, d = x.shape
            hd = d // H
            qkv = x @ iw.T + ib
            q, k, v = jnp.split(qkv, 3, axis=-1)
            rs = lambda t: t.reshape(b, s, H, hd).transpose(0, 2, 1, 3)
            q, k, v = (rs(q), rs(k), rs(v))
            scale = jnp.asarray(hd, x.dtype) ** 0.5
            scores = jnp.einsum('bhqd,bhkd->bhqk', q, k) / scale
            attn = jax.nn.softmax(scores, axis=-1)
            o = jnp.einsum('bhqk,bhkd->bhqd', attn, v).transpose(0, 2, 1, 3).reshape(b, s, d)
            o = o @ ow.T + ob
            x = _layernorm(x + o, n1w, n1b)
            ff = jax.nn.relu(x @ l1w.T + l1b) @ l2w.T + l2b
            return _layernorm(x + ff, n2w, n2b)
        gate_logits = x.mean(axis=1) @ gate_w.T + gate_b
        _, top_idx = jax.lax.top_k(gate_logits, K)
        gate_weights = jax.nn.softmax(gate_logits, axis=-1)
        mask = jnp.zeros_like(gate_weights).at[jnp.arange(x.shape[0])[:, None], top_idx].set(1.0)
        expert_outs = jax.vmap(_encoder_layer, in_axes=(None, 0, 0, 0, 0, 0, 0, 0, 0, 0, 0, 0, 0))(x, in_proj_w, in_proj_b, out_proj_w, out_proj_b, lin1_w, lin1_b, lin2_w, lin2_b, ln1_w, ln1_b, ln2_w, ln2_b)
        return jnp.einsum('be,ebsd->bsd', gate_weights * mask, expert_outs)
    x = x + _L0_attn_ref(_layernorm(x, axis=-1), L0_attn_ln_g, L0_attn_ln_b, L0_attn_w_qkv, L0_attn_b_qkv, L0_attn_w_gate, L0_attn_b_gate, L0_attn_w_proj, L0_attn_b_proj)
    x = x + _L0_xattn_ref(_layernorm(x, axis=-1), ctx_1024, ctx_1024, mask_Bx1x1xS2_ik0, mask_1x1xSxS2_ik0, L0_xattn_Wq, L0_xattn_bq, L0_xattn_Wk, L0_xattn_bk, L0_xattn_Wv, L0_xattn_bv)
    x = x + _L0_ffn_ref(_layernorm(x, axis=-1), L0_ffn_router_w, L0_ffn_expert_bias, L0_ffn_w1, L0_ffn_w3, L0_ffn_w2, L0_ffn_sw1, L0_ffn_sw3, L0_ffn_sw2)
    x = x + _L1_attn_ref(_layernorm(x, axis=-1), L1_attn_Wq, L1_attn_Wk, L1_attn_Wv, L1_attn_Wg, L1_attn_bg, L1_attn_Wo, L1_attn_ln1_w, L1_attn_ln1_b, L1_attn_ln2_w, L1_attn_ln2_b, L1_attn_W1, L1_attn_b1, L1_attn_W2, L1_attn_b2)
    x = x + _L1_xattn_ref(_layernorm(x, axis=-1), ctx_1024, L1_xattn_w_sim, L1_xattn_b_sim, L1_xattn_W_qv, L1_xattn_b_qv)
    x = x + _L1_ffn_ref(_layernorm(x, axis=-1), L1_ffn_in_proj_w, L1_ffn_in_proj_b, L1_ffn_out_proj_w, L1_ffn_out_proj_b, L1_ffn_ln1_w, L1_ffn_ln1_b, L1_ffn_lin1_w, L1_ffn_lin1_b, L1_ffn_lin2_w, L1_ffn_lin2_b, L1_ffn_ln2_w, L1_ffn_ln2_b, L1_ffn_gate_w, L1_ffn_gate_b)
    return x

_drawn_inputs = setup_inputs


def setup_inputs(seed=0):
    import zlib

    import numpy as np

    out = dict(_drawn_inputs(seed))
    spreads = {'L0_attn_ln_g': (1.0, 0.2),
     'L0_attn_ln_b': (0.0, 0.1),
     'L0_attn_b_qkv': (0.0, 0.1),
     'L0_attn_b_gate': (0.0, 0.1),
     'L0_attn_b_proj': (0.0, 0.1),
     'L0_xattn_bq': (0.0, 0.1),
     'L0_xattn_bk': (0.0, 0.1),
     'L0_xattn_bv': (0.0, 0.1),
     'L0_ffn_expert_bias': (0.0, 0.1),
     'L1_attn_bg': (-0.5, 0.2),
     'L1_attn_ln1_w': (1.0, 0.2),
     'L1_attn_ln1_b': (0.0, 0.1),
     'L1_attn_ln2_w': (1.0, 0.2),
     'L1_attn_ln2_b': (0.0, 0.1),
     'L1_attn_b1': (0.0, 0.1),
     'L1_attn_b2': (0.0, 0.1),
     'L1_ffn_ln1_w': (1.0, 0.2),
     'L1_ffn_ln1_b': (0.0, 0.1),
     'L1_ffn_ln2_w': (1.0, 0.2),
     'L1_ffn_ln2_b': (0.0, 0.1)}
    factors = {}
    for name, (base, spread) in spreads.items():
        noise = np.random.default_rng([zlib.crc32(name.encode()), seed]).standard_normal(out[name].shape)
        drawn = base * np.exp(spread * noise) if base else spread * noise
        out[name] = jnp.asarray(drawn.astype(out[name].dtype))
    for name, factor in factors.items():
        out[name] = (out[name] * factor).astype(out[name].dtype)
    return out
```

```python
from contextlib import ExitStack

import concourse.bass as bass
from concourse import mybir

F32 = mybir.dt.float32
BF16 = mybir.dt.bfloat16
I32 = mybir.dt.int32
ALU = mybir.AluOpType
ACT = mybir.ActivationFunctionType
AX = mybir.AxisListType

B, T, D = 4, 512, 128
CT = 77
H, HD = 16, 8
TT = T // 128
NE, HID = 8, 256
NSH = 2
GH, GD = 16, 64
HP = GH // 2
CH = 64
NC = T // CH
FFN = 512
EX, PICK = 4, 2
PAIRS = B * PICK
EPS = 1e-5
HALF = 64

VEC = {}


def _columns(table, *names):
    at = 0
    for name, n in names:
        table[name] = (at, n)
        at += n
    return at


N_VEC = _columns(VEC, ("ln_g", 1), ("ln_b", 1), ("a_bq", 1), ("a_bk", 1), ("b_gate", 1), ("b_proj", 1),
                 ("x_bq", 1), ("x_bk", 1), ("bg", HP), ("ln1_w", 1), ("ln1_b", 1), ("ln2_w", 1),
                 ("ln2_b", 1), ("b1", FFN // 128), ("b2", 1), ("w1", 1), ("w2", 1), ("w3", 1), ("b_qv", 1))
W_L0 = {}
N_W0 = _columns(W_L0, ("a_wq", D), ("a_wk", D), ("a_wv", D), ("w_gate", D), ("w_proj", D),
                ("x_wq", D), ("x_wk", D), ("x_wv", D), ("router", NE))
W_L1 = {}
N_W1 = _columns(W_L1, ("g_wq", HP * 128), ("g_wk", HP * 128), ("g_wv", HP * 128), ("g_wg", HP * 128),
                ("g_wo", HP * 128), ("f_w1", FFN), ("f_w2", FFN), ("w_qv", 4 * D), ("gate_w", EX))
W_EX = {}
N_WX = _columns(W_EX, ("wq", D), ("wk", D), ("wv", D), ("wo", D), ("l1", FFN), ("l2", FFN),
                ("bq", 1), ("bk", 1), ("ob", 1), ("n1w", 1), ("n1b", 1), ("l1b", FFN // 128), ("l2b", 1),
                ("n2w", 1), ("n2b", 1))
ROW = {}
N_ROW = _columns(ROW, ("a_bv", D), ("x_bv", D), ("router_b", NE), ("gate_b", EX), ("b_sim", 1))
ME = {}
N_ME = _columns(ME, ("w1", HID), ("w3", HID), ("w2", 2 * D))

PARTS = 3
SPLIT = PARTS * PARTS * HD
MAXROW = 96
KROWS = MAXROW + 1


class Signal:

    def __init__(self, ctx, nc, name):
        self.sem = ctx.enter_context(nc.semaphore(name))
        self.base = 0

    def __call__(self, n):
        return self.sem, self.base + n

    def close(self, n):
        self.base += n


def dram_view(t, offset, dims):
    return bass.AP(t.tensor, t.offset + offset, [list(d) for d in dims])


class Chip:

    def __init__(self, ctx, nc):
        self.ctx, self.nc = ctx, nc
        self.signals, self.named = {}, {}
        self.PS = ctx.enter_context(nc.psum_tensor("PS", [128, 8, 512], F32))
        self.x = self.sb("x_res", [128, B, T])
        self.y = self.sb("y_norm", [128, B, T])
        self.sq = self.sb("ln_sq", [128, B, T])
        self.rs = self.sb("ln_rs", [128, B, T])
        self.vec = self.sb("vec", [128, N_VEC])
        self.w1 = self.sb("w_l1", [128, N_W1])
        self.rows = self.sb("rows", [128, N_ROW])
        self.center = self.sb("center", [128, 128])
        self.mean = self.sb("mean", [128, 128])
        self.ident = self.sb("ident", [128, 128])
        self.ones = self.sb("ones", [128, 128])
        self.eps = self.sb("eps", [128, 1])

    def sb(self, name, shape, dt=F32, ctx=None):
        self.named[name] = self.named.get(name, 0) + 1
        if self.named[name] > 1:
            name = f"{name}_{self.named[name]}"
        return (ctx or self.ctx).enter_context(self.nc.sbuf_tensor(name, shape, dt))

    def semaphore_for(self, name):
        if name not in self.signals:
            self.signals[name] = Signal(self.ctx, self.nc, name)
        return self.signals[name]

    def v(self, name, k=0):
        return self.vec[:, VEC[name][0] + k:VEC[name][0] + k + 1]


def norm_pe(c, pe, source, run=0, came=None):
    centered, squared, spread = c.semaphore_for("ln_centered"), c.semaphore_for("ln_squared"), c.semaphore_for("ln_spread")
    for b in range(B):
        if came:
            pe.wait_ge(*came(b + 1))
        pe.matmul(c.PS[:, b, :], c.center[:, :], source[:, b, :], start=True, stop=True)\
            .then_inc(centered.sem, 1)
    for b in range(B):
        pe.wait_ge(*squared(run * B + b + 1))
        pe.matmul(c.PS[:, B + b, :], c.mean[:, :], c.sq[:, b, :], start=True, stop=True)\
            .then_inc(spread.sem, 1)


def norm_act(c, act, run=0):
    centered, squared, spread = c.semaphore_for("ln_centered"), c.semaphore_for("ln_squared"), c.semaphore_for("ln_spread")
    logged, scale = c.semaphore_for("ln_logged"), c.semaphore_for("ln_scale")
    for b in range(B):
        act.wait_ge(*centered(run * B + b + 1))
        act.activation(c.sq[:, b, :], c.PS[:, b, :], ACT.Square).then_inc(squared.sem, 1)
    for b in range(B):
        act.wait_ge(*spread(run * B + b + 1))
        act.activation(c.rs[:, b, :], c.PS[:, B + b, :], ACT.Ln, bias=c.eps[:, :]).then_inc(logged.sem, 1)
    for b in range(B):
        act.wait_ge(*logged(run * B + b + 1))
        act.activation(c.rs[:, b, :], c.rs[:, b, :], ACT.Exp, scale=-0.5).then_inc(scale.sem, 1)


def norm_dve(c, dve, dest, run=0, gain=None, shift=None):
    scale, normed, scaled = c.semaphore_for("ln_scale"), c.semaphore_for("ln_normed"), c.semaphore_for("ln_scaled")
    for b in range(B):
        dve.wait_ge(*scale(run * B + b + 1))
        dve.tensor_tensor(dest[:, b, :], c.PS[:, b, :], c.rs[:, b, :], ALU.mult).then_inc(normed.sem, 1)
        if gain is not None:
            dve.wait_ge(*normed(run * B + b + 1))
            dve.tensor_scalar(dest[:, b, :], dest[:, b, :], gain, shift, ALU.mult, ALU.add)\
                .then_inc(scaled.sem, 1)


def norm_close(c, runs=1, scaled=0):
    for name in ("ln_centered", "ln_squared", "ln_spread", "ln_logged", "ln_scale", "ln_normed"):
        c.semaphore_for(name).close(B * runs)
    c.semaphore_for("ln_scaled").close(B * scaled)


def stage_setup(c, ins):
    loaded = c.semaphore_for("setup_loaded")
    made = c.semaphore_for("const_made")
    with c.nc.Block() as block:
        @block.sync
        def _(sp):
            sp.dma_start(c.x[:, :, :], ins["x"]).then_inc(loaded.sem, 16)
            sp.dma_start(c.vec[:, :], ins["vec"]).then_inc(loaded.sem, 16)
            sp.dma_start(c.rows[:, :], ins["rows"].partition_broadcast(128)).then_inc(loaded.sem, 16)
            sp.dma_start(c.w1[:, :], ins["w_l1"]).then_inc(loaded.sem, 16)

        @block.gpsimd
        def _(pool):
            pool.memset(c.ident[:, :], 0.0).then_inc(made.sem, 1)
            pool.memset(c.ones[:, :], 1.0).then_inc(made.sem, 1)
            pool.memset(c.mean[:, :], 1.0 / D).then_inc(made.sem, 1)
            pool.memset(c.center[:, :], -1.0 / D).then_inc(made.sem, 1)
            pool.memset(c.eps[:, :], EPS).then_inc(made.sem, 1)
            pool.wait_ge(*made(5))
            pool.affine_select(out=c.ident[:, :], in_=c.ident[:, :], compare_op=ALU.not_equal, fill=1.0,
                               base=0, pattern=[[-1, 128]], channel_multiplier=1).then_inc(made.sem, 1)
            pool.affine_select(out=c.center[:, :], in_=c.center[:, :], compare_op=ALU.not_equal,
                               fill=1.0 - 1.0 / D, base=0, pattern=[[-1, 128]], channel_multiplier=1)\
                .then_inc(made.sem, 1)
            pool.wait_ge(*made(7))

        @block.vector
        def _(dve):
            dve.wait_ge(*loaded(4 * 16))
    made.close(7)


def attention_core(c, items, causal, q_parts, k_parts, max_rows, sums, values):
    nc, PS = c.nc, c.PS
    loaded = [c.semaphore_for("qk_loaded_even"), c.semaphore_for("qk_loaded_odd")]
    scored, drained = c.semaphore_for("at_scored"), c.semaphore_for("at_drained")
    drained_v, masked, summed = c.semaphore_for("at_drained_v"), c.semaphore_for("at_masked"), c.semaphore_for("at_summed")
    copied, zeroed = c.semaphore_for("at_sum_copied"), c.semaphore_for("at_zeroed")
    sent = [c.semaphore_for("at_sum_sent_even"), c.semaphore_for("at_sum_sent_odd")]
    nscored, maxed, turned = c.semaphore_for("mx_scored"), c.semaphore_for("mx_found"), c.semaphore_for("mx_turned")
    mcast, msent = c.semaphore_for("mx_cast"), c.semaphore_for("mx_sent")
    mloaded = [c.semaphore_for("mx_loaded_even"), c.semaphore_for("mx_loaded_odd")]
    primed = c.semaphore_for("at_primed")
    G = H // 4
    STEPS = G * TT
    ctx = ExitStack()
    with ctx:
        qs = c.sb("q_split", [128, 2, H, T], BF16, ctx)
        ks = c.sb("k_split", [128, 2, H, T], BF16, ctx)
        probs = c.sb("probs", [128, 2, 4, T], F32, ctx)
        osum = c.sb("o_sum", [128, 2, G, T], F32, ctx)
        zero = c.sb("zero512", [128, T], F32, ctx)
        tri = c.sb("tri", [128, 128], F32, ctx)
        if not causal:
            mx = c.sb("mx", [128, 2, H * TT], F32, ctx)
            mrow = c.sb("mx_row", [H * TT, 2, 128], BF16, ctx)

        block = ctx.enter_context(nc.Block())

        def drain_wait(e, n, s):
            t = n * STEPS + s
            if causal:
                e.wait_ge(*masked(t + 1))
            else:
                e.wait_ge(*drained(2 * t + 2))

        @block.sync
        def _(sp):
            def load(n):
                if n >= 2:
                    sp.wait_ge(*scored((n - 1) * 2 * STEPS))
                else:
                    sp.wait_ge(*primed(4))
                for i in range(PARTS):
                    sp.dma_start(ks[24 * i:24 * i + 24, n % 2, :, :],
                                 dram_view(k_parts, n * PARTS * D * T, [(H * T, 24), (1, H * T)])
                                 ).then_inc(loaded[n % 2].sem, 16)
                    for j in range(PARTS):
                        r = 24 * i + 8 * j
                        sp.dma_start(qs[r:r + 8, n % 2, :, :],
                                     dram_view(q_parts, (n * PARTS + i) * D * T, [(H * T, 8), (1, H * T)])
                                     ).then_inc(loaded[n % 2].sem, 16)

            def send_max(n):
                sp.wait_ge(*mcast(n + 1))
                sp.dma_start(dram_view(max_rows, n * H * T, [(128, H * TT), (1, 128)]), mrow[:, n % 2, :])\
                    .then_inc(msent.sem, 16)
                sp.wait_ge(*msent(16 * (n + 1)))
                sp.dma_start(qs[MAXROW:MAXROW + 1, n % 2, :, :],
                             dram_view(max_rows, n * H * T, [(H * T, 1), (1, H * T)]))\
                    .then_inc(mloaded[n % 2].sem, 16)

            load(0)
            if not causal:
                load(1)
                send_max(0)
            for n in range(items):
                if causal:
                    if n + 1 < items:
                        load(n + 1)
                else:
                    if n + 1 < items:
                        send_max(n + 1)
                sp.wait_ge(*copied(G * (n + 1)))
                for j in range(4):
                    sp.dma_start(dram_view(sums, (n * 4 + j) * 9 * G * T, [(G * T, 9), (1, G * T)]),
                                 osum[32 * j:32 * j + 9, n % 2, :, :]).then_inc(sent[n % 2].sem, 16)
                if not causal and n + 2 < items:
                    load(n + 2)
            for k in range(2):
                sp.wait_ge(*sent[k](64 * (items // 2)))

        @block.gpsimd
        def _(pool):
            pool.memset(qs[:, :, :, :], 0.0).then_inc(primed.sem, 1)
            pool.memset(ks[:, :, :, :], 0.0).then_inc(primed.sem, 1)
            pool.memset(zero[:, :], 0.0).then_inc(primed.sem, 1)
            pool.memset(tri[:, :], 1.0).then_inc(primed.sem, 1)
            pool.wait_ge(*primed(4))
            pool.memset(ks[MAXROW:MAXROW + 1, :, :, :], 1.0).then_inc(zeroed.sem, 1)
            pool.wait_ge(*zeroed(1))
            pool.affine_select(out=tri[:, :], in_=tri[:, :], compare_op=ALU.is_ge, fill=0.0,
                               base=0, pattern=[[1, 128]], channel_multiplier=-1).then_inc(zeroed.sem, 1)
            if causal:
                pool.wait_ge(*zeroed(2))
                for t in range(items * STEPS):
                    q0 = 128 * (t % TT)
                    pool.wait_ge(*drained(t + 1))
                    pool.wait_ge(*drained_v(t + 1))
                    block_of = probs[:, t % 2, :, q0:q0 + 128]
                    pool.tensor_tensor(block_of, block_of, tri[:, :].unsqueeze(1).to_broadcast([128, 4, 128]),
                                       ALU.mult).then_inc(masked.sem, 1)

        @block.tensor
        def _(pe):
            pe.wait_ge(*primed(4))
            pe.wait_ge(*zeroed(2))
            for o in range(2):
                pe.matmul(PS[:, 4 + o, :], zero[:, 0:128], zero[:, :], start=True, stop=True)

            def max_pass(n, i):
                u = n * H * TT + i
                if u >= 2:
                    pe.wait_ge(*maxed(u - 1))
                h, qt = i // TT, i % TT
                pe.matmul(PS[:, 6 + i % 2, :], qs[0:SPLIT, n % 2, h, 128 * qt:128 * qt + 128],
                          ks[0:SPLIT, n % 2, h, :], start=True, stop=True).then_inc(nscored.sem, 1)

            def turn_max(n):
                pe.wait_ge(*maxed((n + 1) * H * TT))
                pe.transpose(PS[0:H * TT, 6, 0:128], mx[:, n % 2, :], c.ident[:, :]).then_inc(turned.sem, 1)

            def scores(n, s):
                g, kt = s // TT, s % TT
                q0 = 128 * kt if causal else 0
                t = n * STEPS + s
                for half in range(2):
                    if t >= 1:
                        if causal:
                            pe.wait_ge(*(drained, drained_v)[half](t))
                        else:
                            pe.wait_ge(*drained(2 * t - 1 + half))
                    for jj in range(2):
                        h = 4 * g + 2 * half + jj
                        rows = SPLIT if causal else KROWS
                        mm = pe.matmul(PS[:, 2 * half + jj, q0:T], ks[0:rows, n % 2, h, 128 * kt:128 * kt + 128],
                                       qs[0:rows, n % 2, h, q0:T], start=True, stop=True)
                    mm.then_inc(scored.sem, 1)

            def sum_up(n, s):
                g, kt = s // TT, s % TT
                q0 = 128 * kt if causal else 0
                t = n * STEPS + s
                drain_wait(pe, n, s)
                if kt == 0 and n * G + g >= 2:
                    pe.wait_ge(*copied(n * G + g - 1))
                for j in range(4):
                    mm = pe.matmul(PS[32 * j:32 * j + 9, 4 + g % 2, q0:T], values[:, n, kt, 4 * g + j, :],
                                   probs[:, t % 2, j, q0:T], start=(kt == 0), stop=(kt == TT - 1),
                                   skip_group_check=True)
                mm.then_inc(summed.sem, 1)

            if not causal:
                pe.wait_ge(*loaded[0](16 * 12))
                for i in range(H * TT):
                    max_pass(0, i)
                turn_max(0)
            for n in range(items):
                ahead = not causal and n + 1 < items
                if ahead:
                    pe.wait_ge(*loaded[(n + 1) % 2](16 * 12 * ((n + 1) // 2 + 1)))
                    pe.wait_ge(*mcast(n + 1))
                pe.wait_ge(*loaded[n % 2](16 * 12 * (n // 2 + 1)))
                if not causal:
                    pe.wait_ge(*mloaded[n % 2](16 * (n // 2 + 1)))
                for s in range(STEPS):
                    scores(n, s)
                    if ahead:
                        for i in range(4):
                            max_pass(n + 1, 4 * s + i)
                    if s:
                        sum_up(n, s - 1)
                sum_up(n, STEPS - 1)
                if ahead:
                    turn_max(n + 1)

        @block.scalar
        def _(act):
            act.preload_act_table_set("natural_log_exp_and_others")
            act.wait_ge(*primed(4))

            def cast_max(n):
                act.wait_ge(*turned(n + 1))
                if n >= 2:
                    act.wait_ge(*msent(16 * (n - 1)))
                act.activation(mrow[:, n % 2, :], PS[0:H * TT, 6, 0:128], ACT.Copy, scale=-1.0)\
                    .then_inc(mcast.sem, 1)

            if not causal:
                cast_max(0)
            for n in range(items):
                for s in range(STEPS):
                    t = n * STEPS + s
                    g, kt = s // TT, s % TT
                    q0 = 128 * kt if causal else 0
                    for half in range(1 if causal else 2):
                        act.wait_ge(*scored(2 * t + half + 1))
                        if t >= 2:
                            act.wait_ge(*summed(t - 1))
                        act.activation(probs[:, t % 2, 2 * half:2 * half + 2, q0:T],
                                       PS[:, 2 * half:2 * half + 2, q0:T],
                                       ACT.Copy if causal else ACT.Exp).then_inc(drained.sem, 1)
                if not causal and n + 1 < items:
                    cast_max(n + 1)

        @block.vector
        def _(dve):
            dve.wait_ge(*zeroed(2))

            def find_max(n, i):
                dve.wait_ge(*nscored(n * H * TT + i + 1))
                if i == 0 and n >= 2:
                    dve.wait_ge(*turned(n - 1))
                dve.tensor_reduce(mx[:, n % 2, i:i + 1], PS[:, 6 + i % 2, :], AX.X, ALU.max)\
                    .then_inc(maxed.sem, 1)

            def copy_sums(n, g):
                dve.wait_ge(*summed(n * STEPS + TT * (g + 1)))
                if g == 0 and n >= 2:
                    dve.wait_ge(*sent[n % 2](64 * (n // 2)))
                dve.tensor_copy(osum[:, n % 2, g, :], PS[:, 4 + g % 2, :]).then_inc(copied.sem, 1)

            if not causal:
                for i in range(H * TT):
                    find_max(0, i)
            for n in range(items):
                for s in range(STEPS):
                    t = n * STEPS + s
                    g, kt = s // TT, s % TT
                    if causal:
                        dve.wait_ge(*scored(2 * t + 2))
                        if t >= 2:
                            dve.wait_ge(*summed(t - 1))
                        dve.tensor_copy(probs[:, t % 2, 2:4, 128 * kt:T], PS[:, 2:4, 128 * kt:T])\
                            .then_inc(drained_v.sem, 1)
                    elif n + 1 < items:
                        for i in range(4):
                            find_max(n + 1, 4 * s + i)
                    if kt == 0 and s:
                        copy_sums(n, g - 1)
                copy_sums(n, G - 1)

    for s, n in ((loaded[0], 8 * 12 * items), (loaded[1], 8 * 12 * items), (scored, 2 * STEPS * items), (drained, (1 if causal else 2) * STEPS * items),
                 (summed, STEPS * items), (copied, G * items), (sent[0], 32 * items),
                 (sent[1], 32 * items), (zeroed, 2), (primed, 4)):
        s.close(n)
    if causal:
        masked.close(STEPS * items)
        drained_v.close(STEPS * items)
    else:
        for s, n in ((nscored, H * TT * items), (maxed, H * TT * items), (turned, items), (mcast, items),
                     (msent, 16 * items), (mloaded[0], 8 * items), (mloaded[1], 8 * items)):
            s.close(n)


def stage_linear_attention(c, ins, scratch):
    nc, PS = c.nc, c.PS
    w_came = c.semaphore_for("w_came")
    second = c.semaphore_for("a_second_norm")
    gated, gsum, glog, gscale, gate = (c.semaphore_for(n) for n in ("a_gate_raw", "a_gate_mean", "a_gate_log",
                                                            "a_gate_scale", "a_gate"))
    sigm = c.semaphore_for("a_sigmoid")
    proj, qk, low, ex, elu = (c.semaphore_for(n) for n in ("a_proj", "a_qk", "a_low", "a_exp", "a_elu"))
    hi, rest, mid, last, vals = (c.semaphore_for(n) for n in ("s_high", "s_rest", "s_middle", "s_last", "at_values"))
    stored = [c.semaphore_for("s_stored_q"), c.semaphore_for("s_stored_k")]
    outer = ExitStack()
    with outer:
        values = c.sb("a_values", [128, B, TT, H, 9], F32, outer)
        w0 = c.sb("w_l0", [128, N_W0], F32, outer)

        def w(name, n=D):
            at = W_L0[name][0]
            return w0[:, at:at + n]

        ctx = ExitStack()
        with ctx:
            z = c.sb("a_z", [128, B, T], F32, ctx)
            gs = c.sb("a_gs", [128, B, T], F32, ctx)
            qkf = c.sb("a_qkf", [128, 2, T], F32, ctx)
            neg = c.sb("a_neg", [128, 2, T], F32, ctx)
            parts = c.sb("a_parts", [128, 2, PARTS, T], BF16, ctx)
            res = c.sb("a_res", [128, 2, T], F32, ctx)
            block = ctx.enter_context(nc.Block())

            @block.sync
            def _(sp):
                sp.dma_start(w0[:, :], ins["w_l0"]).then_inc(w_came.sem, 16)
                for u in range(2 * B):
                    sp.wait_ge(*last(u + 1))
                    dest = scratch["q_parts"] if u % 2 == 0 else scratch["k_parts"]
                    sp.dma_start(dram_view(dest, (u // 2) * PARTS * D * T, [(T, 128), (D * T, PARTS), (1, T)]),
                                 parts[:, u % 2, :, :]).then_inc(stored[u % 2].sem, 16)
                for s in stored:
                    sp.wait_ge(*s(16 * B))

            @block.tensor
            def _(pe):
                norm_pe(c, pe, c.x)
                norm_pe(c, pe, c.y, 1, c.semaphore_for("ln_normed"))
                pe.wait_ge(*w_came(16))
                for b in range(B):
                    pe.wait_ge(*second(b + 1))
                    pe.matmul(PS[:, b, :], w("w_gate"), c.y[:, b, :], start=True, stop=True).then_inc(gated.sem, 1)
                for b in range(B):
                    pe.wait_ge(*sigm(b + 1))
                    pe.matmul(PS[:, B + b, :], c.mean[:, :], gs[:, b, :], start=True, stop=True).then_inc(gsum.sem, 1)
                for b in range(B):
                    if b == 0:
                        pe.wait_ge(*sigm(B))
                    else:
                        pe.wait_ge(*qk(2 * b))
                        pe.wait_ge(*vals(b))
                    pe.matmul(PS[:, 0, :], w("a_wq"), z[:, b, :], start=True, stop=True).then_inc(proj.sem, 1)
                    pe.matmul(PS[:, 1, :], w("a_wk"), z[:, b, :], start=True, stop=True).then_inc(proj.sem, 1)
                    for kt in range(TT):
                        mm = pe.matmul(PS[:, 2, 128 * kt:128 * kt + 128], z[:, b, 128 * kt:128 * kt + 128],
                                       w("a_wv"), start=True, stop=True)
                    mm.then_inc(proj.sem, 1)

            @block.scalar
            def _(act):
                act.preload_act_table_set("natural_log_exp_and_others")
                norm_act(c, act)
                norm_act(c, act, 1)
                for b in range(B):
                    act.wait_ge(*gated(b + 1))
                    act.activation(gs[:, b, :], PS[:, b, :], ACT.Sigmoid, bias=c.v("b_gate")).then_inc(sigm.sem, 1)
                for b in range(B):
                    act.wait_ge(*gsum(b + 1))
                    act.activation(c.rs[:, b, :], PS[:, B + b, :], ACT.Ln, bias=c.eps[:, :]).then_inc(glog.sem, 1)
                for b in range(B):
                    act.wait_ge(*glog(b + 1))
                    act.activation(c.rs[:, b, :], c.rs[:, b, :], ACT.Exp, scale=-1.0).then_inc(gscale.sem, 1)
                for u in range(2 * B):
                    act.wait_ge(*low(u + 1))
                    act.activation(neg[:, u % 2, :], neg[:, u % 2, :], ACT.Exp).then_inc(ex.sem, 1)
                    act.wait_ge(*elu(u + 1))
                    if u >= 2:
                        act.wait_ge(*stored[u % 2](16 * (u // 2)))
                    act.activation(parts[:, u % 2, 0, :], qkf[:, u % 2, :], ACT.Copy).then_inc(hi.sem, 1)
                    act.wait_ge(*rest(u + 1))
                    act.activation(parts[:, u % 2, 1, :], res[:, u % 2, :], ACT.Copy).then_inc(mid.sem, 1)

            @block.gpsimd
            def _(pool):
                pool.memset(values[:, :, :, :, 8:9], 1.0).then_inc(c.semaphore_for("at_ones").sem, 1)

            @block.vector
            def _(dve):
                norm_dve(c, dve, c.y)
                scale = c.semaphore_for("ln_scale")
                for b in range(B):
                    dve.wait_ge(*scale(B + b + 1))
                    dve.tensor_tensor(z[:, b, :], PS[:, b, :], c.rs[:, b, :], ALU.mult)\
                        .then_inc(c.semaphore_for("ln_normed").sem, 1)
                    dve.wait_ge(*c.semaphore_for("ln_normed")(B + b + 1))
                    dve.tensor_scalar(z[:, b, :], z[:, b, :], c.v("ln_g"), c.v("ln_b"), ALU.mult, ALU.add)\
                        .then_inc(second.sem, 1)
                for b in range(B):
                    dve.wait_ge(*gscale(b + 1))
                    dve.tensor_tensor(gs[:, b, :], gs[:, b, :], c.rs[:, b, :], ALU.mult).then_inc(gate.sem, 1)
                dve.wait_ge(*gate(B))
                bv = ROW["a_bv"][0]
                for b in range(B):
                    for k in range(2):
                        u = 2 * b + k
                        dve.wait_ge(*proj(3 * b + k + 1))
                        dve.scalar_tensor_tensor(out=qkf[:, k, :], in0=PS[:, k, :], scalar=c.v(("a_bq", "a_bk")[k]),
                                                 in1=gs[:, b, :], op0=ALU.add, op1=ALU.mult).then_inc(qk.sem, 1)
                        dve.wait_ge(*qk(u + 1))
                        dve.tensor_scalar(neg[:, k, :], qkf[:, k, :], 0.0, None, ALU.min).then_inc(low.sem, 1)
                        if k == 0:
                            dve.wait_ge(*proj(3 * b + 3))
                            dve.tensor_tensor(values[:, b, :, :, 0:8],
                                              PS[:, 2, :].rearrange("p (k h d) -> p k h d", k=TT, d=HD),
                                              c.rows[:, bv:bv + D].rearrange("p (h d) -> p h d", d=HD)
                                              .unsqueeze(1).to_broadcast([128, TT, H, HD]), ALU.add).then_inc(vals.sem, 1)
                        dve.wait_ge(*ex(u + 1))
                        dve.scalar_tensor_tensor(out=qkf[:, k, :], in0=qkf[:, k, :], scalar=0.0, in1=neg[:, k, :],
                                                 op0=ALU.max, op1=ALU.add).then_inc(elu.sem, 1)
                        dve.wait_ge(*hi(u + 1))
                        dve.tensor_tensor(res[:, k, :], qkf[:, k, :], parts[:, k, 0, :], ALU.subtract)\
                            .then_inc(rest.sem, 1)
                        dve.wait_ge(*mid(u + 1))
                        dve.tensor_tensor(parts[:, k, 2, :], res[:, k, :], parts[:, k, 1, :], ALU.subtract)\
                            .then_inc(last.sem, 1)
        norm_close(c, 2)
        for s, n in ((second, B), (gated, B), (gsum, B), (glog, B), (gscale, B), (gate, B), (sigm, B), (proj, 3 * B),
                     (qk, 2 * B), (low, 2 * B), (ex, 2 * B), (elu, 2 * B), (hi, 2 * B), (rest, 2 * B), (mid, 2 * B),
                     (last, 2 * B), (vals, B), (stored[0], 16 * B), (stored[1], 16 * B), (w_came, 16)):
            s.close(n)
        attention_core(c, B, True, scratch["q_parts"], scratch["k_parts"], None, scratch["sums"], values)
        finish_attention(c, scratch, w("w_proj"), 1e-5, c.v("b_proj"))


def fetch_sums(sp, sums, items, num, den, fetched):
    G = H // 4
    for n in range(items):
        for j in range(4):
            at = (n * 4 + j) * 9 * G * T
            sp.dma_start(num[32 * j:32 * j + 32, n, :], dram_view(sums, at, [(T, 32), (1, T)]))\
                .then_inc(fetched[n].sem, 16)
            sp.dma_start(den[32 * j:32 * j + 32, n, :],
                         dram_view(sums, at + 8 * G * T, [(0, 8), (T, G), (1, T)])).then_inc(fetched[n].sem, 16)


def stage_cross_attention(c, ins, scratch):
    nc, PS = c.nc, c.PS
    G = H // 4
    w_came, made = c.semaphore_for("w_came"), c.semaphore_for("const_made")
    proj, kq, spread_k, vals = (c.semaphore_for(n) for n in ("x_proj", "x_biased", "x_k_spread", "at_values"))
    capped = c.semaphore_for("x_cap")
    scored, mined, maxed, subbed, exped = (c.semaphore_for(n) for n in ("x_scored", "x_masked", "x_max", "x_shifted", "x_exp"))
    turned, moved, summed, copied = (c.semaphore_for(n) for n in ("x_turned", "x_moved", "x_summed", "x_sum_copied"))
    sent = [c.semaphore_for("at_sum_sent_even"), c.semaphore_for("at_sum_sent_odd")]
    outer = ExitStack()
    with outer:
        w0 = c.sb("x_w", [128, N_W0], F32, outer)
        q = c.sb("x_q", [128, B, T], F32, outer)
        kx = c.sb("x_kx", [128, B, H, CT], F32, outer)
        vx = c.sb("x_vx", [CT, B, H, 9], F32, outer)
        cap = c.sb("x_cap", [128, B, TT, CT], F32, outer)
        perm = c.sb("x_perm", [128, 128], F32, outer)

        def w(name, n=D):
            at = W_L0[name][0]
            return w0[:, at:at + n]

        ctx = ExitStack()
        with ctx:
            cx = c.sb("x_ctx", [128, B, CT], F32, ctx)
            kb = c.sb("x_kb", [128, B, CT], F32, ctx)
            hm = c.sb("x_head", [128, H], F32, ctx)
            padi = c.sb("x_padi", [128, B, CT], I32, ctx)
            subi = c.sb("x_subi", [128, TT, CT], I32, ctx)
            pad = c.sb("x_pad", [128, B, CT], F32, ctx)
            sub = c.sb("x_sub", [128, TT, CT], F32, ctx)
            block = ctx.enter_context(nc.Block())

            @block.sync
            def _(sp):
                sp.dma_start(w0[:, :], ins["w_l0"]).then_inc(w_came.sem, 16)
                sp.dma_start(cx[:, :, :], ins["ctx"]).then_inc(w_came.sem, 16)
                sp.dma_start(padi[:, :, :], ins["pad_mask"].rearrange("b t -> (b t)").partition_broadcast(128))\
                    .then_inc(w_came.sem, 16)
                sp.dma_start(subi[:, :, :], ins["sub_mask"].rearrange("(k p) t -> p k t", p=128))\
                    .then_inc(w_came.sem, 16)
                sp.dma_start(perm[:, :], ins["perm"]).then_inc(w_came.sem, 16)

            @block.tensor
            def _(pe):
                norm_pe(c, pe, c.x)
                pe.wait_ge(*w_came(80))
                normed = c.semaphore_for("ln_normed")
                pe.wait_ge(*normed(B))
                for b in range(B):
                    pe.matmul(PS[:, b, :], w("x_wq"), c.y[:, b, :], start=True, stop=True).then_inc(proj.sem, 1)
                pe.matmul(PS[:, 4, 0:B * CT], w("x_wk"), cx[:, :, :].rearrange("p b t -> p (b t)"),
                          start=True, stop=True).then_inc(proj.sem, 1)
                for b in range(B):
                    mm = pe.matmul(PS[0:CT, 5, D * b:D * b + D], cx[:, b, :], w("x_wv"), start=True, stop=True)
                mm.then_inc(proj.sem, 1)

            @block.scalar
            def _(act):
                act.preload_act_table_set("natural_log_exp_and_others")
                norm_act(c, act)

            @block.gpsimd
            def _(pool):
                pool.memset(hm[:, :], 1.0).then_inc(made.sem, 1)
                pool.wait_ge(*made(1))
                pool.affine_select(out=hm[:, :], in_=hm[:, :], compare_op=ALU.is_ge, fill=0.0, base=0,
                                   pattern=[[-HD, H]], channel_multiplier=1).then_inc(made.sem, 1)
                pool.wait_ge(*made(2))
                pool.affine_select(out=hm[:, :], in_=hm[:, :], compare_op=ALU.is_ge, fill=0.0, base=HD - 1,
                                   pattern=[[HD, H]], channel_multiplier=-1).then_inc(made.sem, 1)
                pool.memset(vx[:, :, :, 8:9], 1.0).then_inc(made.sem, 1)

            @block.vector
            def _(dve):
                dve.wait_ge(*w_came(80))
                dve.tensor_scalar(pad[:, :, :], padi[:, :, :], 0, None, ALU.not_equal).then_inc(capped.sem, 1)
                dve.tensor_scalar(sub[:, :, :], subi[:, :, :], 0, None, ALU.not_equal).then_inc(capped.sem, 1)
                dve.wait_ge(*capped(2))
                for b in range(B):
                    dve.tensor_tensor(cap[:, b, :, :], sub[:, :, :],
                                      pad[:, b, :].unsqueeze(1).to_broadcast([128, TT, CT]), ALU.mult)\
                        .then_inc(capped.sem, 1)
                dve.wait_ge(*capped(2 + B))
                dve.tensor_scalar(cap[:, :, :, :], cap[:, :, :, :], 3e38, -1e9, ALU.mult, ALU.add)\
                    .then_inc(capped.sem, 1)
                norm_dve(c, dve, c.y)
                dve.wait_ge(*proj(B + 1))
                dve.tensor_scalar(kb[:, :, :], PS[:, 4, 0:B * CT].rearrange("p (b t) -> p b t", b=B), c.v("x_bk"), None,
                                  ALU.add).then_inc(kq.sem, 1)
                dve.wait_ge(*proj(B + 2))
                bv = ROW["x_bv"][0]
                dve.wait_ge(*made(4))
                dve.tensor_tensor(vx[:, :, :, 0:8], PS[0:CT, 5, :].rearrange("p (b h d) -> p b h d", b=B, d=HD),
                                  c.rows[0:CT, bv:bv + D].rearrange("p (h d) -> p h d", d=HD).unsqueeze(1)
                                  .to_broadcast([CT, B, H, HD]), ALU.add).then_inc(vals.sem, 1)
                dve.wait_ge(*kq(1))
                for b in range(B):
                    dve.tensor_tensor(kx[:, b, :, :], kb[:, b, :].unsqueeze(1).to_broadcast([128, H, CT]),
                                      hm[:, :].unsqueeze(2).to_broadcast([128, H, CT]), ALU.mult)\
                        .then_inc(spread_k.sem, 1)
                for b in range(B):
                    dve.tensor_scalar(q[:, b, :], PS[:, b, :], c.v("x_bq"), float(HD) ** -0.5, ALU.add, ALU.mult)\
                        .then_inc(kq.sem, 1)
                dve.wait_ge(*kq(1 + B))
        norm_close(c)
        for s, n in ((w_came, 80), (proj, B + 2), (kq, B + 1), (spread_k, B), (vals, 1), (capped, 3 + B)):
            s.close(n)
        made.close(4)

        ctx = ExitStack()
        with ctx:
            sc = c.sb("x_sc", [128, 2, H, CT], F32, ctx)
            mx = c.sb("x_mx", [128, 2, H], F32, ctx)
            pt = c.sb("x_pt", [CT, 2, 4, 128], F32, ctx)
            osum = c.sb("x_osum", [128, 2, G, T], F32, ctx)
            zero = c.sb("x_zero", [128, T], F32, ctx)
            U = B * TT
            zeroed = c.semaphore_for("at_zeroed")
            block = ctx.enter_context(nc.Block())

            @block.tensor
            def _(pe):
                pe.wait_ge(*zeroed(1))
                for o in range(2):
                    pe.matmul(PS[:, 6 + o, :], zero[:, 0:128], zero[:, :], start=True, stop=True)

                def scores(u):
                    b, qt = u // TT, u % TT
                    if u:
                        pe.wait_ge(*mined(u))
                    for g in range(G):
                        mm = pe.matmul(PS[:, g, 0:4 * CT], q[:, b, 128 * qt:128 * qt + 128],
                                       kx[:, b, 4 * g:4 * g + 4, :].rearrange("p h t -> p (h t)"),
                                       start=True, stop=True)
                    mm.then_inc(scored.sem, 1)

                def sum_up(u, g):
                    b = u // TT
                    k = u * G + g
                    pe.wait_ge(*moved(k + 1))
                    if g == 0 and u >= 2:
                        pe.wait_ge(*copied(u - 1))
                    for j in range(4):
                        mm = pe.matmul(PS[32 * j:32 * j + 9, 6 + u % 2, 128 * g:128 * g + 128],
                                       vx[:, b, 4 * g + j, :], pt[:, k % 2, j, :], start=True, stop=True,
                                       skip_group_check=True)
                    mm.then_inc(summed.sem, 1)

                scores(0)
                for u in range(U):
                    if u + 1 < U:
                        scores(u + 1)
                    pe.wait_ge(*exped(u + 1))
                    for g in range(G):
                        k = u * G + g
                        if k >= 2:
                            pe.wait_ge(*moved(k - 1))
                        for j in range(4):
                            mm = pe.transpose(PS[0:CT, 4 + k % 2, 128 * j:128 * j + 128], sc[:, u % 2, 4 * g + j, :],
                                              c.ident[:, :])
                        mm.then_inc(turned.sem, 1)
                        if g:
                            sum_up(u, g - 1)
                    sum_up(u, G - 1)

            @block.gpsimd
            def _(pool):
                pool.memset(zero[:, :], 0.0).then_inc(zeroed.sem, 1)
                for u in range(U):
                    pool.wait_ge(*maxed(u + 1))
                    pool.tensor_tensor(sc[:, u % 2, :, :], sc[:, u % 2, :, :],
                                       mx[:, u % 2, :].unsqueeze(2).to_broadcast([128, H, CT]), ALU.subtract)\
                        .then_inc(subbed.sem, 1)

            @block.scalar
            def _(act):
                act.preload_act_table_set("natural_log_exp_and_others")
                for u in range(U):
                    act.wait_ge(*subbed(u + 1))
                    act.activation(sc[:, u % 2, :, :], sc[:, u % 2, :, :], ACT.Exp).then_inc(exped.sem, 1)
                    for g in range(G):
                        k = u * G + g
                        act.wait_ge(*turned(k + 1))
                        if k >= 2:
                            act.wait_ge(*summed(k - 1))
                        act.activation(pt[:, k % 2, :, :], PS[0:CT, 4 + k % 2, :].rearrange("p (j q) -> p j q", j=4),
                                       ACT.Copy).then_inc(moved.sem, 1)

            @block.vector
            def _(dve):
                def copy_sums(u):
                    b, qt = u // TT, u % TT
                    dve.wait_ge(*summed(G * (u + 1)))
                    if qt == 0 and b >= 2:
                        dve.wait_ge(*sent[b % 2](64 * (b // 2)))
                    dve.tensor_copy(osum[:, b % 2, :, 128 * qt:128 * qt + 128],
                                    PS[:, 6 + u % 2, :].rearrange("p (g q) -> p g q", g=G)).then_inc(copied.sem, 1)

                for u in range(U):
                    b, qt = u // TT, u % TT
                    dve.wait_ge(*scored(u + 1))
                    if u >= 2:
                        dve.wait_ge(*turned(G * (u - 1)))
                    dve.tensor_tensor(sc[:, u % 2, :, :].rearrange("p (g h) t -> p g h t", g=G),
                                      PS[:, 0:4, 0:4 * CT].rearrange("p g (h t) -> p g h t", h=4),
                                      cap[:, b, qt, :].unsqueeze(1).unsqueeze(1).to_broadcast([128, G, 4, CT]),
                                      ALU.min).then_inc(mined.sem, 1)
                    dve.wait_ge(*mined(u + 1))
                    dve.tensor_reduce(mx[:, u % 2, :], sc[:, u % 2, :, :], AX.X, ALU.max).then_inc(maxed.sem, 1)
                    if u:
                        copy_sums(u - 1)
                copy_sums(U - 1)

            @block.sync
            def _(sp):
                for b in range(B):
                    sp.wait_ge(*copied(TT * (b + 1)))
                    for j in range(4):
                        sp.dma_start(dram_view(scratch["sums"], (b * 4 + j) * 9 * G * T, [(G * T, 9), (1, G * T)]),
                                     osum[32 * j:32 * j + 9, b % 2, :, :]).then_inc(sent[b % 2].sem, 16)
                for s in sent:
                    sp.wait_ge(*s(64 * (B // 2)))
        for s, n in ((scored, U), (mined, U), (maxed, U), (subbed, U), (exped, U), (turned, U * G), (moved, U * G),
                     (summed, U * G), (copied, U), (sent[0], 32 * B), (sent[1], 32 * B), (zeroed, 1)):
            s.close(n)
        finish_attention(c, scratch, perm[:, :], None, None)


def finish_attention(c, scratch, weight, shift, bias):
    nc, PS = c.nc, c.PS
    fetched = [c.semaphore_for(f"o_fetched{n}") for n in range(B)]
    inverted, divided, projected, added = (c.semaphore_for(n) for n in ("o_inverted", "o_divided", "o_projected", "x_added"))
    ctx = ExitStack()
    with ctx:
        num = c.sb("o_num", [128, B, T], F32, ctx)
        den = c.sb("o_den", [128, B, T], F32, ctx)
        block = ctx.enter_context(nc.Block())

        @block.sync
        def _(sp):
            fetch_sums(sp, scratch["sums"], B, num, den, fetched)

        @block.tensor
        def _(pe):
            for b in range(B):
                pe.wait_ge(*divided(b + 1))
                pe.matmul(PS[:, b, :], weight, num[:, b, :], start=True, stop=True).then_inc(projected.sem, 1)

        @block.vector
        def _(dve):
            for b in range(B):
                dve.wait_ge(*fetched[b](128))
                dve.tensor_scalar(den[:, b, :], den[:, b, :], shift or 0.0, None, ALU.add).then_inc(inverted.sem, 1)
                dve.wait_ge(*inverted(2 * b + 1))
                dve.reciprocal(den[:, b, :], den[:, b, :]).then_inc(inverted.sem, 1)
                dve.wait_ge(*inverted(2 * b + 2))
                dve.tensor_tensor(num[:, b, :], num[:, b, :], den[:, b, :], ALU.mult).then_inc(divided.sem, 1)
            for b in range(B):
                dve.wait_ge(*projected(b + 1))
                dve.scalar_tensor_tensor(out=c.x[:, b, :], in0=PS[:, b, :], scalar=0.0 if bias is None else bias,
                                         in1=c.x[:, b, :], op0=ALU.add, op1=ALU.add).then_inc(added.sem, 1)
            dve.wait_ge(*added(B))
    for s, n in (*((f, 128) for f in fetched), (inverted, 2 * B), (divided, B), (projected, B), (added, B)):
        s.close(n)


def stage_experts(c, ins, scratch):
    nc, PS = c.nc, c.PS
    ALL = NSH + NE
    NT = B * TT
    ROUTED = NSH
    w_came, made, normed = c.semaphore_for("w_came"), c.semaphore_for("const_made"), c.semaphore_for("ln_normed")
    routed, step, exped, turned, moved, stored = (c.semaphore_for(n) for n in (
        "m_logits", "m_route_step", "m_exp", "m_turned", "m_turned_copy", "m_weights_stored"))
    slot_came = [c.semaphore_for("m_slot_even"), c.semaphore_for("m_slot_odd")]
    up, silu, gated, wide, summed, added = (c.semaphore_for(n) for n in (
        "m_up", "m_silu", "m_gated", "m_weighted", "m_down", "x_added"))
    outer = ExitStack()
    with outer:
        ctx = ExitStack()
        with ctx:
            rw = c.sb("m_router", [128, NE], F32, ctx)
            lg = c.sb("m_lg", [128, NT, NE], F32, ctx)
            ex = c.sb("m_ex", [128, NT, NE], F32, ctx)
            small = c.sb("m_small", [128, 4, NT], F32, ctx)
            gt = c.sb("m_gt", [128, NT, NE, NE], F32, ctx)
            eq = c.sb("m_eq", [128, NT, NE, NE], F32, ctx)
            low = c.sb("m_low", [128, NE, NE], F32, ctx)
            cwt = c.sb("m_cwt", [NE, B, T], F32, ctx)
            block = ctx.enter_context(nc.Block())
            a, n = W_L0["router"]

            @block.sync
            def _(sp):
                sp.dma_start(rw[:, :], ins["w_l0"][:, a:a + n]).then_inc(w_came.sem, 16)
                sp.wait_ge(*moved(B))
                sp.dma_start(scratch["combine"], cwt[:, :, :].rearrange("e b t -> e (b t)")).then_inc(stored.sem, 16)
                sp.wait_ge(*stored(16))

            @block.gpsimd
            def _(pool):
                pool.memset(low[:, :, :], 1.0).then_inc(made.sem, 1)
                pool.wait_ge(*made(1))
                pool.affine_select(out=low[:, :, :], in_=low[:, :, :], compare_op=ALU.is_ge, fill=0.0, base=-1,
                                   pattern=[[1, NE], [-1, NE]], channel_multiplier=0).then_inc(made.sem, 1)

            @block.tensor
            def _(pe):
                norm_pe(c, pe, c.x)
                pe.wait_ge(*w_came(16))
                pe.wait_ge(*normed(B))
                for i in range(NT):
                    mm = pe.matmul(PS[:, 0, NE * i:NE * i + NE], c.y[:, i // TT, 128 * (i % TT):128 * (i % TT) + 128],
                                   rw[:, :], start=True, stop=True)
                mm.then_inc(routed.sem, 1)
                pe.wait_ge(*step(12))
                for i in range(NT):
                    mm = pe.transpose(PS[0:NE, i // TT, 128 * (i % TT):128 * (i % TT) + 128], ex[:, i, :], c.ident[:, :])
                    if i % TT == TT - 1:
                        mm.then_inc(turned.sem, 1)

            @block.scalar
            def _(act):
                act.preload_act_table_set("natural_log_exp_and_others")
                norm_act(c, act)
                act.wait_ge(*step(8))
                act.activation(ex[:, :, :], ex[:, :, :], ACT.Exp).then_inc(exped.sem, 1)
                for b in range(B):
                    act.wait_ge(*turned(b + 1))
                    act.activation(cwt[:, b, :], PS[0:NE, b, :], ACT.Copy).then_inc(moved.sem, 1)

            @block.vector
            def _(dve):
                norm_dve(c, dve, c.y)
                dve.wait_ge(*routed(1))
                rb = ROW["router_b"][0]
                dve.tensor_tensor(lg[:, :, :], PS[:, 0, 0:NT * NE].rearrange("p (i e) -> p i e", e=NE),
                                  c.rows[:, rb:rb + NE].unsqueeze(1).to_broadcast([128, NT, NE]), ALU.add)\
                    .then_inc(step.sem, 1)
                dve.wait_ge(*step(1))
                other = lg[:, :, :].unsqueeze(2).to_broadcast([128, NT, NE, NE])
                own = lg[:, :, :].unsqueeze(3).to_broadcast([128, NT, NE, NE])
                dve.tensor_tensor(gt[:, :, :, :], other, own, ALU.is_gt).then_inc(step.sem, 1)
                dve.tensor_tensor(eq[:, :, :, :], other, own, ALU.is_equal).then_inc(step.sem, 1)
                dve.wait_ge(*made(2))
                dve.wait_ge(*step(3))
                dve.tensor_tensor(eq[:, :, :, :], eq[:, :, :, :],
                                  low[:, :, :].unsqueeze(1).to_broadcast([128, NT, NE, NE]), ALU.mult)\
                    .then_inc(step.sem, 1)
                dve.wait_ge(*step(4))
                dve.tensor_tensor(gt[:, :, :, :], gt[:, :, :, :], eq[:, :, :, :], ALU.add).then_inc(step.sem, 1)
                dve.tensor_reduce(small[:, 0, :], lg[:, :, :], AX.X, ALU.max).then_inc(step.sem, 1)
                dve.wait_ge(*step(6))
                dve.tensor_reduce(eq[:, :, :, 0], gt[:, :, :, :], AX.X, ALU.add).then_inc(step.sem, 1)
                dve.tensor_tensor(ex[:, :, :], lg[:, :, :], small[:, 0, :].unsqueeze(2).to_broadcast([128, NT, NE]),
                                  ALU.subtract).then_inc(step.sem, 1)
                dve.wait_ge(*step(8))
                dve.wait_ge(*exped(1))
                dve.scalar_tensor_tensor(out=ex[:, :, :], in0=eq[:, :, :, 0], scalar=1.5, in1=ex[:, :, :],
                                         op0=ALU.is_lt, op1=ALU.mult).then_inc(step.sem, 1)
                dve.wait_ge(*step(9))
                dve.tensor_reduce(small[:, 1, :], ex[:, :, :], AX.X, ALU.add).then_inc(step.sem, 1)
                dve.wait_ge(*step(10))
                dve.reciprocal(small[:, 2, :], small[:, 1, :]).then_inc(step.sem, 1)
                dve.wait_ge(*step(11))
                dve.tensor_tensor(ex[:, :, :], ex[:, :, :], small[:, 2, :].unsqueeze(2).to_broadcast([128, NT, NE]),
                                  ALU.mult).then_inc(step.sem, 1)
        norm_close(c)
        for s, n in ((w_came, 16), (made, 2), (routed, 1), (step, 12), (exped, 1), (turned, B), (moved, B), (stored, 16)):
            s.close(n)

        ctx = ExitStack()
        with ctx:
            slot = c.sb("m_slot", [128, 2, N_ME], F32, ctx)
            cw = c.sb("m_cw", [128, 2, B, T], F32, ctx)
            yw = c.sb("m_yw", [128, 2, B, T], F32, ctx)
            sl = c.sb("m_sl", [128, 2, T], F32, ctx)
            gb = c.sb("m_gb", [128, 2, T], F32, ctx)
            block = ctx.enter_context(nc.Block())
            STEPS = 2 * B
            LOOPED = NE // 2 - 1

            def w(par, name, m):
                at = ME[name][0] + 128 * m
                return slot[:, par, at:at + 128]

            @block.sync
            def _(sp):
                def load(e, par, routed_one):
                    if not (isinstance(e, int) and e < 2):
                        sp.wait_ge(*summed(STEPS * e - STEPS))
                    sp.dma_start(slot[:, par, :], ins["moe"][e, :, :] if isinstance(e, int) else
                                 ins["moe"][bass.ds(e, 1), :, :].rearrange("a p n -> (a p) n"))\
                        .then_inc(slot_came[par].sem, 16)
                    if routed_one:
                        row = e - ROUTED
                        src = scratch["combine"][row:row + 1, :] if isinstance(e, int) else \
                            scratch["combine"][bass.ds(row, 1), :]
                        sp.dma_start(cw[:, par, :, :].rearrange("p b t -> p (b t)"),
                                     src.to_broadcast([128, B * T])).then_inc(slot_came[par].sem, 16)

                for e in range(NSH):
                    load(e, e % 2, False)
                with sp.Fori(0, LOOPED) as i:
                    for par in range(2):
                        load(2 * i + (NSH + par), par, True)
                for e in range(ALL - 2, ALL):
                    load(e, e % 2, True)

            def came(e, par):
                return slot_came[par]((e - par) * 16 + 16) if not isinstance(e, int) or e >= NSH else slot_came[par](16)

            @block.gpsimd
            def _(pool):
                def weigh(e, par):
                    pool.wait_ge(*came(e, par))
                    pool.wait_ge(*up(STEPS * e - STEPS))
                    for b in range(B):
                        pool.tensor_tensor(yw[:, par, b, :], c.y[:, b, :], cw[:, par, b, :], ALU.mult)\
                            .then_inc(wide.sem, 1)

                with pool.Fori(0, LOOPED) as i:
                    for par in range(2):
                        weigh(2 * i + (NSH + par), par)
                for e in range(ALL - 2, ALL):
                    weigh(e, e % 2)

            @block.tensor
            def _(pe):
                def down(e, par, s, first=False, last=False):
                    b, m = s // 2, s % 2
                    pe.wait_ge(*gated(STEPS * e + (s + 1)))
                    pe.matmul(PS[:, 4 + b, :], w(par, "w2", m), gb[:, m, :], start=first and m == 0,
                              stop=last and m == 1, skip_group_check=True).then_inc(summed.sem, 1)

                def expert(e, par, first=False, last=False, fixed=True):
                    pe.wait_ge(*came(e, par))
                    for s in range(STEPS):
                        b, m = s // 2, s % 2
                        begun = not (first and s < 2)
                        if begun:
                            pe.wait_ge(*silu(STEPS * e + (s - 1)))
                        pe.matmul(PS[:, m, :], w(par, "w1", m), c.y[:, b, :], start=True, stop=True)
                        if begun:
                            pe.wait_ge(*gated(STEPS * e + (s - 1)))
                        routed_one = not fixed or e >= NSH
                        if routed_one and m == 0:
                            pe.wait_ge(*wide(B * e + (b + 1 - B * NSH)))
                        pe.matmul(PS[:, 2 + m, :], w(par, "w3", m), yw[:, par, b, :] if routed_one else c.y[:, b, :],
                                  start=True, stop=True).then_inc(up.sem, 1)
                        if s:
                            down(e, par, s - 1, first, last)
                        elif not first:
                            down(e - 1, 1 - par, STEPS - 1)

                expert(0, 0, first=True)
                expert(1, 1)
                with pe.Fori(0, LOOPED) as i:
                    for par in range(2):
                        expert(2 * i + (NSH + par), par, fixed=False)
                expert(ALL - 2, 0)
                expert(ALL - 1, 1, last=True)
                down(ALL - 1, 1, STEPS - 1, last=True)

            @block.scalar
            def _(act):
                act.preload_act_table_set("natural_log_exp_and_others")
                def expert(e, first=False):
                    for s in range(STEPS):
                        act.wait_ge(*up(STEPS * e + (s + 1)))
                        if not (first and s < 2):
                            act.wait_ge(*gated(STEPS * e + (s - 1)))
                        act.activation(sl[:, s % 2, :], PS[:, s % 2, :], ACT.Silu).then_inc(silu.sem, 1)

                expert(0, True)
                expert(1)
                with act.Fori(0, LOOPED) as i:
                    for par in range(2):
                        expert(2 * i + (NSH + par))
                expert(ALL - 2)
                expert(ALL - 1)

            @block.vector
            def _(dve):
                def expert(e, first=False):
                    for s in range(STEPS):
                        dve.wait_ge(*silu(STEPS * e + (s + 1)))
                        if not (first and s < 2):
                            dve.wait_ge(*summed(STEPS * e + (s - 1)))
                        dve.tensor_tensor(gb[:, s % 2, :], sl[:, s % 2, :], PS[:, 2 + s % 2, :], ALU.mult)\
                            .then_inc(gated.sem, 1)

                expert(0, True)
                expert(1)
                with dve.Fori(0, LOOPED) as i:
                    for par in range(2):
                        expert(2 * i + (NSH + par))
                expert(ALL - 2)
                expert(ALL - 1)
                dve.wait_ge(*summed(STEPS * ALL))
                for b in range(B):
                    dve.tensor_tensor(c.x[:, b, :], c.x[:, b, :], PS[:, 4 + b, :], ALU.add).then_inc(added.sem, 1)
                dve.wait_ge(*added(B))
        per = (16 + 32 * NE // 2)
        for s, n in ((slot_came[0], per), (slot_came[1], per), (up, STEPS * ALL), (silu, STEPS * ALL),
                     (gated, STEPS * ALL), (wide, B * NE), (summed, STEPS * ALL), (added, B)):
            s.close(n)


def stage_gated_attention(c, ins, scratch):
    nc, PS = c.nc, c.PS
    made, normed = c.semaphore_for("const_made"), c.semaphore_for("ln_normed")
    scaled = c.semaphore_for("ln_scaled")
    outer = ExitStack()
    with outer:
        z = c.sb("g_z", [128, B, T], F32, outer)
        ctx = ExitStack()
        with ctx:
            def buf(name, shape, dt=F32):
                return c.sb("g_" + name, shape, dt, ctx)

            xb = buf("xb", [128, T])
            sqq, sqk, e1, t1, lga = (buf(n, [128, T]) for n in ("sqq", "sqk", "e1", "t1", "lga"))
            rq, rk, te, de, dd, dec, kdt, oe = (buf(n, [128, T]) for n in ("rq", "rk", "te", "de", "dd", "dec", "kdt", "oe"))
            dg = buf("dg", [128, NC])
            cum, eq, qn, kn, kd = (buf(n, [128, 2, T]) for n in ("cum", "eq", "qn", "kn", "kd"))
            le, lo, re, ro = (buf(n, [128, 2, T]) for n in ("le", "lo", "re", "ro"))
            reset = buf("reset", [128, T])
            late = buf("late", [128, CH])
            eye = buf("eye", [128, CH])
            pair, swap = buf("pair", [128, 128]), buf("swap", [128, 128])
            nbg = buf("nbg", [128, HP])
            ln256 = buf("ln256", [128, 1])

            (proj, sq, ex, vm, nrm, ln, rr, tt, la, cm, eqs, tes, des, qk, kds, qds) = (c.semaphore_for("g_" + n) for n in (
                "projected", "squared", "exp", "values", "norm", "norm_log", "norm_scale", "one_plus", "log",
                "cumulated", "decay", "to_end", "end_decay", "normalised", "k_decayed", "q_decayed"))
            (lm, sc, kt, dst, dms, decs, ktm, kv, am, st, om, oes, acc, res, xbs) = (c.semaphore_for("g_" + n) for n in (
                "mean_log", "scored", "k_turned", "pair_log", "pair_masked", "pair_decay", "k_moved", "chunk_state",
                "weighted", "state", "out", "out_copied", "out_projected", "residual", "x_copied"))

            def wl(name, hp):
                at = W_L1[name][0] + 128 * hp
                return c.w1[:, at:at + 128]

            with nc.Block() as block:
                @block.gpsimd
                def _(pool):
                    pool.memset(reset[:, :], 1.0).then_inc(made.sem, 1)
                    pool.memset(pair[:, :], 0.0).then_inc(made.sem, 1)
                    pool.memset(swap[:, :], 0.0).then_inc(made.sem, 1)
                    pool.memset(late[:, :], 0.0).then_inc(made.sem, 1)
                    pool.memset(eye[:, :], 0.0).then_inc(made.sem, 1)
                    pool.memset(ln256[:, :], 5.545177444479562).then_inc(made.sem, 1)
                    pool.memset(le[:, :, :], 0.0).then_inc(made.sem, 1)
                    pool.memset(lo[:, :, :], 0.0).then_inc(made.sem, 1)
                    pool.wait_ge(*made(8))
                    pool.memset(reset[:, :].rearrange("p (n t) -> p n t", t=CH)[:, :, 0:1], 0.0).then_inc(made.sem, 1)
                    pool.wait_ge(*made(9))
                    for p in (0, HALF):
                        pool.memset(pair[p:p + HALF, p:p + HALF], 1.0).then_inc(made.sem, 1)
                        pool.memset(swap[p:p + HALF, HALF - p:CH + HALF - p], 1.0 / GD).then_inc(made.sem, 1)
                    pool.wait_ge(*made(13))
                    for p in (0, HALF):
                        pool.affine_select(out=late[p:p + HALF, :], in_=late[p:p + HALF, :], compare_op=ALU.is_ge,
                                           fill=1e30, base=0, pattern=[[1, CH]], channel_multiplier=-1)\
                            .then_inc(made.sem, 1)
                        pool.affine_select(out=eye[p:p + HALF, :], in_=eye[p:p + HALF, :], compare_op=ALU.not_equal,
                                           fill=1.0, base=0, pattern=[[-1, CH]], channel_multiplier=1)\
                            .then_inc(made.sem, 1)

                @block.tensor
                def _(pe):
                    norm_pe(c, pe, c.x)
                    norm_pe(c, pe, c.y, 1, normed)

                @block.scalar
                def _(act):
                    act.preload_act_table_set("natural_log_exp_and_others")
                    norm_act(c, act)
                    norm_act(c, act, 1)

                @block.vector
                def _(dve):
                    a, n = VEC["bg"]
                    dve.tensor_scalar(nbg[:, :], c.vec[:, a:a + n], -1.0, None, ALU.mult).then_inc(res.sem, 1)
                    norm_dve(c, dve, c.y)
                    norm_dve(c, dve, z, 1, c.v("ln1_w"), c.v("ln1_b"))
            norm_close(c, 2, 1)
            res.close(1)
            made.close(17)

            block = ctx.enter_context(nc.Block())

            def chunks(t):
                return t.rearrange("p (n t) -> p n t", t=CH)

            @block.tensor
            def _(pe):
                def front(u, hp):
                    if hp == 0:
                        pe.wait_ge(*xbs(u_batch(u) + 1))
                    pe.wait_ge(*qk(2 * u))
                    pe.matmul(PS[:, 0, :], wl("g_wq", hp), xb[:, :], start=True, stop=True).then_inc(proj.sem, 1)
                    pe.matmul(PS[:, 1, :], wl("g_wk", hp), xb[:, :], start=True, stop=True).then_inc(proj.sem, 1)
                    pe.wait_ge(*ln(2 * u))
                    pe.matmul(PS[:, 2, :], wl("g_wg", hp), xb[:, :], start=True, stop=True).then_inc(proj.sem, 1)
                    for n in range(NC):
                        for head in range(2):
                            p = HALF * (1 - head)
                            mm = pe.matmul(PS[p:p + HALF, 3, CH * n:CH * n + CH], xb[:, CH * n:CH * n + CH],
                                           wl("g_wv", hp)[:, GD * head:GD * head + GD], start=True, stop=True,
                                           skip_group_check=True)
                    mm.then_inc(proj.sem, 1)

                def norms(u, before):
                    pe.wait_ge(*sq(2 * u + 2))
                    pe.wait_ge(*ex(u + 1))
                    pe.matmul(PS[:, 2, :], pair[:, :], sqq[:, :], start=True, stop=True).then_inc(nrm.sem, 1)
                    pe.wait_ge(*vm(2 * u + 2))
                    if before is not None:
                        states_ready(before)
                    pe.matmul(PS[:, 3, :], pair[:, :], sqk[:, :], start=True, stop=True).then_inc(nrm.sem, 1)

                def back(u, k):
                    pe.wait_ge(*cm(u + 1))
                    pe.wait_ge(*st(14 * u))
                    pe.wait_ge(*qk(2 * u + 2))
                    pe.wait_ge(*am(2 * u))
                    pe.wait_ge(*kds(u + 1))
                    pe.wait_ge(*oes(u))
                    pe.matmul(PS[:, 4, :], swap[:, :], cum[:, k, :], start=True, stop=True).then_inc(lm.sem, 1)
                    for n in range(NC):
                        for head in range(2):
                            p, o = HALF * head, HALF * (1 - head)
                            mm = pe.matmul(PS[o:o + HALF, 5, CH * n:CH * n + CH],
                                           kn[p:p + HALF, k, CH * n:CH * n + CH], qn[p:p + HALF, k, CH * n:CH * n + CH],
                                           start=True, stop=True, skip_group_check=True)
                    mm.then_inc(sc.sem, 1)
                    for n in range(NC):
                        for head in range(2):
                            p, o = HALF * head, HALF * (1 - head)
                            mm = pe.matmul(PS[o:o + HALF, 6, CH * n:CH * n + CH],
                                           kd[p:p + HALF, k, CH * n:CH * n + CH], eye[p:p + HALF, :],
                                           start=True, stop=True, skip_group_check=True)
                    mm.then_inc(kt.sem, 1)

                def states_ready(u):
                    pe.wait_ge(*dst(3 * u + 3))
                    pe.wait_ge(*ktm(u + 1))
                    pe.wait_ge(*vm(2 * u + 2))

                def states(u, k):
                    for n in range(NC):
                        for head, v in ((0, le), (1, lo)):
                            p, o = HALF * head, HALF * (1 - head)
                            mm = pe.matmul(PS[p:p + HALF, 4, CH * n:CH * n + CH],
                                           kdt[o:o + HALF, CH * n:CH * n + CH], v[o:o + HALF, k, CH * n:CH * n + CH],
                                           start=True, stop=True, skip_group_check=True)
                    mm.then_inc(kv.sem, 1)
                    pe.wait_ge(*am(2 * u + 2))
                    pe.wait_ge(*qds(2 * u + 2))
                    pe.wait_ge(*st(14 * u + 14))
                    for n in range(NC):
                        for head, left, right in ((0, le, re), (1, lo, ro)):
                            p = HALF * head
                            mm = pe.matmul(PS[p:p + HALF, 6, CH * n:CH * n + CH], left[:, k, CH * n:CH * n + CH],
                                           right[:, k, CH * n:CH * n + CH], start=True, stop=True,
                                           skip_group_check=True)
                    mm.then_inc(om.sem, 1)

                def project(u, hp):
                    pe.wait_ge(*oes(u + 1))
                    if hp == 0:
                        pe.wait_ge(*res(u_batch(u)))
                    pe.matmul(PS[:, 7, :], wl("g_wo", hp), oe[:, :], start=(hp == 0), stop=(hp == HP - 1))\
                        .then_inc(acc.sem, 1)

                with pe.Fori(0, B) as b:
                    u_batch = lambda u: b
                    for hp in range(HP + 1):
                        u = b * HP + hp
                        if hp < HP:
                            front(u, hp)
                        if hp:
                            back(b * HP + (hp - 1), (hp - 1) % 2)
                        w = b * HP + (hp - 1)
                        if hp < HP:
                            norms(u, w if hp else None)
                        else:
                            states_ready(w)
                            project(b * HP + (HP - 2), HP - 2)
                        if hp:
                            states(w, (hp - 1) % 2)
                            if hp != HP - 1:
                                project(w, hp - 1)

            @block.scalar
            def _(act):
                act.preload_act_table_set("natural_log_exp_and_others")
                def early(u, hp):
                    k = hp % 2
                    act.wait_ge(*proj(4 * u + 1))
                    act.activation(sqq[:, :], PS[:, 0, :], ACT.Square).then_inc(sq.sem, 1)
                    act.wait_ge(*proj(4 * u + 2))
                    act.activation(sqk[:, :], PS[:, 1, :], ACT.Square).then_inc(sq.sem, 1)
                    act.wait_ge(*proj(4 * u + 3))
                    act.activation(e1[:, :], PS[:, 2, :], ACT.Exp, scale=-1.0, bias=nbg[:, hp:hp + 1]).then_inc(ex.sem, 1)
                    act.wait_ge(*proj(4 * u + 4))
                    act.activation(lo[0:HALF, k, :], PS[0:HALF, 3, :], ACT.Copy).then_inc(vm.sem, 1)
                    act.activation(le[HALF:128, k, :], PS[HALF:128, 3, :], ACT.Copy).then_inc(vm.sem, 1)

                def late_part(u, k):
                    act.wait_ge(*kt(u + 1))
                    act.activation(kdt[:, :], PS[:, 6, :], ACT.Copy).then_inc(ktm.sem, 1)
                    act.wait_ge(*dms(u + 1))
                    act.activation(dec[:, :], dd[:, :], ACT.Exp, scale=-1.0).then_inc(decs.sem, 1)

                def middle(u):
                    act.wait_ge(*tt(u + 1))
                    act.activation(lga[:, :], t1[:, :], ACT.Ln).then_inc(la.sem, 1)
                    for i, r in enumerate((rq, rk)):
                        act.wait_ge(*nrm(2 * u + i + 1))
                        act.activation(r[:, :], PS[:, 2 + i, :], ACT.Ln, scale=65536.0).then_inc(ln.sem, 1)
                    for i, r in enumerate((rq, rk)):
                        act.wait_ge(*ln(2 * u + i + 1))
                        act.activation(r[:, :], r[:, :], ACT.Exp, scale=-0.5, bias=ln256[:, :]).then_inc(rr.sem, 1)

                def outs(u):
                    act.wait_ge(*om(u + 1))
                    act.activation(oe[:, :], PS[:, 6, :], ACT.Copy).then_inc(oes.sem, 1)

                def decays(u, k):
                    act.wait_ge(*cm(u + 1))
                    act.activation(eq[:, k, :], cum[:, k, :], ACT.Exp, scale=-1.0).then_inc(eqs.sem, 1)
                    act.wait_ge(*tes(u + 1))
                    act.activation(de[:, :], te[:, :], ACT.Exp).then_inc(des.sem, 1)

                with act.Fori(0, B) as b:
                    for hp in range(HP + 1):
                        u, w = b * HP + hp, b * HP + (hp - 1)
                        if hp == 0:
                            act.wait_ge(*proj(b * 4 * HP))
                            act.activation(xb[:, :], z[:, bass.ds(b, 1), :].rearrange("p a t -> p (a t)"), ACT.Copy)\
                                .then_inc(xbs.sem, 1)
                        if hp < HP:
                            early(u, hp)
                        if hp:
                            late_part(w, (hp - 1) % 2)
                        if hp < HP:
                            middle(u)
                        if hp:
                            outs(w)
                        if hp < HP:
                            decays(u, hp % 2)

            @block.vector
            def _(dve):
                def pair_log(u):
                    dve.wait_ge(*lm(u + 1))
                    dve.tensor_tensor(chunks(dd[:, :]), chunks(PS[:, 4, :]),
                                      eye[:, :].unsqueeze(1).to_broadcast([128, NC, CH]), ALU.mult).then_inc(dst.sem, 1)
                    dve.wait_ge(*dst(3 * u + 1))
                    dve.tensor_reduce(dg[:, :], chunks(dd[:, :]), AX.X, ALU.add).then_inc(dst.sem, 1)
                    dve.wait_ge(*dst(3 * u + 2))
                    dve.tensor_tensor(chunks(dd[:, :]), chunks(PS[:, 4, :]),
                                      dg[:, :].unsqueeze(2).to_broadcast([128, NC, CH]), ALU.subtract)\
                        .then_inc(dst.sem, 1)

                def plus(u):
                    dve.wait_ge(*ex(u + 1))
                    dve.tensor_scalar(t1[:, :], e1[:, :], 1.0, 1e6, ALU.add, ALU.min).then_inc(tt.sem, 1)

                def weigh(u, k):
                    dve.wait_ge(*sc(u + 1))
                    dve.wait_ge(*decs(u + 1))
                    dve.tensor_tensor(ro[0:HALF, k, :], PS[0:HALF, 5, :], dec[0:HALF, :], ALU.mult).then_inc(am.sem, 1)
                    dve.tensor_tensor(re[HALF:128, k, :], PS[HALF:128, 5, :], dec[HALF:128, :], ALU.mult)\
                        .then_inc(am.sem, 1)

                def cumulate(u, k):
                    dve.wait_ge(*la(u + 1))
                    dve.tensor_tensor_scan(cum[:, k, :], reset[:, :], lga[:, :], 0.0, ALU.mult, ALU.add)\
                        .then_inc(cm.sem, 1)

                def chain(u, k):
                    dve.wait_ge(*kv(u + 1))
                    for n in range(NC - 1):
                        if n:
                            dve.wait_ge(*st(14 * u + 2 * n))
                        for p, s in ((0, le), (HALF, lo)):
                            dve.scalar_tensor_tensor(out=s[p:p + HALF, k, CH * n + CH:CH * n + 2 * CH],
                                                     in0=s[p:p + HALF, k, CH * n:CH * n + CH],
                                                     scalar=eq[p:p + HALF, k, CH * n + CH - 1:CH * n + CH],
                                                     in1=PS[p:p + HALF, 4, CH * n:CH * n + CH],
                                                     op0=ALU.mult, op1=ALU.add).then_inc(st.sem, 1)

                def normalise(u, k):
                    for i, (r, to) in enumerate(((rq, qn), (rk, kn))):
                        dve.wait_ge(*rr(2 * u + i + 1))
                        dve.scalar_tensor_tensor(out=to[:, k, :], in0=r[:, :], scalar=1e12, in1=PS[:, i, :],
                                                 op0=ALU.min, op1=ALU.mult).then_inc(qk.sem, 1)

                with dve.Fori(0, B) as b:
                    for hp in range(HP + 1):
                        u, w = b * HP + hp, b * HP + (hp - 1)
                        if hp:
                            pair_log(w)
                        if hp < HP:
                            plus(u)
                        if hp:
                            weigh(w, (hp - 1) % 2)
                        if hp < HP:
                            cumulate(u, hp % 2)
                        if hp:
                            chain(w, (hp - 1) % 2)
                        if hp < HP:
                            normalise(u, hp % 2)
                    dve.wait_ge(*acc(b * HP + HP))
                    zb = z[:, bass.ds(b, 1), :].rearrange("p a t -> p (a t)")
                    dve.tensor_tensor(zb, c.y[:, bass.ds(b, 1), :].rearrange("p a t -> p (a t)"), PS[:, 7, :], ALU.add)\
                        .then_inc(res.sem, 1)

            @block.gpsimd
            def _(pool):
                def mask(u):
                    pool.wait_ge(*dst(3 * u + 3))
                    pool.tensor_tensor(chunks(dd[:, :]), chunks(dd[:, :]),
                                       late[:, :].unsqueeze(1).to_broadcast([128, NC, CH]), ALU.add).then_inc(dms.sem, 1)

                def to_end(u, k):
                    pool.wait_ge(*cm(u + 1))
                    pool.tensor_tensor(chunks(te[:, :]), chunks(cum[:, k, :]),
                                       chunks(cum[:, k, :])[:, :, CH - 1:CH].to_broadcast([128, NC, CH]), ALU.subtract)\
                        .then_inc(tes.sem, 1)

                def decayed(u, k):
                    pool.wait_ge(*qk(2 * u + 2))
                    pool.wait_ge(*eqs(u + 1))
                    pool.wait_ge(*tes(u + 1))
                    pool.tensor_tensor(re[0:HALF, k, :], qn[0:HALF, k, :], eq[0:HALF, k, :], ALU.mult)\
                        .then_inc(qds.sem, 1)
                    pool.wait_ge(*qds(2 * u + 1))
                    pool.tensor_tensor(ro[HALF:128, k, :], qn[HALF:128, k, :], eq[HALF:128, k, :], ALU.mult)\
                        .then_inc(qds.sem, 1)
                    pool.wait_ge(*qds(2 * u + 2))
                    pool.wait_ge(*des(u + 1))
                    pool.tensor_tensor(kd[:, k, :], kn[:, k, :], de[:, :], ALU.mult).then_inc(kds.sem, 1)

                with pool.Fori(0, B) as b:
                    for hp in range(HP + 1):
                        u, w = b * HP + hp, b * HP + (hp - 1)
                        if hp:
                            mask(w)
                        if hp < HP:
                            to_end(u, hp % 2)
                            decayed(u, hp % 2)
        U = B * HP
        for s, n in ((proj, 4 * U), (sq, 2 * U), (ex, U), (vm, 2 * U), (nrm, 2 * U), (ln, 2 * U), (rr, 2 * U), (tt, U),
                     (la, U), (cm, U), (eqs, U), (tes, U), (des, U), (qk, 2 * U), (kds, U), (qds, 2 * U), (lm, U),
                     (sc, U), (kt, U), (dst, 3 * U), (dms, U), (decs, U), (ktm, U), (kv, U), (am, 2 * U), (st, 14 * U),
                     (om, U), (oes, U), (acc, U), (res, B), (xbs, B)):
            s.close(n)

        hidden, bent, down, added = (c.semaphore_for(n) for n in ("f_hidden", "f_gelu", "f_down", "x_added"))
        M = FFN // 128
        ctx = ExitStack()
        with ctx:
            hb = c.sb("f_hb", [128, 4, T], F32, ctx)
            block = ctx.enter_context(nc.Block())

            def mlp_down(pe, k):
                b, m = k // M, k % M
                at = W_L1["f_w2"][0] + 128 * m
                pe.wait_ge(*bent(k + 1))
                pe.matmul(PS[:, 4 + b, :], c.w1[:, at:at + 128], hb[:, m, :], start=(m == 0), stop=(m == M - 1),
                          skip_group_check=True).then_inc(down.sem, 1)

            @block.tensor
            def _(pe):
                norm_pe(c, pe, z)
                for k in range(B * M):
                    b, m = k // M, k % M
                    pe.wait_ge(*scaled(b + 1))
                    if k == 0:
                        pe.wait_ge(*scaled(B))
                    if k >= 4:
                        pe.wait_ge(*bent(k - 3))
                    pe.matmul(PS[:, m, :], c.w1[:, W_L1["f_w1"][0] + 128 * m:W_L1["f_w1"][0] + 128 * m + 128],
                              c.y[:, b, :], start=True, stop=True).then_inc(hidden.sem, 1)
                    if k:
                        mlp_down(pe, k - 1)
                mlp_down(pe, B * M - 1)

            @block.scalar
            def _(act):
                act.preload_act_table_set("natural_log_exp_and_others")
                norm_act(c, act)
                for k in range(B * M):
                    act.wait_ge(*hidden(k + 1))
                    if k >= 4:
                        act.wait_ge(*down(k - 3))
                    act.activation(hb[:, k % M, :], PS[:, k % M, :], ACT.Gelu, bias=c.v("b1", k % M)).then_inc(bent.sem, 1)

            @block.vector
            def _(dve):
                norm_dve(c, dve, c.y, 0, c.v("ln2_w"), c.v("ln2_b"))
                for b in range(B):
                    dve.tensor_tensor(c.x[:, b, :], c.x[:, b, :], z[:, b, :], ALU.add).then_inc(added.sem, 1)
                for b in range(B):
                    dve.wait_ge(*down(M * (b + 1)))
                    dve.wait_ge(*added(b + 1))
                    dve.scalar_tensor_tensor(out=c.x[:, b, :], in0=PS[:, 4 + b, :], scalar=c.v("b2"), in1=c.x[:, b, :],
                                             op0=ALU.add, op1=ALU.add).then_inc(added.sem, 1)
                dve.wait_ge(*added(2 * B))
        norm_close(c, 1, 1)
        for s, n in ((hidden, B * M), (bent, B * M), (down, B * M), (added, 2 * B)):
            s.close(n)


def stage_context_mix(c, ins, scratch):
    nc, PS = c.nc, c.PS
    NT = B * TT
    came, normed, added = c.semaphore_for("w_came"), c.semaphore_for("ln_normed"), c.semaphore_for("x_added")
    rhs, side, sim, mxs, sub, exped, red = (c.semaphore_for("b_" + n) for n in (
        "weighted_ctx", "side", "similar", "max", "shifted", "exp", "reduced"))
    turned, moved, hats, hat, mixed = (c.semaphore_for("b_" + n) for n in ("turned", "moved", "hat_raw", "hat", "mixed"))
    peak, peaks = c.semaphore_for("b_peak"), c.semaphore_for("b_peak_steps")
    ctx = ExitStack()
    with ctx:
        cx = c.sb("b_ctx", [128, B, CT], F32, ctx)
        ck = c.sb("b_ctx_tok", [CT, B, D], F32, ctx)
        cr = c.sb("b_cr", [128, B, CT], F32, ctx)
        srow = c.sb("b_srow", [1, B, CT], F32, ctx)
        a = c.sb("b_a", [128, NT, CT], F32, ctx)
        mx = c.sb("b_mx", [128, NT], F32, ctx)
        rs = c.sb("b_rs", [128, 4, NT], F32, ctx)
        at = c.sb("b_at", [CT, B, T], F32, ctx)
        hq = c.sb("b_hq", [128, B, T], F32, ctx)
        eh = c.sb("b_eh", [128, B, T], F32, ctx)
        et = c.sb("b_et", [128, NT, D], F32, ctx)
        mt = c.sb("b_mt", [NT, 128], F32, ctx)
        mt1 = c.sb("b_mt1", [NT, 1], F32, ctx)
        m1 = c.sb("b_m1", [1, 2, NT], F32, ctx)
        hc = c.sb("b_hc", [128, B], F32, ctx)
        block = ctx.enter_context(nc.Block())
        SUMW = 4 * CT

        def per_batch(t):
            return t.rearrange("p (b k) -> p b k", b=B)

        @block.sync
        def _(sp):
            sp.dma_start(cx[:, :, :], ins["ctx"]).then_inc(came.sem, 16)
            sp.dma_start(ck[:, :, :], ins["ctx_tok"]).then_inc(came.sem, 16)

        @block.tensor
        def _(pe):
            pe.wait_ge(*came(32))
            pe.matmul(PS[0:1, 7, 0:B * CT], c.v("w2"), cx[:, :, :].rearrange("p b t -> p (b t)"), start=True, stop=True)\
                .then_inc(side.sem, 1)
            pe.wait_ge(*side(2))
            norm_pe(c, pe, c.x)
            pe.wait_ge(*normed(B))
            pe.wait_ge(*rhs(1))
            for b in range(B):
                for k in range(TT):
                    pe.matmul(PS[:, b, CT * k:CT * k + CT], c.y[:, b, 128 * k:128 * k + 128], cr[:, b, :],
                              start=True, stop=False)
                    mm = pe.matmul(PS[:, b, CT * k:CT * k + CT], c.ones[0:1, :], srow[:, b, :], start=False, stop=True)
                mm.then_inc(sim.sem, 1)
            for b in range(B):
                pe.wait_ge(*red(3 + b + 1))
                for k in range(TT):
                    mm = pe.transpose(PS[0:CT, 4 + b, 128 * k:128 * k + 128], a[:, TT * b + k, :], c.ident[:, :])
                mm.then_inc(turned.sem, 1)
            for b in range(B):
                pe.wait_ge(*moved(b + 1))
                pe.matmul(PS[:, b, :], ck[:, b, :], at[:, b, :], start=True, stop=True).then_inc(hats.sem, 1)
            for b in range(B):
                for k in range(TT):
                    mm = pe.transpose(PS[:, 4 + b, 128 * k:128 * k + 128], c.y[:, b, 128 * k:128 * k + 128], c.ident[:, :])
                mm.then_inc(turned.sem, 1)
            pe.wait_ge(*hat(1))
            pe.transpose(PS[0:NT, 0, 0:128], mx[:, :], c.ident[:, :]).then_inc(peak.sem, 1)
            pe.wait_ge(*peaks(1))
            pe.transpose(PS[0:1, 0, 128:128 + NT], mt1[:, :], c.ident[0:NT, 0:NT]).then_inc(peak.sem, 1)
            pe.wait_ge(*peaks(3))
            pe.matmul(PS[:, 0, 160:160 + NT], c.ones[0:1, :], m1[0:1, 1, :], start=True, stop=True).then_inc(peak.sem, 1)
            pe.wait_ge(*peaks(5))
            pe.matmul(PS[:, 0, 192:192 + NT], c.ones[:, :], rs[:, 2, :], start=True, stop=True).then_inc(peak.sem, 1)
            pe.wait_ge(*peaks(8))
            pe.wait_ge(*moved(2 * B))
            for b in range(B):
                for k in range(TT):
                    i = TT * b + k
                    mm = pe.matmul(PS[:, 0, 224 + b:225 + b], et[:, i, :], rs[:, 2, i:i + 1], start=(k == 0),
                                   stop=(k == TT - 1))
            mm.then_inc(peak.sem, 1)
            W = W_L1["w_qv"][0]
            for b in range(B):
                pe.wait_ge(*hat(2 * B + b + 1))
                for part, src in enumerate((c.y, hq, eh, c.sq)):
                    mm = pe.matmul(PS[:, 4 + b, :], c.w1[:, W + D * part:W + D * part + D], src[:, b, :],
                                   start=(part == 0), stop=(part == 3))
                mm.then_inc(mixed.sem, 1)

        @block.scalar
        def _(act):
            act.preload_act_table_set("natural_log_exp_and_others")
            norm_act(c, act)
            act.wait_ge(*sub(1))
            act.activation(a[:, :, :], a[:, :, :], ACT.Exp).then_inc(exped.sem, 1)
            for b in range(B):
                act.wait_ge(*turned(b + 1))
                act.activation(at[:, b, :], PS[0:CT, 4 + b, :], ACT.Copy).then_inc(moved.sem, 1)
            for b in range(B):
                act.wait_ge(*turned(B + b + 1))
                act.activation(et[:, TT * b:TT * b + TT, :], PS[:, 4 + b, :].rearrange("p (k d) -> p k d", k=TT), ACT.Copy)\
                    .then_inc(moved.sem, 1)
            act.wait_ge(*peaks(4))
            act.activation(rs[:, 2, :], rs[:, 2, :], ACT.Exp).then_inc(peaks.sem, 1)

        @block.vector
        def _(dve):
            dve.wait_ge(*came(32))
            dve.wait_ge(*side(1))
            bs = ROW["b_sim"][0]
            dve.tensor_scalar(srow[:, :, :], PS[0:1, 7, 0:B * CT].rearrange("p (b t) -> p b t", b=B),
                              c.rows[0:1, bs:bs + 1], None, ALU.add).then_inc(side.sem, 1)
            dve.tensor_scalar(cr[:, :, :], cx[:, :, :], c.v("w3"), c.v("w1"), ALU.mult, ALU.add).then_inc(rhs.sem, 1)
            norm_dve(c, dve, c.y)
            dve.wait_ge(*sim(B))
            sims = PS[:, 0:B, 0:SUMW].rearrange("p b (k t) -> p b k t", k=TT)
            dve.tensor_reduce(per_batch(mx[:, :]), sims, AX.X, ALU.max).then_inc(mxs.sem, 1)
            dve.wait_ge(*mxs(1))
            dve.tensor_tensor(a[:, :, :].rearrange("p (b k) t -> p b k t", b=B), sims,
                              per_batch(mx[:, :]).unsqueeze(3).to_broadcast([128, B, TT, CT]), ALU.subtract)\
                .then_inc(sub.sem, 1)
            dve.wait_ge(*exped(1))
            dve.tensor_reduce(rs[:, 0, :], a[:, :, :], AX.X, ALU.add).then_inc(red.sem, 1)
            dve.wait_ge(*red(1))
            dve.reciprocal(rs[:, 1, :], rs[:, 0, :]).then_inc(red.sem, 1)
            dve.wait_ge(*red(2))
            dve.tensor_copy(rs[:, 3, :], rs[:, 1, :]).then_inc(red.sem, 1)
            for b in range(B):
                dve.tensor_tensor(a[:, TT * b:TT * b + TT, :], a[:, TT * b:TT * b + TT, :],
                                  rs[:, 1, TT * b:TT * b + TT].unsqueeze(2).to_broadcast([128, TT, CT]), ALU.mult)\
                    .then_inc(red.sem, 1)
            for b in range(B):
                dve.wait_ge(*hats(b + 1))
                dve.tensor_copy(hq[:, b, :], PS[:, b, :]).then_inc(hat.sem, 1)
            dve.wait_ge(*peak(1))
            dve.tensor_reduce(mt1[:, :], PS[0:NT, 0, 0:128], AX.X, ALU.max).then_inc(peaks.sem, 1)
            dve.wait_ge(*peak(2))
            dve.tensor_reduce(m1[0:1, 0, 0:B], per_batch(PS[0:1, 0, 128:128 + NT]), AX.X, ALU.max).then_inc(peaks.sem, 1)
            dve.wait_ge(*peaks(2))
            dve.tensor_copy(per_batch(m1[0:1, 1, :]), m1[0:1, 0, 0:B].unsqueeze(2).to_broadcast([1, B, TT]))\
                .then_inc(peaks.sem, 1)
            dve.wait_ge(*peak(3))
            dve.tensor_tensor(rs[:, 2, :], mx[:, :], PS[:, 0, 160:160 + NT], ALU.subtract).then_inc(peaks.sem, 1)
            dve.wait_ge(*peak(4))
            dve.tensor_reduce(rs[:, 0, 0:B], per_batch(PS[:, 0, 192:192 + NT]), AX.X, ALU.add).then_inc(peaks.sem, 1)
            dve.wait_ge(*peaks(6))
            dve.reciprocal(rs[:, 0, 0:B], rs[:, 0, 0:B]).then_inc(peaks.sem, 1)
            dve.wait_ge(*peaks(7))
            dve.tensor_tensor(per_batch(rs[:, 2, :]), per_batch(rs[:, 2, :]),
                              rs[:, 0, 0:B].unsqueeze(2).to_broadcast([128, B, TT]), ALU.mult).then_inc(peaks.sem, 1)
            for b in range(B):
                dve.wait_ge(*hat(b + 1))
                dve.tensor_tensor(eh[:, b, :], c.y[:, b, :], hq[:, b, :], ALU.mult).then_inc(hat.sem, 1)
            dve.wait_ge(*peak(5))
            dve.tensor_copy(hc[:, :], PS[:, 0, 224:224 + B]).then_inc(peaks.sem, 1)
            dve.wait_ge(*peaks(9))
            for b in range(B):
                dve.tensor_scalar(c.sq[:, b, :], c.y[:, b, :], hc[:, b:b + 1], None, ALU.mult).then_inc(hat.sem, 1)
            for b in range(B):
                dve.wait_ge(*mixed(b + 1))
                dve.scalar_tensor_tensor(out=c.x[:, b, :], in0=PS[:, 4 + b, :], scalar=c.v("b_qv"), in1=c.x[:, b, :],
                                         op0=ALU.add, op1=ALU.add).then_inc(added.sem, 1)
            dve.wait_ge(*added(B))
    norm_close(c)
    for s, n in ((came, 32), (rhs, 1), (side, 2), (sim, B), (mxs, 1), (sub, 1), (exped, 1), (red, 3 + B), (turned, 2 * B),
                 (moved, 2 * B), (hats, B), (hat, 3 * B), (mixed, B), (peak, 5), (peaks, 9), (added, B)):
        s.close(n)


def stage_encoders(c, ins, scratch):
    nc, PS = c.nc, c.PS
    normed, made, added = c.semaphore_for("ln_normed"), c.semaphore_for("const_made"), c.semaphore_for("x_added")
    logit, pick, pexp, wide = (c.semaphore_for("e_" + n) for n in ("logits", "pick", "gate_exp", "gate_wide"))
    number = c.semaphore_for("e_number_stored")
    outer = ExitStack()
    with outer:
        wp = c.sb("e_wp", [128, PAIRS], F32, outer)
        num_i = c.sb("e_num", [1, PAIRS], I32, outer)
        values = c.sb("e_values", [128, PAIRS, TT, H, 9], F32, outer)
        ctx = ExitStack()
        with ctx:
            mean = c.sb("e_mean", [128, B], F32, ctx)
            lg = c.sb("e_lg", [1, B, EX], F32, ctx)
            gp = c.sb("e_gp", [1, B, EX], F32, ctx)
            cmp = c.sb("e_cmp", [1, B, EX, EX], F32, ctx)
            eq = c.sb("e_eq", [1, B, EX, EX], F32, ctx)
            low = c.sb("e_low", [1, EX, EX], F32, ctx)
            iot = c.sb("e_iota", [1, B, EX], F32, ctx)
            sel = c.sb("e_sel", [1, B, EX], F32, ctx)
            t4 = c.sb("e_t4", [1, B, EX], F32, ctx)
            sm = c.sb("e_sm", [1, 4, B], F32, ctx)
            nf = c.sb("e_nf", [1, B, PICK], F32, ctx)
            wf = c.sb("e_wf", [1, B, PICK], F32, ctx)
            block = ctx.enter_context(nc.Block())

            @block.gpsimd
            def _(pool):
                pool.memset(low[:, :, :], 1.0).then_inc(made.sem, 1)
                for e in range(EX):
                    pool.memset(iot[:, :, e:e + 1], float(e)).then_inc(made.sem, 1)
                pool.memset(values[:, :, :, :, 8:9], 1.0).then_inc(made.sem, 1)
                pool.wait_ge(*made(2 + EX))
                pool.affine_select(out=low[:, :, :], in_=low[:, :, :], compare_op=ALU.is_ge, fill=0.0, base=-1,
                                   pattern=[[1, EX], [-1, EX]], channel_multiplier=0).then_inc(made.sem, 1)
                pool.wait_ge(*made(3 + EX))

            @block.tensor
            def _(pe):
                norm_pe(c, pe, c.x)
                pe.wait_ge(*pick(B))
                gw = W_L1["gate_w"][0]
                for b in range(B):
                    mm = pe.matmul(PS[0:1, 0, EX * b:EX * b + EX], mean[:, b:b + 1], c.w1[:, gw:gw + EX],
                                   start=True, stop=True)
                mm.then_inc(logit.sem, 1)
                pe.wait_ge(*wide(1))
                pe.matmul(PS[:, 1, 0:PAIRS], c.ones[0:1, :], wf[:, :, :].rearrange("p b k -> p (b k)"), start=True,
                          stop=True).then_inc(logit.sem, 1)

            @block.scalar
            def _(act):
                act.preload_act_table_set("natural_log_exp_and_others")
                norm_act(c, act)
                act.wait_ge(*pick(B + 3))
                act.activation(gp[:, :, :], gp[:, :, :], ACT.Exp).then_inc(pexp.sem, 1)

            @block.vector
            def _(dve):
                norm_dve(c, dve, c.y)
                for b in range(B):
                    dve.wait_ge(*normed(b + 1))
                    dve.tensor_reduce(mean[:, b:b + 1], c.y[:, b, :], AX.X, ALU.add).then_inc(pick.sem, 1)
                dve.wait_ge(*logit(1))
                dve.wait_ge(*made(3 + EX))
                gb = ROW["gate_b"][0]
                dve.scalar_tensor_tensor(out=lg[:, :, :], in0=PS[0:1, 0, 0:B * EX].rearrange("p (b e) -> p b e", e=EX),
                                         scalar=1.0 / T, in1=c.rows[0:1, gb:gb + EX].unsqueeze(1).to_broadcast([1, B, EX]),
                                         op0=ALU.mult, op1=ALU.add).then_inc(pick.sem, 1)
                dve.wait_ge(*pick(B + 1))
                dve.tensor_reduce(sm[:, 0, :], lg[:, :, :], AX.X, ALU.max).then_inc(pick.sem, 1)
                dve.wait_ge(*pick(B + 2))
                dve.tensor_tensor(gp[:, :, :], lg[:, :, :], sm[:, 0, :].unsqueeze(2).to_broadcast([1, B, EX]),
                                  ALU.subtract).then_inc(pick.sem, 1)
                other = lg[:, :, :].unsqueeze(2).to_broadcast([1, B, EX, EX])
                own = lg[:, :, :].unsqueeze(3).to_broadcast([1, B, EX, EX])
                dve.tensor_tensor(cmp[:, :, :, :], other, own, ALU.is_gt).then_inc(pick.sem, 1)
                dve.tensor_tensor(eq[:, :, :, :], other, own, ALU.is_equal).then_inc(pick.sem, 1)
                dve.wait_ge(*pick(B + 5))
                dve.tensor_tensor(eq[:, :, :, :], eq[:, :, :, :], low[:, :, :].unsqueeze(1).to_broadcast([1, B, EX, EX]),
                                  ALU.mult).then_inc(pick.sem, 1)
                dve.wait_ge(*pick(B + 6))
                dve.tensor_tensor(cmp[:, :, :, :], cmp[:, :, :, :], eq[:, :, :, :], ALU.add).then_inc(pick.sem, 1)
                dve.wait_ge(*pick(B + 7))
                dve.tensor_reduce(t4[:, :, :], cmp[:, :, :, :], AX.X, ALU.add).then_inc(pick.sem, 1)
                dve.wait_ge(*pick(B + 8))
                dve.tensor_scalar(sel[:, :, :], t4[:, :, :], PICK - 0.5, None, ALU.is_lt).then_inc(pick.sem, 1)
                dve.wait_ge(*pick(B + 9))
                dve.tensor_tensor(t4[:, :, :], sel[:, :, :], iot[:, :, :], ALU.mult).then_inc(pick.sem, 1)
                dve.wait_ge(*pick(B + 10))
                dve.tensor_reduce(nf[:, :, 1], t4[:, :, :], AX.X, ALU.max).then_inc(pick.sem, 1)
                dve.wait_ge(*pick(B + 11))
                dve.tensor_scalar(t4[:, :, :], iot[:, :, :], -1.0, float(EX), ALU.mult, ALU.add).then_inc(pick.sem, 1)
                dve.wait_ge(*pick(B + 12))
                dve.tensor_tensor(t4[:, :, :], t4[:, :, :], sel[:, :, :], ALU.mult).then_inc(pick.sem, 1)
                dve.wait_ge(*pick(B + 13))
                dve.tensor_reduce(nf[:, :, 0], t4[:, :, :], AX.X, ALU.max).then_inc(pick.sem, 1)
                dve.wait_ge(*pick(B + 14))
                dve.tensor_scalar(nf[:, :, 0], nf[:, :, 0], -1.0, float(EX), ALU.mult, ALU.add).then_inc(pick.sem, 1)
                dve.wait_ge(*pick(B + 15))
                dve.tensor_copy(num_i[:, :], nf[:, :, :].rearrange("p b k -> p (b k)")).then_inc(pick.sem, 1)
                dve.wait_ge(*pexp(1))
                dve.tensor_reduce(sm[:, 1, :], gp[:, :, :], AX.X, ALU.add).then_inc(pick.sem, 1)
                dve.wait_ge(*pick(B + 17))
                dve.reciprocal(sm[:, 2, :], sm[:, 1, :]).then_inc(pick.sem, 1)
                dve.wait_ge(*pick(B + 18))
                dve.tensor_tensor(gp[:, :, :], gp[:, :, :], sm[:, 2, :].unsqueeze(2).to_broadcast([1, B, EX]), ALU.mult)\
                    .then_inc(pick.sem, 1)
                dve.wait_ge(*pick(B + 19))
                for k in range(PICK):
                    dve.tensor_tensor(t4[:, :, :], iot[:, :, :], nf[:, :, k:k + 1].to_broadcast([1, B, EX]), ALU.is_equal)\
                        .then_inc(pick.sem, 1)
                    dve.wait_ge(*pick(B + 20 + 3 * k))
                    dve.tensor_tensor(t4[:, :, :], t4[:, :, :], gp[:, :, :], ALU.mult).then_inc(pick.sem, 1)
                    dve.wait_ge(*pick(B + 21 + 3 * k))
                    dve.tensor_reduce(wf[:, :, k], t4[:, :, :], AX.X, ALU.add).then_inc(pick.sem, 1)
                    dve.wait_ge(*pick(B + 22 + 3 * k))
                dve.nop().then_inc(wide.sem, 1)
                dve.wait_ge(*logit(2))
                dve.tensor_copy(wp[:, :], PS[:, 1, 0:PAIRS]).then_inc(wide.sem, 1)
                dve.wait_ge(*wide(2))
        norm_close(c)
        for s, n in ((logit, 2), (pick, B + 25), (pexp, 1), (wide, 2), (made, 3 + EX)):
            s.close(n)

        slot_came = [c.semaphore_for("e_slot_even"), c.semaphore_for("e_slot_odd")]
        stored = [c.semaphore_for("s_stored_q"), c.semaphore_for("s_stored_k")]
        proj, bias, hi, rest, mid, last, vals = (c.semaphore_for(n) for n in (
            "e_proj", "e_biased", "s_high", "s_rest", "s_middle", "s_last", "at_values"))
        NV = W_EX["bq"][0]
        NQ = 3 * D
        ctx = ExitStack()
        with ctx:
            ws = c.sb("e_ws", [128, 2, NQ], F32, ctx)
            bs = c.sb("e_bs", [128, 2, 2], F32, ctx)
            bv = c.sb("e_bv", [128, 2, D], F32, ctx)
            qkf = c.sb("e_qkf", [128, 2, T], F32, ctx)
            res = c.sb("e_res", [128, 2, T], F32, ctx)
            parts = c.sb("e_parts", [128, 2, PARTS, T], BF16, ctx)
            block = ctx.enter_context(nc.Block())

            @block.sync
            def _(sp):
                def load(n):
                    if n >= 2:
                        sp.wait_ge(*bias(2 * n - 2))
                        sp.wait_ge(*vals(n - 1))
                    e = sp.value_load(num_i[0:1, n:n + 1], min_val=0, max_val=EX - 1)
                    src = ins["w_ex"][bass.ds(e, 1), :, :].rearrange("a p n -> (a p) n")
                    sp.dma_start(ws[:, n % 2, :], src[:, 0:NQ]).then_inc(slot_came[n % 2].sem, 16)
                    sp.dma_start(bs[:, n % 2, :], src[:, NV:NV + 2]).then_inc(slot_came[n % 2].sem, 16)
                    sp.dma_start(bv[:, n % 2, :], ins["bv_ex"][bass.ds(e, 1), :].to_broadcast([128, D]))\
                        .then_inc(slot_came[n % 2].sem, 16)

                load(0)
                for n in range(PAIRS):
                    if n + 1 < PAIRS:
                        load(n + 1)
                    for k, dest in enumerate((scratch["q_parts"], scratch["k_parts"])):
                        sp.wait_ge(*last(2 * n + k + 1))
                        sp.dma_start(dram_view(dest, n * PARTS * D * T, [(T, 128), (D * T, PARTS), (1, T)]),
                                     parts[:, k, :, :]).then_inc(stored[k].sem, 16)
                for s in stored:
                    sp.wait_ge(*s(16 * PAIRS))

            @block.tensor
            def _(pe):
                for n in range(PAIRS):
                    o = 3 * (n % 2)
                    pe.wait_ge(*slot_came[n % 2](48 * (n // 2 + 1)))
                    if n >= 2:
                        pe.wait_ge(*bias(2 * n - 2))
                        pe.wait_ge(*vals(n - 1))
                    yb = c.y[:, n // PICK, :]
                    pe.matmul(PS[:, o, :], ws[:, n % 2, 0:D], yb, start=True, stop=True).then_inc(proj.sem, 1)
                    pe.matmul(PS[:, o + 1, :], ws[:, n % 2, D:2 * D], yb, start=True, stop=True).then_inc(proj.sem, 1)
                    for kt in range(TT):
                        mm = pe.matmul(PS[:, o + 2, 128 * kt:128 * kt + 128], yb[:, 128 * kt:128 * kt + 128],
                                       ws[:, n % 2, 2 * D:3 * D], start=True, stop=True)
                    mm.then_inc(proj.sem, 1)

            @block.scalar
            def _(act):
                for u in range(2 * PAIRS):
                    act.wait_ge(*bias(u + 1))
                    if u >= 2:
                        act.wait_ge(*stored[u % 2](16 * (u // 2)))
                    act.activation(parts[:, u % 2, 0, :], qkf[:, u % 2, :], ACT.Copy).then_inc(hi.sem, 1)
                    act.wait_ge(*rest(u + 1))
                    act.activation(parts[:, u % 2, 1, :], res[:, u % 2, :], ACT.Copy).then_inc(mid.sem, 1)

            @block.vector
            def _(dve):
                for n in range(PAIRS):
                    o = 3 * (n % 2)
                    for k in range(2):
                        u = 2 * n + k
                        dve.wait_ge(*proj(3 * n + k + 1))
                        dve.tensor_scalar(qkf[:, k, :], PS[:, o + k, :], bs[:, n % 2, k:k + 1],
                                          float(HD) ** -0.5 if k == 0 else 1.0, ALU.add, ALU.mult).then_inc(bias.sem, 1)
                    dve.wait_ge(*proj(3 * n + 3))
                    dve.tensor_tensor(values[:, n, :, :, 0:8], PS[:, o + 2, :].rearrange("p (k h d) -> p k h d", k=TT, d=HD),
                                      bv[:, n % 2, :].rearrange("p (h d) -> p h d", d=HD).unsqueeze(1)
                                      .to_broadcast([128, TT, H, HD]), ALU.add).then_inc(vals.sem, 1)
                    for k in range(2):
                        u = 2 * n + k
                        dve.wait_ge(*hi(u + 1))
                        dve.tensor_tensor(res[:, k, :], qkf[:, k, :], parts[:, k, 0, :], ALU.subtract).then_inc(rest.sem, 1)
                        dve.wait_ge(*mid(u + 1))
                        dve.tensor_tensor(parts[:, k, 2, :], res[:, k, :], parts[:, k, 1, :], ALU.subtract)\
                            .then_inc(last.sem, 1)

        P2 = PAIRS // 2
        for s, n in ((slot_came[0], 48 * P2), (slot_came[1], 48 * P2), (proj, 3 * PAIRS), (bias, 2 * PAIRS),
                     (hi, 2 * PAIRS), (rest, 2 * PAIRS), (mid, 2 * PAIRS), (last, 2 * PAIRS), (vals, PAIRS),
                     (stored[0], 16 * PAIRS), (stored[1], 16 * PAIRS)):
            s.close(n)

        attention_core(c, PAIRS, False, scratch["q_parts"], scratch["k_parts"], scratch["max_rows"],
                       scratch["sums"], values)

        SLOTS = 2 * PICK
        came = [c.semaphore_for(f"e_layer{k}") for k in range(SLOTS)]
        prod = [c.semaphore_for(f"e_products{k}") for k in range(PICK)]
        curve = [c.semaphore_for(f"e_curves{k}") for k in range(PICK)]
        vec = [c.semaphore_for(f"e_sums{k}") for k in range(PICK)]
        NP, NA, NVS = 13, 10, 9
        NR = N_WX - 3 * D
        M = FFN // 128
        ctx = ExitStack()
        with ctx:
            wl = c.sb("e_wl", [128, SLOTS, NR], F32, ctx)
            num = c.sb("e_o_num", [128, SLOTS, T], F32, ctx)
            den = c.sb("e_o_den", [128, SLOTS, T], F32, ctx)
            t1 = c.sb("e_t1", [128, PICK, T], F32, ctx)
            sq = c.sb("e_sq", [128, PICK, T], F32, ctx)
            x1 = c.sb("e_x1", [128, PICK, T], F32, ctx)
            hb = c.sb("e_hb", [128, PICK, M, T], F32, ctx)
            block = ctx.enter_context(nc.Block())

            def at(name, slot, k=0, n=128):
                a = W_EX[name][0] - 3 * D + k
                return wl[:, slot, a:a + n]

            def batches(e, emit):
                with e.Fori(0, B // 2) as j:
                    for half in range(2):
                        emit(2 * j + half, half, j)

            @block.sync
            def _(sp):
                G = H // 4

                def load(b, half, j):
                    for k in range(PICK):
                        slot = PICK * half + k
                        n = PICK * b + k
                        e = sp.value_load(num_i[0:1, bass.ds(n, 1)], min_val=0, max_val=EX - 1)
                        src = ins["w_ex"][bass.ds(e, 1), :, :].rearrange("a p n -> (a p) n")
                        sp.dma_start(wl[:, slot, :], src[:, 3 * D:N_WX]).then_inc(came[slot].sem, 16)
                        for r in range(4):
                            rows = 9 * G
                            at_row = n * 4 * rows + r * rows
                            sp.dma_start(num[32 * r:32 * r + 32, slot, :], scratch["sums"][bass.ds(at_row, 32), :])\
                                .then_inc(came[slot].sem, 16)
                            sp.dma_start(den[32 * r:32 * r + 32, slot, :],
                                         scratch["sums"][bass.ds(at_row + 8 * G, G), :].unsqueeze(0)
                                         .to_broadcast([8, G, T])).then_inc(came[slot].sem, 16)

                for b in range(2):
                    load(b, b, 0)
                for b in range(2, B):
                    for k in range(PICK):
                        sp.wait_ge(*vec[k](NVS * (b - 1)))
                    load(b, b % 2, 0)

            def item_came(e, b, half, k, j):
                e.wait_ge(*came[PICK * half + k](16 * 9 * j + 16 * 9))

            @block.tensor
            def _(pe):
                def mm(k, bank, left, right, start=True, stop=True):
                    pe.matmul(PS[:, 4 * k + bank, :], left, right, start=start, stop=stop,
                              skip_group_check=True).then_inc(prod[k].sem, 1)

                def batch(b, half, j):
                    both = range(PICK)
                    slot = lambda k: PICK * half + k
                    for k in both:
                        item_came(pe, b, half, k, j)
                        pe.wait_ge(*vec[k](NVS * b + 2))
                        mm(k, 0, at("wo", slot(k)), num[:, slot(k), :])
                    for k in both:
                        pe.wait_ge(*vec[k](NVS * b + 3))
                        mm(k, 1, c.center[:, :], t1[:, k, :])
                    for k in both:
                        pe.wait_ge(*curve[k](NA * b + 1))
                        mm(k, 2, c.mean[:, :], sq[:, k, :])
                    for k in both:
                        pe.wait_ge(*vec[k](NVS * b + 5))
                        mm(k, 0, at("l1", slot(k), 0), x1[:, k, :])
                        mm(k, 2, at("l1", slot(k), 128), x1[:, k, :])
                    for m in range(2):
                        for k in both:
                            pe.wait_ge(*curve[k](NA * b + 4 + m))
                            mm(k, 3, at("l2", slot(k), 128 * m), hb[:, k, m, :], m == 0, False)
                            mm(k, 2 * m, at("l1", slot(k), 128 * (m + 2)), x1[:, k, :])
                    for m in range(2, M):
                        for k in both:
                            pe.wait_ge(*curve[k](NA * b + 4 + m))
                            mm(k, 3, at("l2", slot(k), 128 * m), hb[:, k, m, :], False, m == M - 1)
                    for k in both:
                        pe.wait_ge(*vec[k](NVS * b + 6))
                        mm(k, 1, c.center[:, :], t1[:, k, :])
                    for k in both:
                        pe.wait_ge(*curve[k](NA * b + 8))
                        mm(k, 2, c.mean[:, :], sq[:, k, :])

                batches(pe, batch)

            @block.scalar
            def _(act):
                act.preload_act_table_set("natural_log_exp_and_others")

                def batch(b, half, j):
                    both = range(PICK)

                    def norm(first, centre, spread):
                        for k in both:
                            act.wait_ge(*prod[k](NP * b + centre))
                            act.activation(sq[:, k, :], PS[:, 4 * k + 1, :], ACT.Square).then_inc(curve[k].sem, 1)
                        for k in both:
                            act.wait_ge(*prod[k](NP * b + spread))
                            act.activation(sq[:, k, :], PS[:, 4 * k + 2, :], ACT.Ln, bias=c.eps[:, :])\
                                .then_inc(curve[k].sem, 1)
                        for k in both:
                            act.wait_ge(*curve[k](NA * b + first + 1))
                            act.activation(sq[:, k, :], sq[:, k, :], ACT.Exp, scale=-0.5).then_inc(curve[k].sem, 1)

                    norm(1, 2, 3)
                    for m, up in enumerate((4, 5, 7, 9)):
                        for k in both:
                            act.wait_ge(*prod[k](NP * b + up))
                            act.activation(hb[:, k, m, :], PS[:, 4 * k + 2 * (m % 2), :], ACT.Relu,
                                           bias=at("l1b", PICK * half + k, m, 1)).then_inc(curve[k].sem, 1)
                    norm(8, 12, 13)

                batches(act, batch)

            @block.vector
            def _(dve):
                def batch(b, half, j):
                    both = range(PICK)
                    slot = lambda k: PICK * half + k
                    yb = c.y[:, bass.ds(b, 1), :].rearrange("p a t -> p (a t)")
                    xb = c.x[:, bass.ds(b, 1), :].rearrange("p a t -> p (a t)")
                    for k in both:
                        item_came(dve, b, half, k, j)
                        dve.reciprocal(den[:, slot(k), :], den[:, slot(k), :]).then_inc(vec[k].sem, 1)
                    for k in both:
                        dve.wait_ge(*vec[k](NVS * b + 1))
                        dve.tensor_tensor(num[:, slot(k), :], num[:, slot(k), :], den[:, slot(k), :], ALU.mult)\
                            .then_inc(vec[k].sem, 1)
                    for k in both:
                        dve.wait_ge(*prod[k](NP * b + 1))
                        dve.scalar_tensor_tensor(out=t1[:, k, :], in0=PS[:, 4 * k, :], scalar=at("ob", slot(k), 0, 1),
                                                 in1=yb, op0=ALU.add, op1=ALU.add).then_inc(vec[k].sem, 1)

                    def norm(curves, done, w, shift):
                        for k in both:
                            dve.wait_ge(*curve[k](NA * b + curves))
                            dve.tensor_tensor(x1[:, k, :], PS[:, 4 * k + 1, :], sq[:, k, :], ALU.mult)\
                                .then_inc(vec[k].sem, 1)
                        for k in both:
                            dve.wait_ge(*vec[k](NVS * b + done))
                            dve.tensor_scalar(x1[:, k, :], x1[:, k, :], at(w, slot(k), 0, 1), at(shift, slot(k), 0, 1),
                                              ALU.mult, ALU.add).then_inc(vec[k].sem, 1)

                    norm(3, 4, "n1w", "n1b")
                    for k in both:
                        dve.wait_ge(*prod[k](NP * b + 11))
                        dve.wait_ge(*vec[k](NVS * b + 5))
                        dve.scalar_tensor_tensor(out=t1[:, k, :], in0=PS[:, 4 * k + 3, :], scalar=at("l2b", slot(k), 0, 1),
                                                 in1=x1[:, k, :], op0=ALU.add, op1=ALU.add).then_inc(vec[k].sem, 1)
                    norm(10, 7, "n2w", "n2b")
                    for k in both:
                        dve.wait_ge(*vec[k](NVS * b + 8))
                        if k:
                            dve.wait_ge(*vec[k - 1](NVS * b + 9))
                        dve.scalar_tensor_tensor(out=xb, in0=x1[:, k, :], scalar=wp[:, bass.ds(PICK * b + k, 1)],
                                                 in1=xb, op0=ALU.mult, op1=ALU.add).then_inc(vec[k].sem, 1)

                batches(dve, batch)
        for s in came:
            s.close(16 * 9 * B // 2)
        for k in range(PICK):
            prod[k].close(NP * B)
            curve[k].close(NA * B)
            vec[k].close(NVS * B)


def stage_out(c, out):
    written = c.semaphore_for("out_written")
    with c.nc.Block() as block:
        @block.sync
        def _(sp):
            sp.dma_start(out, c.x[:, :, :]).then_inc(written.sem, 16)
            sp.wait_ge(*written(16))


def decoder(nc, ins, out, upto=6, since=0):
    scratch = {
        "q_parts": nc.dram_tensor("q_parts", (PAIRS * PARTS * D, T), BF16).ap(),
        "k_parts": nc.dram_tensor("k_parts", (PAIRS * PARTS * D, T), BF16).ap(),
        "sums": nc.dram_tensor("head_sums", (PAIRS * 4 * 9 * (H // 4), T), F32).ap(),
        "combine": nc.dram_tensor("combine", (NE, B * T), F32).ap(),
        "max_rows": nc.dram_tensor("max_rows", (PAIRS * H, T), BF16).ap(),
    }
    ctx = ExitStack()
    with ctx:
        c = Chip(ctx, nc)
        stage_setup(c, ins)
        stages = [stage_linear_attention, stage_cross_attention, stage_experts,
                  stage_gated_attention, stage_context_mix, stage_encoders]
        for stage in stages[since:upto]:
            stage(c, ins, scratch)
        stage_out(c, out)


_INPUTS = ("x", "vec", "rows", "w_l0", "w_l1", "w_ex", "bv_ex", "moe", "ctx", "ctx_tok", "pad_mask", "sub_mask",
           "perm")


def arrange(i):
    import numpy as np
    a = {k: np.asarray(v) for k, v in i.items()}
    dh = np.arange(D).reshape(H, HD).T.reshape(-1)
    jrg = np.arange(D).reshape(H // 4, 4, HD).transpose(1, 2, 0).reshape(-1)
    col = lambda v: v.reshape(-1, 128).T
    put = np.concatenate
    A, G, E = "L0_attn_", "L1_attn_", "L1_ffn_"
    bqkv, wqkv = a[A + "b_qkv"], a[A + "w_qkv"]
    vec = put([col(a[A + "ln_g"]), col(a[A + "ln_b"]), col(bqkv[:D][dh]), col(bqkv[D:2 * D][dh]),
               col(a[A + "b_gate"][dh]), col(a[A + "b_proj"]), col(a["L0_xattn_bq"]), col(a["L0_xattn_bk"]),
               col(a[G + "bg"]), col(a[G + "ln1_w"]), col(a[G + "ln1_b"]), col(a[G + "ln2_w"]), col(a[G + "ln2_b"]),
               col(a[G + "b1"]), col(a[G + "b2"]), col(a["L1_xattn_w_sim"]), col(a["L1_xattn_b_qv"])], 1)
    rows = put([bqkv[2 * D:], a["L0_xattn_bv"], a["L0_ffn_expert_bias"], a[E + "gate_b"], a["L1_xattn_b_sim"]])
    w_l0 = put([wqkv[:, :D][:, dh], wqkv[:, D:2 * D][:, dh], wqkv[:, 2 * D:], a[A + "w_gate"][:, dh],
                a[A + "w_proj"][jrg], a["L0_xattn_Wq"].T, a["L0_xattn_Wk"].T, a["L0_xattn_Wv"].T,
                a["L0_ffn_router_w"].T], 1)
    tiles = lambda w: w.reshape(-1, 128, w.shape[1]).transpose(1, 0, 2).reshape(128, -1)
    w_l1 = put([a[G + "Wq"], a[G + "Wk"], a[G + "Wv"], a[G + "Wg"], tiles(a[G + "Wo"]), a[G + "W1"],
                tiles(a[G + "W2"]), tiles(a["L1_xattn_W_qv"]), a[E + "gate_w"].T], 1)
    w_ex, bv_ex = [], []
    for e in range(EX):
        iw, ib = a[E + "in_proj_w"][e], a[E + "in_proj_b"][e]
        w_ex.append(put([iw[:D][dh].T, iw[D:2 * D][dh].T, iw[2 * D:].T, a[E + "out_proj_w"][e].T[jrg],
                         a[E + "lin1_w"][e].T, tiles(a[E + "lin2_w"][e].T), col(ib[:D][dh]), col(ib[D:2 * D][dh]),
                         col(a[E + "out_proj_b"][e]), col(a[E + "ln1_w"][e]), col(a[E + "ln1_b"][e]),
                         col(a[E + "lin1_b"][e]), col(a[E + "lin2_b"][e]), col(a[E + "ln2_w"][e]),
                         col(a[E + "ln2_b"][e])], 1))
        bv_ex.append(ib[2 * D:])
    M = "L0_ffn_"
    moe = []
    for w1, w3, w2 in ((a[M + "sw1"], a[M + "sw3"], a[M + "sw2"]), (a[M + "w1"], a[M + "w3"], a[M + "w2"])):
        for e in range(len(w1)):
            moe.append(put([w1[e].T, w3[e].T, tiles(w2[e].T)], 1))
    out = {
        "x": a["x"].transpose(2, 0, 1), "vec": vec, "rows": rows, "w_l0": w_l0, "w_l1": w_l1,
        "w_ex": np.stack(w_ex), "bv_ex": np.stack(bv_ex), "moe": np.stack(moe),
        "ctx": a["ctx_1024"].transpose(2, 0, 1), "ctx_tok": a["ctx_1024"].transpose(1, 0, 2),
        "pad_mask": a["mask_Bx1x1xS2_ik0"].reshape(B, CT), "sub_mask": a["mask_1x1xSxS2_ik0"].reshape(T, CT),
        "perm": np.eye(D, dtype=np.float32)[jrg],
    }
    return {k: np.ascontiguousarray(v) for k, v in out.items()}


def kernel(**inputs):
    import numpy as np
    import concourse.bacc as bacc
    from concourse import mybir as my
    from concourse.bass_utils import run_bass_kernel_spmd as run

    nc = bacc.Bacc("TRN2", target_bir_lowering=False, num_devices=1)
    arrays = arrange(inputs)
    aps = {k: nc.dram_tensor(f"in_{k}", arrays[k].shape, my.dt.from_np(arrays[k].dtype), kind="ExternalInput").ap()
           for k in _INPUTS}
    out = nc.dram_tensor("out_x", (D, B, T), F32, kind="ExternalOutput").ap()
    decoder(nc, aps, out)
    r = run(nc, [{f"in_{k}": arrays[k] for k in _INPUTS}], core_ids=[0])
    return np.ascontiguousarray(r.results[0]["out_x"].transpose(1, 2, 0))
```

```python
from contextlib import ExitStack

import concourse.bass as bass
from concourse import mybir

F32 = mybir.dt.float32
BF16 = mybir.dt.bfloat16
I32 = mybir.dt.int32
ALU = mybir.AluOpType
ACT = mybir.ActivationFunctionType
AX = mybir.AxisListType

B, T, D = 4, 512, 128
CT = 77
H, HD = 16, 8
TT = T // 128
NE, HID = 8, 256
NSH = 2
GH, GD = 16, 64
HP = GH // 2
CH = 64
NC = T // CH
FFN = 512
EX, PICK = 4, 2
PAIRS = B * PICK
EPS = 1e-5
HALF = 64

VEC = {}


def _columns(table, *names):
    at = 0
    for name, n in names:
        table[name] = (at, n)
        at += n
    return at


N_VEC = _columns(VEC, ("ln_g", 1), ("ln_b", 1), ("a_bq", 1), ("a_bk", 1), ("b_gate", 1), ("b_proj", 1),
                 ("x_bq", 1), ("x_bk", 1), ("bg", HP), ("ln1_w", 1), ("ln1_b", 1), ("ln2_w", 1),
                 ("ln2_b", 1), ("b1", FFN // 128), ("b2", 1), ("w1", 1), ("w2", 1), ("w3", 1), ("b_qv", 1))
W_L0 = {}
N_W0 = _columns(W_L0, ("a_wq", D), ("a_wk", D), ("a_wv", D), ("w_gate", D), ("w_proj", D),
                ("x_wq", D), ("x_wk", D), ("x_wv", D), ("router", NE))
W_L1 = {}
N_W1 = _columns(W_L1, ("g_wq", HP * 128), ("g_wk", HP * 128), ("g_wv", HP * 128), ("g_wg", HP * 128),
                ("g_wo", HP * 128), ("f_w1", FFN), ("f_w2", FFN), ("w_qv", 4 * D), ("gate_w", EX))
W_EX = {}
N_WX = _columns(W_EX, ("wq", D), ("wk", D), ("wv", D), ("wo", D), ("l1", FFN), ("l2", FFN),
                ("bq", 1), ("bk", 1), ("ob", 1), ("n1w", 1), ("n1b", 1), ("l1b", FFN // 128), ("l2b", 1),
                ("n2w", 1), ("n2b", 1))
ROW = {}
N_ROW = _columns(ROW, ("a_bv", D), ("x_bv", D), ("router_b", NE), ("gate_b", EX), ("b_sim", 1))
ME = {}
N_ME = _columns(ME, ("w1", HID), ("w3", HID), ("w2", 2 * D))

PARTS = 3
SPLIT = PARTS * PARTS * HD
MAXROW = SPLIT
KROWS = MAXROW + 1


class Signal:

    def __init__(self, ctx, nc, name):
        self.sem = ctx.enter_context(nc.semaphore(name))
        self.base = 0

    def __call__(self, n):
        return self.sem, self.base + n

    def close(self, n):
        self.base += n


def dram_view(t, offset, dims):
    return bass.AP(t.tensor, t.offset + offset, [list(d) for d in dims])


class Chip:

    def __init__(self, ctx, nc):
        self.ctx, self.nc = ctx, nc
        self.signals, self.named = {}, {}
        self.PS = ctx.enter_context(nc.psum_tensor("PS", [128, 8, 512], F32))
        self.x = self.sb("x_res", [128, B, T])
        self.y = self.sb("y_norm", [128, B, T])
        self.sq = self.sb("ln_sq", [128, B, T])
        self.rs = self.sb("ln_rs", [128, B, T])
        self.vec = self.sb("vec", [128, N_VEC])
        self.w1 = self.sb("w_l1", [128, N_W1])
        self.rows = self.sb("rows", [128, N_ROW])
        self.center = self.sb("center", [128, 128])
        self.mean = self.sb("mean", [128, 128])
        self.ident = self.sb("ident", [128, 128])
        self.ones = self.sb("ones", [128, 128])
        self.eps = self.sb("eps", [128, 1])

    def sb(self, name, shape, dt=F32, ctx=None):
        self.named[name] = self.named.get(name, 0) + 1
        if self.named[name] > 1:
            name = f"{name}_{self.named[name]}"
        return (ctx or self.ctx).enter_context(self.nc.sbuf_tensor(name, shape, dt))

    def semaphore_for(self, name):
        if name not in self.signals:
            self.signals[name] = Signal(self.ctx, self.nc, name)
        return self.signals[name]

    def v(self, name, k=0):
        return self.vec[:, VEC[name][0] + k:VEC[name][0] + k + 1]


def norm_pe(c, pe, source, run=0, came=None):
    centered, squared, spread = c.semaphore_for("ln_centered"), c.semaphore_for("ln_squared"), c.semaphore_for("ln_spread")
    for b in range(B):
        if came:
            pe.wait_ge(*came(b + 1))
        pe.matmul(c.PS[:, b, :], c.center[:, :], source[:, b, :], start=True, stop=True)\
            .then_inc(centered.sem, 1)
    for b in range(B):
        pe.wait_ge(*squared(run * B + b + 1))
        pe.matmul(c.PS[:, B + b, :], c.mean[:, :], c.sq[:, b, :], start=True, stop=True)\
            .then_inc(spread.sem, 1)


def norm_act(c, act, run=0):
    centered, squared, spread = c.semaphore_for("ln_centered"), c.semaphore_for("ln_squared"), c.semaphore_for("ln_spread")
    logged, scale = c.semaphore_for("ln_logged"), c.semaphore_for("ln_scale")
    for b in range(B):
        act.wait_ge(*centered(run * B + b + 1))
        act.activation(c.sq[:, b, :], c.PS[:, b, :], ACT.Square).then_inc(squared.sem, 1)
    for b in range(B):
        act.wait_ge(*spread(run * B + b + 1))
        act.activation(c.rs[:, b, :], c.PS[:, B + b, :], ACT.Ln, bias=c.eps[:, :]).then_inc(logged.sem, 1)
    for b in range(B):
        act.wait_ge(*logged(run * B + b + 1))
        act.activation(c.rs[:, b, :], c.rs[:, b, :], ACT.Exp, scale=-0.5).then_inc(scale.sem, 1)


def norm_dve(c, dve, dest, run=0, gain=None, shift=None):
    scale, normed, scaled = c.semaphore_for("ln_scale"), c.semaphore_for("ln_normed"), c.semaphore_for("ln_scaled")
    for b in range(B):
        dve.wait_ge(*scale(run * B + b + 1))
        dve.tensor_tensor(dest[:, b, :], c.PS[:, b, :], c.rs[:, b, :], ALU.mult).then_inc(normed.sem, 1)
        if gain is not None:
            dve.wait_ge(*normed(run * B + b + 1))
            dve.tensor_scalar(dest[:, b, :], dest[:, b, :], gain, shift, ALU.mult, ALU.add)\
                .then_inc(scaled.sem, 1)


def norm_close(c, runs=1, scaled=0):
    for name in ("ln_centered", "ln_squared", "ln_spread", "ln_logged", "ln_scale", "ln_normed"):
        c.semaphore_for(name).close(B * runs)
    c.semaphore_for("ln_scaled").close(B * scaled)


def stage_setup(c, ins):
    loaded = c.semaphore_for("setup_loaded")
    made = c.semaphore_for("const_made")
    with c.nc.Block() as block:
        @block.sync
        def _(sp):
            sp.dma_start(c.x[:, :, :], ins["x"]).then_inc(loaded.sem, 16)
            sp.dma_start(c.vec[:, :], ins["vec"]).then_inc(loaded.sem, 16)
            sp.dma_start(c.rows[:, :], ins["rows"].partition_broadcast(128)).then_inc(loaded.sem, 16)
            sp.dma_start(c.w1[:, :], ins["w_l1"]).then_inc(loaded.sem, 16)

        @block.gpsimd
        def _(pool):
            pool.memset(c.ident[:, :], 0.0).then_inc(made.sem, 1)
            pool.memset(c.ones[:, :], 1.0).then_inc(made.sem, 1)
            pool.memset(c.mean[:, :], 1.0 / D).then_inc(made.sem, 1)
            pool.memset(c.center[:, :], -1.0 / D).then_inc(made.sem, 1)
            pool.memset(c.eps[:, :], EPS).then_inc(made.sem, 1)
            pool.wait_ge(*made(5))
            pool.affine_select(out=c.ident[:, :], in_=c.ident[:, :], compare_op=ALU.not_equal, fill=1.0,
                               base=0, pattern=[[-1, 128]], channel_multiplier=1).then_inc(made.sem, 1)
            pool.affine_select(out=c.center[:, :], in_=c.center[:, :], compare_op=ALU.not_equal,
                               fill=1.0 - 1.0 / D, base=0, pattern=[[-1, 128]], channel_multiplier=1)\
                .then_inc(made.sem, 1)
            pool.wait_ge(*made(7))

        @block.vector
        def _(dve):
            dve.wait_ge(*loaded(4 * 16))
    made.close(7)


G = H // 4
STEPS = G * TT
QK_LOADS = PARTS * (PARTS + 1)


def load_split(sp, qs, ks, at, q_parts, k_parts, n, came):
    for i in range(PARTS):
        sp.dma_start(ks[24 * i:24 * i + 24, at, :, :],
                     dram_view(k_parts, n * PARTS * D * T, [(H * T, 24), (1, H * T)])).then_inc(came.sem, 16)
        for j in range(PARTS):
            r = 24 * i + 8 * j
            sp.dma_start(qs[r:r + 8, at, :, :],
                         dram_view(q_parts, (n * PARTS + i) * D * T, [(H * T, 8), (1, H * T)])).then_inc(came.sem, 16)


def send_sums(sp, sums, osum, n, sent):
    for j in range(4):
        sp.dma_start(dram_view(sums, (n * 4 + j) * 9 * G * T, [(G * T, 9), (1, G * T)]),
                     osum[n % 2][32 * j:32 * j + 9, :, :]).then_inc(sent[n % 2].sem, 16)


def linear_core(c, items, q_parts, k_parts, sums, values):
    nc, PS = c.nc, c.PS
    loaded = [c.semaphore_for("qk_loaded_0"), c.semaphore_for("qk_loaded_1")]
    scored, edged, drained = c.semaphore_for("at_scored"), c.semaphore_for("at_edged"), c.semaphore_for("at_drained")
    summed, copied, made = c.semaphore_for("at_summed"), c.semaphore_for("at_sum_copied"), c.semaphore_for("const_made")
    sent = [c.semaphore_for("at_sum_sent_even"), c.semaphore_for("at_sum_sent_odd")]
    BANKS = ((0, 1), (2, 3), (6, 7))
    NP = 3
    UNITS = 2 * STEPS
    ctx = ExitStack()
    with ctx:
        qs = c.sb("q_split", [128, 2, H, T], BF16, ctx)
        ks = c.sb("k_split", [128, 2, H, T], BF16, ctx)
        probs = c.sb("probs", [128, NP, 4, T], F32, ctx)
        osum = [c.rs, c.sb("o_sum", [128, G, T], F32, ctx)]
        zero = c.sb("zero512", [128, T], F32, ctx)
        tri = c.sb("tri", [128, 128], F32, ctx)
        block = ctx.enter_context(nc.Block())

        def drains(v):
            whole, rest = v // (2 * TT), v % (2 * TT)
            return whole * (2 * TT - 2) + min(rest, 2 * TT - 2)

        def place(v):
            return BANKS[v % 3][0], (v // 2) % NP, 128 * (v // 2 % TT)

        @block.sync
        def _(sp):
            load_split(sp, qs, ks, 0, q_parts, k_parts, 0, loaded[0])
            for n in range(items):
                if n + 1 < items:
                    if n >= 1:
                        sp.wait_ge(*scored(n * UNITS))
                    load_split(sp, qs, ks, (n + 1) % 2, q_parts, k_parts, n + 1, loaded[(n + 1) % 2])
                sp.wait_ge(*copied(G * (n + 1)))
                send_sums(sp, sums, osum, n, sent)
            for k in range(2):
                sp.wait_ge(*sent[k](64 * (items // 2)))

        @block.gpsimd
        def _(pool):
            pool.memset(zero[:, :], 0.0).then_inc(made.sem, 1)
            pool.memset(tri[:, :], 1.0).then_inc(made.sem, 1)
            pool.wait_ge(*made(2))
            pool.affine_select(out=tri[:, :], in_=tri[:, :], compare_op=ALU.is_ge, fill=0.0,
                               base=0, pattern=[[1, 128]], channel_multiplier=-1).then_inc(made.sem, 1)

        @block.tensor
        def _(pe):
            pe.wait_ge(*made(2))
            for o in range(2):
                pe.matmul(PS[:, 4 + o, :], zero[:, 0:128], zero[:, :], start=True, stop=True)

            def scores(v):
                bank, _, q0 = place(v)
                n, g = v // UNITS, v // 2 // TT % G
                if v >= 3:
                    pe.wait_ge(*edged(v - 2))
                    pe.wait_ge(*drained(drains(v - 2)))
                for jj in range(2):
                    h = 4 * g + 2 * (v % 2) + jj
                    mm = pe.matmul(PS[:, bank + jj, q0:T], ks[0:SPLIT, n % 2, h, q0:q0 + 128],
                                   qs[0:SPLIT, n % 2, h, q0:T], start=True, stop=True)
                mm.then_inc(scored.sem, 1)

            def sum_up(t):
                _, at, q0 = place(2 * t)
                n, g, kt = t // STEPS, t // TT % G, t % TT
                pe.wait_ge(*edged(2 * t + 2))
                pe.wait_ge(*drained(drains(2 * t + 2)))
                if kt == 0 and n * G + g >= 2:
                    pe.wait_ge(*copied(n * G + g - 1))
                for j in range(4):
                    mm = pe.matmul(PS[32 * j:32 * j + 9, 4 + g % 2, q0:T], values[:, n, kt, 4 * g + j, :],
                                   probs[:, at, j, q0:T], start=(kt == 0), stop=(kt == TT - 1),
                                   skip_group_check=True)
                mm.then_inc(summed.sem, 1)

            for t in range(items * STEPS):
                if t % STEPS == 0:
                    n = t // STEPS
                    pe.wait_ge(*loaded[n % 2](16 * QK_LOADS * (n // 2 + 1)))
                scores(2 * t)
                scores(2 * t + 1)
                if t:
                    sum_up(t - 1)
            sum_up(items * STEPS - 1)

        @block.vector
        def _(dve):
            def copy_sums(group):
                n, g = group // G, group % G
                dve.wait_ge(*summed(TT * (group + 1)))
                if g == 0 and n >= 2:
                    dve.wait_ge(*sent[n % 2](64 * (n // 2)))
                dve.tensor_copy(osum[n % 2][:, g, :], PS[:, 4 + g % 2, :]).then_inc(copied.sem, 1)

            dve.wait_ge(*made(3))
            for v in range(items * UNITS):
                bank, at, q0 = place(v)
                t, h = v // 2, 2 * (v % 2)
                dve.wait_ge(*scored(v + 1))
                if t >= NP:
                    dve.wait_ge(*summed(t - NP + 1))
                dve.tensor_tensor(probs[:, at, h:h + 2, q0:q0 + 128], PS[:, bank:bank + 2, q0:q0 + 128],
                                  tri[:, :].unsqueeze(1).to_broadcast([128, 2, 128]), ALU.mult).then_inc(edged.sem, 1)
                if v % (2 * TT) == 5 and t >= TT:
                    copy_sums(t // TT - 1)
            copy_sums(items * G - 1)

        @block.scalar
        def _(act):
            act.preload_act_table_set("natural_log_exp_and_others")
            for v in range(items * UNITS):
                bank, at, q0 = place(v)
                h = 2 * (v % 2)
                act.wait_ge(*edged(v + 1))
                if q0 + 128 < T:
                    act.activation(probs[:, at, h:h + 2, q0 + 128:T], PS[:, bank:bank + 2, q0 + 128:T], ACT.Copy)\
                        .then_inc(drained.sem, 1)

    for s, n in ((loaded[0], 8 * QK_LOADS * items), (loaded[1], 8 * QK_LOADS * items), (scored, UNITS * items),
                 (edged, UNITS * items), (drained, drains(UNITS * items)), (summed, STEPS * items), (copied, G * items),
                 (sent[0], 32 * items), (sent[1], 32 * items), (made, 3)):
        s.close(n)


def softmax_core(c, items, q_parts, k_parts, max_rows, sums, values):
    nc, PS = c.nc, c.PS
    NQ = 3
    MAXES = H * TT
    READY = STEPS - 4
    loaded = [c.semaphore_for(f"qk_loaded_{k}") for k in range(NQ)]
    scored, drained = c.semaphore_for("at_scored"), c.semaphore_for("at_drained")
    summed, copied, made = c.semaphore_for("at_summed"), c.semaphore_for("at_sum_copied"), c.semaphore_for("const_made")
    sent = [c.semaphore_for("at_sum_sent_even"), c.semaphore_for("at_sum_sent_odd")]
    nscored, maxed, turned = c.semaphore_for("mx_scored"), c.semaphore_for("mx_found"), c.semaphore_for("mx_turned")
    mcast, msent = c.semaphore_for("mx_cast"), c.semaphore_for("mx_sent")
    mloaded = [c.semaphore_for("mx_loaded_even"), c.semaphore_for("mx_loaded_odd")]
    ones_came = c.semaphore_for("at_ones_came")

    def found_by(t):
        if t < READY:
            return MAXES + -(-MAXES * (t + 1) // READY)
        return min(items * MAXES, 2 * MAXES + (MAXES // STEPS) * (t + 1 - READY))

    ctx = ExitStack()
    with ctx:
        qs = c.sb("q_split", [128, NQ, H, T], BF16, ctx)
        ks = c.sb("k_split", [128, NQ, H, T], BF16, ctx)
        probs = c.sb("probs", [128, 2, 4, T], F32, ctx)
        osum = [c.rs, c.sb("o_sum", [128, G, T], F32, ctx)]
        zero, mx = c.sq[:, 0, :], c.sq[:, 1, 0:2 * MAXES].rearrange("p (n i) -> p n i", i=MAXES)
        one_row = c.sb("one_row", [128, H * T // 128], BF16, ctx)
        mrow = c.sb("mx_row", [MAXES, 2, 128], BF16, ctx)
        block = ctx.enter_context(nc.Block())

        @block.sync
        def _(sp):
            def load(n):
                if n >= NQ:
                    sp.wait_ge(*scored((n - NQ + 1) * 2 * STEPS))
                load_split(sp, qs, ks, n % NQ, q_parts, k_parts, n, loaded[n % NQ])

            def send_max(n):
                sp.wait_ge(*mcast(n + 1))
                sp.dma_start(dram_view(max_rows, n * H * T, [(128, MAXES), (1, 128)]), mrow[:, n % 2, :])\
                    .then_inc(msent.sem, 16)
                sp.wait_ge(*msent(16 * (n + 1)))
                sp.dma_start(qs[MAXROW:MAXROW + 1, n % NQ, :, :],
                             dram_view(max_rows, n * H * T, [(H * T, 1), (1, H * T)]))\
                    .then_inc(mloaded[n % 2].sem, 16)

            load(0)
            load(1)
            sp.wait_ge(*made(2))
            for k in range(NQ):
                sp.dma_start(ks[MAXROW:MAXROW + 1, k, :, :], one_row[:, :]).then_inc(ones_came.sem, 16)
            load(2)
            send_max(0)
            for n in range(items):
                if n + 1 < items:
                    send_max(n + 1)
                sp.wait_ge(*copied(G * (n + 1)))
                send_sums(sp, sums, osum, n, sent)
                if n + NQ < items:
                    load(n + NQ)
            for k in range(2):
                sp.wait_ge(*sent[k](64 * (items // 2)))

        @block.gpsimd
        def _(pool):
            pool.memset(zero, 0.0).then_inc(made.sem, 1)
            pool.memset(one_row[:, :], 1.0).then_inc(made.sem, 1)

        @block.tensor
        def _(pe):
            pe.wait_ge(*made(2))
            for o in range(2):
                pe.matmul(PS[:, 4 + o, :], zero[:, 0:128], zero, start=True, stop=True)

            def max_pass(u):
                n, i = u // MAXES, u % MAXES
                h, qt = i // TT, i % TT
                if i == 0:
                    pe.wait_ge(*loaded[n % NQ](16 * QK_LOADS * (n // NQ + 1)))
                    if n:
                        pe.wait_ge(*mcast(n))
                if u >= 2:
                    pe.wait_ge(*maxed(u - 1))
                pe.matmul(PS[:, 6 + i % 2, :], qs[0:SPLIT, n % NQ, h, 128 * qt:128 * qt + 128],
                          ks[0:SPLIT, n % NQ, h, :], start=True, stop=True).then_inc(nscored.sem, 1)

            def turn_max(n):
                pe.wait_ge(*maxed((n + 1) * MAXES))
                pe.transpose(PS[0:MAXES, 6, 0:128], mx[:, n % 2, :], c.ident[:, :]).then_inc(turned.sem, 1)

            def scores(t, half):
                n, g, kt = t // STEPS, t // TT % G, t % TT
                if t >= 1:
                    pe.wait_ge(*drained(2 * t - 1 + half))
                for jj in range(2):
                    h = 4 * g + 2 * half + jj
                    mm = pe.matmul(PS[:, 2 * half + jj, :], ks[0:KROWS, n % NQ, h, 128 * kt:128 * kt + 128],
                                   qs[0:KROWS, n % NQ, h, :], start=True, stop=True)
                mm.then_inc(scored.sem, 1)

            def sum_up(t):
                n, g, kt = t // STEPS, t // TT % G, t % TT
                pe.wait_ge(*drained(2 * t + 2))
                if kt == 0 and n * G + g >= 2:
                    pe.wait_ge(*copied(n * G + g - 1))
                for j in range(4):
                    mm = pe.matmul(PS[32 * j:32 * j + 9, 4 + g % 2, :], values[:, n, kt, 4 * g + j, :],
                                   probs[:, t % 2, j, :], start=(kt == 0), stop=(kt == TT - 1),
                                   skip_group_check=True)
                mm.then_inc(summed.sem, 1)

            for u in range(MAXES):
                max_pass(u)
            turn_max(0)
            for t in range(items * STEPS):
                n = t // STEPS
                if t % STEPS == 0:
                    if n == 0:
                        pe.wait_ge(*ones_came(16 * NQ))
                    pe.wait_ge(*mloaded[n % 2](16 * (n // 2 + 1)))
                ahead = list(range(found_by(t - 1), found_by(t)))
                turning = found_by(t) != found_by(t - 1) and found_by(t) % MAXES == 0

                def some(k):
                    for u in ahead[k * len(ahead) // 4:(k + 1) * len(ahead) // 4]:
                        max_pass(u)

                scores(t, 0)
                some(0)
                scores(t, 1)
                some(1)
                some(2)
                if t:
                    sum_up(t - 1)
                some(3)
                if turning:
                    turn_max(found_by(t) // MAXES - 1)
            sum_up(items * STEPS - 1)

        @block.scalar
        def _(act):
            act.preload_act_table_set("natural_log_exp_and_others")

            def cast_max(n):
                act.wait_ge(*turned(n + 1))
                if n >= 2:
                    act.wait_ge(*msent(16 * (n - 1)))
                act.activation(mrow[:, n % 2, :], PS[0:MAXES, 6, 0:128], ACT.Copy, scale=-1.0)\
                    .then_inc(mcast.sem, 1)

            cast_max(0)
            for t in range(items * STEPS):
                for half in range(2):
                    act.wait_ge(*scored(2 * t + half + 1))
                    if t >= 2:
                        act.wait_ge(*summed(t - 1))
                    act.activation(probs[:, t % 2, 2 * half:2 * half + 2, :], PS[:, 2 * half:2 * half + 2, :],
                                   ACT.Exp).then_inc(drained.sem, 1)
                if t % STEPS == READY - 1 and t // STEPS + 1 < items:
                    cast_max(t // STEPS + 1)

        @block.vector
        def _(dve):
            def find_max(u):
                n, i = u // MAXES, u % MAXES
                dve.wait_ge(*nscored(u + 1))
                if i == 0 and n >= 2:
                    dve.wait_ge(*turned(n - 1))
                dve.tensor_reduce(mx[:, n % 2, i:i + 1], PS[:, 6 + i % 2, :], AX.X, ALU.max).then_inc(maxed.sem, 1)

            def copy_sums(group):
                n, g = group // G, group % G
                dve.wait_ge(*summed(TT * (group + 1)))
                if g == 0 and n >= 2:
                    dve.wait_ge(*sent[n % 2](64 * (n // 2)))
                dve.tensor_copy(osum[n % 2][:, g, :], PS[:, 4 + g % 2, :]).then_inc(copied.sem, 1)

            for u in range(MAXES):
                find_max(u)
            for t in range(items * STEPS):
                for u in range(found_by(t - 1), found_by(t)):
                    find_max(u)
                if t % TT == 0 and t:
                    copy_sums(t // TT - 1)
            copy_sums(items * G - 1)

    TM = items * MAXES
    for s, n in ((scored, 2 * STEPS * items), (drained, 2 * STEPS * items), (summed, STEPS * items),
                 (copied, G * items), (sent[0], 32 * items), (sent[1], 32 * items), (made, 2), (nscored, TM),
                 (maxed, TM), (turned, items), (mcast, items), (msent, 16 * items), (ones_came, 16 * NQ),
                 (mloaded[0], 8 * items), (mloaded[1], 8 * items)):
        s.close(n)
    for k in range(NQ):
        loaded[k].close(16 * QK_LOADS * len(range(k, items, NQ)))


def stage_linear_attention(c, ins, scratch):
    nc, PS = c.nc, c.PS
    w_came = c.semaphore_for("w_came")
    second = c.semaphore_for("a_second_norm")
    gated, gsum, glog, gscale, gate = (c.semaphore_for(n) for n in ("a_gate_raw", "a_gate_mean", "a_gate_log",
                                                            "a_gate_scale", "a_gate"))
    sigm = c.semaphore_for("a_sigmoid")
    proj, qk, low, ex, elu = (c.semaphore_for(n) for n in ("a_proj", "a_qk", "a_low", "a_exp", "a_elu"))
    hi, rest, mid, last, vals = (c.semaphore_for(n) for n in ("s_high", "s_rest", "s_middle", "s_last", "at_values"))
    stored = [c.semaphore_for("s_stored_q"), c.semaphore_for("s_stored_k")]
    outer = ExitStack()
    with outer:
        values = c.sb("a_values", [128, B, TT, H, 9], F32, outer)
        w0 = c.sb("w_l0", [128, N_W0], F32, outer)

        def w(name, n=D):
            at = W_L0[name][0]
            return w0[:, at:at + n]

        ctx = ExitStack()
        with ctx:
            z = c.sb("a_z", [128, B, T], F32, ctx)
            gs = c.sb("a_gs", [128, B, T], F32, ctx)
            qkf = c.sb("a_qkf", [128, 2, T], F32, ctx)
            neg = c.sb("a_neg", [128, 2, T], F32, ctx)
            parts = c.sb("a_parts", [128, 2, PARTS, T], BF16, ctx)
            res = c.sb("a_res", [128, 2, T], F32, ctx)
            block = ctx.enter_context(nc.Block())

            @block.sync
            def _(sp):
                sp.dma_start(w0[:, :], ins["w_l0"]).then_inc(w_came.sem, 16)
                for u in range(2 * B):
                    sp.wait_ge(*last(u + 1))
                    dest = scratch["q_parts"] if u % 2 == 0 else scratch["k_parts"]
                    sp.dma_start(dram_view(dest, (u // 2) * PARTS * D * T, [(T, 128), (D * T, PARTS), (1, T)]),
                                 parts[:, u % 2, :, :]).then_inc(stored[u % 2].sem, 16)
                for s in stored:
                    sp.wait_ge(*s(16 * B))

            @block.tensor
            def _(pe):
                norm_pe(c, pe, c.x)
                norm_pe(c, pe, c.y, 1, c.semaphore_for("ln_normed"))
                pe.wait_ge(*w_came(16))
                for b in range(B):
                    pe.wait_ge(*second(b + 1))
                    pe.matmul(PS[:, b, :], w("w_gate"), c.y[:, b, :], start=True, stop=True).then_inc(gated.sem, 1)
                for b in range(B):
                    pe.wait_ge(*sigm(b + 1))
                    pe.matmul(PS[:, B + b, :], c.mean[:, :], gs[:, b, :], start=True, stop=True).then_inc(gsum.sem, 1)
                for b in range(B):
                    if b == 0:
                        pe.wait_ge(*sigm(B))
                    else:
                        pe.wait_ge(*qk(2 * b))
                        pe.wait_ge(*vals(b))
                    pe.matmul(PS[:, 0, :], w("a_wq"), z[:, b, :], start=True, stop=True).then_inc(proj.sem, 1)
                    pe.matmul(PS[:, 1, :], w("a_wk"), z[:, b, :], start=True, stop=True).then_inc(proj.sem, 1)
                    for kt in range(TT):
                        mm = pe.matmul(PS[:, 2, 128 * kt:128 * kt + 128], z[:, b, 128 * kt:128 * kt + 128],
                                       w("a_wv"), start=True, stop=True)
                    mm.then_inc(proj.sem, 1)

            @block.scalar
            def _(act):
                act.preload_act_table_set("natural_log_exp_and_others")
                norm_act(c, act)
                norm_act(c, act, 1)
                for b in range(B):
                    act.wait_ge(*gated(b + 1))
                    act.activation(gs[:, b, :], PS[:, b, :], ACT.Sigmoid, bias=c.v("b_gate")).then_inc(sigm.sem, 1)
                for b in range(B):
                    act.wait_ge(*gsum(b + 1))
                    act.activation(c.rs[:, b, :], PS[:, B + b, :], ACT.Ln, bias=c.eps[:, :]).then_inc(glog.sem, 1)
                for b in range(B):
                    act.wait_ge(*glog(b + 1))
                    act.activation(c.rs[:, b, :], c.rs[:, b, :], ACT.Exp, scale=-1.0).then_inc(gscale.sem, 1)
                for u in range(2 * B):
                    act.wait_ge(*low(u + 1))
                    act.activation(neg[:, u % 2, :], neg[:, u % 2, :], ACT.Exp).then_inc(ex.sem, 1)
                    act.wait_ge(*elu(u + 1))
                    if u >= 2:
                        act.wait_ge(*stored[u % 2](16 * (u // 2)))
                    act.activation(parts[:, u % 2, 0, :], qkf[:, u % 2, :], ACT.Copy).then_inc(hi.sem, 1)
                    act.wait_ge(*rest(u + 1))
                    act.activation(parts[:, u % 2, 1, :], res[:, u % 2, :], ACT.Copy).then_inc(mid.sem, 1)

            @block.gpsimd
            def _(pool):
                pool.memset(values[:, :, :, :, 8:9], 1.0).then_inc(c.semaphore_for("at_ones").sem, 1)

            @block.vector
            def _(dve):
                norm_dve(c, dve, c.y)
                scale = c.semaphore_for("ln_scale")
                for b in range(B):
                    dve.wait_ge(*scale(B + b + 1))
                    dve.tensor_tensor(z[:, b, :], PS[:, b, :], c.rs[:, b, :], ALU.mult)\
                        .then_inc(c.semaphore_for("ln_normed").sem, 1)
                    dve.wait_ge(*c.semaphore_for("ln_normed")(B + b + 1))
                    dve.tensor_scalar(z[:, b, :], z[:, b, :], c.v("ln_g"), c.v("ln_b"), ALU.mult, ALU.add)\
                        .then_inc(second.sem, 1)
                for b in range(B):
                    dve.wait_ge(*gscale(b + 1))
                    dve.tensor_tensor(gs[:, b, :], gs[:, b, :], c.rs[:, b, :], ALU.mult).then_inc(gate.sem, 1)
                dve.wait_ge(*gate(B))
                bv = ROW["a_bv"][0]
                for b in range(B):
                    for k in range(2):
                        u = 2 * b + k
                        dve.wait_ge(*proj(3 * b + k + 1))
                        dve.scalar_tensor_tensor(out=qkf[:, k, :], in0=PS[:, k, :], scalar=c.v(("a_bq", "a_bk")[k]),
                                                 in1=gs[:, b, :], op0=ALU.add, op1=ALU.mult).then_inc(qk.sem, 1)
                        dve.wait_ge(*qk(u + 1))
                        dve.tensor_scalar(neg[:, k, :], qkf[:, k, :], 0.0, None, ALU.min).then_inc(low.sem, 1)
                        if k == 0:
                            dve.wait_ge(*proj(3 * b + 3))
                            dve.tensor_tensor(values[:, b, :, :, 0:8],
                                              PS[:, 2, :].rearrange("p (k h d) -> p k h d", k=TT, d=HD),
                                              c.rows[:, bv:bv + D].rearrange("p (h d) -> p h d", d=HD)
                                              .unsqueeze(1).to_broadcast([128, TT, H, HD]), ALU.add).then_inc(vals.sem, 1)
                        dve.wait_ge(*ex(u + 1))
                        dve.scalar_tensor_tensor(out=qkf[:, k, :], in0=qkf[:, k, :], scalar=0.0, in1=neg[:, k, :],
                                                 op0=ALU.max, op1=ALU.add).then_inc(elu.sem, 1)
                        dve.wait_ge(*hi(u + 1))
                        dve.tensor_tensor(res[:, k, :], qkf[:, k, :], parts[:, k, 0, :], ALU.subtract)\
                            .then_inc(rest.sem, 1)
                        dve.wait_ge(*mid(u + 1))
                        dve.tensor_tensor(parts[:, k, 2, :], res[:, k, :], parts[:, k, 1, :], ALU.subtract)\
                            .then_inc(last.sem, 1)
        norm_close(c, 2)
        for s, n in ((second, B), (gated, B), (gsum, B), (glog, B), (gscale, B), (gate, B), (sigm, B), (proj, 3 * B),
                     (qk, 2 * B), (low, 2 * B), (ex, 2 * B), (elu, 2 * B), (hi, 2 * B), (rest, 2 * B), (mid, 2 * B),
                     (last, 2 * B), (vals, B), (stored[0], 16 * B), (stored[1], 16 * B), (w_came, 16)):
            s.close(n)
        linear_core(c, B, scratch["q_parts"], scratch["k_parts"], scratch["sums"], values)
        finish_attention(c, scratch, w("w_proj"), 1e-5, c.v("b_proj"))


def fetch_sums(sp, sums, items, num, den, fetched):
    for n in range(items):
        for j in range(4):
            at = (n * 4 + j) * 9 * G * T
            sp.dma_start(num[32 * j:32 * j + 32, n, :], dram_view(sums, at, [(T, 32), (1, T)]))\
                .then_inc(fetched[n].sem, 16)
            sp.dma_start(den[32 * j:32 * j + 32, n, :],
                         dram_view(sums, at + 8 * G * T, [(0, 8), (T, G), (1, T)])).then_inc(fetched[n].sem, 16)


def stage_cross_attention(c, ins, scratch):
    nc, PS = c.nc, c.PS
    w_came, made = c.semaphore_for("w_came"), c.semaphore_for("const_made")
    proj, kq, spread_k, vals = (c.semaphore_for(n) for n in ("x_proj", "x_biased", "x_k_spread", "at_values"))
    capped = c.semaphore_for("x_cap")
    scored, mined, maxed, subbed, exped = (c.semaphore_for(n) for n in ("x_scored", "x_masked", "x_max", "x_shifted", "x_exp"))
    turned, moved, summed, copied = (c.semaphore_for(n) for n in ("x_turned", "x_moved", "x_summed", "x_sum_copied"))
    sent = [c.semaphore_for("at_sum_sent_even"), c.semaphore_for("at_sum_sent_odd")]
    outer = ExitStack()
    with outer:
        w0 = c.sb("x_w", [128, N_W0], F32, outer)
        q = c.sb("x_q", [128, B, T], F32, outer)
        kx = c.sb("x_kx", [128, B, H, CT], F32, outer)
        vx = c.sb("x_vx", [CT, B, H, 9], F32, outer)
        cap = c.sb("x_cap", [128, B, TT, CT], F32, outer)
        perm = c.sb("x_perm", [128, 128], F32, outer)

        def w(name, n=D):
            at = W_L0[name][0]
            return w0[:, at:at + n]

        ctx = ExitStack()
        with ctx:
            cx = c.sb("x_ctx", [128, B, CT], F32, ctx)
            kb = c.sb("x_kb", [128, B, CT], F32, ctx)
            hm = c.sb("x_head", [128, H], F32, ctx)
            padi = c.sb("x_padi", [128, B, CT], I32, ctx)
            subi = c.sb("x_subi", [128, TT, CT], I32, ctx)
            pad = c.sb("x_pad", [128, B, CT], F32, ctx)
            sub = c.sb("x_sub", [128, TT, CT], F32, ctx)
            block = ctx.enter_context(nc.Block())

            @block.sync
            def _(sp):
                sp.dma_start(w0[:, :], ins["w_l0"]).then_inc(w_came.sem, 16)
                sp.dma_start(cx[:, :, :], ins["ctx"]).then_inc(w_came.sem, 16)
                sp.dma_start(padi[:, :, :], ins["pad_mask"].rearrange("b t -> (b t)").partition_broadcast(128))\
                    .then_inc(w_came.sem, 16)
                sp.dma_start(subi[:, :, :], ins["sub_mask"].rearrange("(k p) t -> p k t", p=128))\
                    .then_inc(w_came.sem, 16)
                sp.dma_start(perm[:, :], ins["perm"]).then_inc(w_came.sem, 16)

            @block.tensor
            def _(pe):
                norm_pe(c, pe, c.x)
                pe.wait_ge(*w_came(80))
                normed = c.semaphore_for("ln_normed")
                pe.wait_ge(*normed(B))
                for b in range(B):
                    pe.matmul(PS[:, b, :], w("x_wq"), c.y[:, b, :], start=True, stop=True).then_inc(proj.sem, 1)
                pe.matmul(PS[:, 4, 0:B * CT], w("x_wk"), cx[:, :, :].rearrange("p b t -> p (b t)"),
                          start=True, stop=True).then_inc(proj.sem, 1)
                for b in range(B):
                    mm = pe.matmul(PS[0:CT, 5, D * b:D * b + D], cx[:, b, :], w("x_wv"), start=True, stop=True)
                mm.then_inc(proj.sem, 1)

            @block.scalar
            def _(act):
                act.preload_act_table_set("natural_log_exp_and_others")
                norm_act(c, act)

            @block.gpsimd
            def _(pool):
                pool.memset(hm[:, :], 1.0).then_inc(made.sem, 1)
                pool.wait_ge(*made(1))
                pool.affine_select(out=hm[:, :], in_=hm[:, :], compare_op=ALU.is_ge, fill=0.0, base=0,
                                   pattern=[[-HD, H]], channel_multiplier=1).then_inc(made.sem, 1)
                pool.wait_ge(*made(2))
                pool.affine_select(out=hm[:, :], in_=hm[:, :], compare_op=ALU.is_ge, fill=0.0, base=HD - 1,
                                   pattern=[[HD, H]], channel_multiplier=-1).then_inc(made.sem, 1)
                pool.memset(vx[:, :, :, 8:9], 1.0).then_inc(made.sem, 1)

            @block.vector
            def _(dve):
                dve.wait_ge(*w_came(80))
                dve.tensor_scalar(pad[:, :, :], padi[:, :, :], 0, None, ALU.not_equal).then_inc(capped.sem, 1)
                dve.tensor_scalar(sub[:, :, :], subi[:, :, :], 0, None, ALU.not_equal).then_inc(capped.sem, 1)
                dve.wait_ge(*capped(2))
                for b in range(B):
                    dve.tensor_tensor(cap[:, b, :, :], sub[:, :, :],
                                      pad[:, b, :].unsqueeze(1).to_broadcast([128, TT, CT]), ALU.mult)\
                        .then_inc(capped.sem, 1)
                dve.wait_ge(*capped(2 + B))
                dve.tensor_scalar(cap[:, :, :, :], cap[:, :, :, :], 3e38, -1e9, ALU.mult, ALU.add)\
                    .then_inc(capped.sem, 1)
                norm_dve(c, dve, c.y)
                dve.wait_ge(*proj(B + 1))
                dve.tensor_scalar(kb[:, :, :], PS[:, 4, 0:B * CT].rearrange("p (b t) -> p b t", b=B), c.v("x_bk"), None,
                                  ALU.add).then_inc(kq.sem, 1)
                dve.wait_ge(*proj(B + 2))
                bv = ROW["x_bv"][0]
                dve.wait_ge(*made(4))
                dve.tensor_tensor(vx[:, :, :, 0:8], PS[0:CT, 5, :].rearrange("p (b h d) -> p b h d", b=B, d=HD),
                                  c.rows[0:CT, bv:bv + D].rearrange("p (h d) -> p h d", d=HD).unsqueeze(1)
                                  .to_broadcast([CT, B, H, HD]), ALU.add).then_inc(vals.sem, 1)
                dve.wait_ge(*kq(1))
                for b in range(B):
                    dve.tensor_tensor(kx[:, b, :, :], kb[:, b, :].unsqueeze(1).to_broadcast([128, H, CT]),
                                      hm[:, :].unsqueeze(2).to_broadcast([128, H, CT]), ALU.mult)\
                        .then_inc(spread_k.sem, 1)
                for b in range(B):
                    dve.tensor_scalar(q[:, b, :], PS[:, b, :], c.v("x_bq"), float(HD) ** -0.5, ALU.add, ALU.mult)\
                        .then_inc(kq.sem, 1)
                dve.wait_ge(*kq(1 + B))
        norm_close(c)
        for s, n in ((w_came, 80), (proj, B + 2), (kq, B + 1), (spread_k, B), (vals, 1), (capped, 3 + B)):
            s.close(n)
        made.close(4)

        ctx = ExitStack()
        with ctx:
            sc = c.sb("x_sc", [128, 2, H, CT], F32, ctx)
            mx = c.sb("x_mx", [128, 2, H], F32, ctx)
            pt = c.sb("x_pt", [CT, 2, 4, 128], F32, ctx)
            osum = c.sb("x_osum", [128, 2, G, T], F32, ctx)
            zero = c.sb("x_zero", [128, T], F32, ctx)
            U = B * TT
            zeroed = c.semaphore_for("at_zeroed")
            block = ctx.enter_context(nc.Block())

            @block.tensor
            def _(pe):
                pe.wait_ge(*zeroed(1))
                for o in range(2):
                    pe.matmul(PS[:, 6 + o, :], zero[:, 0:128], zero[:, :], start=True, stop=True)

                def scores(u):
                    b, qt = u // TT, u % TT
                    if u:
                        pe.wait_ge(*mined(u))
                    for g in range(G):
                        mm = pe.matmul(PS[:, g, 0:4 * CT], q[:, b, 128 * qt:128 * qt + 128],
                                       kx[:, b, 4 * g:4 * g + 4, :].rearrange("p h t -> p (h t)"),
                                       start=True, stop=True)
                    mm.then_inc(scored.sem, 1)

                def sum_up(u, g):
                    b = u // TT
                    k = u * G + g
                    pe.wait_ge(*moved(k + 1))
                    if g == 0 and u >= 2:
                        pe.wait_ge(*copied(u - 1))
                    for j in range(4):
                        mm = pe.matmul(PS[32 * j:32 * j + 9, 6 + u % 2, 128 * g:128 * g + 128],
                                       vx[:, b, 4 * g + j, :], pt[:, k % 2, j, :], start=True, stop=True,
                                       skip_group_check=True)
                    mm.then_inc(summed.sem, 1)

                scores(0)
                for u in range(U):
                    if u + 1 < U:
                        scores(u + 1)
                    pe.wait_ge(*exped(u + 1))
                    for g in range(G):
                        k = u * G + g
                        if k >= 2:
                            pe.wait_ge(*moved(k - 1))
                        for j in range(4):
                            mm = pe.transpose(PS[0:CT, 4 + k % 2, 128 * j:128 * j + 128], sc[:, u % 2, 4 * g + j, :],
                                              c.ident[:, :])
                        mm.then_inc(turned.sem, 1)
                        if g:
                            sum_up(u, g - 1)
                    sum_up(u, G - 1)

            @block.gpsimd
            def _(pool):
                pool.memset(zero[:, :], 0.0).then_inc(zeroed.sem, 1)
                for u in range(U):
                    pool.wait_ge(*maxed(u + 1))
                    pool.tensor_tensor(sc[:, u % 2, :, :], sc[:, u % 2, :, :],
                                       mx[:, u % 2, :].unsqueeze(2).to_broadcast([128, H, CT]), ALU.subtract)\
                        .then_inc(subbed.sem, 1)

            @block.scalar
            def _(act):
                act.preload_act_table_set("natural_log_exp_and_others")
                for u in range(U):
                    act.wait_ge(*subbed(u + 1))
                    act.activation(sc[:, u % 2, :, :], sc[:, u % 2, :, :], ACT.Exp).then_inc(exped.sem, 1)
                    for g in range(G):
                        k = u * G + g
                        act.wait_ge(*turned(k + 1))
                        if k >= 2:
                            act.wait_ge(*summed(k - 1))
                        act.activation(pt[:, k % 2, :, :], PS[0:CT, 4 + k % 2, :].rearrange("p (j q) -> p j q", j=4),
                                       ACT.Copy).then_inc(moved.sem, 1)

            @block.vector
            def _(dve):
                def copy_sums(u):
                    b, qt = u // TT, u % TT
                    dve.wait_ge(*summed(G * (u + 1)))
                    if qt == 0 and b >= 2:
                        dve.wait_ge(*sent[b % 2](64 * (b // 2)))
                    dve.tensor_copy(osum[:, b % 2, :, 128 * qt:128 * qt + 128],
                                    PS[:, 6 + u % 2, :].rearrange("p (g q) -> p g q", g=G)).then_inc(copied.sem, 1)

                for u in range(U):
                    b, qt = u // TT, u % TT
                    dve.wait_ge(*scored(u + 1))
                    if u >= 2:
                        dve.wait_ge(*turned(G * (u - 1)))
                    dve.tensor_tensor(sc[:, u % 2, :, :].rearrange("p (g h) t -> p g h t", g=G),
                                      PS[:, 0:4, 0:4 * CT].rearrange("p g (h t) -> p g h t", h=4),
                                      cap[:, b, qt, :].unsqueeze(1).unsqueeze(1).to_broadcast([128, G, 4, CT]),
                                      ALU.min).then_inc(mined.sem, 1)
                    dve.wait_ge(*mined(u + 1))
                    dve.tensor_reduce(mx[:, u % 2, :], sc[:, u % 2, :, :], AX.X, ALU.max).then_inc(maxed.sem, 1)
                    if u:
                        copy_sums(u - 1)
                copy_sums(U - 1)

            @block.sync
            def _(sp):
                for b in range(B):
                    sp.wait_ge(*copied(TT * (b + 1)))
                    for j in range(4):
                        sp.dma_start(dram_view(scratch["sums"], (b * 4 + j) * 9 * G * T, [(G * T, 9), (1, G * T)]),
                                     osum[32 * j:32 * j + 9, b % 2, :, :]).then_inc(sent[b % 2].sem, 16)
                for s in sent:
                    sp.wait_ge(*s(64 * (B // 2)))
        for s, n in ((scored, U), (mined, U), (maxed, U), (subbed, U), (exped, U), (turned, U * G), (moved, U * G),
                     (summed, U * G), (copied, U), (sent[0], 32 * B), (sent[1], 32 * B), (zeroed, 1)):
            s.close(n)
        finish_attention(c, scratch, perm[:, :], None, None)


def finish_attention(c, scratch, weight, shift, bias):
    nc, PS = c.nc, c.PS
    fetched = [c.semaphore_for(f"o_fetched{n}") for n in range(B)]
    inverted, divided, projected, added = (c.semaphore_for(n) for n in ("o_inverted", "o_divided", "o_projected", "x_added"))
    ctx = ExitStack()
    with ctx:
        num = c.sb("o_num", [128, B, T], F32, ctx)
        den = c.sb("o_den", [128, B, T], F32, ctx)
        block = ctx.enter_context(nc.Block())

        @block.sync
        def _(sp):
            fetch_sums(sp, scratch["sums"], B, num, den, fetched)

        @block.tensor
        def _(pe):
            for b in range(B):
                pe.wait_ge(*divided(b + 1))
                pe.matmul(PS[:, b, :], weight, num[:, b, :], start=True, stop=True).then_inc(projected.sem, 1)

        @block.vector
        def _(dve):
            for b in range(B):
                dve.wait_ge(*fetched[b](128))
                dve.tensor_scalar(den[:, b, :], den[:, b, :], shift or 0.0, None, ALU.add).then_inc(inverted.sem, 1)
                dve.wait_ge(*inverted(2 * b + 1))
                dve.reciprocal(den[:, b, :], den[:, b, :]).then_inc(inverted.sem, 1)
                dve.wait_ge(*inverted(2 * b + 2))
                dve.tensor_tensor(num[:, b, :], num[:, b, :], den[:, b, :], ALU.mult).then_inc(divided.sem, 1)
            for b in range(B):
                dve.wait_ge(*projected(b + 1))
                dve.scalar_tensor_tensor(out=c.x[:, b, :], in0=PS[:, b, :], scalar=0.0 if bias is None else bias,
                                         in1=c.x[:, b, :], op0=ALU.add, op1=ALU.add).then_inc(added.sem, 1)
            dve.wait_ge(*added(B))
    for s, n in (*((f, 128) for f in fetched), (inverted, 2 * B), (divided, B), (projected, B), (added, B)):
        s.close(n)


def stage_experts(c, ins, scratch):
    nc, PS = c.nc, c.PS
    ALL = NSH + NE
    NT = B * TT
    ROUTED = NSH
    w_came, made, normed = c.semaphore_for("w_came"), c.semaphore_for("const_made"), c.semaphore_for("ln_normed")
    routed, step, exped, turned, moved, stored = (c.semaphore_for(n) for n in (
        "m_logits", "m_route_step", "m_exp", "m_turned", "m_turned_copy", "m_weights_stored"))
    slot_came = [c.semaphore_for("m_slot_even"), c.semaphore_for("m_slot_odd")]
    up, silu, gated, wide, summed, added = (c.semaphore_for(n) for n in (
        "m_up", "m_silu", "m_gated", "m_weighted", "m_down", "x_added"))
    outer = ExitStack()
    with outer:
        ctx = ExitStack()
        with ctx:
            rw = c.sb("m_router", [128, NE], F32, ctx)
            lg = c.sb("m_lg", [128, NT, NE], F32, ctx)
            ex = c.sb("m_ex", [128, NT, NE], F32, ctx)
            small = c.sb("m_small", [128, 4, NT], F32, ctx)
            gt = c.sb("m_gt", [128, NT, NE, NE], F32, ctx)
            eq = c.sb("m_eq", [128, NT, NE, NE], F32, ctx)
            low = c.sb("m_low", [128, NE, NE], F32, ctx)
            cwt = c.sb("m_cwt", [NE, B, T], F32, ctx)
            block = ctx.enter_context(nc.Block())
            a, n = W_L0["router"]

            @block.sync
            def _(sp):
                sp.dma_start(rw[:, :], ins["w_l0"][:, a:a + n]).then_inc(w_came.sem, 16)
                sp.wait_ge(*moved(B))
                sp.dma_start(scratch["combine"], cwt[:, :, :].rearrange("e b t -> e (b t)")).then_inc(stored.sem, 16)
                sp.wait_ge(*stored(16))

            @block.gpsimd
            def _(pool):
                pool.memset(low[:, :, :], 1.0).then_inc(made.sem, 1)
                pool.wait_ge(*made(1))
                pool.affine_select(out=low[:, :, :], in_=low[:, :, :], compare_op=ALU.is_ge, fill=0.0, base=-1,
                                   pattern=[[1, NE], [-1, NE]], channel_multiplier=0).then_inc(made.sem, 1)

            @block.tensor
            def _(pe):
                norm_pe(c, pe, c.x)
                pe.wait_ge(*w_came(16))
                pe.wait_ge(*normed(B))
                for i in range(NT):
                    mm = pe.matmul(PS[:, 0, NE * i:NE * i + NE], c.y[:, i // TT, 128 * (i % TT):128 * (i % TT) + 128],
                                   rw[:, :], start=True, stop=True)
                mm.then_inc(routed.sem, 1)
                pe.wait_ge(*step(12))
                for i in range(NT):
                    mm = pe.transpose(PS[0:NE, i // TT, 128 * (i % TT):128 * (i % TT) + 128], ex[:, i, :], c.ident[:, :])
                    if i % TT == TT - 1:
                        mm.then_inc(turned.sem, 1)

            @block.scalar
            def _(act):
                act.preload_act_table_set("natural_log_exp_and_others")
                norm_act(c, act)
                act.wait_ge(*step(8))
                act.activation(ex[:, :, :], ex[:, :, :], ACT.Exp).then_inc(exped.sem, 1)
                for b in range(B):
                    act.wait_ge(*turned(b + 1))
                    act.activation(cwt[:, b, :], PS[0:NE, b, :], ACT.Copy).then_inc(moved.sem, 1)

            @block.vector
            def _(dve):
                norm_dve(c, dve, c.y)
                dve.wait_ge(*routed(1))
                rb = ROW["router_b"][0]
                dve.tensor_tensor(lg[:, :, :], PS[:, 0, 0:NT * NE].rearrange("p (i e) -> p i e", e=NE),
                                  c.rows[:, rb:rb + NE].unsqueeze(1).to_broadcast([128, NT, NE]), ALU.add)\
                    .then_inc(step.sem, 1)
                dve.wait_ge(*step(1))
                other = lg[:, :, :].unsqueeze(2).to_broadcast([128, NT, NE, NE])
                own = lg[:, :, :].unsqueeze(3).to_broadcast([128, NT, NE, NE])
                dve.tensor_tensor(gt[:, :, :, :], other, own, ALU.is_gt).then_inc(step.sem, 1)
                dve.tensor_tensor(eq[:, :, :, :], other, own, ALU.is_equal).then_inc(step.sem, 1)
                dve.wait_ge(*made(2))
                dve.wait_ge(*step(3))
                dve.tensor_tensor(eq[:, :, :, :], eq[:, :, :, :],
                                  low[:, :, :].unsqueeze(1).to_broadcast([128, NT, NE, NE]), ALU.mult)\
                    .then_inc(step.sem, 1)
                dve.wait_ge(*step(4))
                dve.tensor_tensor(gt[:, :, :, :], gt[:, :, :, :], eq[:, :, :, :], ALU.add).then_inc(step.sem, 1)
                dve.tensor_reduce(small[:, 0, :], lg[:, :, :], AX.X, ALU.max).then_inc(step.sem, 1)
                dve.wait_ge(*step(6))
                dve.tensor_reduce(eq[:, :, :, 0], gt[:, :, :, :], AX.X, ALU.add).then_inc(step.sem, 1)
                dve.tensor_tensor(ex[:, :, :], lg[:, :, :], small[:, 0, :].unsqueeze(2).to_broadcast([128, NT, NE]),
                                  ALU.subtract).then_inc(step.sem, 1)
                dve.wait_ge(*step(8))
                dve.wait_ge(*exped(1))
                dve.scalar_tensor_tensor(out=ex[:, :, :], in0=eq[:, :, :, 0], scalar=1.5, in1=ex[:, :, :],
                                         op0=ALU.is_lt, op1=ALU.mult).then_inc(step.sem, 1)
                dve.wait_ge(*step(9))
                dve.tensor_reduce(small[:, 1, :], ex[:, :, :], AX.X, ALU.add).then_inc(step.sem, 1)
                dve.wait_ge(*step(10))
                dve.reciprocal(small[:, 2, :], small[:, 1, :]).then_inc(step.sem, 1)
                dve.wait_ge(*step(11))
                dve.tensor_tensor(ex[:, :, :], ex[:, :, :], small[:, 2, :].unsqueeze(2).to_broadcast([128, NT, NE]),
                                  ALU.mult).then_inc(step.sem, 1)
        norm_close(c)
        for s, n in ((w_came, 16), (made, 2), (routed, 1), (step, 12), (exped, 1), (turned, B), (moved, B), (stored, 16)):
            s.close(n)

        ctx = ExitStack()
        with ctx:
            slot = c.sb("m_slot", [128, 2, N_ME], F32, ctx)
            cw = c.sb("m_cw", [128, 2, B, T], F32, ctx)
            yw = c.sb("m_yw", [128, 2, B, T], F32, ctx)
            sl = c.sb("m_sl", [128, 2, T], F32, ctx)
            gb = c.sb("m_gb", [128, 2, T], F32, ctx)
            block = ctx.enter_context(nc.Block())
            STEPS = 2 * B
            LOOPED = NE // 2 - 1

            def w(par, name, m):
                at = ME[name][0] + 128 * m
                return slot[:, par, at:at + 128]

            @block.sync
            def _(sp):
                def load(e, par, routed_one):
                    if not (isinstance(e, int) and e < 2):
                        sp.wait_ge(*summed(STEPS * e - STEPS))
                    sp.dma_start(slot[:, par, :], ins["moe"][e, :, :] if isinstance(e, int) else
                                 ins["moe"][bass.ds(e, 1), :, :].rearrange("a p n -> (a p) n"))\
                        .then_inc(slot_came[par].sem, 16)
                    if routed_one:
                        row = e - ROUTED
                        src = scratch["combine"][row:row + 1, :] if isinstance(e, int) else \
                            scratch["combine"][bass.ds(row, 1), :]
                        sp.dma_start(cw[:, par, :, :].rearrange("p b t -> p (b t)"),
                                     src.to_broadcast([128, B * T])).then_inc(slot_came[par].sem, 16)

                for e in range(NSH):
                    load(e, e % 2, False)
                with sp.Fori(0, LOOPED) as i:
                    for par in range(2):
                        load(2 * i + (NSH + par), par, True)
                for e in range(ALL - 2, ALL):
                    load(e, e % 2, True)

            def came(e, par):
                return slot_came[par]((e - par) * 16 + 16) if not isinstance(e, int) or e >= NSH else slot_came[par](16)

            @block.gpsimd
            def _(pool):
                def weigh(e, par):
                    pool.wait_ge(*came(e, par))
                    pool.wait_ge(*up(STEPS * e - STEPS))
                    for b in range(B):
                        pool.tensor_tensor(yw[:, par, b, :], c.y[:, b, :], cw[:, par, b, :], ALU.mult)\
                            .then_inc(wide.sem, 1)

                with pool.Fori(0, LOOPED) as i:
                    for par in range(2):
                        weigh(2 * i + (NSH + par), par)
                for e in range(ALL - 2, ALL):
                    weigh(e, e % 2)

            @block.tensor
            def _(pe):
                def down(e, par, s, first=False, last=False):
                    b, m = s // 2, s % 2
                    pe.wait_ge(*gated(STEPS * e + (s + 1)))
                    pe.matmul(PS[:, 4 + b, :], w(par, "w2", m), gb[:, m, :], start=first and m == 0,
                              stop=last and m == 1, skip_group_check=True).then_inc(summed.sem, 1)

                def expert(e, par, first=False, last=False, fixed=True):
                    pe.wait_ge(*came(e, par))
                    for s in range(STEPS):
                        b, m = s // 2, s % 2
                        begun = not (first and s < 2)
                        if begun:
                            pe.wait_ge(*silu(STEPS * e + (s - 1)))
                        pe.matmul(PS[:, m, :], w(par, "w1", m), c.y[:, b, :], start=True, stop=True)
                        if begun:
                            pe.wait_ge(*gated(STEPS * e + (s - 1)))
                        routed_one = not fixed or e >= NSH
                        if routed_one and m == 0:
                            pe.wait_ge(*wide(B * e + (b + 1 - B * NSH)))
                        pe.matmul(PS[:, 2 + m, :], w(par, "w3", m), yw[:, par, b, :] if routed_one else c.y[:, b, :],
                                  start=True, stop=True).then_inc(up.sem, 1)
                        if s:
                            down(e, par, s - 1, first, last)
                        elif not first:
                            down(e - 1, 1 - par, STEPS - 1)

                expert(0, 0, first=True)
                expert(1, 1)
                with pe.Fori(0, LOOPED) as i:
                    for par in range(2):
                        expert(2 * i + (NSH + par), par, fixed=False)
                expert(ALL - 2, 0)
                expert(ALL - 1, 1, last=True)
                down(ALL - 1, 1, STEPS - 1, last=True)

            @block.scalar
            def _(act):
                act.preload_act_table_set("natural_log_exp_and_others")
                def expert(e, first=False):
                    for s in range(STEPS):
                        act.wait_ge(*up(STEPS * e + (s + 1)))
                        if not (first and s < 2):
                            act.wait_ge(*gated(STEPS * e + (s - 1)))
                        act.activation(sl[:, s % 2, :], PS[:, s % 2, :], ACT.Silu).then_inc(silu.sem, 1)

                expert(0, True)
                expert(1)
                with act.Fori(0, LOOPED) as i:
                    for par in range(2):
                        expert(2 * i + (NSH + par))
                expert(ALL - 2)
                expert(ALL - 1)

            @block.vector
            def _(dve):
                def expert(e, first=False):
                    for s in range(STEPS):
                        dve.wait_ge(*silu(STEPS * e + (s + 1)))
                        if not (first and s < 2):
                            dve.wait_ge(*summed(STEPS * e + (s - 1)))
                        dve.tensor_tensor(gb[:, s % 2, :], sl[:, s % 2, :], PS[:, 2 + s % 2, :], ALU.mult)\
                            .then_inc(gated.sem, 1)

                expert(0, True)
                expert(1)
                with dve.Fori(0, LOOPED) as i:
                    for par in range(2):
                        expert(2 * i + (NSH + par))
                expert(ALL - 2)
                expert(ALL - 1)
                dve.wait_ge(*summed(STEPS * ALL))
                for b in range(B):
                    dve.tensor_tensor(c.x[:, b, :], c.x[:, b, :], PS[:, 4 + b, :], ALU.add).then_inc(added.sem, 1)
                dve.wait_ge(*added(B))
        per = (16 + 32 * NE // 2)
        for s, n in ((slot_came[0], per), (slot_came[1], per), (up, STEPS * ALL), (silu, STEPS * ALL),
                     (gated, STEPS * ALL), (wide, B * NE), (summed, STEPS * ALL), (added, B)):
            s.close(n)


def stage_gated_attention(c, ins, scratch):
    nc, PS = c.nc, c.PS
    made, normed = c.semaphore_for("const_made"), c.semaphore_for("ln_normed")
    scaled = c.semaphore_for("ln_scaled")
    outer = ExitStack()
    with outer:
        z = c.sb("g_z", [128, B, T], F32, outer)
        ctx = ExitStack()
        with ctx:
            def buf(name, shape, dt=F32):
                return c.sb("g_" + name, shape, dt, ctx)

            xb = buf("xb", [128, T])
            sqq, sqk, e1, t1, lga = (buf(n, [128, T]) for n in ("sqq", "sqk", "e1", "t1", "lga"))
            rq, rk, te, de, dd, dec, kdt, oe = (buf(n, [128, T]) for n in ("rq", "rk", "te", "de", "dd", "dec", "kdt", "oe"))
            dg = buf("dg", [128, NC])
            cum, eq, qn, kn, kd = (buf(n, [128, 2, T]) for n in ("cum", "eq", "qn", "kn", "kd"))
            LB = 4
            le, lo = (buf(n, [128, LB, T]) for n in ("le", "lo"))
            re, ro = (buf(n, [128, 2, T]) for n in ("re", "ro"))
            reset = buf("reset", [128, T])
            late = buf("late", [128, CH])
            eye = buf("eye", [128, CH])
            pair, swap = buf("pair", [128, 128]), buf("swap", [128, 128])
            nbg = buf("nbg", [128, HP])
            ln256 = buf("ln256", [128, 1])
            first = buf("first", [128, 4])

            (proj, sq, ex, vm, nrm, ln, rr, tt, la, cm, eqs, tes, des, qk, kds, qds) = (c.semaphore_for("g_" + n) for n in (
                "projected", "squared", "exp", "values", "norm", "norm_log", "norm_scale", "one_plus", "log",
                "cumulated", "decay", "to_end", "end_decay", "normalised", "k_decayed", "q_decayed"))
            (lm, sc, kt, dst, dms, decs, ktm, kv, am, st, om, oes, acc, res, xbs) = (c.semaphore_for("g_" + n) for n in (
                "mean_log", "scored", "k_turned", "pair_log", "pair_masked", "pair_decay", "k_moved", "chunk_state",
                "weighted", "state", "out", "out_copied", "out_projected", "residual", "x_copied"))

            def wl(name, hp):
                at = W_L1[name][0] + 128 * hp
                return c.w1[:, at:at + 128]

            with nc.Block() as block:
                @block.gpsimd
                def _(pool):
                    pool.memset(reset[:, :], 1.0).then_inc(made.sem, 1)
                    pool.memset(pair[:, :], 0.0).then_inc(made.sem, 1)
                    pool.memset(swap[:, :], 0.0).then_inc(made.sem, 1)
                    pool.memset(late[:, :], 0.0).then_inc(made.sem, 1)
                    pool.memset(eye[:, :], 0.0).then_inc(made.sem, 1)
                    pool.memset(ln256[:, :], 5.545177444479562).then_inc(made.sem, 1)
                    pool.memset(le[:, :, :], 0.0).then_inc(made.sem, 1)
                    pool.memset(lo[:, :, :], 0.0).then_inc(made.sem, 1)
                    pool.wait_ge(*made(8))
                    pool.memset(reset[:, :].rearrange("p (n t) -> p n t", t=CH)[:, :, 0:1], 0.0).then_inc(made.sem, 1)
                    pool.wait_ge(*made(9))
                    for p in (0, HALF):
                        pool.memset(pair[p:p + HALF, p:p + HALF], 1.0).then_inc(made.sem, 1)
                        pool.memset(swap[p:p + HALF, HALF - p:CH + HALF - p], 1.0 / GD).then_inc(made.sem, 1)
                    pool.wait_ge(*made(13))
                    for p in (0, HALF):
                        pool.affine_select(out=late[p:p + HALF, :], in_=late[p:p + HALF, :], compare_op=ALU.is_ge,
                                           fill=1e30, base=0, pattern=[[1, CH]], channel_multiplier=-1)\
                            .then_inc(made.sem, 1)
                        pool.affine_select(out=eye[p:p + HALF, :], in_=eye[p:p + HALF, :], compare_op=ALU.not_equal,
                                           fill=1.0, base=0, pattern=[[-1, CH]], channel_multiplier=1)\
                            .then_inc(made.sem, 1)

                @block.tensor
                def _(pe):
                    norm_pe(c, pe, c.x)
                    norm_pe(c, pe, c.y, 1, normed)

                @block.scalar
                def _(act):
                    act.preload_act_table_set("natural_log_exp_and_others")
                    norm_act(c, act)
                    norm_act(c, act, 1)

                @block.vector
                def _(dve):
                    for k, s in enumerate((st, am, oes, res)):
                        dve.memset(first[:, k:k + 1], 0.0).then_inc(s.sem, 1)
                    a, n = VEC["bg"]
                    dve.tensor_scalar(nbg[:, :], c.vec[:, a:a + n], -1.0, None, ALU.mult).then_inc(res.sem, 1)
                    norm_dve(c, dve, c.y)
                    norm_dve(c, dve, z, 1, c.v("ln1_w"), c.v("ln1_b"))
            norm_close(c, 2, 1)
            for s, n in ((st, 1), (am, 1), (oes, 1), (res, 2)):
                s.close(n)
            made.close(17)

            block = ctx.enter_context(nc.Block())

            def chunks(t):
                return t.rearrange("p (n t) -> p n t", t=CH)

            @block.tensor
            def _(pe):
                def front(u, hp):
                    pe.wait_ge(*ln(2 * u))
                    pe.matmul(PS[:, 2, :], wl("g_wg", hp), xb[:, :], start=True, stop=True).then_inc(proj.sem, 1)
                    for n in range(NC):
                        for head in range(2):
                            p = HALF * (1 - head)
                            mm = pe.matmul(PS[p:p + HALF, 3, CH * n:CH * n + CH], xb[:, CH * n:CH * n + CH],
                                           wl("g_wv", hp)[:, GD * head:GD * head + GD], start=True, stop=True,
                                           skip_group_check=True)
                    mm.then_inc(proj.sem, 1)
                    pe.wait_ge(*qk(2 * u))
                    pe.matmul(PS[:, 0, :], wl("g_wq", hp), xb[:, :], start=True, stop=True).then_inc(proj.sem, 1)
                    pe.matmul(PS[:, 1, :], wl("g_wk", hp), xb[:, :], start=True, stop=True).then_inc(proj.sem, 1)

                def norms(u, before):
                    pe.wait_ge(*sq(2 * u + 1))
                    pe.wait_ge(*ex(u + 1))
                    pe.matmul(PS[:, 2, :], pair[:, :], sqq[:, :], start=True, stop=True).then_inc(nrm.sem, 1)
                    pe.wait_ge(*sq(2 * u + 2))
                    pe.wait_ge(*vm(2 * u + 2))
                    if before is not None:
                        turned_ready(before)
                    pe.matmul(PS[:, 3, :], pair[:, :], sqk[:, :], start=True, stop=True).then_inc(nrm.sem, 1)

                def scores(u, k, before):
                    pe.wait_ge(*cm(u + 1))
                    pe.wait_ge(*st(14 * u))
                    pe.wait_ge(*qk(2 * u + 2))
                    pe.wait_ge(*am(2 * u))
                    pe.matmul(PS[:, 4, :], swap[:, :], cum[:, k, :], start=True, stop=True).then_inc(lm.sem, 1)
                    for n in range(NC):
                        for head in range(2):
                            p, o = HALF * head, HALF * (1 - head)
                            mm = pe.matmul(PS[o:o + HALF, 5, CH * n:CH * n + CH],
                                           kn[p:p + HALF, k, CH * n:CH * n + CH], qn[p:p + HALF, k, CH * n:CH * n + CH],
                                           start=True, stop=True, skip_group_check=True)
                    mm.then_inc(sc.sem, 1)
                    if before is not None:
                        turn_ready(u)
                        project(u - 1, before)

                def turn_ready(u):
                    pe.wait_ge(*kds(u + 1))
                    pe.wait_ge(*oes(u))

                def turned_ready(u):
                    pe.wait_ge(*dst(3 * u + 3))
                    pe.wait_ge(*ktm(u + 1))

                def turn_keys(k):
                    for n in range(NC):
                        for head in range(2):
                            p, o = HALF * head, HALF * (1 - head)
                            mm = pe.matmul(PS[o:o + HALF, 6, CH * n:CH * n + CH],
                                           kd[p:p + HALF, k, CH * n:CH * n + CH], eye[p:p + HALF, :],
                                           start=True, stop=True, skip_group_check=True)
                    mm.then_inc(kt.sem, 1)

                def chunk_states(k):
                    for n in range(NC):
                        for head, v in ((0, le), (1, lo)):
                            p, o = HALF * head, HALF * (1 - head)
                            mm = pe.matmul(PS[p:p + HALF, 4, CH * n:CH * n + CH],
                                           kdt[o:o + HALF, CH * n:CH * n + CH], v[o:o + HALF, k, CH * n:CH * n + CH],
                                           start=True, stop=True, skip_group_check=True)
                    mm.then_inc(kv.sem, 1)

                def outputs(u, k, kl):
                    pe.wait_ge(*am(2 * u + 2))
                    pe.wait_ge(*qds(2 * u + 2))
                    pe.wait_ge(*st(14 * u + 14))
                    for n in range(NC):
                        for head, left, right in ((0, le, re), (1, lo, ro)):
                            p = HALF * head
                            mm = pe.matmul(PS[p:p + HALF, 6, CH * n:CH * n + CH], left[:, kl, CH * n:CH * n + CH],
                                           right[:, k, CH * n:CH * n + CH], start=True, stop=True,
                                           skip_group_check=True)
                    mm.then_inc(om.sem, 1)

                def project(u, hp):
                    pe.wait_ge(*oes(u + 1))
                    pe.matmul(PS[:, 7, :], wl("g_wo", hp), oe[:, :], start=(hp == 0), stop=(hp == HP - 1))\
                        .then_inc(acc.sem, 1)

                def batch(b, last):
                    for hp in range(HP):
                        u = b * HP + hp
                        if hp == 0:
                            turn_ready(u)
                        elif hp == 1:
                            pe.wait_ge(*res(b))
                        scores(u, hp % 2, hp - 1 if hp else None)
                        turn_keys(hp % 2)
                        if not (last and hp == HP - 1):
                            norms(u + 1, u)
                        else:
                            turned_ready(u)
                        chunk_states(hp % LB)
                        if not (last and hp >= HP - 2):
                            if hp == HP - 2:
                                pe.wait_ge(*xbs(b + 2))
                            front(u + 2, (hp + 2) % HP)
                        outputs(u, hp % 2, hp % LB)
                    project(b * HP + (HP - 1), HP - 1)

                pe.wait_ge(*xbs(1))
                front(0, 0)
                norms(0, None)
                front(1, 1)
                with pe.Fori(0, B - 1) as b:
                    batch(b, False)
                batch(B - 1, True)

            @block.scalar
            def _(act):
                act.preload_act_table_set("natural_log_exp_and_others")

                def take_batch(b):
                    act.activation(xb[:, :], z[:, bass.ds(b, 1), :].rearrange("p a t -> p (a t)"), ACT.Copy)\
                        .then_inc(xbs.sem, 1)

                def early(u, hp):
                    kl = hp % LB
                    act.wait_ge(*proj(4 * u + 1))
                    act.activation(e1[:, :], PS[:, 2, :], ACT.Exp, scale=-1.0, bias=nbg[:, hp:hp + 1]).then_inc(ex.sem, 1)
                    act.wait_ge(*proj(4 * u + 2))
                    act.activation(lo[0:HALF, kl, :], PS[0:HALF, 3, :], ACT.Copy).then_inc(vm.sem, 1)
                    act.activation(le[HALF:128, kl, :], PS[HALF:128, 3, :], ACT.Copy).then_inc(vm.sem, 1)
                    act.wait_ge(*proj(4 * u + 3))
                    act.activation(sqq[:, :], PS[:, 0, :], ACT.Square).then_inc(sq.sem, 1)
                    act.wait_ge(*proj(4 * u + 4))
                    act.activation(sqk[:, :], PS[:, 1, :], ACT.Square).then_inc(sq.sem, 1)

                def log_gate(u):
                    act.wait_ge(*tt(u + 1))
                    act.activation(lga[:, :], t1[:, :], ACT.Ln).then_inc(la.sem, 1)

                def late_part(u):
                    act.wait_ge(*dms(u + 1))
                    act.activation(dec[:, :], dd[:, :], ACT.Exp, scale=-1.0).then_inc(decs.sem, 1)
                    act.wait_ge(*kt(u + 1))
                    act.activation(kdt[:, :], PS[:, 6, :], ACT.Copy).then_inc(ktm.sem, 1)

                def scales(u):
                    for i, r in enumerate((rq, rk)):
                        act.wait_ge(*nrm(2 * u + i + 1))
                        act.activation(r[:, :], PS[:, 2 + i, :], ACT.Ln, scale=65536.0).then_inc(ln.sem, 1)
                    for i, r in enumerate((rq, rk)):
                        act.wait_ge(*ln(2 * u + i + 1))
                        act.activation(r[:, :], r[:, :], ACT.Exp, scale=-0.5, bias=ln256[:, :]).then_inc(rr.sem, 1)

                def outs(u):
                    act.wait_ge(*om(u + 1))
                    act.activation(oe[:, :], PS[:, 6, :], ACT.Copy).then_inc(oes.sem, 1)

                def decays(u, k):
                    act.wait_ge(*cm(u + 1))
                    act.activation(eq[:, k, :], cum[:, k, :], ACT.Exp, scale=-1.0).then_inc(eqs.sem, 1)
                    act.wait_ge(*tes(u + 1))
                    act.activation(de[:, :], te[:, :], ACT.Exp).then_inc(des.sem, 1)

                def batch(b, last):
                    for hp in range(HP):
                        u = b * HP + hp
                        more, ahead = not (last and hp == HP - 1), not (last and hp >= HP - 2)
                        if more:
                            log_gate(u + 1)
                        late_part(u)
                        if more:
                            decays(u + 1, (hp + 1) % 2)
                            scales(u + 1)
                        if hp == HP - 2 and not last:
                            act.wait_ge(*proj(b * 4 * HP + 4 * HP))
                            take_batch(b + 1)
                        if ahead:
                            early(u + 2, (hp + 2) % HP)
                        outs(u)

                take_batch(0)
                early(0, 0)
                log_gate(0)
                scales(0)
                decays(0, 0)
                early(1, 1)
                with act.Fori(0, B - 1) as b:
                    batch(b, False)
                batch(B - 1, True)

            @block.vector
            def _(dve):
                def pair_log(u):
                    dve.wait_ge(*lm(u + 1))
                    dve.tensor_tensor(chunks(dd[:, :]), chunks(PS[:, 4, :]),
                                      eye[:, :].unsqueeze(1).to_broadcast([128, NC, CH]), ALU.mult).then_inc(dst.sem, 1)
                    dve.wait_ge(*dst(3 * u + 1))
                    dve.tensor_reduce(dg[:, :], chunks(dd[:, :]), AX.X, ALU.add).then_inc(dst.sem, 1)
                    dve.wait_ge(*dst(3 * u + 2))
                    dve.tensor_tensor(chunks(dd[:, :]), chunks(PS[:, 4, :]),
                                      dg[:, :].unsqueeze(2).to_broadcast([128, NC, CH]), ALU.subtract)\
                        .then_inc(dst.sem, 1)

                def plus(u):
                    dve.wait_ge(*ex(u + 1))
                    dve.tensor_scalar(t1[:, :], e1[:, :], 1.0, 1e6, ALU.add, ALU.min).then_inc(tt.sem, 1)

                def weigh(u, k):
                    dve.wait_ge(*sc(u + 1))
                    dve.wait_ge(*decs(u + 1))
                    dve.tensor_tensor(ro[0:HALF, k, :], PS[0:HALF, 5, :], dec[0:HALF, :], ALU.mult).then_inc(am.sem, 1)
                    dve.tensor_tensor(re[HALF:128, k, :], PS[HALF:128, 5, :], dec[HALF:128, :], ALU.mult)\
                        .then_inc(am.sem, 1)

                def cumulate(u, k):
                    dve.wait_ge(*la(u + 1))
                    dve.tensor_tensor_scan(cum[:, k, :], reset[:, :], lga[:, :], 0.0, ALU.mult, ALU.add)\
                        .then_inc(cm.sem, 1)

                def chain(u, k, kl):
                    dve.wait_ge(*kv(u + 1))
                    for n in range(NC - 1):
                        if n:
                            dve.wait_ge(*st(14 * u + 2 * n))
                        for p, s in ((0, le), (HALF, lo)):
                            dve.scalar_tensor_tensor(out=s[p:p + HALF, kl, CH * n + CH:CH * n + 2 * CH],
                                                     in0=s[p:p + HALF, kl, CH * n:CH * n + CH],
                                                     scalar=eq[p:p + HALF, k, CH * n + CH - 1:CH * n + CH],
                                                     in1=PS[p:p + HALF, 4, CH * n:CH * n + CH],
                                                     op0=ALU.mult, op1=ALU.add).then_inc(st.sem, 1)

                def normalise(u, k):
                    for i, (r, to) in enumerate(((rq, qn), (rk, kn))):
                        dve.wait_ge(*rr(2 * u + i + 1))
                        dve.scalar_tensor_tensor(out=to[:, k, :], in0=r[:, :], scalar=1e12, in1=PS[:, i, :],
                                                 op0=ALU.min, op1=ALU.mult).then_inc(qk.sem, 1)

                def batch(b, last):
                    for hp in range(HP):
                        u = b * HP + hp
                        more = not (last and hp == HP - 1)
                        if more:
                            plus(u + 1)
                        pair_log(u)
                        if more:
                            cumulate(u + 1, (hp + 1) % 2)
                        weigh(u, hp % 2)
                        if more:
                            normalise(u + 1, (hp + 1) % 2)
                        chain(u, hp % 2, hp % LB)
                    dve.wait_ge(*acc(b * HP + HP))
                    zb = z[:, bass.ds(b, 1), :].rearrange("p a t -> p (a t)")
                    dve.tensor_tensor(zb, c.y[:, bass.ds(b, 1), :].rearrange("p a t -> p (a t)"), PS[:, 7, :], ALU.add)\
                        .then_inc(res.sem, 1)

                plus(0)
                cumulate(0, 0)
                normalise(0, 0)
                with dve.Fori(0, B - 1) as b:
                    batch(b, False)
                batch(B - 1, True)

            @block.gpsimd
            def _(pool):
                def mask(u):
                    pool.wait_ge(*dst(3 * u + 3))
                    pool.tensor_tensor(chunks(dd[:, :]), chunks(dd[:, :]),
                                       late[:, :].unsqueeze(1).to_broadcast([128, NC, CH]), ALU.add).then_inc(dms.sem, 1)

                def to_end(u, k):
                    pool.wait_ge(*cm(u + 1))
                    pool.tensor_tensor(chunks(te[:, :]), chunks(cum[:, k, :]),
                                       chunks(cum[:, k, :])[:, :, CH - 1:CH].to_broadcast([128, NC, CH]), ALU.subtract)\
                        .then_inc(tes.sem, 1)

                def decayed(u, k):
                    pool.wait_ge(*qk(2 * u + 2))
                    pool.wait_ge(*eqs(u + 1))
                    pool.wait_ge(*tes(u + 1))
                    pool.tensor_tensor(re[0:HALF, k, :], qn[0:HALF, k, :], eq[0:HALF, k, :], ALU.mult)\
                        .then_inc(qds.sem, 1)
                    pool.wait_ge(*qds(2 * u + 1))
                    pool.tensor_tensor(ro[HALF:128, k, :], qn[HALF:128, k, :], eq[HALF:128, k, :], ALU.mult)\
                        .then_inc(qds.sem, 1)
                    pool.wait_ge(*qds(2 * u + 2))
                    pool.wait_ge(*des(u + 1))
                    pool.tensor_tensor(kd[:, k, :], kn[:, k, :], de[:, :], ALU.mult).then_inc(kds.sem, 1)

                def batch(b, last):
                    for hp in range(HP):
                        u = b * HP + hp
                        mask(u)
                        if not (last and hp == HP - 1):
                            to_end(u + 1, (hp + 1) % 2)
                            decayed(u + 1, (hp + 1) % 2)

                to_end(0, 0)
                decayed(0, 0)
                with pool.Fori(0, B - 1) as b:
                    batch(b, False)
                batch(B - 1, True)
        U = B * HP
        for s, n in ((proj, 4 * U), (sq, 2 * U), (ex, U), (vm, 2 * U), (nrm, 2 * U), (ln, 2 * U), (rr, 2 * U), (tt, U),
                     (la, U), (cm, U), (eqs, U), (tes, U), (des, U), (qk, 2 * U), (kds, U), (qds, 2 * U), (lm, U),
                     (sc, U), (kt, U), (dst, 3 * U), (dms, U), (decs, U), (ktm, U), (kv, U), (am, 2 * U), (st, 14 * U),
                     (om, U), (oes, U), (acc, U), (res, B), (xbs, B)):
            s.close(n)

        hidden, bent, down, added = (c.semaphore_for(n) for n in ("f_hidden", "f_gelu", "f_down", "x_added"))
        M = FFN // 128
        ctx = ExitStack()
        with ctx:
            hb = c.sb("f_hb", [128, 4, T], F32, ctx)
            block = ctx.enter_context(nc.Block())

            def mlp_down(pe, k):
                b, m = k // M, k % M
                at = W_L1["f_w2"][0] + 128 * m
                pe.wait_ge(*bent(k + 1))
                pe.matmul(PS[:, 4 + b, :], c.w1[:, at:at + 128], hb[:, m, :], start=(m == 0), stop=(m == M - 1),
                          skip_group_check=True).then_inc(down.sem, 1)

            @block.tensor
            def _(pe):
                norm_pe(c, pe, z)
                for k in range(B * M):
                    b, m = k // M, k % M
                    pe.wait_ge(*scaled(b + 1))
                    if k == 0:
                        pe.wait_ge(*scaled(B))
                    if k >= 4:
                        pe.wait_ge(*bent(k - 3))
                    pe.matmul(PS[:, m, :], c.w1[:, W_L1["f_w1"][0] + 128 * m:W_L1["f_w1"][0] + 128 * m + 128],
                              c.y[:, b, :], start=True, stop=True).then_inc(hidden.sem, 1)
                    if k:
                        mlp_down(pe, k - 1)
                mlp_down(pe, B * M - 1)

            @block.scalar
            def _(act):
                act.preload_act_table_set("natural_log_exp_and_others")
                norm_act(c, act)
                for k in range(B * M):
                    act.wait_ge(*hidden(k + 1))
                    if k >= 4:
                        act.wait_ge(*down(k - 3))
                    act.activation(hb[:, k % M, :], PS[:, k % M, :], ACT.Gelu, bias=c.v("b1", k % M)).then_inc(bent.sem, 1)

            @block.vector
            def _(dve):
                norm_dve(c, dve, c.y, 0, c.v("ln2_w"), c.v("ln2_b"))
                for b in range(B):
                    dve.tensor_tensor(c.x[:, b, :], c.x[:, b, :], z[:, b, :], ALU.add).then_inc(added.sem, 1)
                for b in range(B):
                    dve.wait_ge(*down(M * (b + 1)))
                    dve.wait_ge(*added(b + 1))
                    dve.scalar_tensor_tensor(out=c.x[:, b, :], in0=PS[:, 4 + b, :], scalar=c.v("b2"), in1=c.x[:, b, :],
                                             op0=ALU.add, op1=ALU.add).then_inc(added.sem, 1)
                dve.wait_ge(*added(2 * B))
        norm_close(c, 1, 1)
        for s, n in ((hidden, B * M), (bent, B * M), (down, B * M), (added, 2 * B)):
            s.close(n)


def stage_context_mix(c, ins, scratch):
    nc, PS = c.nc, c.PS
    NT = B * TT
    came, normed, added = c.semaphore_for("w_came"), c.semaphore_for("ln_normed"), c.semaphore_for("x_added")
    rhs, side, sim, mxs, sub, exped, red = (c.semaphore_for("b_" + n) for n in (
        "weighted_ctx", "side", "similar", "max", "shifted", "exp", "reduced"))
    turned, moved, hats, hat, mixed = (c.semaphore_for("b_" + n) for n in ("turned", "moved", "hat_raw", "hat", "mixed"))
    peak, peaks = c.semaphore_for("b_peak"), c.semaphore_for("b_peak_steps")
    ctx = ExitStack()
    with ctx:
        cx = c.sb("b_ctx", [128, B, CT], F32, ctx)
        ck = c.sb("b_ctx_tok", [CT, B, D], F32, ctx)
        cr = c.sb("b_cr", [128, B, CT], F32, ctx)
        srow = c.sb("b_srow", [1, B, CT], F32, ctx)
        a = c.sb("b_a", [128, NT, CT], F32, ctx)
        mx = c.sb("b_mx", [128, NT], F32, ctx)
        rs = c.sb("b_rs", [128, 4, NT], F32, ctx)
        at = c.sb("b_at", [CT, B, T], F32, ctx)
        hq = c.sb("b_hq", [128, B, T], F32, ctx)
        eh = c.sb("b_eh", [128, B, T], F32, ctx)
        et = c.sb("b_et", [128, NT, D], F32, ctx)
        mt = c.sb("b_mt", [NT, 128], F32, ctx)
        mt1 = c.sb("b_mt1", [NT, 1], F32, ctx)
        m1 = c.sb("b_m1", [1, 2, NT], F32, ctx)
        hc = c.sb("b_hc", [128, B], F32, ctx)
        block = ctx.enter_context(nc.Block())
        SUMW = 4 * CT

        def per_batch(t):
            return t.rearrange("p (b k) -> p b k", b=B)

        @block.sync
        def _(sp):
            sp.dma_start(cx[:, :, :], ins["ctx"]).then_inc(came.sem, 16)
            sp.dma_start(ck[:, :, :], ins["ctx_tok"]).then_inc(came.sem, 16)

        @block.tensor
        def _(pe):
            pe.wait_ge(*came(32))
            pe.matmul(PS[0:1, 7, 0:B * CT], c.v("w2"), cx[:, :, :].rearrange("p b t -> p (b t)"), start=True, stop=True)\
                .then_inc(side.sem, 1)
            pe.wait_ge(*side(2))
            norm_pe(c, pe, c.x)
            pe.wait_ge(*normed(B))
            pe.wait_ge(*rhs(1))
            for b in range(B):
                for k in range(TT):
                    pe.matmul(PS[:, b, CT * k:CT * k + CT], c.y[:, b, 128 * k:128 * k + 128], cr[:, b, :],
                              start=True, stop=False)
                    mm = pe.matmul(PS[:, b, CT * k:CT * k + CT], c.ones[0:1, :], srow[:, b, :], start=False, stop=True)
                mm.then_inc(sim.sem, 1)
            for b in range(B):
                pe.wait_ge(*red(3 + b + 1))
                for k in range(TT):
                    mm = pe.transpose(PS[0:CT, 4 + b, 128 * k:128 * k + 128], a[:, TT * b + k, :], c.ident[:, :])
                mm.then_inc(turned.sem, 1)
            for b in range(B):
                pe.wait_ge(*moved(b + 1))
                pe.matmul(PS[:, b, :], ck[:, b, :], at[:, b, :], start=True, stop=True).then_inc(hats.sem, 1)
            for b in range(B):
                for k in range(TT):
                    mm = pe.transpose(PS[:, 4 + b, 128 * k:128 * k + 128], c.y[:, b, 128 * k:128 * k + 128], c.ident[:, :])
                mm.then_inc(turned.sem, 1)
            pe.wait_ge(*hat(1))
            pe.transpose(PS[0:NT, 0, 0:128], mx[:, :], c.ident[:, :]).then_inc(peak.sem, 1)
            pe.wait_ge(*peaks(1))
            pe.transpose(PS[0:1, 0, 128:128 + NT], mt1[:, :], c.ident[0:NT, 0:NT]).then_inc(peak.sem, 1)
            pe.wait_ge(*peaks(3))
            pe.matmul(PS[:, 0, 160:160 + NT], c.ones[0:1, :], m1[0:1, 1, :], start=True, stop=True).then_inc(peak.sem, 1)
            pe.wait_ge(*peaks(5))
            pe.matmul(PS[:, 0, 192:192 + NT], c.ones[:, :], rs[:, 2, :], start=True, stop=True).then_inc(peak.sem, 1)
            pe.wait_ge(*peaks(8))
            pe.wait_ge(*moved(2 * B))
            for b in range(B):
                for k in range(TT):
                    i = TT * b + k
                    mm = pe.matmul(PS[:, 0, 224 + b:225 + b], et[:, i, :], rs[:, 2, i:i + 1], start=(k == 0),
                                   stop=(k == TT - 1))
            mm.then_inc(peak.sem, 1)
            W = W_L1["w_qv"][0]
            for b in range(B):
                pe.wait_ge(*hat(2 * B + b + 1))
                for part, src in enumerate((c.y, hq, eh, c.sq)):
                    mm = pe.matmul(PS[:, 4 + b, :], c.w1[:, W + D * part:W + D * part + D], src[:, b, :],
                                   start=(part == 0), stop=(part == 3))
                mm.then_inc(mixed.sem, 1)

        @block.scalar
        def _(act):
            act.preload_act_table_set("natural_log_exp_and_others")
            norm_act(c, act)
            act.wait_ge(*sub(1))
            act.activation(a[:, :, :], a[:, :, :], ACT.Exp).then_inc(exped.sem, 1)
            for b in range(B):
                act.wait_ge(*turned(b + 1))
                act.activation(at[:, b, :], PS[0:CT, 4 + b, :], ACT.Copy).then_inc(moved.sem, 1)
            for b in range(B):
                act.wait_ge(*turned(B + b + 1))
                act.activation(et[:, TT * b:TT * b + TT, :], PS[:, 4 + b, :].rearrange("p (k d) -> p k d", k=TT), ACT.Copy)\
                    .then_inc(moved.sem, 1)
            act.wait_ge(*peaks(4))
            act.activation(rs[:, 2, :], rs[:, 2, :], ACT.Exp).then_inc(peaks.sem, 1)

        @block.vector
        def _(dve):
            dve.wait_ge(*came(32))
            dve.wait_ge(*side(1))
            bs = ROW["b_sim"][0]
            dve.tensor_scalar(srow[:, :, :], PS[0:1, 7, 0:B * CT].rearrange("p (b t) -> p b t", b=B),
                              c.rows[0:1, bs:bs + 1], None, ALU.add).then_inc(side.sem, 1)
            dve.tensor_scalar(cr[:, :, :], cx[:, :, :], c.v("w3"), c.v("w1"), ALU.mult, ALU.add).then_inc(rhs.sem, 1)
            norm_dve(c, dve, c.y)
            dve.wait_ge(*sim(B))
            sims = PS[:, 0:B, 0:SUMW].rearrange("p b (k t) -> p b k t", k=TT)
            dve.tensor_reduce(per_batch(mx[:, :]), sims, AX.X, ALU.max).then_inc(mxs.sem, 1)
            dve.wait_ge(*mxs(1))
            dve.tensor_tensor(a[:, :, :].rearrange("p (b k) t -> p b k t", b=B), sims,
                              per_batch(mx[:, :]).unsqueeze(3).to_broadcast([128, B, TT, CT]), ALU.subtract)\
                .then_inc(sub.sem, 1)
            dve.wait_ge(*exped(1))
            dve.tensor_reduce(rs[:, 0, :], a[:, :, :], AX.X, ALU.add).then_inc(red.sem, 1)
            dve.wait_ge(*red(1))
            dve.reciprocal(rs[:, 1, :], rs[:, 0, :]).then_inc(red.sem, 1)
            dve.wait_ge(*red(2))
            dve.tensor_copy(rs[:, 3, :], rs[:, 1, :]).then_inc(red.sem, 1)
            for b in range(B):
                dve.tensor_tensor(a[:, TT * b:TT * b + TT, :], a[:, TT * b:TT * b + TT, :],
                                  rs[:, 1, TT * b:TT * b + TT].unsqueeze(2).to_broadcast([128, TT, CT]), ALU.mult)\
                    .then_inc(red.sem, 1)
            for b in range(B):
                dve.wait_ge(*hats(b + 1))
                dve.tensor_copy(hq[:, b, :], PS[:, b, :]).then_inc(hat.sem, 1)
            dve.wait_ge(*peak(1))
            dve.tensor_reduce(mt1[:, :], PS[0:NT, 0, 0:128], AX.X, ALU.max).then_inc(peaks.sem, 1)
            dve.wait_ge(*peak(2))
            dve.tensor_reduce(m1[0:1, 0, 0:B], per_batch(PS[0:1, 0, 128:128 + NT]), AX.X, ALU.max).then_inc(peaks.sem, 1)
            dve.wait_ge(*peaks(2))
            dve.tensor_copy(per_batch(m1[0:1, 1, :]), m1[0:1, 0, 0:B].unsqueeze(2).to_broadcast([1, B, TT]))\
                .then_inc(peaks.sem, 1)
            dve.wait_ge(*peak(3))
            dve.tensor_tensor(rs[:, 2, :], mx[:, :], PS[:, 0, 160:160 + NT], ALU.subtract).then_inc(peaks.sem, 1)
            dve.wait_ge(*peak(4))
            dve.tensor_reduce(rs[:, 0, 0:B], per_batch(PS[:, 0, 192:192 + NT]), AX.X, ALU.add).then_inc(peaks.sem, 1)
            dve.wait_ge(*peaks(6))
            dve.reciprocal(rs[:, 0, 0:B], rs[:, 0, 0:B]).then_inc(peaks.sem, 1)
            dve.wait_ge(*peaks(7))
            dve.tensor_tensor(per_batch(rs[:, 2, :]), per_batch(rs[:, 2, :]),
                              rs[:, 0, 0:B].unsqueeze(2).to_broadcast([128, B, TT]), ALU.mult).then_inc(peaks.sem, 1)
            for b in range(B):
                dve.wait_ge(*hat(b + 1))
                dve.tensor_tensor(eh[:, b, :], c.y[:, b, :], hq[:, b, :], ALU.mult).then_inc(hat.sem, 1)
            dve.wait_ge(*peak(5))
            dve.tensor_copy(hc[:, :], PS[:, 0, 224:224 + B]).then_inc(peaks.sem, 1)
            dve.wait_ge(*peaks(9))
            for b in range(B):
                dve.tensor_scalar(c.sq[:, b, :], c.y[:, b, :], hc[:, b:b + 1], None, ALU.mult).then_inc(hat.sem, 1)
            for b in range(B):
                dve.wait_ge(*mixed(b + 1))
                dve.scalar_tensor_tensor(out=c.x[:, b, :], in0=PS[:, 4 + b, :], scalar=c.v("b_qv"), in1=c.x[:, b, :],
                                         op0=ALU.add, op1=ALU.add).then_inc(added.sem, 1)
            dve.wait_ge(*added(B))
    norm_close(c)
    for s, n in ((came, 32), (rhs, 1), (side, 2), (sim, B), (mxs, 1), (sub, 1), (exped, 1), (red, 3 + B), (turned, 2 * B),
                 (moved, 2 * B), (hats, B), (hat, 3 * B), (mixed, B), (peak, 5), (peaks, 9), (added, B)):
        s.close(n)


def stage_encoders(c, ins, scratch):
    nc, PS = c.nc, c.PS
    normed, made, added = c.semaphore_for("ln_normed"), c.semaphore_for("const_made"), c.semaphore_for("x_added")
    logit, pick, pexp, wide = (c.semaphore_for("e_" + n) for n in ("logits", "pick", "gate_exp", "gate_wide"))
    number = c.semaphore_for("e_number_stored")
    outer = ExitStack()
    with outer:
        wp = c.sb("e_wp", [128, PAIRS], F32, outer)
        num_i = c.sb("e_num", [1, PAIRS], I32, outer)
        values = c.sb("e_values", [128, PAIRS, TT, H, 9], F32, outer)
        ctx = ExitStack()
        with ctx:
            mean = c.sb("e_mean", [128, B], F32, ctx)
            lg = c.sb("e_lg", [1, B, EX], F32, ctx)
            gp = c.sb("e_gp", [1, B, EX], F32, ctx)
            cmp = c.sb("e_cmp", [1, B, EX, EX], F32, ctx)
            eq = c.sb("e_eq", [1, B, EX, EX], F32, ctx)
            low = c.sb("e_low", [1, EX, EX], F32, ctx)
            iot = c.sb("e_iota", [1, B, EX], F32, ctx)
            sel = c.sb("e_sel", [1, B, EX], F32, ctx)
            t4 = c.sb("e_t4", [1, B, EX], F32, ctx)
            sm = c.sb("e_sm", [1, 4, B], F32, ctx)
            nf = c.sb("e_nf", [1, B, PICK], F32, ctx)
            wf = c.sb("e_wf", [1, B, PICK], F32, ctx)
            block = ctx.enter_context(nc.Block())

            @block.gpsimd
            def _(pool):
                pool.memset(low[:, :, :], 1.0).then_inc(made.sem, 1)
                for e in range(EX):
                    pool.memset(iot[:, :, e:e + 1], float(e)).then_inc(made.sem, 1)
                pool.memset(values[:, :, :, :, 8:9], 1.0).then_inc(made.sem, 1)
                pool.wait_ge(*made(2 + EX))
                pool.affine_select(out=low[:, :, :], in_=low[:, :, :], compare_op=ALU.is_ge, fill=0.0, base=-1,
                                   pattern=[[1, EX], [-1, EX]], channel_multiplier=0).then_inc(made.sem, 1)
                pool.wait_ge(*made(3 + EX))

            @block.tensor
            def _(pe):
                norm_pe(c, pe, c.x)
                pe.wait_ge(*pick(B))
                gw = W_L1["gate_w"][0]
                for b in range(B):
                    mm = pe.matmul(PS[0:1, 0, EX * b:EX * b + EX], mean[:, b:b + 1], c.w1[:, gw:gw + EX],
                                   start=True, stop=True)
                mm.then_inc(logit.sem, 1)
                pe.wait_ge(*wide(1))
                pe.matmul(PS[:, 1, 0:PAIRS], c.ones[0:1, :], wf[:, :, :].rearrange("p b k -> p (b k)"), start=True,
                          stop=True).then_inc(logit.sem, 1)

            @block.scalar
            def _(act):
                act.preload_act_table_set("natural_log_exp_and_others")
                norm_act(c, act)
                act.wait_ge(*pick(B + 3))
                act.activation(gp[:, :, :], gp[:, :, :], ACT.Exp).then_inc(pexp.sem, 1)

            @block.vector
            def _(dve):
                norm_dve(c, dve, c.y)
                for b in range(B):
                    dve.wait_ge(*normed(b + 1))
                    dve.tensor_reduce(mean[:, b:b + 1], c.y[:, b, :], AX.X, ALU.add).then_inc(pick.sem, 1)
                dve.wait_ge(*logit(1))
                dve.wait_ge(*made(3 + EX))
                gb = ROW["gate_b"][0]
                dve.scalar_tensor_tensor(out=lg[:, :, :], in0=PS[0:1, 0, 0:B * EX].rearrange("p (b e) -> p b e", e=EX),
                                         scalar=1.0 / T, in1=c.rows[0:1, gb:gb + EX].unsqueeze(1).to_broadcast([1, B, EX]),
                                         op0=ALU.mult, op1=ALU.add).then_inc(pick.sem, 1)
                dve.wait_ge(*pick(B + 1))
                dve.tensor_reduce(sm[:, 0, :], lg[:, :, :], AX.X, ALU.max).then_inc(pick.sem, 1)
                dve.wait_ge(*pick(B + 2))
                dve.tensor_tensor(gp[:, :, :], lg[:, :, :], sm[:, 0, :].unsqueeze(2).to_broadcast([1, B, EX]),
                                  ALU.subtract).then_inc(pick.sem, 1)
                other = lg[:, :, :].unsqueeze(2).to_broadcast([1, B, EX, EX])
                own = lg[:, :, :].unsqueeze(3).to_broadcast([1, B, EX, EX])
                dve.tensor_tensor(cmp[:, :, :, :], other, own, ALU.is_gt).then_inc(pick.sem, 1)
                dve.tensor_tensor(eq[:, :, :, :], other, own, ALU.is_equal).then_inc(pick.sem, 1)
                dve.wait_ge(*pick(B + 5))
                dve.tensor_tensor(eq[:, :, :, :], eq[:, :, :, :], low[:, :, :].unsqueeze(1).to_broadcast([1, B, EX, EX]),
                                  ALU.mult).then_inc(pick.sem, 1)
                dve.wait_ge(*pick(B + 6))
                dve.tensor_tensor(cmp[:, :, :, :], cmp[:, :, :, :], eq[:, :, :, :], ALU.add).then_inc(pick.sem, 1)
                dve.wait_ge(*pick(B + 7))
                dve.tensor_reduce(t4[:, :, :], cmp[:, :, :, :], AX.X, ALU.add).then_inc(pick.sem, 1)
                dve.wait_ge(*pick(B + 8))
                dve.tensor_scalar(sel[:, :, :], t4[:, :, :], PICK - 0.5, None, ALU.is_lt).then_inc(pick.sem, 1)
                dve.wait_ge(*pick(B + 9))
                dve.tensor_tensor(t4[:, :, :], sel[:, :, :], iot[:, :, :], ALU.mult).then_inc(pick.sem, 1)
                dve.wait_ge(*pick(B + 10))
                dve.tensor_reduce(nf[:, :, 1], t4[:, :, :], AX.X, ALU.max).then_inc(pick.sem, 1)
                dve.wait_ge(*pick(B + 11))
                dve.tensor_scalar(t4[:, :, :], iot[:, :, :], -1.0, float(EX), ALU.mult, ALU.add).then_inc(pick.sem, 1)
                dve.wait_ge(*pick(B + 12))
                dve.tensor_tensor(t4[:, :, :], t4[:, :, :], sel[:, :, :], ALU.mult).then_inc(pick.sem, 1)
                dve.wait_ge(*pick(B + 13))
                dve.tensor_reduce(nf[:, :, 0], t4[:, :, :], AX.X, ALU.max).then_inc(pick.sem, 1)
                dve.wait_ge(*pick(B + 14))
                dve.tensor_scalar(nf[:, :, 0], nf[:, :, 0], -1.0, float(EX), ALU.mult, ALU.add).then_inc(pick.sem, 1)
                dve.wait_ge(*pick(B + 15))
                dve.tensor_copy(num_i[:, :], nf[:, :, :].rearrange("p b k -> p (b k)")).then_inc(pick.sem, 1)
                dve.wait_ge(*pexp(1))
                dve.tensor_reduce(sm[:, 1, :], gp[:, :, :], AX.X, ALU.add).then_inc(pick.sem, 1)
                dve.wait_ge(*pick(B + 17))
                dve.reciprocal(sm[:, 2, :], sm[:, 1, :]).then_inc(pick.sem, 1)
                dve.wait_ge(*pick(B + 18))
                dve.tensor_tensor(gp[:, :, :], gp[:, :, :], sm[:, 2, :].unsqueeze(2).to_broadcast([1, B, EX]), ALU.mult)\
                    .then_inc(pick.sem, 1)
                dve.wait_ge(*pick(B + 19))
                for k in range(PICK):
                    dve.tensor_tensor(t4[:, :, :], iot[:, :, :], nf[:, :, k:k + 1].to_broadcast([1, B, EX]), ALU.is_equal)\
                        .then_inc(pick.sem, 1)
                    dve.wait_ge(*pick(B + 20 + 3 * k))
                    dve.tensor_tensor(t4[:, :, :], t4[:, :, :], gp[:, :, :], ALU.mult).then_inc(pick.sem, 1)
                    dve.wait_ge(*pick(B + 21 + 3 * k))
                    dve.tensor_reduce(wf[:, :, k], t4[:, :, :], AX.X, ALU.add).then_inc(pick.sem, 1)
                    dve.wait_ge(*pick(B + 22 + 3 * k))
                dve.nop().then_inc(wide.sem, 1)
                dve.wait_ge(*logit(2))
                dve.tensor_copy(wp[:, :], PS[:, 1, 0:PAIRS]).then_inc(wide.sem, 1)
                dve.wait_ge(*wide(2))
        norm_close(c)
        for s, n in ((logit, 2), (pick, B + 25), (pexp, 1), (wide, 2), (made, 3 + EX)):
            s.close(n)

        slot_came = [c.semaphore_for("e_slot_even"), c.semaphore_for("e_slot_odd")]
        stored = [c.semaphore_for("s_stored_q"), c.semaphore_for("s_stored_k")]
        proj, bias, hi, rest, mid, last, vals = (c.semaphore_for(n) for n in (
            "e_proj", "e_biased", "s_high", "s_rest", "s_middle", "s_last", "at_values"))
        NV = W_EX["bq"][0]
        NQ = 3 * D
        ctx = ExitStack()
        with ctx:
            ws = c.sb("e_ws", [128, 2, NQ], F32, ctx)
            bs = c.sb("e_bs", [128, 2, 2], F32, ctx)
            bv = c.sb("e_bv", [128, 2, D], F32, ctx)
            qkf = c.sb("e_qkf", [128, 2, T], F32, ctx)
            res = c.sb("e_res", [128, 2, T], F32, ctx)
            parts = c.sb("e_parts", [128, 2, PARTS, T], BF16, ctx)
            block = ctx.enter_context(nc.Block())

            @block.sync
            def _(sp):
                def load(n):
                    if n >= 2:
                        sp.wait_ge(*bias(2 * n - 2))
                        sp.wait_ge(*vals(n - 1))
                    e = sp.value_load(num_i[0:1, n:n + 1], min_val=0, max_val=EX - 1)
                    src = ins["w_ex"][bass.ds(e, 1), :, :].rearrange("a p n -> (a p) n")
                    sp.dma_start(ws[:, n % 2, :], src[:, 0:NQ]).then_inc(slot_came[n % 2].sem, 16)
                    sp.dma_start(bs[:, n % 2, :], src[:, NV:NV + 2]).then_inc(slot_came[n % 2].sem, 16)
                    sp.dma_start(bv[:, n % 2, :], ins["bv_ex"][bass.ds(e, 1), :].to_broadcast([128, D]))\
                        .then_inc(slot_came[n % 2].sem, 16)

                load(0)
                for n in range(PAIRS):
                    if n + 1 < PAIRS:
                        load(n + 1)
                    for k, dest in enumerate((scratch["q_parts"], scratch["k_parts"])):
                        sp.wait_ge(*last(2 * n + k + 1))
                        sp.dma_start(dram_view(dest, n * PARTS * D * T, [(T, 128), (D * T, PARTS), (1, T)]),
                                     parts[:, k, :, :]).then_inc(stored[k].sem, 16)
                for s in stored:
                    sp.wait_ge(*s(16 * PAIRS))

            @block.tensor
            def _(pe):
                for n in range(PAIRS):
                    o = 3 * (n % 2)
                    pe.wait_ge(*slot_came[n % 2](48 * (n // 2 + 1)))
                    if n >= 2:
                        pe.wait_ge(*bias(2 * n - 2))
                        pe.wait_ge(*vals(n - 1))
                    yb = c.y[:, n // PICK, :]
                    pe.matmul(PS[:, o, :], ws[:, n % 2, 0:D], yb, start=True, stop=True).then_inc(proj.sem, 1)
                    pe.matmul(PS[:, o + 1, :], ws[:, n % 2, D:2 * D], yb, start=True, stop=True).then_inc(proj.sem, 1)
                    for kt in range(TT):
                        mm = pe.matmul(PS[:, o + 2, 128 * kt:128 * kt + 128], yb[:, 128 * kt:128 * kt + 128],
                                       ws[:, n % 2, 2 * D:3 * D], start=True, stop=True)
                    mm.then_inc(proj.sem, 1)

            @block.scalar
            def _(act):
                for u in range(2 * PAIRS):
                    act.wait_ge(*bias(u + 1))
                    if u >= 2:
                        act.wait_ge(*stored[u % 2](16 * (u // 2)))
                    act.activation(parts[:, u % 2, 0, :], qkf[:, u % 2, :], ACT.Copy).then_inc(hi.sem, 1)
                    act.wait_ge(*rest(u + 1))
                    act.activation(parts[:, u % 2, 1, :], res[:, u % 2, :], ACT.Copy).then_inc(mid.sem, 1)

            @block.vector
            def _(dve):
                for n in range(PAIRS):
                    o = 3 * (n % 2)
                    for k in range(2):
                        u = 2 * n + k
                        dve.wait_ge(*proj(3 * n + k + 1))
                        dve.tensor_scalar(qkf[:, k, :], PS[:, o + k, :], bs[:, n % 2, k:k + 1],
                                          float(HD) ** -0.5 if k == 0 else 1.0, ALU.add, ALU.mult).then_inc(bias.sem, 1)
                    dve.wait_ge(*proj(3 * n + 3))
                    dve.tensor_tensor(values[:, n, :, :, 0:8], PS[:, o + 2, :].rearrange("p (k h d) -> p k h d", k=TT, d=HD),
                                      bv[:, n % 2, :].rearrange("p (h d) -> p h d", d=HD).unsqueeze(1)
                                      .to_broadcast([128, TT, H, HD]), ALU.add).then_inc(vals.sem, 1)
                    for k in range(2):
                        u = 2 * n + k
                        dve.wait_ge(*hi(u + 1))
                        dve.tensor_tensor(res[:, k, :], qkf[:, k, :], parts[:, k, 0, :], ALU.subtract).then_inc(rest.sem, 1)
                        dve.wait_ge(*mid(u + 1))
                        dve.tensor_tensor(parts[:, k, 2, :], res[:, k, :], parts[:, k, 1, :], ALU.subtract)\
                            .then_inc(last.sem, 1)

        P2 = PAIRS // 2
        for s, n in ((slot_came[0], 48 * P2), (slot_came[1], 48 * P2), (proj, 3 * PAIRS), (bias, 2 * PAIRS),
                     (hi, 2 * PAIRS), (rest, 2 * PAIRS), (mid, 2 * PAIRS), (last, 2 * PAIRS), (vals, PAIRS),
                     (stored[0], 16 * PAIRS), (stored[1], 16 * PAIRS)):
            s.close(n)

        softmax_core(c, PAIRS, scratch["q_parts"], scratch["k_parts"], scratch["max_rows"],
                     scratch["sums"], values)

        SLOTS = 2 * PICK
        came = [c.semaphore_for(f"e_layer{k}") for k in range(SLOTS)]
        prod = [c.semaphore_for(f"e_products{k}") for k in range(PICK)]
        curve = [c.semaphore_for(f"e_curves{k}") for k in range(PICK)]
        vec = [c.semaphore_for(f"e_sums{k}") for k in range(PICK)]
        NP, NA, NVS = 13, 10, 9
        NR = N_WX - 3 * D
        M = FFN // 128
        ctx = ExitStack()
        with ctx:
            wl = c.sb("e_wl", [128, SLOTS, NR], F32, ctx)
            num = c.sb("e_o_num", [128, SLOTS, T], F32, ctx)
            den = c.sb("e_o_den", [128, SLOTS, T], F32, ctx)
            t1 = c.sb("e_t1", [128, PICK, T], F32, ctx)
            sq = c.sb("e_sq", [128, PICK, T], F32, ctx)
            x1 = c.sb("e_x1", [128, PICK, T], F32, ctx)
            hb = c.sb("e_hb", [128, PICK, M, T], F32, ctx)
            block = ctx.enter_context(nc.Block())

            def at(name, slot, k=0, n=128):
                a = W_EX[name][0] - 3 * D + k
                return wl[:, slot, a:a + n]

            def batches(e, emit):
                with e.Fori(0, B // 2) as j:
                    for half in range(2):
                        emit(2 * j + half, half, j)

            @block.sync
            def _(sp):
                def load(b, half, j):
                    for k in range(PICK):
                        slot = PICK * half + k
                        n = PICK * b + k
                        e = sp.value_load(num_i[0:1, bass.ds(n, 1)], min_val=0, max_val=EX - 1)
                        src = ins["w_ex"][bass.ds(e, 1), :, :].rearrange("a p n -> (a p) n")
                        sp.dma_start(wl[:, slot, :], src[:, 3 * D:N_WX]).then_inc(came[slot].sem, 16)
                        for r in range(4):
                            rows = 9 * G
                            at_row = n * 4 * rows + r * rows
                            sp.dma_start(num[32 * r:32 * r + 32, slot, :], scratch["sums"][bass.ds(at_row, 32), :])\
                                .then_inc(came[slot].sem, 16)
                            sp.dma_start(den[32 * r:32 * r + 32, slot, :],
                                         scratch["sums"][bass.ds(at_row + 8 * G, G), :].unsqueeze(0)
                                         .to_broadcast([8, G, T])).then_inc(came[slot].sem, 16)

                for b in range(2):
                    load(b, b, 0)
                for b in range(2, B):
                    for k in range(PICK):
                        sp.wait_ge(*vec[k](NVS * (b - 1)))
                    load(b, b % 2, 0)

            def item_came(e, b, half, k, j):
                e.wait_ge(*came[PICK * half + k](16 * 9 * j + 16 * 9))

            @block.tensor
            def _(pe):
                def mm(k, bank, left, right, start=True, stop=True):
                    pe.matmul(PS[:, 4 * k + bank, :], left, right, start=start, stop=stop,
                              skip_group_check=True).then_inc(prod[k].sem, 1)

                def batch(b, half, j):
                    both = range(PICK)
                    slot = lambda k: PICK * half + k
                    for k in both:
                        item_came(pe, b, half, k, j)
                        pe.wait_ge(*vec[k](NVS * b + 2))
                        mm(k, 0, at("wo", slot(k)), num[:, slot(k), :])
                    for k in both:
                        pe.wait_ge(*vec[k](NVS * b + 3))
                        mm(k, 1, c.center[:, :], t1[:, k, :])
                    for k in both:
                        pe.wait_ge(*curve[k](NA * b + 1))
                        mm(k, 2, c.mean[:, :], sq[:, k, :])
                    for k in both:
                        pe.wait_ge(*vec[k](NVS * b + 5))
                        mm(k, 0, at("l1", slot(k), 0), x1[:, k, :])
                        mm(k, 2, at("l1", slot(k), 128), x1[:, k, :])
                    for m in range(2):
                        for k in both:
                            pe.wait_ge(*curve[k](NA * b + 4 + m))
                            mm(k, 3, at("l2", slot(k), 128 * m), hb[:, k, m, :], m == 0, False)
                            mm(k, 2 * m, at("l1", slot(k), 128 * (m + 2)), x1[:, k, :])
                    for m in range(2, M):
                        for k in both:
                            pe.wait_ge(*curve[k](NA * b + 4 + m))
                            mm(k, 3, at("l2", slot(k), 128 * m), hb[:, k, m, :], False, m == M - 1)
                    for k in both:
                        pe.wait_ge(*vec[k](NVS * b + 6))
                        mm(k, 1, c.center[:, :], t1[:, k, :])
                    for k in both:
                        pe.wait_ge(*curve[k](NA * b + 8))
                        mm(k, 2, c.mean[:, :], sq[:, k, :])

                batches(pe, batch)

            @block.scalar
            def _(act):
                act.preload_act_table_set("natural_log_exp_and_others")

                def batch(b, half, j):
                    both = range(PICK)

                    def norm(first, centre, spread):
                        for k in both:
                            act.wait_ge(*prod[k](NP * b + centre))
                            act.activation(sq[:, k, :], PS[:, 4 * k + 1, :], ACT.Square).then_inc(curve[k].sem, 1)
                        for k in both:
                            act.wait_ge(*prod[k](NP * b + spread))
                            act.activation(sq[:, k, :], PS[:, 4 * k + 2, :], ACT.Ln, bias=c.eps[:, :])\
                                .then_inc(curve[k].sem, 1)
                        for k in both:
                            act.wait_ge(*curve[k](NA * b + first + 1))
                            act.activation(sq[:, k, :], sq[:, k, :], ACT.Exp, scale=-0.5).then_inc(curve[k].sem, 1)

                    norm(1, 2, 3)
                    for m, up in enumerate((4, 5, 7, 9)):
                        for k in both:
                            act.wait_ge(*prod[k](NP * b + up))
                            act.activation(hb[:, k, m, :], PS[:, 4 * k + 2 * (m % 2), :], ACT.Relu,
                                           bias=at("l1b", PICK * half + k, m, 1)).then_inc(curve[k].sem, 1)
                    norm(8, 12, 13)

                batches(act, batch)

            @block.vector
            def _(dve):
                def batch(b, half, j):
                    both = range(PICK)
                    slot = lambda k: PICK * half + k
                    yb = c.y[:, bass.ds(b, 1), :].rearrange("p a t -> p (a t)")
                    xb = c.x[:, bass.ds(b, 1), :].rearrange("p a t -> p (a t)")
                    for k in both:
                        item_came(dve, b, half, k, j)
                        dve.reciprocal(den[:, slot(k), :], den[:, slot(k), :]).then_inc(vec[k].sem, 1)
                    for k in both:
                        dve.wait_ge(*vec[k](NVS * b + 1))
                        dve.tensor_tensor(num[:, slot(k), :], num[:, slot(k), :], den[:, slot(k), :], ALU.mult)\
                            .then_inc(vec[k].sem, 1)
                    for k in both:
                        dve.wait_ge(*prod[k](NP * b + 1))
                        dve.scalar_tensor_tensor(out=t1[:, k, :], in0=PS[:, 4 * k, :], scalar=at("ob", slot(k), 0, 1),
                                                 in1=yb, op0=ALU.add, op1=ALU.add).then_inc(vec[k].sem, 1)

                    def norm(curves, done, w, shift):
                        for k in both:
                            dve.wait_ge(*curve[k](NA * b + curves))
                            dve.tensor_tensor(x1[:, k, :], PS[:, 4 * k + 1, :], sq[:, k, :], ALU.mult)\
                                .then_inc(vec[k].sem, 1)
                        for k in both:
                            dve.wait_ge(*vec[k](NVS * b + done))
                            dve.tensor_scalar(x1[:, k, :], x1[:, k, :], at(w, slot(k), 0, 1), at(shift, slot(k), 0, 1),
                                              ALU.mult, ALU.add).then_inc(vec[k].sem, 1)

                    norm(3, 4, "n1w", "n1b")
                    for k in both:
                        dve.wait_ge(*prod[k](NP * b + 11))
                        dve.wait_ge(*vec[k](NVS * b + 5))
                        dve.scalar_tensor_tensor(out=t1[:, k, :], in0=PS[:, 4 * k + 3, :], scalar=at("l2b", slot(k), 0, 1),
                                                 in1=x1[:, k, :], op0=ALU.add, op1=ALU.add).then_inc(vec[k].sem, 1)
                    norm(10, 7, "n2w", "n2b")
                    for k in both:
                        dve.wait_ge(*vec[k](NVS * b + 8))
                        if k:
                            dve.wait_ge(*vec[k - 1](NVS * b + 9))
                        dve.scalar_tensor_tensor(out=xb, in0=x1[:, k, :], scalar=wp[:, bass.ds(PICK * b + k, 1)],
                                                 in1=xb, op0=ALU.mult, op1=ALU.add).then_inc(vec[k].sem, 1)

                batches(dve, batch)
        for s in came:
            s.close(16 * 9 * B // 2)
        for k in range(PICK):
            prod[k].close(NP * B)
            curve[k].close(NA * B)
            vec[k].close(NVS * B)


def stage_out(c, out):
    written = c.semaphore_for("out_written")
    with c.nc.Block() as block:
        @block.sync
        def _(sp):
            sp.dma_start(out, c.x[:, :, :]).then_inc(written.sem, 16)
            sp.wait_ge(*written(16))


def decoder(nc, ins, out, upto=6, since=0):
    scratch = {
        "q_parts": nc.dram_tensor("q_parts", (PAIRS * PARTS * D, T), BF16).ap(),
        "k_parts": nc.dram_tensor("k_parts", (PAIRS * PARTS * D, T), BF16).ap(),
        "sums": nc.dram_tensor("head_sums", (PAIRS * 4 * 9 * (H // 4), T), F32).ap(),
        "combine": nc.dram_tensor("combine", (NE, B * T), F32).ap(),
        "max_rows": nc.dram_tensor("max_rows", (PAIRS * H, T), BF16).ap(),
    }
    ctx = ExitStack()
    with ctx:
        c = Chip(ctx, nc)
        stage_setup(c, ins)
        stages = [stage_linear_attention, stage_cross_attention, stage_experts,
                  stage_gated_attention, stage_context_mix, stage_encoders]
        for stage in stages[since:upto]:
            stage(c, ins, scratch)
        stage_out(c, out)


_INPUTS = ("x", "vec", "rows", "w_l0", "w_l1", "w_ex", "bv_ex", "moe", "ctx", "ctx_tok", "pad_mask", "sub_mask",
           "perm")


def arrange(i):
    import numpy as np
    a = {k: np.asarray(v) for k, v in i.items()}
    dh = np.arange(D).reshape(H, HD).T.reshape(-1)
    jrg = np.arange(D).reshape(H // 4, 4, HD).transpose(1, 2, 0).reshape(-1)
    col = lambda v: v.reshape(-1, 128).T
    put = np.concatenate
    A, G, E = "L0_attn_", "L1_attn_", "L1_ffn_"
    bqkv, wqkv = a[A + "b_qkv"], a[A + "w_qkv"]
    vec = put([col(a[A + "ln_g"]), col(a[A + "ln_b"]), col(bqkv[:D][dh]), col(bqkv[D:2 * D][dh]),
               col(a[A + "b_gate"][dh]), col(a[A + "b_proj"]), col(a["L0_xattn_bq"]), col(a["L0_xattn_bk"]),
               col(a[G + "bg"]), col(a[G + "ln1_w"]), col(a[G + "ln1_b"]), col(a[G + "ln2_w"]), col(a[G + "ln2_b"]),
               col(a[G + "b1"]), col(a[G + "b2"]), col(a["L1_xattn_w_sim"]), col(a["L1_xattn_b_qv"])], 1)
    rows = put([bqkv[2 * D:], a["L0_xattn_bv"], a["L0_ffn_expert_bias"], a[E + "gate_b"], a["L1_xattn_b_sim"]])
    w_l0 = put([wqkv[:, :D][:, dh], wqkv[:, D:2 * D][:, dh], wqkv[:, 2 * D:], a[A + "w_gate"][:, dh],
                a[A + "w_proj"][jrg], a["L0_xattn_Wq"].T, a["L0_xattn_Wk"].T, a["L0_xattn_Wv"].T,
                a["L0_ffn_router_w"].T], 1)
    tiles = lambda w: w.reshape(-1, 128, w.shape[1]).transpose(1, 0, 2).reshape(128, -1)
    w_l1 = put([a[G + "Wq"], a[G + "Wk"], a[G + "Wv"], a[G + "Wg"], tiles(a[G + "Wo"]), a[G + "W1"],
                tiles(a[G + "W2"]), tiles(a["L1_xattn_W_qv"]), a[E + "gate_w"].T], 1)
    w_ex, bv_ex = [], []
    for e in range(EX):
        iw, ib = a[E + "in_proj_w"][e], a[E + "in_proj_b"][e]
        w_ex.append(put([iw[:D][dh].T, iw[D:2 * D][dh].T, iw[2 * D:].T, a[E + "out_proj_w"][e].T[jrg],
                         a[E + "lin1_w"][e].T, tiles(a[E + "lin2_w"][e].T), col(ib[:D][dh]), col(ib[D:2 * D][dh]),
                         col(a[E + "out_proj_b"][e]), col(a[E + "ln1_w"][e]), col(a[E + "ln1_b"][e]),
                         col(a[E + "lin1_b"][e]), col(a[E + "lin2_b"][e]), col(a[E + "ln2_w"][e]),
                         col(a[E + "ln2_b"][e])], 1))
        bv_ex.append(ib[2 * D:])
    M = "L0_ffn_"
    moe = []
    for w1, w3, w2 in ((a[M + "sw1"], a[M + "sw3"], a[M + "sw2"]), (a[M + "w1"], a[M + "w3"], a[M + "w2"])):
        for e in range(len(w1)):
            moe.append(put([w1[e].T, w3[e].T, tiles(w2[e].T)], 1))
    out = {
        "x": a["x"].transpose(2, 0, 1), "vec": vec, "rows": rows, "w_l0": w_l0, "w_l1": w_l1,
        "w_ex": np.stack(w_ex), "bv_ex": np.stack(bv_ex), "moe": np.stack(moe),
        "ctx": a["ctx_1024"].transpose(2, 0, 1), "ctx_tok": a["ctx_1024"].transpose(1, 0, 2),
        "pad_mask": a["mask_Bx1x1xS2_ik0"].reshape(B, CT), "sub_mask": a["mask_1x1xSxS2_ik0"].reshape(T, CT),
        "perm": np.eye(D, dtype=np.float32)[jrg],
    }
    return {k: np.ascontiguousarray(v) for k, v in out.items()}


def kernel(**inputs):
    import numpy as np
    import concourse.bacc as bacc
    from concourse import mybir as my
    from concourse.bass_utils import run_bass_kernel_spmd as run

    nc = bacc.Bacc("TRN2", target_bir_lowering=False, num_devices=1)
    arrays = arrange(inputs)
    aps = {k: nc.dram_tensor(f"in_{k}", arrays[k].shape, my.dt.from_np(arrays[k].dtype), kind="ExternalInput").ap()
           for k in _INPUTS}
    out = nc.dram_tensor("out_x", (D, B, T), F32, kind="ExternalOutput").ap()
    decoder(nc, aps, out)
    r = run(nc, [{f"in_{k}": arrays[k] for k in _INPUTS}], core_ids=[0])
    return np.ascontiguousarray(r.results[0]["out_x"].transpose(1, 2, 0))
```

```python
from contextlib import ExitStack

import concourse.bass as bass
from concourse import mybir

F32 = mybir.dt.float32
BF16 = mybir.dt.bfloat16
I32 = mybir.dt.int32
ALU = mybir.AluOpType
ACT = mybir.ActivationFunctionType
AX = mybir.AxisListType

B, T, D = 4, 512, 128
CT = 77
H, HD = 16, 8
TT = T // 128
NE, HID = 8, 256
NSH = 2
GH, GD = 16, 64
HP = GH // 2
CH = 64
NC = T // CH
FFN = 512
EX, PICK = 4, 2
PAIRS = B * PICK
EPS = 1e-5
HALF = 64

VEC = {}


def _columns(table, *names):
    at = 0
    for name, n in names:
        table[name] = (at, n)
        at += n
    return at


N_VEC = _columns(VEC, ("ln_g", 1), ("ln_b", 1), ("a_bq", 1), ("a_bk", 1), ("b_gate", 1), ("b_proj", 1),
                 ("x_bq", 1), ("x_bk", 1), ("bg", HP), ("ln1_w", 1), ("ln1_b", 1), ("ln2_w", 1),
                 ("ln2_b", 1), ("b1", FFN // 128), ("b2", 1), ("w1", 1), ("w2", 1), ("w3", 1), ("b_qv", 1))
W_L0 = {}
N_W0 = _columns(W_L0, ("a_wq", D), ("a_wk", D), ("a_wv", D), ("w_gate", D), ("w_proj", D),
                ("x_wq", D), ("x_wk", D), ("x_wv", D), ("router", NE))
W_L1 = {}
N_W1 = _columns(W_L1, ("g_wq", HP * 128), ("g_wk", HP * 128), ("g_wv", HP * 128), ("g_wg", HP * 128),
                ("g_wo", HP * 128), ("f_w1", FFN), ("f_w2", FFN), ("w_qv", 4 * D), ("gate_w", EX))
W_EX = {}
N_WX = _columns(W_EX, ("wq", D), ("wk", D), ("wv", D), ("wo", D), ("l1", FFN), ("l2", FFN),
                ("bq", 1), ("bk", 1), ("ob", 1), ("n1w", 1), ("n1b", 1), ("l1b", FFN // 128), ("l2b", 1),
                ("n2w", 1), ("n2b", 1))
ROW = {}
N_ROW = _columns(ROW, ("a_bv", D), ("x_bv", D), ("router_b", NE), ("gate_b", EX), ("b_sim", 1))
ME = {}
N_ME = _columns(ME, ("w1", HID), ("w3", HID), ("w2", 2 * D))

PARTS = 3
SPLIT = PARTS * PARTS * HD
MAXROW = SPLIT
KROWS = MAXROW + 1


class Signal:

    def __init__(self, ctx, nc, name):
        self.sem = ctx.enter_context(nc.semaphore(name))
        self.base = 0

    def __call__(self, n):
        return self.sem, self.base + n

    def close(self, n):
        self.base += n


def dram_view(t, offset, dims):
    return bass.AP(t.tensor, t.offset + offset, [list(d) for d in dims])


class Chip:

    def __init__(self, ctx, nc):
        self.ctx, self.nc = ctx, nc
        self.signals, self.named = {}, {}
        self.PS = ctx.enter_context(nc.psum_tensor("PS", [128, 8, 512], F32))
        self.x = self.sb("x_res", [128, B, T])
        self.y = self.sb("y_norm", [128, B, T])
        self.sq = self.sb("ln_sq", [128, B, T])
        self.rs = self.sb("ln_rs", [128, B, T])
        self.vec = self.sb("vec", [128, N_VEC])
        self.w1 = self.sb("w_l1", [128, N_W1])
        self.rows = self.sb("rows", [128, N_ROW])
        self.center = self.sb("center", [128, 128])
        self.mean = self.sb("mean", [128, 128])
        self.ident = self.sb("ident", [128, 128])
        self.ones = self.sb("ones", [128, 128])
        self.eps = self.sb("eps", [128, 1])

    def sb(self, name, shape, dt=F32, ctx=None):
        self.named[name] = self.named.get(name, 0) + 1
        if self.named[name] > 1:
            name = f"{name}_{self.named[name]}"
        return (ctx or self.ctx).enter_context(self.nc.sbuf_tensor(name, shape, dt))

    def semaphore_for(self, name):
        if name not in self.signals:
            self.signals[name] = Signal(self.ctx, self.nc, name)
        return self.signals[name]

    def v(self, name, k=0):
        return self.vec[:, VEC[name][0] + k:VEC[name][0] + k + 1]


def norm_pe(c, pe, source, run=0, came=None):
    centered, squared, spread = c.semaphore_for("ln_centered"), c.semaphore_for("ln_squared"), c.semaphore_for("ln_spread")

    def center(b):
        if came:
            pe.wait_ge(*came(b + 1))
        pe.matmul(c.PS[:, b, :], c.center[:, :], source[:, b, :], start=True, stop=True)\
            .then_inc(centered.sem, 1)

    center(0)
    for b in range(B):
        if b + 1 < B:
            center(b + 1)
        pe.wait_ge(*squared(run * B + b + 1))
        pe.matmul(c.PS[:, B + b, :], c.mean[:, :], c.sq[:, b, :], start=True, stop=True)\
            .then_inc(spread.sem, 1)


def norm_act(c, act, run=0):
    centered, squared, spread = c.semaphore_for("ln_centered"), c.semaphore_for("ln_squared"), c.semaphore_for("ln_spread")
    logged, scale = c.semaphore_for("ln_logged"), c.semaphore_for("ln_scale")

    def square(b):
        act.wait_ge(*centered(run * B + b + 1))
        act.activation(c.sq[:, b, :], c.PS[:, b, :], ACT.Square).then_inc(squared.sem, 1)

    square(0)
    for b in range(B):
        if b + 1 < B:
            square(b + 1)
        act.wait_ge(*spread(run * B + b + 1))
        act.activation(c.rs[:, b, :], c.PS[:, B + b, :], ACT.Ln, bias=c.eps[:, :]).then_inc(logged.sem, 1)
        act.wait_ge(*logged(run * B + b + 1))
        act.activation(c.rs[:, b, :], c.rs[:, b, :], ACT.Exp, scale=-0.5).then_inc(scale.sem, 1)


def norm_dve(c, dve, dest, run=0, gain=None, shift=None):
    scale, normed, scaled = c.semaphore_for("ln_scale"), c.semaphore_for("ln_normed"), c.semaphore_for("ln_scaled")
    for b in range(B):
        dve.wait_ge(*scale(run * B + b + 1))
        dve.tensor_tensor(dest[:, b, :], c.PS[:, b, :], c.rs[:, b, :], ALU.mult).then_inc(normed.sem, 1)
        if gain is not None:
            dve.wait_ge(*normed(run * B + b + 1))
            dve.tensor_scalar(dest[:, b, :], dest[:, b, :], gain, shift, ALU.mult, ALU.add)\
                .then_inc(scaled.sem, 1)


def norm_close(c, runs=1, scaled=0):
    for name in ("ln_centered", "ln_squared", "ln_spread", "ln_logged", "ln_scale", "ln_normed"):
        c.semaphore_for(name).close(B * runs)
    c.semaphore_for("ln_scaled").close(B * scaled)


def stage_setup(c, ins):
    x_came, vec_came = [c.semaphore_for(f"arrived_{b}") for b in range(B)], c.semaphore_for("vectors_came")
    made = c.semaphore_for("const_made")
    with c.nc.Block() as block:
        @block.sync
        def _(sp):
            for b in range(B):
                sp.dma_start(c.x[:, b, :], ins["x"][:, b, :]).then_inc(x_came[b].sem, 16)
            sp.dma_start(c.vec[:, :], ins["vec"]).then_inc(vec_came.sem, 16)
            sp.dma_start(c.rows[:, :], ins["rows"].partition_broadcast(128)).then_inc(vec_came.sem, 16)

        @block.gpsimd
        def _(pool):
            pool.memset(c.ident[:, :], 0.0).then_inc(made.sem, 1)
            pool.memset(c.ones[:, :], 1.0).then_inc(made.sem, 1)
            pool.memset(c.mean[:, :], 1.0 / D).then_inc(made.sem, 1)
            pool.memset(c.center[:, :], -1.0 / D).then_inc(made.sem, 1)
            pool.memset(c.eps[:, :], EPS).then_inc(made.sem, 1)
            pool.wait_ge(*made(5))
            pool.affine_select(out=c.ident[:, :], in_=c.ident[:, :], compare_op=ALU.not_equal, fill=1.0,
                               base=0, pattern=[[-1, 128]], channel_multiplier=1).then_inc(made.sem, 1)
            pool.affine_select(out=c.center[:, :], in_=c.center[:, :], compare_op=ALU.not_equal,
                               fill=1.0 - 1.0 / D, base=0, pattern=[[-1, 128]], channel_multiplier=1)\
                .then_inc(made.sem, 1)
            pool.wait_ge(*made(7))
    made.close(7)


G = H // 4
STEPS = G * TT
QK_LOADS = PARTS * (PARTS + 1)


def load_split(sp, qs, ks, at, q_parts, k_parts, n, came):
    for i in range(PARTS):
        sp.dma_start(ks[24 * i:24 * i + 24, at, :, :],
                     dram_view(k_parts, n * PARTS * D * T, [(H * T, 24), (1, H * T)])).then_inc(came.sem, 16)
        for j in range(PARTS):
            r = 24 * i + 8 * j
            sp.dma_start(qs[r:r + 8, at, :, :],
                         dram_view(q_parts, (n * PARTS + i) * D * T, [(H * T, 8), (1, H * T)])).then_inc(came.sem, 16)


def send_sums(sp, sums, osum, n, sent):
    for j in range(4):
        sp.dma_start(dram_view(sums, (n * 4 + j) * 9 * G * T, [(G * T, 9), (1, G * T)]),
                     osum[n % 2][32 * j:32 * j + 9, :, :]).then_inc(sent[n % 2].sem, 16)


class Closing:

    def __init__(self, c, ctx, sums, weight, shift, bias):
        self.c, self.sums, self.weight, self.shift, self.bias = c, sums, weight, shift, bias
        self.num = c.sb("o_num", [128, B, T], F32, ctx)
        self.den = c.sb("o_den", [128, B, T], F32, ctx)
        self.fetched = [c.semaphore_for(f"arrived_{n}") for n in range(B)]
        self.shifted, self.inverted, self.divided, self.projected, self.added = (c.semaphore_for(n) for n in (
            "o_shifted", "o_inverted", "o_divided", "o_projected", "x_added"))

    def fetch(self, sp, n):
        for j in range(4):
            at = (n * 4 + j) * 9 * G * T
            sp.dma_start(self.num[32 * j:32 * j + 32, n, :], dram_view(self.sums, at, [(T, 32), (1, T)]))\
                .then_inc(self.fetched[n].sem, 16)
            sp.dma_start(self.den[32 * j:32 * j + 32, n, :],
                         dram_view(self.sums, at + 8 * G * T, [(0, 8), (T, G), (1, T)]))\
                .then_inc(self.fetched[n].sem, 16)

    def invert(self, dve, n, quarter):
        part = self.den[:, n, 128 * quarter:128 * quarter + 128]
        if quarter == 0:
            dve.wait_ge(*self.fetched[n](128))
        if self.shift is not None:
            dve.tensor_scalar(part, part, self.shift, None, ALU.add).then_inc(self.shifted.sem, 1)
            dve.wait_ge(*self.shifted(TT * n + quarter + 1))
        dve.reciprocal(part, part).then_inc(self.inverted.sem, 1)

    def divide(self, e, n):
        e.wait_ge(*self.inverted(TT * (n + 1)))
        e.tensor_tensor(self.num[:, n, :], self.num[:, n, :], self.den[:, n, :], ALU.mult)\
            .then_inc(self.divided.sem, 1)

    def project(self, pe, n):
        pe.wait_ge(*self.divided(n + 1))
        pe.matmul(self.c.PS[:, n, :], self.weight, self.num[:, n, :], start=True, stop=True)\
            .then_inc(self.projected.sem, 1)

    def add(self, dve, n):
        x = self.c.x[:, n, :]
        dve.wait_ge(*self.projected(n + 1))
        dve.scalar_tensor_tensor(out=x, in0=self.c.PS[:, n, :], scalar=0.0 if self.bias is None else self.bias,
                                 in1=x, op0=ALU.add, op1=ALU.add).then_inc(self.added.sem, 1)

    def close(self):
        for s, n in (*((f, 128) for f in self.fetched), (self.shifted, 0 if self.shift is None else TT * B),
                     (self.inverted, TT * B), (self.divided, B), (self.projected, B), (self.added, B)):
            s.close(n)


def linear_core(c, items, qs, ks, stored, q_parts, k_parts, sums, values, weight, shift, bias):
    nc, PS = c.nc, c.PS
    loaded = [c.semaphore_for("qk_loaded_0"), c.semaphore_for("qk_loaded_1")]
    scored, edged, drained = c.semaphore_for("at_scored"), c.semaphore_for("at_edged"), c.semaphore_for("at_drained")
    summed, copied, made = c.semaphore_for("at_summed"), c.semaphore_for("at_sum_copied"), c.semaphore_for("const_made")
    sent = [c.semaphore_for("at_sum_sent_even"), c.semaphore_for("at_sum_sent_odd")]
    BANKS = ((0, 1), (2, 3), (6, 7))
    NP = 3
    UNITS = 2 * STEPS
    ctx = ExitStack()
    with ctx:
        probs = c.sb("probs", [128, NP, 4, T], F32, ctx)
        osum = [c.rs, c.sb("o_sum", [128, G, T], F32, ctx)]
        zero = c.sb("zero512", [128, T], F32, ctx)
        tri = c.sb("tri", [128, 128], F32, ctx)
        closing = Closing(c, ctx, sums, weight, shift, bias)
        block = ctx.enter_context(nc.Block())

        def drains(v):
            whole, rest = v // (2 * TT), v % (2 * TT)
            return whole * (2 * TT - 2) + min(rest, 2 * TT - 2)

        def place(v):
            return BANKS[v % 3][0], (v // 2) % NP, 128 * (v // 2 % TT)

        @block.sync
        def _(sp):
            for n in range(items):
                if n == 1:
                    for s in stored:
                        sp.wait_ge(*s(0))
                if 1 <= n < items - 1:
                    sp.wait_ge(*scored(n * UNITS))
                    load_split(sp, qs, ks, (n + 1) % 2, q_parts, k_parts, n + 1, loaded[(n + 1) % 2])
                sp.wait_ge(*copied(G * (n + 1)))
                send_sums(sp, sums, osum, n, sent)
                sp.wait_ge(*sent[n % 2](64 * (n // 2 + 1)))
                closing.fetch(sp, n)

        @block.gpsimd
        def _(pool):
            pool.memset(zero[:, :], 0.0).then_inc(made.sem, 1)
            pool.memset(tri[:, :], 1.0).then_inc(made.sem, 1)
            pool.wait_ge(*made(2))
            pool.affine_select(out=tri[:, :], in_=tri[:, :], compare_op=ALU.is_ge, fill=0.0,
                               base=0, pattern=[[1, 128]], channel_multiplier=-1).then_inc(made.sem, 1)
            for n in range(items):
                closing.divide(pool, n)

        @block.tensor
        def _(pe):
            pe.wait_ge(*made(2))
            for o in range(2):
                pe.matmul(PS[:, 4 + o, :], zero[:, 0:128], zero[:, :], start=True, stop=True)

            def scores(v):
                bank, _, q0 = place(v)
                n, g = v // UNITS, v // 2 // TT % G
                if v >= 3:
                    pe.wait_ge(*edged(v - 2))
                    pe.wait_ge(*drained(drains(v - 2)))
                for jj in range(2):
                    h = 4 * g + 2 * (v % 2) + jj
                    mm = pe.matmul(PS[:, bank + jj, q0:T], ks[0:SPLIT, n % 2, h, q0:q0 + 128],
                                   qs[0:SPLIT, n % 2, h, q0:T], start=True, stop=True)
                mm.then_inc(scored.sem, 1)

            def sum_up(t):
                _, at, q0 = place(2 * t)
                n, g, kt = t // STEPS, t // TT % G, t % TT
                pe.wait_ge(*edged(2 * t + 2))
                pe.wait_ge(*drained(drains(2 * t + 2)))
                if kt == 0 and n * G + g >= 2:
                    pe.wait_ge(*copied(n * G + g - 1))
                for j in range(4):
                    mm = pe.matmul(PS[32 * j:32 * j + 9, 4 + g % 2, q0:T], values[:, n, kt, 4 * g + j, :],
                                   probs[:, at, j, q0:T], start=(kt == 0), stop=(kt == TT - 1),
                                   skip_group_check=True)
                mm.then_inc(summed.sem, 1)

            for t in range(items * STEPS):
                if t % STEPS == 0:
                    n = t // STEPS
                    pe.wait_ge(*loaded[n % 2](16 * QK_LOADS * (n // 2 + 1)))
                scores(2 * t)
                scores(2 * t + 1)
                if t:
                    sum_up(t - 1)
            sum_up(items * STEPS - 1)
            for n in range(items):
                closing.project(pe, n)

        @block.vector
        def _(dve):
            def copy_sums(group):
                n, g = group // G, group % G
                dve.wait_ge(*summed(TT * (group + 1)))
                if g == 0 and n >= 2:
                    dve.wait_ge(*sent[n % 2](64 * (n // 2)))
                dve.tensor_copy(osum[n % 2][:, g, :], PS[:, 4 + g % 2, :]).then_inc(copied.sem, 1)

            dve.wait_ge(*made(3))
            for v in range(items * UNITS):
                bank, at, q0 = place(v)
                t, h = v // 2, 2 * (v % 2)
                dve.wait_ge(*scored(v + 1))
                if t >= NP:
                    dve.wait_ge(*summed(t - NP + 1))
                dve.tensor_tensor(probs[:, at, h:h + 2, q0:q0 + 128], PS[:, bank:bank + 2, q0:q0 + 128],
                                  tri[:, :].unsqueeze(1).to_broadcast([128, 2, 128]), ALU.mult).then_inc(edged.sem, 1)
                if v % (2 * TT) == 5 and t >= TT:
                    copy_sums(t // TT - 1)
                if t >= STEPS and v % UNITS in (22, 25, 28, 31):
                    closing.invert(dve, t // STEPS - 1, (v % UNITS - 22) // 3)
            copy_sums(items * G - 1)
            for quarter in range(TT):
                closing.invert(dve, items - 1, quarter)
            for n in range(items):
                closing.add(dve, n)

        @block.scalar
        def _(act):
            act.preload_act_table_set("natural_log_exp_and_others")
            for v in range(items * UNITS):
                bank, at, q0 = place(v)
                h = 2 * (v % 2)
                act.wait_ge(*edged(v + 1))
                if q0 + 128 < T:
                    act.activation(probs[:, at, h:h + 2, q0 + 128:T], PS[:, bank:bank + 2, q0 + 128:T], ACT.Copy)\
                        .then_inc(drained.sem, 1)

    for s, n in ((loaded[0], 8 * QK_LOADS * items), (loaded[1], 8 * QK_LOADS * items), (scored, UNITS * items),
                 (edged, UNITS * items), (drained, drains(UNITS * items)), (summed, STEPS * items), (copied, G * items),
                 (sent[0], 32 * items), (sent[1], 32 * items), (made, 3)):
        s.close(n)
    closing.close()


class Projection:

    def __init__(self, c, ctx, items, ins, num_i, scratch, values):
        self.c, self.items, self.ins, self.num_i, self.values = c, items, ins, num_i, values
        self.dests = (scratch["q_parts"], scratch["k_parts"])
        self.came = [c.semaphore_for("weights_came_0"), c.semaphore_for("weights_came_1")]
        self.stored = [c.semaphore_for("s_stored_0"), c.semaphore_for("s_stored_1")]
        self.proj, self.biased, self.hi, self.rest, self.mid, self.last, self.vals = (c.semaphore_for(n) for n in (
            "e_proj", "e_biased", "s_high", "s_rest", "s_middle", "s_last", "at_values"))
        self.w = c.sb("e_ws", [128, 2, 3 * D], F32, ctx)
        self.bs = c.sb("e_bs", [128, 2, 2], F32, ctx)
        self.bv = c.sb("e_bv", [128, 2, D], F32, ctx)
        self.qkf = c.sb("e_qkf", [128, 2, T], F32, ctx)
        self.res = c.sb("e_res", [128, 2, T], F32, ctx)
        self.parts = c.sb("e_parts", [128, 2, PARTS, T], BF16, ctx)

    def products_read(self, e, n):
        e.wait_ge(*self.biased(2 * n))
        e.wait_ge(*self.vals(n))

    def load(self, sp, n):
        if n >= 2:
            self.products_read(sp, n - 1)
        e = sp.value_load(self.num_i[0:1, n:n + 1], min_val=0, max_val=EX - 1)
        src = self.ins["w_ex"][bass.ds(e, 1), :, :].rearrange("a p n -> (a p) n")
        nb = W_EX["bq"][0]
        sp.dma_start(self.w[:, n % 2, :], src[:, 0:3 * D]).then_inc(self.came[n % 2].sem, 16)
        sp.dma_start(self.bs[:, n % 2, :], src[:, nb:nb + 2]).then_inc(self.came[n % 2].sem, 16)
        sp.dma_start(self.bv[:, n % 2, :], self.ins["bv_ex"][bass.ds(e, 1), :].to_broadcast([128, D]))\
            .then_inc(self.came[n % 2].sem, 16)

    def store(self, act, n):
        for k in range(2):
            act.wait_ge(*self.last(2 * n + k + 1))
            act.dma_start(dram_view(self.dests[k], n * PARTS * D * T, [(T, 128), (D * T, PARTS), (1, T)]),
                          self.parts[:, k, :, :]).then_inc(self.stored[k].sem, 16)

    def all_stored(self, sp, n):
        for s in self.stored:
            sp.wait_ge(*s(16 * (n + 1)))

    def products(self, pe, n):
        PS, w = self.c.PS, self.w
        pe.wait_ge(*self.came[n % 2](48 * (n // 2 + 1)))
        if n:
            self.products_read(pe, n)
        yb = self.c.y[:, n // PICK, :]
        for k in range(2):
            pe.matmul(PS[:, k, :], w[:, n % 2, D * k:D * k + D], yb, start=True, stop=True).then_inc(self.proj.sem, 1)
        for kt in range(TT):
            mm = pe.matmul(PS[:, 2, 128 * kt:128 * kt + 128], yb[:, 128 * kt:128 * kt + 128],
                           w[:, n % 2, 2 * D:3 * D], start=True, stop=True)
        mm.then_inc(self.proj.sem, 1)

    def bias(self, dve, n):
        PS = self.c.PS
        for k in range(2):
            dve.wait_ge(*self.proj(3 * n + k + 1))
            if n:
                dve.wait_ge(*self.last(2 * n - 1 + k))
            dve.tensor_scalar(self.qkf[:, k, :], PS[:, k, :], self.bs[:, n % 2, k:k + 1],
                              float(HD) ** -0.5 if k == 0 else 1.0, ALU.add, ALU.mult).then_inc(self.biased.sem, 1)
        dve.wait_ge(*self.proj(3 * n + 3))
        dve.tensor_tensor(self.values[:, n, :, :, 0:8], PS[:, 2, :].rearrange("p (k h d) -> p k h d", k=TT, d=HD),
                          self.bv[:, n % 2, :].rearrange("p (h d) -> p h d", d=HD).unsqueeze(1)
                          .to_broadcast([128, TT, H, HD]), ALU.add).then_inc(self.vals.sem, 1)

    def split_high(self, act, n):
        for k in range(2):
            u = 2 * n + k
            act.wait_ge(*self.biased(u + 1))
            if n:
                act.wait_ge(*self.stored[k](16 * n))
            act.activation(self.parts[:, k, 0, :], self.qkf[:, k, :], ACT.Copy).then_inc(self.hi.sem, 1)
            act.wait_ge(*self.rest(u + 1))
            act.activation(self.parts[:, k, 1, :], self.res[:, k, :], ACT.Copy).then_inc(self.mid.sem, 1)

    def split_low(self, pool, n):
        for k in range(2):
            u = 2 * n + k
            pool.wait_ge(*self.hi(u + 1))
            pool.tensor_tensor(self.res[:, k, :], self.qkf[:, k, :], self.parts[:, k, 0, :], ALU.subtract)\
                .then_inc(self.rest.sem, 1)
            pool.wait_ge(*self.mid(u + 1))
            pool.tensor_tensor(self.parts[:, k, 2, :], self.res[:, k, :], self.parts[:, k, 1, :], ALU.subtract)\
                .then_inc(self.last.sem, 1)

    def close(self):
        n = self.items
        for s, k in ((self.came[0], 24 * n), (self.came[1], 24 * n), (self.proj, 3 * n), (self.biased, 2 * n),
                     (self.hi, 2 * n), (self.rest, 2 * n), (self.mid, 2 * n), (self.last, 2 * n), (self.vals, n),
                     (self.stored[0], 16 * n), (self.stored[1], 16 * n)):
            s.close(k)


def softmax_core(c, items, ins, num_i, scratch, values):
    nc, PS = c.nc, c.PS
    max_rows, sums = scratch["max_rows"], scratch["sums"]
    NQ = 3
    MAXES = H * TT
    READY = STEPS - 4
    loaded = [c.semaphore_for(f"qk_loaded_{k}") for k in range(NQ)]
    scored, drained = c.semaphore_for("at_scored"), c.semaphore_for("at_drained")
    summed, copied, made = c.semaphore_for("at_summed"), c.semaphore_for("at_sum_copied"), c.semaphore_for("const_made")
    sent = [c.semaphore_for("at_sum_sent_even"), c.semaphore_for("at_sum_sent_odd")]
    nscored, maxed, turned = c.semaphore_for("mx_scored"), c.semaphore_for("mx_found"), c.semaphore_for("mx_turned")
    mcast, msent = c.semaphore_for("mx_cast"), c.semaphore_for("mx_sent")
    mloaded = [c.semaphore_for("mx_loaded_even"), c.semaphore_for("mx_loaded_odd")]
    ones_came = c.semaphore_for("at_primed")

    FREE = 5
    BEFORE, AFTER = 3, 2

    def max_bank(u):
        return 8 - FREE + u % FREE if u < MAXES else 6 + u % 2

    def opening(project, maxima, then=None):
        share = -(-MAXES // (items - BEFORE - AFTER + 1))
        for n in range(items):
            if n >= BEFORE:
                for u in range(share * (n - BEFORE), min(MAXES, share * (n - BEFORE + 1))):
                    maxima(u)
            if n == items - AFTER and then:
                then()
            project(n)

    def found_by(t):
        if t < READY:
            return MAXES + -(-MAXES * (t + 1) // READY)
        return min(items * MAXES, 2 * MAXES + (MAXES // STEPS) * (t + 1 - READY))

    ctx = ExitStack()
    with ctx:
        qs = c.sb("q_split", [128, NQ, H, T], BF16, ctx)
        ks = c.sb("k_split", [128, NQ, H, T], BF16, ctx)
        probs = c.w1[:, 0:8 * T].rearrange("p (k j t) -> p k j t", k=2, j=4)
        osum = [c.rs, c.w1[:, 8 * T:12 * T].rearrange("p (g t) -> p g t", g=G)]
        projection = Projection(c, ctx, items, ins, num_i, scratch, values)
        zero, mx = c.sq[:, 0, :], c.sq[:, 1, 0:2 * MAXES].rearrange("p (n i) -> p n i", i=MAXES)
        one_row = c.sb("one_row", [128, H * T // 128], BF16, ctx)
        mrow = c.sb("mx_row", [MAXES, 2, 128], BF16, ctx)
        block = ctx.enter_context(nc.Block())

        @block.sync
        def _(sp):
            def load(n):
                if n >= NQ:
                    sp.wait_ge(*scored((n - NQ + 1) * 2 * STEPS))
                load_split(sp, qs, ks, n % NQ, scratch["q_parts"], scratch["k_parts"], n, loaded[n % NQ])

            def send_max(n):
                sp.wait_ge(*mcast(n + 1))
                sp.dma_start(dram_view(max_rows, n * H * T, [(128, MAXES), (1, 128)]), mrow[:, n % 2, :])\
                    .then_inc(msent.sem, 16)
                sp.wait_ge(*msent(16 * (n + 1)))
                sp.dma_start(qs[MAXROW:MAXROW + 1, n % NQ, :, :],
                             dram_view(max_rows, n * H * T, [(H * T, 1), (1, H * T)]))\
                    .then_inc(mloaded[n % 2].sem, 16)

            projection.load(sp, 0)
            projection.load(sp, 1)
            for n in range(items - 2):
                projection.load(sp, n + 2)
                if n < NQ:
                    projection.all_stored(sp, n)
                    load(n)
            sp.wait_ge(*made(2))
            for k in range(NQ):
                sp.dma_start(ks[MAXROW:MAXROW + 1, k, :, :], one_row[:, :]).then_inc(ones_came.sem, 16)
            send_max(0)
            projection.all_stored(sp, items - 1)
            for n in range(items):
                if n + 1 < items:
                    send_max(n + 1)
                sp.wait_ge(*copied(G * (n + 1)))
                send_sums(sp, sums, osum, n, sent)
                if n + NQ < items:
                    load(n + NQ)
            for k in range(2):
                sp.wait_ge(*sent[k](64 * (items // 2)))

        @block.gpsimd
        def _(pool):
            pool.memset(zero, 0.0).then_inc(made.sem, 1)
            pool.memset(one_row[:, :], 1.0).then_inc(made.sem, 1)
            for n in range(items):
                projection.split_low(pool, n)

        @block.tensor
        def _(pe):
            def max_pass(u):
                n, i = u // MAXES, u % MAXES
                h, qt = i // TT, i % TT
                if i == 0:
                    pe.wait_ge(*loaded[n % NQ](16 * QK_LOADS * (n // NQ + 1)))
                    if n:
                        pe.wait_ge(*mcast(n))
                if u >= FREE:
                    pe.wait_ge(*maxed(u - FREE + 1 if u < MAXES else u - 1))
                pe.matmul(PS[:, max_bank(u), :], qs[0:SPLIT, n % NQ, h, 128 * qt:128 * qt + 128],
                          ks[0:SPLIT, n % NQ, h, :], start=True, stop=True).then_inc(nscored.sem, 1)

            def turn_max(n):
                pe.wait_ge(*maxed((n + 1) * MAXES))
                pe.transpose(PS[0:MAXES, 6, 0:128], mx[:, n % 2, :], c.ident[:, :]).then_inc(turned.sem, 1)

            def scores(t, half):
                n, g, kt = t // STEPS, t // TT % G, t % TT
                if t >= 1:
                    pe.wait_ge(*drained(2 * t - 1 + half))
                for jj in range(2):
                    h = 4 * g + 2 * half + jj
                    mm = pe.matmul(PS[:, 2 * half + jj, :], ks[0:KROWS, n % NQ, h, 128 * kt:128 * kt + 128],
                                   qs[0:KROWS, n % NQ, h, :], start=True, stop=True)
                mm.then_inc(scored.sem, 1)

            def sum_up(t):
                n, g, kt = t // STEPS, t // TT % G, t % TT
                pe.wait_ge(*drained(2 * t + 2))
                if kt == 0 and n * G + g >= 2:
                    pe.wait_ge(*copied(n * G + g - 1))
                for j in range(4):
                    mm = pe.matmul(PS[32 * j:32 * j + 9, 4 + g % 2, :], values[:, n, kt, 4 * g + j, :],
                                   probs[:, t % 2, j, :], start=(kt == 0), stop=(kt == TT - 1),
                                   skip_group_check=True)
                mm.then_inc(summed.sem, 1)

            opening(lambda n: projection.products(pe, n), max_pass, lambda: turn_max(0))
            pe.wait_ge(*made(2))
            for o in range(2):
                pe.matmul(PS[:, 4 + o, :], zero[:, 0:128], zero, start=True, stop=True)
            projection.products_read(pe, items)
            for t in range(items * STEPS):
                n = t // STEPS
                if t % STEPS == 0:
                    if n == 0:
                        pe.wait_ge(*ones_came(16 * NQ))
                    pe.wait_ge(*mloaded[n % 2](16 * (n // 2 + 1)))
                ahead = list(range(found_by(t - 1), found_by(t)))
                turning = found_by(t) != found_by(t - 1) and found_by(t) % MAXES == 0

                def some(k):
                    for u in ahead[k * len(ahead) // 4:(k + 1) * len(ahead) // 4]:
                        max_pass(u)

                scores(t, 0)
                some(0)
                scores(t, 1)
                some(1)
                some(2)
                if t:
                    sum_up(t - 1)
                some(3)
                if turning:
                    turn_max(found_by(t) // MAXES - 1)
            sum_up(items * STEPS - 1)

        @block.scalar
        def _(act):
            act.preload_act_table_set("natural_log_exp_and_others")

            def cast_max(n):
                act.wait_ge(*turned(n + 1))
                if n >= 2:
                    act.wait_ge(*msent(16 * (n - 1)))
                act.activation(mrow[:, n % 2, :], PS[0:MAXES, 6, 0:128], ACT.Copy, scale=-1.0)\
                    .then_inc(mcast.sem, 1)

            for n in range(items):
                if n == items - AFTER:
                    cast_max(0)
                projection.split_high(act, n)
                projection.store(act, n)
            for t in range(items * STEPS):
                for half in range(2):
                    act.wait_ge(*scored(2 * t + half + 1))
                    if t >= 2:
                        act.wait_ge(*summed(t - 1))
                    act.activation(probs[:, t % 2, 2 * half:2 * half + 2, :], PS[:, 2 * half:2 * half + 2, :],
                                   ACT.Exp).then_inc(drained.sem, 1)
                if t % STEPS == READY - 1 and t // STEPS + 1 < items:
                    cast_max(t // STEPS + 1)

        @block.vector
        def _(dve):
            def find_max(u):
                n, i = u // MAXES, u % MAXES
                dve.wait_ge(*nscored(u + 1))
                if i == 0 and n >= 2:
                    dve.wait_ge(*turned(n - 1))
                dve.tensor_reduce(mx[:, n % 2, i:i + 1], PS[:, max_bank(u), :], AX.X, ALU.max).then_inc(maxed.sem, 1)

            def copy_sums(group):
                n, g = group // G, group % G
                dve.wait_ge(*summed(TT * (group + 1)))
                if g == 0 and n >= 2:
                    dve.wait_ge(*sent[n % 2](64 * (n // 2)))
                dve.tensor_copy(osum[n % 2][:, g, :], PS[:, 4 + g % 2, :]).then_inc(copied.sem, 1)

            opening(lambda n: projection.bias(dve, n), find_max)
            for t in range(items * STEPS):
                for u in range(found_by(t - 1), found_by(t)):
                    find_max(u)
                if t % TT == 0 and t:
                    copy_sums(t // TT - 1)
            copy_sums(items * G - 1)

    TM = items * MAXES
    for s, n in ((scored, 2 * STEPS * items), (drained, 2 * STEPS * items), (summed, STEPS * items),
                 (copied, G * items), (sent[0], 32 * items), (sent[1], 32 * items), (made, 2), (nscored, TM),
                 (maxed, TM), (turned, items), (mcast, items), (msent, 16 * items), (ones_came, 16 * NQ),
                 (mloaded[0], 8 * items), (mloaded[1], 8 * items)):
        s.close(n)
    for k in range(NQ):
        loaded[k].close(16 * QK_LOADS * len(range(k, items, NQ)))
    projection.close()


def stage_linear_attention(c, ins, scratch):
    nc, PS = c.nc, c.PS
    w_came = c.semaphore_for("w_came")
    second = c.semaphore_for("a_second_norm")
    gated, gsum, glog, gscale, gate = (c.semaphore_for(n) for n in ("a_gate_raw", "a_gate_mean", "a_gate_log",
                                                            "a_gate_scale", "a_gate"))
    sigm = c.semaphore_for("a_sigmoid")
    proj, qk, low, ex, elu = (c.semaphore_for(n) for n in ("a_proj", "a_qk", "a_low", "a_exp", "a_elu"))
    hi, rest, mid, last, vals = (c.semaphore_for(n) for n in ("s_high", "s_rest", "s_middle", "s_last", "at_values"))
    stored = [c.semaphore_for("s_stored_0"), c.semaphore_for("s_stored_1")]
    outer = ExitStack()
    with outer:
        values = c.sb("a_values", [128, B, TT, H, 9], F32, outer)
        qs = c.sb("q_split", [128, 2, H, T], BF16, outer)
        ks = c.sb("k_split", [128, 2, H, T], BF16, outer)
        parts = c.sb("a_parts", [128, 2, 2, PARTS, T], BF16, outer)
        w0 = c.sb("w_l0", [128, N_W0], F32, outer)

        def w(name, n=D):
            at = W_L0[name][0]
            return w0[:, at:at + n]

        ctx = ExitStack()
        with ctx:
            z = c.sb("a_z", [128, B, T], F32, ctx)
            gs = c.sb("a_gs", [128, B, T], F32, ctx)
            qkf = c.sb("a_qkf", [128, 2, T], F32, ctx)
            neg = c.sb("a_neg", [128, 2, T], F32, ctx)
            res = c.sb("a_res", [128, 2, T], F32, ctx)
            block = ctx.enter_context(nc.Block())

            @block.sync
            def _(sp):
                sp.dma_start(w0[:, :], ins["w_l0"]).then_inc(w_came.sem, 16)
                for u in range(2 * B):
                    sp.wait_ge(*last(u + 1))
                    dest = scratch["q_parts"] if u % 2 == 0 else scratch["k_parts"]
                    sp.dma_start(dram_view(dest, (u // 2) * PARTS * D * T, [(T, 128), (D * T, PARTS), (1, T)]),
                                 parts[:, u // 2 % 2, u % 2, :, :]).then_inc(stored[u // 2 % 2].sem, 16)
                    if u in (3, 5):
                        n = u // 2 - 1
                        sp.wait_ge(*stored[n](32))
                        load_split(sp, qs, ks, n, scratch["q_parts"], scratch["k_parts"], n,
                                   c.semaphore_for(f"qk_loaded_{n}"))

            @block.tensor
            def _(pe):
                norm_pe(c, pe, c.x, came=lambda n: c.semaphore_for(f"arrived_{n - 1}")(16))
                norm_pe(c, pe, c.y, 1, c.semaphore_for("ln_normed"))
                pe.wait_ge(*w_came(16))
                for b in range(B):
                    pe.wait_ge(*second(b + 1))
                    pe.matmul(PS[:, b, :], w("w_gate"), c.y[:, b, :], start=True, stop=True).then_inc(gated.sem, 1)
                for b in range(B):
                    pe.wait_ge(*sigm(b + 1))
                    pe.matmul(PS[:, B + b, :], c.mean[:, :], gs[:, b, :], start=True, stop=True).then_inc(gsum.sem, 1)
                for b in range(B):
                    if b == 0:
                        pe.wait_ge(*sigm(B))
                    else:
                        pe.wait_ge(*qk(2 * b))
                        pe.wait_ge(*vals(b))
                    pe.matmul(PS[:, 0, :], w("a_wq"), z[:, b, :], start=True, stop=True).then_inc(proj.sem, 1)
                    pe.matmul(PS[:, 1, :], w("a_wk"), z[:, b, :], start=True, stop=True).then_inc(proj.sem, 1)
                    for kt in range(TT):
                        mm = pe.matmul(PS[:, 2, 128 * kt:128 * kt + 128], z[:, b, 128 * kt:128 * kt + 128],
                                       w("a_wv"), start=True, stop=True)
                    mm.then_inc(proj.sem, 1)

            @block.scalar
            def _(act):
                act.preload_act_table_set("natural_log_exp_and_others")
                norm_act(c, act)
                norm_act(c, act, 1)
                act.wait_ge(*c.semaphore_for("vectors_came")(32))
                for b in range(B):
                    act.wait_ge(*gated(b + 1))
                    act.activation(gs[:, b, :], PS[:, b, :], ACT.Sigmoid, bias=c.v("b_gate")).then_inc(sigm.sem, 1)
                for b in range(B):
                    act.wait_ge(*gsum(b + 1))
                    act.activation(c.rs[:, b, :], PS[:, B + b, :], ACT.Ln, bias=c.eps[:, :]).then_inc(glog.sem, 1)
                for b in range(B):
                    act.wait_ge(*glog(b + 1))
                    act.activation(c.rs[:, b, :], c.rs[:, b, :], ACT.Exp, scale=-1.0).then_inc(gscale.sem, 1)
                for b in range(B):
                    for k in range(2):
                        act.wait_ge(*low(2 * b + k + 1))
                        act.activation(neg[:, k, :], neg[:, k, :], ACT.Exp).then_inc(ex.sem, 1)
                    for k in range(2):
                        act.wait_ge(*elu(2 * b + k + 1))
                        if b >= 2:
                            act.wait_ge(*stored[b % 2](32 * (b // 2)))
                        act.activation(parts[:, b % 2, k, 0, :], qkf[:, k, :], ACT.Copy).then_inc(hi.sem, 1)
                    for k in range(2):
                        act.wait_ge(*rest(2 * b + k + 1))
                        act.activation(parts[:, b % 2, k, 1, :], res[:, k, :], ACT.Copy).then_inc(mid.sem, 1)

            @block.gpsimd
            def _(pool):
                pool.memset(values[:, :, :, :, 8:9], 1.0).then_inc(c.semaphore_for("at_ones").sem, 1)

            @block.vector
            def _(dve):
                norm_dve(c, dve, c.y)
                scale = c.semaphore_for("ln_scale")
                dve.wait_ge(*c.semaphore_for("vectors_came")(32))
                for b in range(B):
                    dve.wait_ge(*scale(B + b + 1))
                    dve.tensor_tensor(z[:, b, :], PS[:, b, :], c.rs[:, b, :], ALU.mult)\
                        .then_inc(c.semaphore_for("ln_normed").sem, 1)
                    dve.wait_ge(*c.semaphore_for("ln_normed")(B + b + 1))
                    dve.tensor_scalar(z[:, b, :], z[:, b, :], c.v("ln_g"), c.v("ln_b"), ALU.mult, ALU.add)\
                        .then_inc(second.sem, 1)
                for b in range(B):
                    dve.wait_ge(*gscale(b + 1))
                    dve.tensor_tensor(gs[:, b, :], gs[:, b, :], c.rs[:, b, :], ALU.mult).then_inc(gate.sem, 1)
                dve.wait_ge(*gate(B))
                bv = ROW["a_bv"][0]
                for b in range(B):
                    for k in range(2):
                        dve.wait_ge(*proj(3 * b + k + 1))
                        dve.scalar_tensor_tensor(out=qkf[:, k, :], in0=PS[:, k, :], scalar=c.v(("a_bq", "a_bk")[k]),
                                                 in1=gs[:, b, :], op0=ALU.add, op1=ALU.mult).then_inc(qk.sem, 1)
                    for k in range(2):
                        dve.wait_ge(*qk(2 * b + k + 1))
                        dve.tensor_scalar(neg[:, k, :], qkf[:, k, :], 0.0, None, ALU.min).then_inc(low.sem, 1)
                    dve.wait_ge(*proj(3 * b + 3))
                    dve.tensor_tensor(values[:, b, :, :, 0:8],
                                      PS[:, 2, :].rearrange("p (k h d) -> p k h d", k=TT, d=HD),
                                      c.rows[:, bv:bv + D].rearrange("p (h d) -> p h d", d=HD)
                                      .unsqueeze(1).to_broadcast([128, TT, H, HD]), ALU.add).then_inc(vals.sem, 1)
                    for k in range(2):
                        dve.wait_ge(*ex(2 * b + k + 1))
                        dve.scalar_tensor_tensor(out=qkf[:, k, :], in0=qkf[:, k, :], scalar=0.0, in1=neg[:, k, :],
                                                 op0=ALU.max, op1=ALU.add).then_inc(elu.sem, 1)
                    for k in range(2):
                        dve.wait_ge(*hi(2 * b + k + 1))
                        dve.tensor_tensor(res[:, k, :], qkf[:, k, :], parts[:, b % 2, k, 0, :], ALU.subtract)\
                            .then_inc(rest.sem, 1)
                    for k in range(2):
                        dve.wait_ge(*mid(2 * b + k + 1))
                        dve.tensor_tensor(parts[:, b % 2, k, 2, :], res[:, k, :], parts[:, b % 2, k, 1, :], ALU.subtract)\
                            .then_inc(last.sem, 1)
        norm_close(c, 2)
        for b in range(B):
            c.semaphore_for(f"arrived_{b}").close(16)
        for s, n in ((second, B), (gated, B), (gsum, B), (glog, B), (gscale, B), (gate, B), (sigm, B), (proj, 3 * B),
                     (qk, 2 * B), (low, 2 * B), (ex, 2 * B), (elu, 2 * B), (hi, 2 * B), (rest, 2 * B), (mid, 2 * B),
                     (last, 2 * B), (vals, B), (stored[0], 16 * B), (stored[1], 16 * B), (w_came, 16)):
            s.close(n)
        linear_core(c, B, qs, ks, stored, scratch["q_parts"], scratch["k_parts"], scratch["sums"], values,
                    w("w_proj"), 1e-5, c.v("b_proj"))


def stage_cross_attention(c, ins, scratch):
    nc, PS = c.nc, c.PS
    w_came, made = c.semaphore_for("w_came"), c.semaphore_for("const_made")
    proj, kq, spread_k, vals = (c.semaphore_for(n) for n in ("x_proj", "x_biased", "x_k_spread", "at_values"))
    capped = c.semaphore_for("x_cap")
    scored, mined, maxed, subbed, exped = (c.semaphore_for(n) for n in ("at_scored", "x_masked", "x_max", "x_shifted", "x_exp"))
    turned, moved, summed, copied = (c.semaphore_for(n) for n in ("x_turned", "x_moved", "at_summed", "at_sum_copied"))
    sent = [c.semaphore_for("at_sum_sent_even"), c.semaphore_for("at_sum_sent_odd")]
    outer = ExitStack()
    with outer:
        w0 = c.sb("x_w", [128, N_W0], F32, outer)
        q = c.sb("x_q", [128, B, T], F32, outer)
        kx = c.sb("x_kx", [128, B, H, CT], F32, outer)
        vx = c.sb("x_vx", [CT, B, H, 9], F32, outer)
        cap = c.sb("x_cap", [128, B, TT, CT], F32, outer)
        perm = c.sb("x_perm", [128, 128], F32, outer)

        def w(name, n=D):
            at = W_L0[name][0]
            return w0[:, at:at + n]

        ctx = ExitStack()
        with ctx:
            cx = c.sb("x_ctx", [128, B, CT], F32, ctx)
            kb = c.sb("x_kb", [128, B, CT], F32, ctx)
            hm = c.sb("x_head", [128, H], F32, ctx)
            padi = c.sb("x_padi", [128, B, CT], I32, ctx)
            subi = c.sb("x_subi", [128, TT, CT], I32, ctx)
            pad = c.sb("x_pad", [128, B, CT], F32, ctx)
            sub = c.sb("x_sub", [128, TT, CT], F32, ctx)
            NS = 3
            sc = c.sb("x_sc", [128, NS, H, CT], F32, ctx)
            mx = c.sb("x_mx", [128, NS, H], F32, ctx)
            pt = c.sb("x_pt", [CT, 2, 4, 128], F32, ctx)
            osum = c.sb("x_osum", [128, 2, G, T], F32, ctx)
            zero = c.sb("x_zero", [128, T], F32, ctx)
            U = B * TT
            zeroed = c.semaphore_for("at_primed")
            closing = Closing(c, ctx, scratch["sums"], perm[:, :], None, None)
            block = ctx.enter_context(nc.Block())

            def spread_keys(e, b):
                return e.tensor_tensor(kx[:, b, :, :], kb[:, b, :].unsqueeze(1).to_broadcast([128, H, CT]),
                                       hm[:, :].unsqueeze(2).to_broadcast([128, H, CT]), ALU.mult)

            @block.sync
            def _(sp):
                sp.dma_start(w0[:, :], ins["w_l0"]).then_inc(w_came.sem, 16)
                sp.dma_start(cx[:, :, :], ins["ctx"]).then_inc(w_came.sem, 16)
                sp.dma_start(padi[:, :, :], ins["pad_mask"].rearrange("b t -> (b t)").partition_broadcast(128))\
                    .then_inc(w_came.sem, 16)
                sp.dma_start(subi[:, :, :], ins["sub_mask"].rearrange("(k p) t -> p k t", p=128))\
                    .then_inc(w_came.sem, 16)
                sp.dma_start(perm[:, :], ins["perm"]).then_inc(w_came.sem, 16)

                for b in range(B):
                    sp.wait_ge(*copied(TT * (b + 1)))
                    for j in range(4):
                        sp.dma_start(dram_view(scratch["sums"], (b * 4 + j) * 9 * G * T, [(G * T, 9), (1, G * T)]),
                                     osum[32 * j:32 * j + 9, b % 2, :, :]).then_inc(sent[b % 2].sem, 16)
                    sp.wait_ge(*sent[b % 2](64 * (b // 2 + 1)))
                    closing.fetch(sp, b)

            @block.gpsimd
            def _(pool):
                pool.memset(zero[:, :], 0.0).then_inc(zeroed.sem, 1)
                pool.memset(hm[:, :], 1.0).then_inc(made.sem, 1)
                pool.wait_ge(*made(1))
                pool.affine_select(out=hm[:, :], in_=hm[:, :], compare_op=ALU.is_ge, fill=0.0, base=0,
                                   pattern=[[-HD, H]], channel_multiplier=1).then_inc(made.sem, 1)
                pool.wait_ge(*made(2))
                pool.affine_select(out=hm[:, :], in_=hm[:, :], compare_op=ALU.is_ge, fill=0.0, base=HD - 1,
                                   pattern=[[HD, H]], channel_multiplier=-1).then_inc(made.sem, 1)
                pool.memset(vx[:, :, :, 8:9], 1.0).then_inc(made.sem, 1)
                pool.wait_ge(*made(3))
                pool.wait_ge(*kq(1))
                for b in range(B // 2, B):
                    spread_keys(pool, b).then_inc(made.sem, 1)

                for u in range(U):
                    pool.wait_ge(*maxed(u + 1))
                    pool.tensor_tensor(sc[:, u % NS, :, :], sc[:, u % NS, :, :],
                                       mx[:, u % NS, :].unsqueeze(2).to_broadcast([128, H, CT]), ALU.subtract)\
                        .then_inc(subbed.sem, 1)
                    if u % TT == 3 and u > TT:
                        closing.divide(pool, u // TT - 1)
                closing.divide(pool, B - 1)

            @block.tensor
            def _(pe):
                norm_pe(c, pe, c.x)
                pe.wait_ge(*w_came(80))
                normed = c.semaphore_for("ln_normed")
                pe.wait_ge(*normed(B))
                for b in range(B):
                    pe.matmul(PS[:, b, :], w("x_wq"), c.y[:, b, :], start=True, stop=True).then_inc(proj.sem, 1)
                pe.matmul(PS[:, 4, 0:B * CT], w("x_wk"), cx[:, :, :].rearrange("p b t -> p (b t)"),
                          start=True, stop=True).then_inc(proj.sem, 1)
                for b in range(B):
                    mm = pe.matmul(PS[0:CT, 5, D * b:D * b + D], cx[:, b, :], w("x_wv"), start=True, stop=True)
                mm.then_inc(proj.sem, 1)

                pe.wait_ge(*zeroed(1))
                for o in range(2):
                    pe.matmul(PS[:, 6 + o, :], zero[:, 0:128], zero[:, :], start=True, stop=True)

                pe.wait_ge(*kq(1 + B))
                pe.wait_ge(*spread_k(B // 2))
                pe.wait_ge(*vals(1))
                def scores(u):
                    b, qt = u // TT, u % TT
                    if u == TT * (B // 2):
                        pe.wait_ge(*made(4 + B // 2))
                    if u:
                        pe.wait_ge(*mined(u))
                    for g in range(G):
                        mm = pe.matmul(PS[:, g, 0:4 * CT], q[:, b, 128 * qt:128 * qt + 128],
                                       kx[:, b, 4 * g:4 * g + 4, :].rearrange("p h t -> p (h t)"),
                                       start=True, stop=True)
                    mm.then_inc(scored.sem, 1)

                def sum_up(u, g):
                    b = u // TT
                    k = u * G + g
                    pe.wait_ge(*moved(k + 1))
                    if g == 0 and u >= 2:
                        pe.wait_ge(*copied(u - 1))
                    for j in range(4):
                        mm = pe.matmul(PS[32 * j:32 * j + 9, 6 + u % 2, 128 * g:128 * g + 128],
                                       vx[:, b, 4 * g + j, :], pt[:, k % 2, j, :], start=True, stop=True,
                                       skip_group_check=True)
                    mm.then_inc(summed.sem, 1)

                scores(0)
                scores(1)
                for u in range(U):
                    if u + 2 < U:
                        scores(u + 2)
                    pe.wait_ge(*exped(u + 1))
                    for g in range(G):
                        k = u * G + g
                        if k >= 2:
                            pe.wait_ge(*moved(k - 1))
                        for j in range(4):
                            mm = pe.transpose(PS[0:CT, 4 + k % 2, 128 * j:128 * j + 128], sc[:, u % NS, 4 * g + j, :],
                                              c.ident[:, :])
                        mm.then_inc(turned.sem, 1)
                        if g:
                            sum_up(u, g - 1)
                    sum_up(u, G - 1)
                for n in range(B):
                    closing.project(pe, n)

            @block.scalar
            def _(act):
                act.preload_act_table_set("natural_log_exp_and_others")
                norm_act(c, act)

                for u in range(U):
                    act.wait_ge(*subbed(u + 1))
                    act.activation(sc[:, u % NS, :, :], sc[:, u % NS, :, :], ACT.Exp).then_inc(exped.sem, 1)
                    for g in range(G):
                        k = u * G + g
                        act.wait_ge(*turned(k + 1))
                        if k >= 2:
                            act.wait_ge(*summed(k - 1))
                        act.activation(pt[:, k % 2, :, :], PS[0:CT, 4 + k % 2, :].rearrange("p (j q) -> p j q", j=4),
                                       ACT.Copy).then_inc(moved.sem, 1)

            @block.vector
            def _(dve):
                dve.wait_ge(*w_came(80))
                dve.tensor_scalar(pad[:, :, :], padi[:, :, :], 0, None, ALU.not_equal).then_inc(capped.sem, 1)
                dve.tensor_scalar(sub[:, :, :], subi[:, :, :], 0, None, ALU.not_equal).then_inc(capped.sem, 1)
                dve.wait_ge(*capped(2))
                for b in range(B):
                    dve.tensor_tensor(cap[:, b, :, :], sub[:, :, :],
                                      pad[:, b, :].unsqueeze(1).to_broadcast([128, TT, CT]), ALU.mult)\
                        .then_inc(capped.sem, 1)
                dve.wait_ge(*capped(2 + B))
                dve.tensor_scalar(cap[:, :, :, :], cap[:, :, :, :], 3e38, -1e9, ALU.mult, ALU.add)\
                    .then_inc(capped.sem, 1)
                norm_dve(c, dve, c.y)
                dve.wait_ge(*proj(B + 1))
                dve.tensor_scalar(kb[:, :, :], PS[:, 4, 0:B * CT].rearrange("p (b t) -> p b t", b=B), c.v("x_bk"), None,
                                  ALU.add).then_inc(kq.sem, 1)
                dve.wait_ge(*proj(B + 2))
                bv = ROW["x_bv"][0]
                dve.wait_ge(*made(4))
                dve.tensor_tensor(vx[:, :, :, 0:8], PS[0:CT, 5, :].rearrange("p (b h d) -> p b h d", b=B, d=HD),
                                  c.rows[0:CT, bv:bv + D].rearrange("p (h d) -> p h d", d=HD).unsqueeze(1)
                                  .to_broadcast([CT, B, H, HD]), ALU.add).then_inc(vals.sem, 1)
                dve.wait_ge(*kq(1))
                for b in range(B // 2):
                    spread_keys(dve, b).then_inc(spread_k.sem, 1)
                for b in range(B):
                    dve.tensor_scalar(q[:, b, :], PS[:, b, :], c.v("x_bq"), float(HD) ** -0.5, ALU.add, ALU.mult)\
                        .then_inc(kq.sem, 1)
                dve.wait_ge(*kq(1 + B))

                def copy_sums(u):
                    b, qt = u // TT, u % TT
                    dve.wait_ge(*summed(G * (u + 1)))
                    if qt == 0 and b >= 2:
                        dve.wait_ge(*sent[b % 2](64 * (b // 2)))
                    dve.tensor_copy(osum[:, b % 2, :, 128 * qt:128 * qt + 128],
                                    PS[:, 6 + u % 2, :].rearrange("p (g q) -> p g q", g=G)).then_inc(copied.sem, 1)

                for u in range(U):
                    b, qt = u // TT, u % TT
                    dve.wait_ge(*scored(u + 1))
                    if u >= NS:
                        dve.wait_ge(*turned(G * (u - NS + 1)))
                    dve.tensor_tensor(sc[:, u % NS, :, :].rearrange("p (g h) t -> p g h t", g=G),
                                      PS[:, 0:4, 0:4 * CT].rearrange("p g (h t) -> p g h t", h=4),
                                      cap[:, b, qt, :].unsqueeze(1).unsqueeze(1).to_broadcast([128, G, 4, CT]),
                                      ALU.min).then_inc(mined.sem, 1)
                    dve.wait_ge(*mined(u + 1))
                    dve.tensor_reduce(mx[:, u % NS, :], sc[:, u % NS, :, :], AX.X, ALU.max).then_inc(maxed.sem, 1)
                    if u >= 2:
                        copy_sums(u - 2)
                    if b:
                        for quarter in ((), (), (), (0, 1, 2, 3))[qt]:
                            closing.invert(dve, b - 1, quarter)
                copy_sums(U - 2)
                copy_sums(U - 1)
                for quarter in range(TT):
                    closing.invert(dve, B - 1, quarter)
                for n in range(B):
                    closing.add(dve, n)
        norm_close(c)
        for s, n in ((w_came, 80), (proj, B + 2), (kq, B + 1), (spread_k, B // 2), (vals, 1), (capped, 3 + B)):
            s.close(n)
        made.close(4 + B // 2)
        for s, n in ((scored, U), (mined, U), (maxed, U), (subbed, U), (exped, U), (turned, U * G), (moved, U * G),
                     (summed, U * G), (copied, U), (sent[0], 32 * B), (sent[1], 32 * B), (zeroed, 1)):
            s.close(n)
        closing.close()


def stage_experts(c, ins, scratch):
    nc, PS = c.nc, c.PS
    w1_came = c.semaphore_for("w1_came")
    ALL = NSH + NE
    NT = B * TT
    ROUTED = NSH
    w_came, made, normed = c.semaphore_for("w_came"), c.semaphore_for("const_made"), c.semaphore_for("ln_normed")
    routed, step, exped, turned, moved, stored = (c.semaphore_for(n) for n in (
        "m_logits", "m_route_step", "m_exp", "m_turned", "m_turned_copy", "m_weights_stored"))
    slot_came = [c.semaphore_for("weights_came_0"), c.semaphore_for("weights_came_1")]
    up, silu, gated, wide, summed, added = (c.semaphore_for(n) for n in (
        "m_up", "m_silu", "m_gated", "m_weighted", "m_down", "x_added"))
    ctx = ExitStack()
    with ctx:
        rw = c.sb("m_router", [128, NE], F32, ctx)
        lg = c.sb("m_lg", [128, NT, NE], F32, ctx)
        ex = c.sb("m_ex", [128, NT, NE], F32, ctx)
        small = c.sb("m_small", [128, 3, NT], F32, ctx)
        gt = c.sb("m_gt", [128, NT, NE, NE], F32, ctx)
        eq = c.sb("m_eq", [128, NT, NE, NE], F32, ctx)
        low = c.sb("m_low", [128, NE, NE], F32, ctx)
        cwt = c.sb("m_cwt", [128, T], F32, ctx)
        slot = c.sb("m_slot", [128, 2, N_ME], F32, ctx)
        cw = c.sb("m_cw", [128, 2, B, T], F32, ctx)
        yw = c.sb("m_yw", [128, 2, B, T], F32, ctx)
        sl = c.sb("m_sl", [128, 2, T], F32, ctx)
        gb = c.sb("m_gb", [128, 2, T], F32, ctx)
        block = ctx.enter_context(nc.Block())
        STEPS = 2 * B
        LOOPED = NE // 2 - 1
        EXP_AT, TURN_AT = 7, 12

        def w(par, name, m):
            at = ME[name][0] + 128 * m
            return slot[:, par, at:at + 128]

        @block.sync
        def _(sp):
            def load(e, par, routed_one):
                if not (isinstance(e, int) and e < 2):
                    sp.wait_ge(*summed(STEPS * e - STEPS))
                sp.dma_start(slot[:, par, :], ins["moe"][e, :, :] if isinstance(e, int) else
                             ins["moe"][bass.ds(e, 1), :, :].rearrange("a p n -> (a p) n"))\
                    .then_inc(slot_came[par].sem, 16)
                if routed_one:
                    row = e - ROUTED
                    src = scratch["combine"][row:row + 1, :] if isinstance(e, int) else \
                        scratch["combine"][bass.ds(row, 1), :]
                    sp.dma_start(cw[:, par, :, :].rearrange("p b t -> p (b t)"),
                                 src.to_broadcast([128, B * T])).then_inc(slot_came[par].sem, 16)

            a, n = W_L0["router"]
            sp.dma_start(rw[:, :], ins["w_l0"][:, a:a + n]).then_inc(w_came.sem, 16)
            for e in range(NSH):
                load(e, e % 2, False)
            sp.dma_start(c.w1[:, :], ins["w_l1"]).then_inc(w1_came.sem, 16)
            sp.wait_ge(*moved(1))
            for b in range(B):
                sp.dma_start(scratch["combine"][:, T * b:T * b + T], cwt[32 * b:32 * b + NE, :])\
                    .then_inc(stored.sem, 16)
            sp.wait_ge(*stored(16 * B))
            with sp.Fori(0, LOOPED) as i:
                for par in range(2):
                    load(2 * i + (NSH + par), par, True)
            for e in range(ALL - 2, ALL):
                load(e, e % 2, True)
            sp.wait_ge(*w1_came(16))

        def came(e, par):
            return slot_came[par]((e - par) * 16 + 16) if not isinstance(e, int) or e >= NSH else slot_came[par](16)

        @block.gpsimd
        def _(pool):
            pool.memset(low[:, :, :], 1.0).then_inc(made.sem, 1)
            pool.wait_ge(*made(1))
            pool.affine_select(out=low[:, :, :], in_=low[:, :, :], compare_op=ALU.is_ge, fill=0.0, base=-1,
                               pattern=[[1, NE], [-1, NE]], channel_multiplier=0).then_inc(made.sem, 1)

            def weigh(e, par):
                pool.wait_ge(*came(e, par))
                pool.wait_ge(*up(STEPS * e - STEPS))
                for b in range(B):
                    pool.tensor_tensor(yw[:, par, b, :], c.y[:, b, :], cw[:, par, b, :], ALU.mult)\
                        .then_inc(wide.sem, 1)

            with pool.Fori(0, LOOPED) as i:
                for par in range(2):
                    weigh(2 * i + (NSH + par), par)
            for e in range(ALL - 2, ALL):
                weigh(e, e % 2)

        @block.tensor
        def _(pe):
            norm_pe(c, pe, c.x)
            pe.wait_ge(*w_came(16))
            pe.wait_ge(*normed(B))
            for i in range(NT):
                mm = pe.matmul(PS[:, 0, NE * i:NE * i + NE], c.y[:, i // TT, 128 * (i % TT):128 * (i % TT) + 128],
                               rw[:, :], start=True, stop=True)
            mm.then_inc(routed.sem, 1)

            def turn_weights(bank):
                pe.wait_ge(*step(12))
                for i in range(NT):
                    b, k = i // TT, i % TT
                    mm = pe.matmul(PS[32 * b:32 * b + NE, bank, 128 * k:128 * k + 128], ex[:, i, :], c.ident[:, :],
                                   start=True, stop=True, skip_group_check=True)
                mm.then_inc(turned.sem, 1)
                pe.wait_ge(*moved(1))

            def down(e, par, s, first=False, last=False):
                b, m = s // 2, s % 2
                pe.wait_ge(*gated(STEPS * e + (s + 1)))
                pe.matmul(PS[:, 4 + b, :], w(par, "w2", m), gb[:, m, :], start=first and m == 0,
                          stop=last and m == 1, skip_group_check=True).then_inc(summed.sem, 1)

            def expert(e, par, first=False, last=False, shared=False):
                pe.wait_ge(*came(e, par))
                for s in range(STEPS):
                    b, m = s // 2, s % 2
                    begun = not (first and s < 2)
                    if begun:
                        pe.wait_ge(*silu(STEPS * e + (s - 1)))
                    elif s == 0:
                        pe.wait_ge(*step(1))
                    if shared and STEPS * e + s == TURN_AT:
                        turn_weights(m)
                    pe.matmul(PS[:, m, :], w(par, "w1", m), c.y[:, b, :], start=True, stop=True)
                    if begun:
                        pe.wait_ge(*gated(STEPS * e + (s - 1)))
                    if not shared and m == 0:
                        pe.wait_ge(*wide(B * e + (b + 1 - B * NSH)))
                    pe.matmul(PS[:, 2 + m, :], w(par, "w3", m), c.y[:, b, :] if shared else yw[:, par, b, :],
                              start=True, stop=True).then_inc(up.sem, 1)
                    if s:
                        down(e, par, s - 1, first, last)
                    elif not first:
                        down(e - 1, 1 - par, STEPS - 1)

            expert(0, 0, first=True, shared=True)
            expert(1, 1, shared=True)
            with pe.Fori(0, LOOPED) as i:
                for par in range(2):
                    expert(2 * i + (NSH + par), par)
            expert(ALL - 2, 0)
            expert(ALL - 1, 1, last=True)
            down(ALL - 1, 1, STEPS - 1, last=True)

        @block.scalar
        def _(act):
            act.preload_act_table_set("natural_log_exp_and_others")
            norm_act(c, act)

            def expert(e, first=False, shared=False):
                for s in range(STEPS):
                    if shared and STEPS * e + s == EXP_AT:
                        act.wait_ge(*step(8))
                        act.activation(ex[:, :, :], ex[:, :, :], ACT.Exp).then_inc(exped.sem, 1)
                    if shared and STEPS * e + s == TURN_AT:
                        act.wait_ge(*turned(1))
                        act.activation(cwt[:, :], PS[:, s % 2, :], ACT.Copy).then_inc(moved.sem, 1)
                    act.wait_ge(*up(STEPS * e + (s + 1)))
                    if not (first and s < 2):
                        act.wait_ge(*gated(STEPS * e + (s - 1)))
                    act.activation(sl[:, s % 2, :], PS[:, s % 2, :], ACT.Silu).then_inc(silu.sem, 1)

            expert(0, True, True)
            expert(1, False, True)
            with act.Fori(0, LOOPED) as i:
                for par in range(2):
                    expert(2 * i + (NSH + par))
            expert(ALL - 2)
            expert(ALL - 1)

        @block.vector
        def _(dve):
            def route(k):
                other = lg[:, :, :].unsqueeze(2).to_broadcast([128, NT, NE, NE])
                own = lg[:, :, :].unsqueeze(3).to_broadcast([128, NT, NE, NE])
                if k == 0:
                    dve.tensor_tensor(gt[:, :, :, :], other, own, ALU.is_gt).then_inc(step.sem, 1)
                elif k == 1:
                    dve.tensor_tensor(eq[:, :, :, :], other, own, ALU.is_equal).then_inc(step.sem, 1)
                elif k == 2:
                    dve.wait_ge(*made(2))
                    dve.wait_ge(*step(3))
                    dve.tensor_tensor(eq[:, :, :, :], eq[:, :, :, :],
                                      low[:, :, :].unsqueeze(1).to_broadcast([128, NT, NE, NE]), ALU.mult)\
                        .then_inc(step.sem, 1)
                elif k == 3:
                    dve.wait_ge(*step(4))
                    dve.tensor_tensor(gt[:, :, :, :], gt[:, :, :, :], eq[:, :, :, :], ALU.add).then_inc(step.sem, 1)
                elif k == 4:
                    dve.tensor_reduce(small[:, 0, :], lg[:, :, :], AX.X, ALU.max).then_inc(step.sem, 1)
                    dve.wait_ge(*step(6))
                    dve.tensor_reduce(eq[:, :, :, 0], gt[:, :, :, :], AX.X, ALU.add).then_inc(step.sem, 1)
                elif k == 5:
                    dve.tensor_tensor(ex[:, :, :], lg[:, :, :], small[:, 0, :].unsqueeze(2).to_broadcast([128, NT, NE]),
                                      ALU.subtract).then_inc(step.sem, 1)
                elif k == EXP_AT + 1:
                    dve.wait_ge(*step(8))
                    dve.wait_ge(*exped(1))
                    dve.scalar_tensor_tensor(out=ex[:, :, :], in0=eq[:, :, :, 0], scalar=1.5, in1=ex[:, :, :],
                                             op0=ALU.is_lt, op1=ALU.mult).then_inc(step.sem, 1)
                    dve.wait_ge(*step(9))
                    dve.tensor_reduce(small[:, 1, :], ex[:, :, :], AX.X, ALU.add).then_inc(step.sem, 1)
                elif k == EXP_AT + 2:
                    dve.wait_ge(*step(10))
                    dve.reciprocal(small[:, 2, :], small[:, 1, :]).then_inc(step.sem, 1)
                    dve.wait_ge(*step(11))
                    dve.tensor_tensor(ex[:, :, :], ex[:, :, :], small[:, 2, :].unsqueeze(2).to_broadcast([128, NT, NE]),
                                      ALU.mult).then_inc(step.sem, 1)

            norm_dve(c, dve, c.y)
            dve.wait_ge(*routed(1))
            rb = ROW["router_b"][0]
            dve.tensor_tensor(lg[:, :, :], PS[:, 0, 0:NT * NE].rearrange("p (i e) -> p i e", e=NE),
                              c.rows[:, rb:rb + NE].unsqueeze(1).to_broadcast([128, NT, NE]), ALU.add)\
                .then_inc(step.sem, 1)
            dve.wait_ge(*step(1))

            def expert(e, first=False, shared=False):
                for s in range(STEPS):
                    if shared:
                        route(STEPS * e + s)
                    dve.wait_ge(*silu(STEPS * e + (s + 1)))
                    if not (first and s < 2):
                        dve.wait_ge(*summed(STEPS * e + (s - 1)))
                    dve.tensor_tensor(gb[:, s % 2, :], sl[:, s % 2, :], PS[:, 2 + s % 2, :], ALU.mult)\
                        .then_inc(gated.sem, 1)

            expert(0, True, True)
            expert(1, False, True)
            with dve.Fori(0, LOOPED) as i:
                for par in range(2):
                    expert(2 * i + (NSH + par))
            expert(ALL - 2)
            expert(ALL - 1)
            dve.wait_ge(*summed(STEPS * ALL))
            for b in range(B):
                dve.tensor_tensor(c.x[:, b, :], c.x[:, b, :], PS[:, 4 + b, :], ALU.add).then_inc(added.sem, 1)
            dve.wait_ge(*added(B))
    norm_close(c)
    for s, n in ((w_came, 16), (made, 2), (routed, 1), (step, 12), (exped, 1), (turned, 1), (moved, 1),
                 (stored, 16 * B)):
        s.close(n)
    per = (16 + 32 * NE // 2)
    for s, n in ((slot_came[0], per), (slot_came[1], per), (up, STEPS * ALL), (silu, STEPS * ALL),
                 (gated, STEPS * ALL), (wide, B * NE), (summed, STEPS * ALL), (added, B)):
        s.close(n)


def stage_gated_attention(c, ins, scratch):
    nc, PS = c.nc, c.PS
    made, normed = c.semaphore_for("const_made"), c.semaphore_for("ln_normed")
    scaled = c.semaphore_for("ln_scaled")
    outer = ExitStack()
    with outer:
        z = c.sb("g_z", [128, B, T], F32, outer)
        ctx = ExitStack()
        with ctx:
            def buf(name, shape, dt=F32):
                return c.sb("g_" + name, shape, dt, ctx)

            xb = buf("xb", [128, T])
            sqq, sqk, e1, t1, lga = (buf(n, [128, T]) for n in ("sqq", "sqk", "e1", "t1", "lga"))
            rq, rk, te, de, dd, dec, kdt, oe = (buf(n, [128, T]) for n in ("rq", "rk", "te", "de", "dd", "dec", "kdt", "oe"))
            dg = buf("dg", [128, NC])
            cum, eq, qn, kn, kd = (buf(n, [128, 2, T]) for n in ("cum", "eq", "qn", "kn", "kd"))
            LB = 4
            le, lo = (buf(n, [128, LB, T]) for n in ("le", "lo"))
            re, ro = (buf(n, [128, 2, T]) for n in ("re", "ro"))
            reset = buf("reset", [128, T])
            late = buf("late", [128, CH])
            eye = buf("eye", [128, CH])
            pair, swap = buf("pair", [128, 128]), buf("swap", [128, 128])
            nbg = buf("nbg", [128, HP])
            ln256 = buf("ln256", [128, 1])
            first = buf("first", [128, 4])

            (proj, sq, ex, vm, nrm, ln, rr, tt, la, cm, eqs, tes, des, qk, kds, qds) = (c.semaphore_for("g_" + n) for n in (
                "projected", "squared", "exp", "values", "norm", "norm_log", "norm_scale", "one_plus", "log",
                "cumulated", "decay", "to_end", "end_decay", "normalised", "k_decayed", "q_decayed"))
            (lm, sc, kt, dst, dms, decs, ktm, kv, am, st, om, oes, acc, res, xbs) = (c.semaphore_for("g_" + n) for n in (
                "mean_log", "scored", "k_turned", "pair_log", "pair_masked", "pair_decay", "k_moved", "chunk_state",
                "weighted", "state", "out", "out_copied", "out_projected", "residual", "x_copied"))

            def wl(name, hp):
                at = W_L1[name][0] + 128 * hp
                return c.w1[:, at:at + 128]

            for signal, n in ((st, 1), (am, 1), (oes, 1), (res, 2)):
                signal.close(n)
            block = ctx.enter_context(nc.Block())
            CONSTANTS = 17
            hidden, bent, down, added = (c.semaphore_for(n) for n in ("f_hidden", "f_gelu", "f_down", "x_added"))
            M = FFN // 128
            hb = buf("hb", [128, M, T])

            def mlp_down(pe, k):
                b, m = k // M, k % M
                at = W_L1["f_w2"][0] + 128 * m
                pe.wait_ge(*bent(k + 1))
                pe.matmul(PS[:, 4 + b, :], c.w1[:, at:at + 128], hb[:, m, :], start=(m == 0), stop=(m == M - 1),
                          skip_group_check=True).then_inc(down.sem, 1)

            def chunks(t):
                return t.rearrange("p (n t) -> p n t", t=CH)

            @block.tensor
            def _(pe):
                def front(u, hp, then=None):
                    pe.wait_ge(*ln(2 * u))
                    pe.matmul(PS[:, 2, :], wl("g_wg", hp), xb[:, :], start=True, stop=True).then_inc(proj.sem, 1)
                    for n in range(NC):
                        for head in range(2):
                            p = HALF * (1 - head)
                            mm = pe.matmul(PS[p:p + HALF, 3, CH * n:CH * n + CH], xb[:, CH * n:CH * n + CH],
                                           wl("g_wv", hp)[:, GD * head:GD * head + GD], start=True, stop=True,
                                           skip_group_check=True)
                    mm.then_inc(proj.sem, 1)
                    pe.wait_ge(*qk(2 * u))
                    pe.matmul(PS[:, 0, :], wl("g_wq", hp), xb[:, :], start=True, stop=True).then_inc(proj.sem, 1)
                    if then is not None:
                        scores_ready(then)
                    pe.matmul(PS[:, 1, :], wl("g_wk", hp), xb[:, :], start=True, stop=True).then_inc(proj.sem, 1)

                def norms(u, before):
                    pe.wait_ge(*sq(2 * u + 1))
                    pe.wait_ge(*ex(u + 1))
                    pe.matmul(PS[:, 2, :], pair[:, :], sqq[:, :], start=True, stop=True).then_inc(nrm.sem, 1)
                    pe.wait_ge(*sq(2 * u + 2))
                    pe.wait_ge(*vm(2 * u + 2))
                    if before is not None:
                        turned_ready(before)
                    pe.matmul(PS[:, 3, :], pair[:, :], sqk[:, :], start=True, stop=True).then_inc(nrm.sem, 1)

                def mean_log(u, k):
                    pe.wait_ge(*cm(u + 1))
                    pe.wait_ge(*st(14 * u))
                    pe.matmul(PS[:, 4, :], swap[:, :], cum[:, k, :], start=True, stop=True).then_inc(lm.sem, 1)

                def scores_ready(u):
                    pe.wait_ge(*qk(2 * u + 2))
                    if not isinstance(u, int) or u:
                        pe.wait_ge(*am(2 * u))

                def scores(k):
                    for n in range(NC):
                        for head in range(2):
                            p, o = HALF * head, HALF * (1 - head)
                            mm = pe.matmul(PS[o:o + HALF, 5, CH * n:CH * n + CH],
                                           kn[p:p + HALF, k, CH * n:CH * n + CH], qn[p:p + HALF, k, CH * n:CH * n + CH],
                                           start=True, stop=True, skip_group_check=True)
                    mm.then_inc(sc.sem, 1)

                def turn_ready(u):
                    pe.wait_ge(*kds(u + 1))
                    pe.wait_ge(*oes(u))

                def turned_ready(u):
                    pe.wait_ge(*dst(3 * u + 3))
                    pe.wait_ge(*ktm(u + 1))

                def turn_keys(k):
                    for n in range(NC):
                        for head in range(2):
                            p, o = HALF * head, HALF * (1 - head)
                            mm = pe.matmul(PS[o:o + HALF, 6, CH * n:CH * n + CH],
                                           kd[p:p + HALF, k, CH * n:CH * n + CH], eye[p:p + HALF, :],
                                           start=True, stop=True, skip_group_check=True)
                    mm.then_inc(kt.sem, 1)

                def chunk_states(k):
                    for n in range(NC):
                        for head, v in ((0, le), (1, lo)):
                            p, o = HALF * head, HALF * (1 - head)
                            mm = pe.matmul(PS[p:p + HALF, 4, CH * n:CH * n + CH],
                                           kdt[o:o + HALF, CH * n:CH * n + CH], v[o:o + HALF, k, CH * n:CH * n + CH],
                                           start=True, stop=True, skip_group_check=True)
                    mm.then_inc(kv.sem, 1)

                def outputs(u, k, kl):
                    pe.wait_ge(*am(2 * u + 2))
                    pe.wait_ge(*qds(2 * u + 2))
                    pe.wait_ge(*st(14 * u + 14))
                    for n in range(NC):
                        for head, left, right in ((0, le, re), (1, lo, ro)):
                            p = HALF * head
                            mm = pe.matmul(PS[p:p + HALF, 6, CH * n:CH * n + CH], left[:, kl, CH * n:CH * n + CH],
                                           right[:, k, CH * n:CH * n + CH], start=True, stop=True,
                                           skip_group_check=True)
                    mm.then_inc(om.sem, 1)

                def project(u, hp):
                    pe.wait_ge(*oes(u + 1))
                    pe.matmul(PS[:, 7, :], wl("g_wo", hp), oe[:, :], start=(hp == 0), stop=(hp == HP - 1))\
                        .then_inc(acc.sem, 1)

                def batch(b, last):
                    for hp in range(HP):
                        u = b * HP + hp
                        if hp:
                            turn_ready(u)
                            if hp == 1:
                                pe.wait_ge(*res(b))
                            project(u - 1, hp - 1)
                        turn_keys(hp % 2)
                        if not (last and hp == HP - 1):
                            norms(u + 1, u)
                        else:
                            turned_ready(u)
                        chunk_states(hp % LB)
                        if not (last and hp >= HP - 2):
                            if hp == HP - 2:
                                pe.wait_ge(*xbs(b + 2))
                            front(u + 2, (hp + 2) % HP, u + 1)
                        elif hp < HP - 1:
                            scores_ready(u + 1)
                        if not (last and hp == HP - 1):
                            scores((hp + 1) % 2)
                            mean_log(u + 1, (hp + 1) % 2)
                        outputs(u, hp % 2, hp % LB)
                    if not last:
                        turn_ready(b * HP + HP)
                    project(b * HP + (HP - 1), HP - 1)

                norm_pe(c, pe, c.x)
                norm_pe(c, pe, c.y, 1, normed)
                pe.wait_ge(*made(CONSTANTS))
                pe.wait_ge(*scaled(B))
                pe.wait_ge(*xbs(1))
                front(0, 0)
                norms(0, None)
                front(1, 1, 0)
                scores(0)
                pe.wait_ge(*kds(1))
                mean_log(0, 0)
                with pe.Fori(0, B - 1) as b:
                    batch(b, False)
                batch(B - 1, True)

                pe.wait_ge(*res(B))
                norm_pe(c, pe, z, 2)
                for k in range(B * M):
                    b, m = k // M, k % M
                    pe.wait_ge(*scaled(B + b + 1))
                    if k == 0:
                        pe.wait_ge(*scaled(2 * B))
                    if k >= 4:
                        pe.wait_ge(*bent(k - 3))
                    pe.matmul(PS[:, m, :], c.w1[:, W_L1["f_w1"][0] + 128 * m:W_L1["f_w1"][0] + 128 * m + 128],
                              c.y[:, b, :], start=True, stop=True).then_inc(hidden.sem, 1)
                    if k:
                        mlp_down(pe, k - 1)
                mlp_down(pe, B * M - 1)

            @block.scalar
            def _(act):
                act.preload_act_table_set("natural_log_exp_and_others")

                def take_batch(b):
                    act.activation(xb[:, :], z[:, bass.ds(b, 1), :].rearrange("p a t -> p (a t)"), ACT.Copy)\
                        .then_inc(xbs.sem, 1)

                def early(u, hp):
                    kl = hp % LB
                    act.wait_ge(*proj(4 * u + 1))
                    act.activation(e1[:, :], PS[:, 2, :], ACT.Exp, scale=-1.0, bias=nbg[:, hp:hp + 1]).then_inc(ex.sem, 1)
                    act.wait_ge(*proj(4 * u + 2))
                    act.activation(lo[0:HALF, kl, :], PS[0:HALF, 3, :], ACT.Copy).then_inc(vm.sem, 1)
                    act.activation(le[HALF:128, kl, :], PS[HALF:128, 3, :], ACT.Copy).then_inc(vm.sem, 1)
                    act.wait_ge(*proj(4 * u + 3))
                    act.activation(sqq[:, :], PS[:, 0, :], ACT.Square).then_inc(sq.sem, 1)
                    act.wait_ge(*proj(4 * u + 4))
                    act.activation(sqk[:, :], PS[:, 1, :], ACT.Square).then_inc(sq.sem, 1)

                def log_gate(u):
                    act.wait_ge(*tt(u + 1))
                    act.activation(lga[:, :], t1[:, :], ACT.Ln).then_inc(la.sem, 1)

                def turned_keys(u):
                    act.wait_ge(*kt(u + 1))
                    act.activation(kdt[:, :], PS[:, 6, :], ACT.Copy).then_inc(ktm.sem, 1)

                def decay(u):
                    act.wait_ge(*dms(u + 1))
                    act.activation(dec[:, :], dd[:, :], ACT.Exp, scale=-1.0).then_inc(decs.sem, 1)

                def scales(u):
                    for i, r in enumerate((rq, rk)):
                        act.wait_ge(*nrm(2 * u + i + 1))
                        act.activation(r[:, :], PS[:, 2 + i, :], ACT.Ln, scale=65536.0).then_inc(ln.sem, 1)
                    for i, r in enumerate((rq, rk)):
                        act.wait_ge(*ln(2 * u + i + 1))
                        act.activation(r[:, :], r[:, :], ACT.Exp, scale=-0.5, bias=ln256[:, :]).then_inc(rr.sem, 1)

                def outs(u):
                    act.wait_ge(*om(u + 1))
                    act.activation(oe[:, :], PS[:, 6, :], ACT.Copy).then_inc(oes.sem, 1)

                def decays(u, k):
                    act.wait_ge(*cm(u + 1))
                    act.activation(eq[:, k, :], cum[:, k, :], ACT.Exp, scale=-1.0).then_inc(eqs.sem, 1)
                    act.wait_ge(*tes(u + 1))
                    act.activation(de[:, :], te[:, :], ACT.Exp).then_inc(des.sem, 1)

                def batch(b, last):
                    for hp in range(HP):
                        u = b * HP + hp
                        more, ahead = not (last and hp == HP - 1), not (last and hp >= HP - 2)
                        if hp == HP - 2 and not last:
                            act.wait_ge(*proj(b * 4 * HP + 4 * HP))
                            take_batch(b + 1)
                        if more:
                            log_gate(u + 1)
                        turned_keys(u)
                        decay(u)
                        if more:
                            scales(u + 1)
                        if more:
                            decays(u + 1, (hp + 1) % 2)
                        if ahead:
                            early(u + 2, (hp + 2) % HP)
                        outs(u)

                norm_act(c, act)
                norm_act(c, act, 1)
                act.wait_ge(*made(CONSTANTS))
                act.wait_ge(*res(0))
                act.wait_ge(*scaled(1))
                take_batch(0)
                early(0, 0)
                log_gate(0)
                scales(0)
                decays(0, 0)
                early(1, 1)
                with act.Fori(0, B - 1) as b:
                    batch(b, False)
                batch(B - 1, True)

                norm_act(c, act, 2)
                for k in range(B * M):
                    act.wait_ge(*hidden(k + 1))
                    if k >= 4:
                        act.wait_ge(*down(k - 3))
                    act.activation(hb[:, k % M, :], PS[:, k % M, :], ACT.Gelu, bias=c.v("b1", k % M)).then_inc(bent.sem, 1)

            @block.vector
            def _(dve):
                def pair_log(u):
                    dve.wait_ge(*lm(u + 1))
                    dve.tensor_tensor(chunks(dd[:, :]), chunks(PS[:, 4, :]),
                                      eye[:, :].unsqueeze(1).to_broadcast([128, NC, CH]), ALU.mult).then_inc(dst.sem, 1)
                    dve.wait_ge(*dst(3 * u + 1))
                    dve.tensor_reduce(dg[:, :], chunks(dd[:, :]), AX.X, ALU.add).then_inc(dst.sem, 1)
                    dve.wait_ge(*dst(3 * u + 2))
                    dve.tensor_tensor(chunks(dd[:, :]), chunks(PS[:, 4, :]),
                                      dg[:, :].unsqueeze(2).to_broadcast([128, NC, CH]), ALU.subtract)\
                        .then_inc(dst.sem, 1)

                def plus(u):
                    dve.wait_ge(*ex(u + 1))
                    dve.tensor_scalar(t1[:, :], e1[:, :], 1.0, 1e6, ALU.add, ALU.min).then_inc(tt.sem, 1)

                def weigh(u, k):
                    dve.wait_ge(*sc(u + 1))
                    dve.wait_ge(*decs(u + 1))
                    dve.tensor_tensor(ro[0:HALF, k, :], PS[0:HALF, 5, :], dec[0:HALF, :], ALU.mult).then_inc(am.sem, 1)
                    dve.tensor_tensor(re[HALF:128, k, :], PS[HALF:128, 5, :], dec[HALF:128, :], ALU.mult)\
                        .then_inc(am.sem, 1)

                def cumulate(u, k):
                    dve.wait_ge(*la(u + 1))
                    dve.tensor_tensor_scan(cum[:, k, :], reset[:, :], lga[:, :], 0.0, ALU.mult, ALU.add)\
                        .then_inc(cm.sem, 1)

                def chain(u, k, kl):
                    dve.wait_ge(*kv(u + 1))
                    for n in range(NC - 1):
                        if n:
                            dve.wait_ge(*st(14 * u + 2 * n))
                        for p, s in ((0, le), (HALF, lo)):
                            dve.scalar_tensor_tensor(out=s[p:p + HALF, kl, CH * n + CH:CH * n + 2 * CH],
                                                     in0=s[p:p + HALF, kl, CH * n:CH * n + CH],
                                                     scalar=eq[p:p + HALF, k, CH * n + CH - 1:CH * n + CH],
                                                     in1=PS[p:p + HALF, 4, CH * n:CH * n + CH],
                                                     op0=ALU.mult, op1=ALU.add).then_inc(st.sem, 1)

                def normalise(u, k):
                    for i, (r, to) in enumerate(((rq, qn), (rk, kn))):
                        dve.wait_ge(*rr(2 * u + i + 1))
                        dve.scalar_tensor_tensor(out=to[:, k, :], in0=r[:, :], scalar=1e12, in1=PS[:, i, :],
                                                 op0=ALU.min, op1=ALU.mult).then_inc(qk.sem, 1)

                def add_attention(b):
                    dve.wait_ge(*acc(b * HP + HP))
                    zb = z[:, bass.ds(b, 1), :].rearrange("p a t -> p (a t)")
                    dve.tensor_tensor(zb, c.y[:, bass.ds(b, 1), :].rearrange("p a t -> p (a t)"), PS[:, 7, :], ALU.add)\
                        .then_inc(res.sem, 1)

                def pair(u, hp, last=False, before=None):
                    more = not (last and hp == HP - 1)
                    if more:
                        plus(u + 1)
                    pair_log(u)
                    if more:
                        cumulate(u + 1, (hp + 1) % 2)
                    if before is not None:
                        add_attention(before)
                    weigh(u, hp % 2)
                    if more:
                        normalise(u + 1, (hp + 1) % 2)
                    chain(u, hp % 2, hp % LB)

                for k, s in enumerate((st, am, oes, res)):
                    dve.memset(first[:, k:k + 1], 0.0).then_inc(s.sem, 1)
                a, n = VEC["bg"]
                dve.tensor_scalar(nbg[:, :], c.vec[:, a:a + n], -1.0, None, ALU.mult).then_inc(res.sem, 1)
                norm_dve(c, dve, c.y)
                norm_dve(c, dve, z, 1, c.v("ln1_w"), c.v("ln1_b"))
                dve.wait_ge(*made(CONSTANTS))
                plus(0)
                cumulate(0, 0)
                normalise(0, 0)
                pair(0, 0)
                with dve.Fori(0, B - 1) as b:
                    for hp in range(1, HP):
                        pair(b * HP + hp, hp)
                    pair(b * HP + HP, 0, before=b)
                for hp in range(1, HP):
                    pair(HP * (B - 1) + hp, hp, last=True)
                add_attention(B - 1)

                norm_dve(c, dve, c.y, 2, c.v("ln2_w"), c.v("ln2_b"))
                dve.wait_ge(*res(B))
                for b in range(B):
                    dve.tensor_tensor(c.x[:, b, :], c.x[:, b, :], z[:, b, :], ALU.add).then_inc(added.sem, 1)
                for b in range(B):
                    dve.wait_ge(*down(M * (b + 1)))
                    dve.wait_ge(*added(b + 1))
                    dve.scalar_tensor_tensor(out=c.x[:, b, :], in0=PS[:, 4 + b, :], scalar=c.v("b2"), in1=c.x[:, b, :],
                                             op0=ALU.add, op1=ALU.add).then_inc(added.sem, 1)
                dve.wait_ge(*added(2 * B))

            @block.gpsimd
            def _(pool):
                def mask(u):
                    pool.wait_ge(*dst(3 * u + 3))
                    pool.tensor_tensor(chunks(dd[:, :]), chunks(dd[:, :]),
                                       late[:, :].unsqueeze(1).to_broadcast([128, NC, CH]), ALU.add).then_inc(dms.sem, 1)

                def to_end(u, k):
                    pool.wait_ge(*cm(u + 1))
                    pool.tensor_tensor(chunks(te[:, :]), chunks(cum[:, k, :]),
                                       chunks(cum[:, k, :])[:, :, CH - 1:CH].to_broadcast([128, NC, CH]), ALU.subtract)\
                        .then_inc(tes.sem, 1)

                def decayed(u, k):
                    pool.wait_ge(*qk(2 * u + 2))
                    pool.wait_ge(*eqs(u + 1))
                    pool.wait_ge(*tes(u + 1))
                    pool.tensor_tensor(re[0:HALF, k, :], qn[0:HALF, k, :], eq[0:HALF, k, :], ALU.mult)\
                        .then_inc(qds.sem, 1)
                    pool.wait_ge(*qds(2 * u + 1))
                    pool.tensor_tensor(ro[HALF:128, k, :], qn[HALF:128, k, :], eq[HALF:128, k, :], ALU.mult)\
                        .then_inc(qds.sem, 1)
                    pool.wait_ge(*qds(2 * u + 2))
                    pool.wait_ge(*des(u + 1))
                    pool.tensor_tensor(kd[:, k, :], kn[:, k, :], de[:, :], ALU.mult).then_inc(kds.sem, 1)

                def batch(b, last):
                    for hp in range(HP):
                        u = b * HP + hp
                        mask(u)
                        if not (last and hp == HP - 1):
                            to_end(u + 1, (hp + 1) % 2)
                            decayed(u + 1, (hp + 1) % 2)

                pool.memset(reset[:, :], 1.0).then_inc(made.sem, 1)
                pool.memset(pair[:, :], 0.0).then_inc(made.sem, 1)
                pool.memset(swap[:, :], 0.0).then_inc(made.sem, 1)
                pool.memset(late[:, :], 0.0).then_inc(made.sem, 1)
                pool.memset(eye[:, :], 0.0).then_inc(made.sem, 1)
                pool.memset(ln256[:, :], 5.545177444479562).then_inc(made.sem, 1)
                pool.memset(le[:, :, :], 0.0).then_inc(made.sem, 1)
                pool.memset(lo[:, :, :], 0.0).then_inc(made.sem, 1)
                pool.wait_ge(*made(8))
                pool.memset(reset[:, :].rearrange("p (n t) -> p n t", t=CH)[:, :, 0:1], 0.0).then_inc(made.sem, 1)
                pool.wait_ge(*made(9))
                for p in (0, HALF):
                    pool.memset(pair[p:p + HALF, p:p + HALF], 1.0).then_inc(made.sem, 1)
                    pool.memset(swap[p:p + HALF, HALF - p:CH + HALF - p], 1.0 / GD).then_inc(made.sem, 1)
                pool.wait_ge(*made(13))
                for p in (0, HALF):
                    pool.affine_select(out=late[p:p + HALF, :], in_=late[p:p + HALF, :], compare_op=ALU.is_ge,
                                       fill=1e30, base=0, pattern=[[1, CH]], channel_multiplier=-1)\
                        .then_inc(made.sem, 1)
                    pool.affine_select(out=eye[p:p + HALF, :], in_=eye[p:p + HALF, :], compare_op=ALU.not_equal,
                                       fill=1.0, base=0, pattern=[[-1, CH]], channel_multiplier=1)\
                        .then_inc(made.sem, 1)

                to_end(0, 0)
                decayed(0, 0)
                with pool.Fori(0, B - 1) as b:
                    batch(b, False)
                batch(B - 1, True)
        made.close(CONSTANTS)
        U = B * HP
        for s, n in ((proj, 4 * U), (sq, 2 * U), (ex, U), (vm, 2 * U), (nrm, 2 * U), (ln, 2 * U), (rr, 2 * U), (tt, U),
                     (la, U), (cm, U), (eqs, U), (tes, U), (des, U), (qk, 2 * U), (kds, U), (qds, 2 * U), (lm, U),
                     (sc, U), (kt, U), (dst, 3 * U), (dms, U), (decs, U), (ktm, U), (kv, U), (am, 2 * U), (st, 14 * U),
                     (om, U), (oes, U), (acc, U), (res, B), (xbs, B)):
            s.close(n)

        norm_close(c, 3, 2)
        for s, n in ((hidden, B * M), (bent, B * M), (down, B * M), (added, 2 * B)):
            s.close(n)


def stage_context_mix(c, ins, scratch):
    nc, PS = c.nc, c.PS
    NT = B * TT
    came, normed, added = c.semaphore_for("w_came"), c.semaphore_for("ln_normed"), c.semaphore_for("x_added")
    rhs, side, sim, mxs, sub, exped, red = (c.semaphore_for("b_" + n) for n in (
        "weighted_ctx", "side", "similar", "max", "shifted", "exp", "reduced"))
    turned, moved, hats, hat, mixed = (c.semaphore_for("b_" + n) for n in ("turned", "moved", "hat_raw", "hat", "mixed"))
    peak, peaks = c.semaphore_for("b_peak"), c.semaphore_for("b_peak_steps")
    ctx = ExitStack()
    with ctx:
        cx = c.sb("b_ctx", [128, B, CT], F32, ctx)
        ck = c.sb("b_ctx_tok", [CT, B, D], F32, ctx)
        cr = c.sb("b_cr", [128, B, CT], F32, ctx)
        srow = c.sb("b_srow", [1, B, CT], F32, ctx)
        a = c.sb("b_a", [128, NT, CT], F32, ctx)
        mx = c.sb("b_mx", [128, NT], F32, ctx)
        rs = c.sb("b_rs", [128, 4, NT], F32, ctx)
        at = c.sb("b_at", [CT, B, T], F32, ctx)
        hq = c.sb("b_hq", [128, B, T], F32, ctx)
        eh = c.sb("b_eh", [128, B, T], F32, ctx)
        et = c.sb("b_et", [128, NT, D], F32, ctx)
        mt = c.sb("b_mt", [NT, 128], F32, ctx)
        mt1 = c.sb("b_mt1", [NT, 1], F32, ctx)
        m1 = c.sb("b_m1", [1, 2, NT], F32, ctx)
        hc = c.sb("b_hc", [128, B], F32, ctx)
        block = ctx.enter_context(nc.Block())
        SUMW = 4 * CT

        def per_batch(t):
            return t.rearrange("p (b k) -> p b k", b=B)

        @block.sync
        def _(sp):
            sp.dma_start(cx[:, :, :], ins["ctx"]).then_inc(came.sem, 16)
            sp.dma_start(ck[:, :, :], ins["ctx_tok"]).then_inc(came.sem, 16)

        @block.tensor
        def _(pe):
            pe.wait_ge(*came(32))
            pe.matmul(PS[0:1, 7, 0:B * CT], c.v("w2"), cx[:, :, :].rearrange("p b t -> p (b t)"), start=True, stop=True)\
                .then_inc(side.sem, 1)
            pe.wait_ge(*side(2))
            norm_pe(c, pe, c.x)
            pe.wait_ge(*normed(B))
            pe.wait_ge(*rhs(1))
            for b in range(B):
                for k in range(TT):
                    pe.matmul(PS[:, b, CT * k:CT * k + CT], c.y[:, b, 128 * k:128 * k + 128], cr[:, b, :],
                              start=True, stop=False)
                    mm = pe.matmul(PS[:, b, CT * k:CT * k + CT], c.ones[0:1, :], srow[:, b, :], start=False, stop=True)
                mm.then_inc(sim.sem, 1)
            for b in range(B):
                pe.wait_ge(*red(3 + b + 1))
                for k in range(TT):
                    mm = pe.transpose(PS[0:CT, 4 + b, 128 * k:128 * k + 128], a[:, TT * b + k, :], c.ident[:, :])
                mm.then_inc(turned.sem, 1)
            for b in range(B):
                pe.wait_ge(*moved(b + 1))
                pe.matmul(PS[:, b, :], ck[:, b, :], at[:, b, :], start=True, stop=True).then_inc(hats.sem, 1)
            for b in range(B):
                for k in range(TT):
                    mm = pe.transpose(PS[:, 4 + b, 128 * k:128 * k + 128], c.y[:, b, 128 * k:128 * k + 128], c.ident[:, :])
                mm.then_inc(turned.sem, 1)
            pe.wait_ge(*hat(1))
            pe.transpose(PS[0:NT, 0, 0:128], mx[:, :], c.ident[:, :]).then_inc(peak.sem, 1)
            pe.wait_ge(*peaks(1))
            pe.transpose(PS[0:1, 0, 128:128 + NT], mt1[:, :], c.ident[0:NT, 0:NT]).then_inc(peak.sem, 1)
            pe.wait_ge(*peaks(3))
            pe.matmul(PS[:, 0, 160:160 + NT], c.ones[0:1, :], m1[0:1, 1, :], start=True, stop=True).then_inc(peak.sem, 1)
            pe.wait_ge(*peaks(5))
            pe.matmul(PS[:, 0, 192:192 + NT], c.ones[:, :], rs[:, 2, :], start=True, stop=True).then_inc(peak.sem, 1)
            pe.wait_ge(*peaks(8))
            pe.wait_ge(*moved(2 * B))
            for b in range(B):
                for k in range(TT):
                    i = TT * b + k
                    mm = pe.matmul(PS[:, 0, 224 + b:225 + b], et[:, i, :], rs[:, 2, i:i + 1], start=(k == 0),
                                   stop=(k == TT - 1))
            mm.then_inc(peak.sem, 1)
            W = W_L1["w_qv"][0]
            for b in range(B):
                pe.wait_ge(*hat(2 * B + b + 1))
                for part, src in enumerate((c.y, hq, eh, c.sq)):
                    mm = pe.matmul(PS[:, 4 + b, :], c.w1[:, W + D * part:W + D * part + D], src[:, b, :],
                                   start=(part == 0), stop=(part == 3))
                mm.then_inc(mixed.sem, 1)

        @block.scalar
        def _(act):
            act.preload_act_table_set("natural_log_exp_and_others")
            norm_act(c, act)
            act.wait_ge(*sub(1))
            act.activation(a[:, :, :], a[:, :, :], ACT.Exp).then_inc(exped.sem, 1)
            for b in range(B):
                act.wait_ge(*turned(b + 1))
                act.activation(at[:, b, :], PS[0:CT, 4 + b, :], ACT.Copy).then_inc(moved.sem, 1)
            for b in range(B):
                act.wait_ge(*turned(B + b + 1))
                act.activation(et[:, TT * b:TT * b + TT, :], PS[:, 4 + b, :].rearrange("p (k d) -> p k d", k=TT), ACT.Copy)\
                    .then_inc(moved.sem, 1)
            act.wait_ge(*peaks(4))
            act.activation(rs[:, 2, :], rs[:, 2, :], ACT.Exp).then_inc(peaks.sem, 1)

        @block.vector
        def _(dve):
            dve.wait_ge(*came(32))
            dve.wait_ge(*side(1))
            bs = ROW["b_sim"][0]
            dve.tensor_scalar(srow[:, :, :], PS[0:1, 7, 0:B * CT].rearrange("p (b t) -> p b t", b=B),
                              c.rows[0:1, bs:bs + 1], None, ALU.add).then_inc(side.sem, 1)
            dve.tensor_scalar(cr[:, :, :], cx[:, :, :], c.v("w3"), c.v("w1"), ALU.mult, ALU.add).then_inc(rhs.sem, 1)
            norm_dve(c, dve, c.y)
            dve.wait_ge(*sim(B))
            sims = PS[:, 0:B, 0:SUMW].rearrange("p b (k t) -> p b k t", k=TT)
            dve.tensor_reduce(per_batch(mx[:, :]), sims, AX.X, ALU.max).then_inc(mxs.sem, 1)
            dve.wait_ge(*mxs(1))
            dve.tensor_tensor(a[:, :, :].rearrange("p (b k) t -> p b k t", b=B), sims,
                              per_batch(mx[:, :]).unsqueeze(3).to_broadcast([128, B, TT, CT]), ALU.subtract)\
                .then_inc(sub.sem, 1)
            dve.wait_ge(*exped(1))
            dve.tensor_reduce(rs[:, 0, :], a[:, :, :], AX.X, ALU.add).then_inc(red.sem, 1)
            dve.wait_ge(*red(1))
            dve.reciprocal(rs[:, 1, :], rs[:, 0, :]).then_inc(red.sem, 1)
            dve.wait_ge(*red(2))
            dve.tensor_copy(rs[:, 3, :], rs[:, 1, :]).then_inc(red.sem, 1)
            for b in range(B):
                dve.tensor_tensor(a[:, TT * b:TT * b + TT, :], a[:, TT * b:TT * b + TT, :],
                                  rs[:, 1, TT * b:TT * b + TT].unsqueeze(2).to_broadcast([128, TT, CT]), ALU.mult)\
                    .then_inc(red.sem, 1)
            for b in range(B):
                dve.wait_ge(*hats(b + 1))
                dve.tensor_copy(hq[:, b, :], PS[:, b, :]).then_inc(hat.sem, 1)
            dve.wait_ge(*peak(1))
            dve.tensor_reduce(mt1[:, :], PS[0:NT, 0, 0:128], AX.X, ALU.max).then_inc(peaks.sem, 1)
            dve.wait_ge(*peak(2))
            dve.tensor_reduce(m1[0:1, 0, 0:B], per_batch(PS[0:1, 0, 128:128 + NT]), AX.X, ALU.max).then_inc(peaks.sem, 1)
            dve.wait_ge(*peaks(2))
            dve.tensor_copy(per_batch(m1[0:1, 1, :]), m1[0:1, 0, 0:B].unsqueeze(2).to_broadcast([1, B, TT]))\
                .then_inc(peaks.sem, 1)
            dve.wait_ge(*peak(3))
            dve.tensor_tensor(rs[:, 2, :], mx[:, :], PS[:, 0, 160:160 + NT], ALU.subtract).then_inc(peaks.sem, 1)
            dve.wait_ge(*peak(4))
            dve.tensor_reduce(rs[:, 0, 0:B], per_batch(PS[:, 0, 192:192 + NT]), AX.X, ALU.add).then_inc(peaks.sem, 1)
            dve.wait_ge(*peaks(6))
            dve.reciprocal(rs[:, 0, 0:B], rs[:, 0, 0:B]).then_inc(peaks.sem, 1)
            dve.wait_ge(*peaks(7))
            dve.tensor_tensor(per_batch(rs[:, 2, :]), per_batch(rs[:, 2, :]),
                              rs[:, 0, 0:B].unsqueeze(2).to_broadcast([128, B, TT]), ALU.mult).then_inc(peaks.sem, 1)
            for b in range(B):
                dve.wait_ge(*hat(b + 1))
                dve.tensor_tensor(eh[:, b, :], c.y[:, b, :], hq[:, b, :], ALU.mult).then_inc(hat.sem, 1)
            dve.wait_ge(*peak(5))
            dve.tensor_copy(hc[:, :], PS[:, 0, 224:224 + B]).then_inc(peaks.sem, 1)
            dve.wait_ge(*peaks(9))
            for b in range(B):
                dve.tensor_scalar(c.sq[:, b, :], c.y[:, b, :], hc[:, b:b + 1], None, ALU.mult).then_inc(hat.sem, 1)
            for b in range(B):
                dve.wait_ge(*mixed(b + 1))
                dve.scalar_tensor_tensor(out=c.x[:, b, :], in0=PS[:, 4 + b, :], scalar=c.v("b_qv"), in1=c.x[:, b, :],
                                         op0=ALU.add, op1=ALU.add).then_inc(added.sem, 1)
            dve.wait_ge(*added(B))
    norm_close(c)
    for s, n in ((came, 32), (rhs, 1), (side, 2), (sim, B), (mxs, 1), (sub, 1), (exped, 1), (red, 3 + B), (turned, 2 * B),
                 (moved, 2 * B), (hats, B), (hat, 3 * B), (mixed, B), (peak, 5), (peaks, 9), (added, B)):
        s.close(n)


def stage_encoders(c, ins, scratch):
    nc, PS = c.nc, c.PS
    normed, made, added = c.semaphore_for("ln_normed"), c.semaphore_for("const_made"), c.semaphore_for("x_added")
    logit, pick, pexp, wide = (c.semaphore_for("e_" + n) for n in ("logits", "pick", "gate_exp", "gate_wide"))
    outer = ExitStack()
    with outer:
        wp = c.sb("e_wp", [128, PAIRS], F32, outer)
        num_i = c.sb("e_num", [1, PAIRS], I32, outer)
        values = c.sb("e_values", [128, PAIRS, TT, H, 9], F32, outer)
        ctx = ExitStack()
        with ctx:
            mean = c.sb("e_mean", [128, B], F32, ctx)
            lg = c.sb("e_lg", [1, B, EX], F32, ctx)
            gp = c.sb("e_gp", [1, B, EX], F32, ctx)
            cmp = c.sb("e_cmp", [1, B, EX, EX], F32, ctx)
            eq = c.sb("e_eq", [1, B, EX, EX], F32, ctx)
            low = c.sb("e_low", [1, EX, EX], F32, ctx)
            iot = c.sb("e_iota", [1, B, EX], F32, ctx)
            sel = c.sb("e_sel", [1, B, EX], F32, ctx)
            t4 = c.sb("e_t4", [1, B, EX], F32, ctx)
            sm = c.sb("e_sm", [1, 4, B], F32, ctx)
            nf = c.sb("e_nf", [1, B, PICK], F32, ctx)
            wf = c.sb("e_wf", [1, B, PICK], F32, ctx)
            block = ctx.enter_context(nc.Block())

            @block.gpsimd
            def _(pool):
                pool.memset(low[:, :, :], 1.0).then_inc(made.sem, 1)
                for e in range(EX):
                    pool.memset(iot[:, :, e:e + 1], float(e)).then_inc(made.sem, 1)
                pool.memset(values[:, :, :, :, 8:9], 1.0).then_inc(made.sem, 1)
                pool.wait_ge(*made(2 + EX))
                pool.affine_select(out=low[:, :, :], in_=low[:, :, :], compare_op=ALU.is_ge, fill=0.0, base=-1,
                                   pattern=[[1, EX], [-1, EX]], channel_multiplier=0).then_inc(made.sem, 1)
                pool.wait_ge(*made(3 + EX))

            @block.tensor
            def _(pe):
                norm_pe(c, pe, c.x)
                pe.wait_ge(*pick(B))
                gw = W_L1["gate_w"][0]
                for b in range(B):
                    mm = pe.matmul(PS[0:1, 0, EX * b:EX * b + EX], mean[:, b:b + 1], c.w1[:, gw:gw + EX],
                                   start=True, stop=True)
                mm.then_inc(logit.sem, 1)
                pe.wait_ge(*wide(1))
                pe.matmul(PS[:, 1, 0:PAIRS], c.ones[0:1, :], wf[:, :, :].rearrange("p b k -> p (b k)"), start=True,
                          stop=True).then_inc(logit.sem, 1)

            @block.scalar
            def _(act):
                act.preload_act_table_set("natural_log_exp_and_others")
                norm_act(c, act)
                act.wait_ge(*pick(B + 3))
                act.activation(gp[:, :, :], gp[:, :, :], ACT.Exp).then_inc(pexp.sem, 1)

            @block.vector
            def _(dve):
                norm_dve(c, dve, c.y)
                for b in range(B):
                    dve.wait_ge(*normed(b + 1))
                    dve.tensor_reduce(mean[:, b:b + 1], c.y[:, b, :], AX.X, ALU.add).then_inc(pick.sem, 1)
                dve.wait_ge(*logit(1))
                dve.wait_ge(*made(3 + EX))
                gb = ROW["gate_b"][0]
                dve.scalar_tensor_tensor(out=lg[:, :, :], in0=PS[0:1, 0, 0:B * EX].rearrange("p (b e) -> p b e", e=EX),
                                         scalar=1.0 / T, in1=c.rows[0:1, gb:gb + EX].unsqueeze(1).to_broadcast([1, B, EX]),
                                         op0=ALU.mult, op1=ALU.add).then_inc(pick.sem, 1)
                dve.wait_ge(*pick(B + 1))
                dve.tensor_reduce(sm[:, 0, :], lg[:, :, :], AX.X, ALU.max).then_inc(pick.sem, 1)
                dve.wait_ge(*pick(B + 2))
                dve.tensor_tensor(gp[:, :, :], lg[:, :, :], sm[:, 0, :].unsqueeze(2).to_broadcast([1, B, EX]),
                                  ALU.subtract).then_inc(pick.sem, 1)
                other = lg[:, :, :].unsqueeze(2).to_broadcast([1, B, EX, EX])
                own = lg[:, :, :].unsqueeze(3).to_broadcast([1, B, EX, EX])
                dve.tensor_tensor(cmp[:, :, :, :], other, own, ALU.is_gt).then_inc(pick.sem, 1)
                dve.tensor_tensor(eq[:, :, :, :], other, own, ALU.is_equal).then_inc(pick.sem, 1)
                dve.wait_ge(*pick(B + 5))
                dve.tensor_tensor(eq[:, :, :, :], eq[:, :, :, :], low[:, :, :].unsqueeze(1).to_broadcast([1, B, EX, EX]),
                                  ALU.mult).then_inc(pick.sem, 1)
                dve.wait_ge(*pick(B + 6))
                dve.tensor_tensor(cmp[:, :, :, :], cmp[:, :, :, :], eq[:, :, :, :], ALU.add).then_inc(pick.sem, 1)
                dve.wait_ge(*pick(B + 7))
                dve.tensor_reduce(t4[:, :, :], cmp[:, :, :, :], AX.X, ALU.add).then_inc(pick.sem, 1)
                dve.wait_ge(*pick(B + 8))
                dve.tensor_scalar(sel[:, :, :], t4[:, :, :], PICK - 0.5, None, ALU.is_lt).then_inc(pick.sem, 1)
                dve.wait_ge(*pick(B + 9))
                dve.tensor_tensor(t4[:, :, :], sel[:, :, :], iot[:, :, :], ALU.mult).then_inc(pick.sem, 1)
                dve.wait_ge(*pick(B + 10))
                dve.tensor_reduce(nf[:, :, 1], t4[:, :, :], AX.X, ALU.max).then_inc(pick.sem, 1)
                dve.wait_ge(*pick(B + 11))
                dve.tensor_scalar(t4[:, :, :], iot[:, :, :], -1.0, float(EX), ALU.mult, ALU.add).then_inc(pick.sem, 1)
                dve.wait_ge(*pick(B + 12))
                dve.tensor_tensor(t4[:, :, :], t4[:, :, :], sel[:, :, :], ALU.mult).then_inc(pick.sem, 1)
                dve.wait_ge(*pick(B + 13))
                dve.tensor_reduce(nf[:, :, 0], t4[:, :, :], AX.X, ALU.max).then_inc(pick.sem, 1)
                dve.wait_ge(*pick(B + 14))
                dve.tensor_scalar(nf[:, :, 0], nf[:, :, 0], -1.0, float(EX), ALU.mult, ALU.add).then_inc(pick.sem, 1)
                dve.wait_ge(*pick(B + 15))
                dve.tensor_copy(num_i[:, :], nf[:, :, :].rearrange("p b k -> p (b k)")).then_inc(pick.sem, 1)
                dve.wait_ge(*pexp(1))
                dve.tensor_reduce(sm[:, 1, :], gp[:, :, :], AX.X, ALU.add).then_inc(pick.sem, 1)
                dve.wait_ge(*pick(B + 17))
                dve.reciprocal(sm[:, 2, :], sm[:, 1, :]).then_inc(pick.sem, 1)
                dve.wait_ge(*pick(B + 18))
                dve.tensor_tensor(gp[:, :, :], gp[:, :, :], sm[:, 2, :].unsqueeze(2).to_broadcast([1, B, EX]), ALU.mult)\
                    .then_inc(pick.sem, 1)
                dve.wait_ge(*pick(B + 19))
                for k in range(PICK):
                    dve.tensor_tensor(t4[:, :, :], iot[:, :, :], nf[:, :, k:k + 1].to_broadcast([1, B, EX]), ALU.is_equal)\
                        .then_inc(pick.sem, 1)
                    dve.wait_ge(*pick(B + 20 + 3 * k))
                    dve.tensor_tensor(t4[:, :, :], t4[:, :, :], gp[:, :, :], ALU.mult).then_inc(pick.sem, 1)
                    dve.wait_ge(*pick(B + 21 + 3 * k))
                    dve.tensor_reduce(wf[:, :, k], t4[:, :, :], AX.X, ALU.add).then_inc(pick.sem, 1)
                    dve.wait_ge(*pick(B + 22 + 3 * k))
                dve.nop().then_inc(wide.sem, 1)
                dve.wait_ge(*logit(2))
                dve.tensor_copy(wp[:, :], PS[:, 1, 0:PAIRS]).then_inc(wide.sem, 1)
                dve.wait_ge(*wide(2))
        norm_close(c)
        for s, n in ((logit, 2), (pick, B + 25), (pexp, 1), (wide, 2), (made, 3 + EX)):
            s.close(n)

        softmax_core(c, PAIRS, ins, num_i, scratch, values)

        SLOTS = 2 * PICK
        came = [c.semaphore_for(f"arrived_{k}") for k in range(SLOTS)]
        weights_came = [c.semaphore_for(f"weights_came_{k}") for k in range(SLOTS)]
        prod1 = [c.semaphore_for(f"e_first_products{k}") for k in range(PICK)]
        curve1 = [c.semaphore_for(f"e_first_curves{k}") for k in range(PICK)]
        vec1 = [c.semaphore_for(f"e_first_sums{k}") for k in range(PICK)]
        prod2 = [c.semaphore_for(f"e_products{k}") for k in range(PICK)]
        curve2 = [c.semaphore_for(f"e_curves{k}") for k in range(PICK)]
        vec2 = [c.semaphore_for(f"e_sums{k}") for k in range(PICK)]
        ready = [c.semaphore_for(f"e_heads_ready{k}") for k in range(PICK)]
        P1, A1, V1 = 3, 3, 3
        P2, A2, V2 = 10, 7, 4
        NR = N_WX - 3 * D
        M = FFN // 128
        ctx = ExitStack()
        with ctx:
            wl = c.sb("e_wl", [128, SLOTS, NR], F32, ctx)
            num = c.sb("e_o_num", [128, SLOTS, T], F32, ctx)
            den = c.sb("e_o_den", [128, SLOTS, T], F32, ctx)
            t1 = c.sb("e_t1", [128, SLOTS, T], F32, ctx)
            sq = c.sb("e_sq", [128, SLOTS, T], F32, ctx)
            x1 = c.sb("e_x1", [128, SLOTS, T], F32, ctx)
            hb = c.sb("e_hb", [128, PICK, M, T], F32, ctx)
            block = ctx.enter_context(nc.Block())

            def at(name, slot, k=0, n=128):
                a = W_EX[name][0] - 3 * D + k
                return wl[:, slot, a:a + n]

            both = range(PICK)

            def slot(b, k):
                return PICK * (b % 2) + k

            def heads_came(e, b, k):
                e.wait_ge(*came[slot(b, k)](16 * 8 * (b // 2 + 1)))

            @block.sync
            def _(sp):
                def load_weights(b):
                    for k in both:
                        n = PICK * b + k
                        if b >= 2:
                            sp.wait_ge(*vec2[k](V2 * (b - 1)))
                        e = sp.value_load(num_i[0:1, n:n + 1], min_val=0, max_val=EX - 1)
                        src = ins["w_ex"][bass.ds(e, 1), :, :].rearrange("a p n -> (a p) n")
                        sp.dma_start(wl[:, slot(b, k), :], src[:, 3 * D:N_WX])\
                            .then_inc(weights_came[slot(b, k)].sem, 16)

                def load_heads(b):
                    for k in both:
                        if b >= 2:
                            sp.wait_ge(*prod1[k](P1 * (b - 2) + 1))
                        n = PICK * b + k
                        for r in range(4):
                            row = (4 * n + r) * 9 * G
                            sp.dma_start(den[32 * r:32 * r + 32, slot(b, k), :],
                                         scratch["sums"][row + 8 * G:row + 9 * G, :].unsqueeze(0)
                                         .to_broadcast([8, G, T])).then_inc(came[slot(b, k)].sem, 16)
                            sp.dma_start(num[32 * r:32 * r + 32, slot(b, k), :], scratch["sums"][row:row + 32, :])\
                                .then_inc(came[slot(b, k)].sem, 16)

                load_heads(0)
                load_weights(0)
                load_heads(1)
                load_weights(1)
                for b in range(2, B):
                    load_heads(b)
                for b in range(2, B):
                    load_weights(b)

            @block.tensor
            def _(pe):
                def mm(signal, k, bank, left, right, start=True, stop=True):
                    pe.matmul(PS[:, 4 * k + bank, :], left, right, start=start, stop=stop,
                              skip_group_check=True).then_inc(signal[k].sem, 1)

                def heads_projected(b):
                    for k in both:
                        pe.wait_ge(*weights_came[slot(b, k)](16 * (b // 2 + 1)))
                        pe.wait_ge(*ready[k](2 * b + 2))
                        if b:
                            pe.wait_ge(*curve2[k](A2 * (b - 1) + 3))
                        mm(prod1, k, 0, at("wo", slot(b, k)), num[:, slot(b, k), :])

                def first_centred(b):
                    for k in both:
                        pe.wait_ge(*vec1[k](V1 * b + 1))
                        if b:
                            pe.wait_ge(*curve2[k](A2 * (b - 1) + 4))
                        mm(prod1, k, 2, c.center[:, :], t1[:, slot(b, k), :])

                def first_spread(b):
                    for k in both:
                        pe.wait_ge(*curve1[k](A1 * b + 1))
                        mm(prod1, k, 0, c.mean[:, :], sq[:, slot(b, k), :])

                def up(b, k, m):
                    mm(prod2, k, 2 * (m % 2), at("l1", slot(b, k), 128 * m), x1[:, slot(b, k), :])

                def down(b, k, m):
                    pe.wait_ge(*curve2[k](A2 * b + 1 + m))
                    mm(prod2, k, 3, at("l2", slot(b, k), 128 * m), hb[:, k, m, :], m == 0, m == M - 1)

                def mlp(b):
                    for k in both:
                        pe.wait_ge(*vec1[k](V1 * b + 3))
                        pe.wait_ge(*curve1[k](A1 * b + 2))
                        up(b, k, 0)
                        up(b, k, 1)
                    for m in range(2):
                        for k in both:
                            if b and m == 0:
                                pe.wait_ge(*vec2[k](V2 * (b - 1) + 2))
                            down(b, k, m)
                            up(b, k, m + 2)
                    for k in both:
                        down(b, k, 2)
                    if b + 1 < B:
                        heads_projected(b + 1)
                    for k in both:
                        down(b, k, 3)

                def second_centred(b):
                    for k in both:
                        pe.wait_ge(*vec2[k](V2 * b + 1))
                        mm(prod2, k, 3, c.center[:, :], t1[:, slot(b, k), :])

                def second_spread(b):
                    for k in both:
                        pe.wait_ge(*curve2[k](A2 * b + 5))
                        mm(prod2, k, 1, c.mean[:, :], sq[:, slot(b, k), :])

                heads_projected(0)
                first_centred(0)
                first_spread(0)
                for b in range(B):
                    mlp(b)
                    if b + 1 < B:
                        first_centred(b + 1)
                    second_centred(b)
                    if b + 1 < B:
                        first_spread(b + 1)
                    second_spread(b)

            @block.scalar
            def _(act):
                act.preload_act_table_set("natural_log_exp_and_others")

                def square(product, curve, b, bank, at_product):
                    for k in both:
                        act.wait_ge(*product[k](at_product))
                        act.activation(sq[:, slot(b, k), :], PS[:, 4 * k + bank, :], ACT.Square).then_inc(curve[k].sem, 1)

                def log(product, curve, b, bank, at_product):
                    for k in both:
                        act.wait_ge(*product[k](at_product))
                        act.activation(sq[:, slot(b, k), :], PS[:, 4 * k + bank, :], ACT.Ln, bias=c.eps[:, :])\
                            .then_inc(curve[k].sem, 1)

                def root(curve, b, at_curve):
                    for k in both:
                        act.wait_ge(*curve[k](at_curve))
                        act.activation(sq[:, slot(b, k), :], sq[:, slot(b, k), :], ACT.Exp, scale=-0.5)\
                            .then_inc(curve[k].sem, 1)

                square(prod1, curve1, 0, 2, 2)
                log(prod1, curve1, 0, 0, 3)
                root(curve1, 0, 2)
                for b in range(B):
                    for m, tile in enumerate((1, 2, 4, 6)):
                        for k in both:
                            act.wait_ge(*prod2[k](P2 * b + tile))
                            act.activation(hb[:, k, m, :], PS[:, 4 * k + 2 * (m % 2), :], ACT.Relu,
                                           bias=at("l1b", slot(b, k), m, 1)).then_inc(curve2[k].sem, 1)
                    n = b + 1
                    if n < B:
                        square(prod1, curve1, n, 2, P1 * n + 2)
                    square(prod2, curve2, b, 3, P2 * b + 9)
                    if n < B:
                        log(prod1, curve1, n, 0, P1 * n + 3)
                    log(prod2, curve2, b, 1, P2 * b + 10)
                    if n < B:
                        root(curve1, n, A1 * n + 2)
                    root(curve2, b, A2 * b + 6)

            @block.gpsimd
            def _(pool):
                for b in range(B):
                    for k in both:
                        pool.wait_ge(*ready[k](2 * b + 1))
                        pool.tensor_tensor(num[:, slot(b, k), :], num[:, slot(b, k), :], den[:, slot(b, k), :], ALU.mult)\
                            .then_inc(ready[k].sem, 1)

            @block.vector
            def _(dve):
                def invert(b):
                    for k in both:
                        heads_came(dve, b, k)
                        dve.reciprocal(den[:, slot(b, k), :], den[:, slot(b, k), :]).then_inc(ready[k].sem, 1)

                def attended(b):
                    for k in both:
                        dve.wait_ge(*prod1[k](P1 * b + 1))
                        dve.scalar_tensor_tensor(out=t1[:, slot(b, k), :], in0=PS[:, 4 * k, :],
                                                 scalar=at("ob", slot(b, k), 0, 1), in1=c.y[:, b, :],
                                                 op0=ALU.add, op1=ALU.add).then_inc(vec1[k].sem, 1)

                def norm(curve, vec, b, bank, at_curve, at_vec, w, shift):
                    for k in both:
                        x = x1[:, slot(b, k), :]
                        dve.wait_ge(*curve[k](at_curve))
                        dve.tensor_tensor(x, PS[:, 4 * k + bank, :], sq[:, slot(b, k), :], ALU.mult).then_inc(vec[k].sem, 1)
                    for k in both:
                        x = x1[:, slot(b, k), :]
                        dve.wait_ge(*vec[k](at_vec))
                        dve.tensor_scalar(x, x, at(w, slot(b, k), 0, 1), at(shift, slot(b, k), 0, 1), ALU.mult, ALU.add)\
                            .then_inc(vec[k].sem, 1)

                def fed(b):
                    for k in both:
                        dve.wait_ge(*prod2[k](P2 * b + 8))
                        dve.scalar_tensor_tensor(out=t1[:, slot(b, k), :], in0=PS[:, 4 * k + 3, :],
                                                 scalar=at("l2b", slot(b, k), 0, 1), in1=x1[:, slot(b, k), :],
                                                 op0=ALU.add, op1=ALU.add).then_inc(vec2[k].sem, 1)

                def first_norm(b):
                    norm(curve1, vec1, b, 2, A1 * b + 3, V1 * b + 2, "n1w", "n1b")

                invert(0)
                attended(0)
                first_norm(0)
                for b in range(B):
                    n = b + 1
                    if n < B:
                        invert(n)
                        attended(n)
                    for k in both:
                        dve.wait_ge(*vec1[k](V1 * b + 3))
                    fed(b)
                    if n < B:
                        first_norm(n)
                    norm(curve2, vec2, b, 3, A2 * b + 7, V2 * b + 2, "n2w", "n2b")
                    for k in both:
                        dve.wait_ge(*vec2[k](V2 * b + 3))
                        if k:
                            dve.wait_ge(*vec2[k - 1](V2 * b + 4))
                        n_item = PICK * b + k
                        dve.scalar_tensor_tensor(out=c.x[:, b, :], in0=x1[:, slot(b, k), :],
                                                 scalar=wp[:, n_item:n_item + 1], in1=c.x[:, b, :],
                                                 op0=ALU.mult, op1=ALU.add).then_inc(vec2[k].sem, 1)
        for k in range(SLOTS):
            came[k].close(16 * 8 * B // 2)
            weights_came[k].close(16 * B // 2)
        for k in range(PICK):
            for steps, n in ((prod1, P1), (curve1, A1), (vec1, V1), (prod2, P2), (curve2, A2), (vec2, V2)):
                steps[k].close(n * B)
            ready[k].close(2 * B)


def stage_out(c, out):
    written = c.semaphore_for("out_written")
    with c.nc.Block() as block:
        @block.sync
        def _(sp):
            sp.dma_start(out, c.x[:, :, :]).then_inc(written.sem, 16)
            sp.wait_ge(*written(16))


def decoder(nc, ins, out):
    scratch = {
        "q_parts": nc.dram_tensor("q_parts", (PAIRS * PARTS * D, T), BF16).ap(),
        "k_parts": nc.dram_tensor("k_parts", (PAIRS * PARTS * D, T), BF16).ap(),
        "sums": nc.dram_tensor("head_sums", (PAIRS * 4 * 9 * (H // 4), T), F32).ap(),
        "combine": nc.dram_tensor("combine", (NE, B * T), F32).ap(),
        "max_rows": nc.dram_tensor("max_rows", (PAIRS * H, T), BF16).ap(),
    }
    ctx = ExitStack()
    with ctx:
        c = Chip(ctx, nc)
        stage_setup(c, ins)
        stages = [stage_linear_attention, stage_cross_attention, stage_experts,
                  stage_gated_attention, stage_context_mix, stage_encoders]
        for stage in stages:
            stage(c, ins, scratch)
        stage_out(c, out)


_INPUTS = ("x", "vec", "rows", "w_l0", "w_l1", "w_ex", "bv_ex", "moe", "ctx", "ctx_tok", "pad_mask", "sub_mask",
           "perm")


def arrange(i):
    import numpy as np
    a = {k: np.asarray(v) for k, v in i.items()}
    dh = np.arange(D).reshape(H, HD).T.reshape(-1)
    jrg = np.arange(D).reshape(H // 4, 4, HD).transpose(1, 2, 0).reshape(-1)
    col = lambda v: v.reshape(-1, 128).T
    put = np.concatenate
    A, G, E = "L0_attn_", "L1_attn_", "L1_ffn_"
    bqkv, wqkv = a[A + "b_qkv"], a[A + "w_qkv"]
    vec = put([col(a[A + "ln_g"]), col(a[A + "ln_b"]), col(bqkv[:D][dh]), col(bqkv[D:2 * D][dh]),
               col(a[A + "b_gate"][dh]), col(a[A + "b_proj"]), col(a["L0_xattn_bq"]), col(a["L0_xattn_bk"]),
               col(a[G + "bg"]), col(a[G + "ln1_w"]), col(a[G + "ln1_b"]), col(a[G + "ln2_w"]), col(a[G + "ln2_b"]),
               col(a[G + "b1"]), col(a[G + "b2"]), col(a["L1_xattn_w_sim"]), col(a["L1_xattn_b_qv"])], 1)
    rows = put([bqkv[2 * D:], a["L0_xattn_bv"], a["L0_ffn_expert_bias"], a[E + "gate_b"], a["L1_xattn_b_sim"]])
    w_l0 = put([wqkv[:, :D][:, dh], wqkv[:, D:2 * D][:, dh], wqkv[:, 2 * D:], a[A + "w_gate"][:, dh],
                a[A + "w_proj"][jrg], a["L0_xattn_Wq"].T, a["L0_xattn_Wk"].T, a["L0_xattn_Wv"].T,
                a["L0_ffn_router_w"].T], 1)
    tiles = lambda w: w.reshape(-1, 128, w.shape[1]).transpose(1, 0, 2).reshape(128, -1)
    w_l1 = put([a[G + "Wq"], a[G + "Wk"], a[G + "Wv"], a[G + "Wg"], tiles(a[G + "Wo"]), a[G + "W1"],
                tiles(a[G + "W2"]), tiles(a["L1_xattn_W_qv"]), a[E + "gate_w"].T], 1)
    w_ex, bv_ex = [], []
    for e in range(EX):
        iw, ib = a[E + "in_proj_w"][e], a[E + "in_proj_b"][e]
        w_ex.append(put([iw[:D][dh].T, iw[D:2 * D][dh].T, iw[2 * D:].T, a[E + "out_proj_w"][e].T[jrg],
                         a[E + "lin1_w"][e].T, tiles(a[E + "lin2_w"][e].T), col(ib[:D][dh]), col(ib[D:2 * D][dh]),
                         col(a[E + "out_proj_b"][e]), col(a[E + "ln1_w"][e]), col(a[E + "ln1_b"][e]),
                         col(a[E + "lin1_b"][e]), col(a[E + "lin2_b"][e]), col(a[E + "ln2_w"][e]),
                         col(a[E + "ln2_b"][e])], 1))
        bv_ex.append(ib[2 * D:])
    M = "L0_ffn_"
    moe = []
    for w1, w3, w2 in ((a[M + "sw1"], a[M + "sw3"], a[M + "sw2"]), (a[M + "w1"], a[M + "w3"], a[M + "w2"])):
        for e in range(len(w1)):
            moe.append(put([w1[e].T, w3[e].T, tiles(w2[e].T)], 1))
    out = {
        "x": a["x"].transpose(2, 0, 1), "vec": vec, "rows": rows, "w_l0": w_l0, "w_l1": w_l1,
        "w_ex": np.stack(w_ex), "bv_ex": np.stack(bv_ex), "moe": np.stack(moe),
        "ctx": a["ctx_1024"].transpose(2, 0, 1), "ctx_tok": a["ctx_1024"].transpose(1, 0, 2),
        "pad_mask": a["mask_Bx1x1xS2_ik0"].reshape(B, CT), "sub_mask": a["mask_1x1xSxS2_ik0"].reshape(T, CT),
        "perm": np.eye(D, dtype=np.float32)[jrg],
    }
    return {k: np.ascontiguousarray(v) for k, v in out.items()}


def kernel(**inputs):
    import numpy as np
    import concourse.bacc as bacc
    from concourse import mybir as my
    from concourse.bass_utils import run_bass_kernel_spmd as run

    nc = bacc.Bacc("TRN2", target_bir_lowering=False, num_devices=1)
    arrays = arrange(inputs)
    aps = {k: nc.dram_tensor(f"in_{k}", arrays[k].shape, my.dt.from_np(arrays[k].dtype), kind="ExternalInput").ap()
           for k in _INPUTS}
    out = nc.dram_tensor("out_x", (D, B, T), F32, kind="ExternalOutput").ap()
    decoder(nc, aps, out)
    r = run(nc, [{f"in_{k}": arrays[k] for k in _INPUTS}], core_ids=[0])
    return np.ascontiguousarray(r.results[0]["out_x"].transpose(1, 2, 0))
```
